# Optimizing a Trainium2 kernel written in Bass

```python
import numpy as np
import jax
import jax.numpy as jnp

def _softmax(x, axis=-1):
    return jax.nn.softmax(x, axis=axis)

def _gelu(x):
    return jax.nn.gelu(x, approximate=True)

def _silu(x):
    return jax.nn.silu(x)

def _sigmoid(x):
    return jax.nn.sigmoid(x)

def _layernorm(x, axis=-1, eps=1e-05):
    m = jnp.mean(x, axis=axis, keepdims=True)
    v = jnp.var(x, axis=axis, keepdims=True)
    return (x - m) / jnp.sqrt(v + eps)

def _scatter_add(tgt, idx, src, axis=0):
    return tgt.at[idx].add(src)

def _segment_sum(src, seg, n):
    return jax.ops.segment_sum(src, seg, n)
kernel_name = 'mk_early_fusion_embed_d4_tok_img1024_r4_740cde'

def setup_inputs(seed: int=0):
    np.random.seed(seed)
    _w = jnp.asarray

    def _rec_inputs():
        import jax
        import jax.numpy as jnp
        _rk = jax.random.key(seed)
        x = -0.00016672 + 0.999947 * jax.random.normal(jax.random.fold_in(_rk, 1), (4, 3, 96, 96), jnp.float32)
        x_txt = jax.random.randint(jax.random.fold_in(_rk, 51), (4, 512), 0, 31993, jnp.int32)
        return (x, x_txt)
    x, x_txt = _rec_inputs()

    def _L0_tok_setup():
        import jax, jax.numpy as jnp
        import numpy as np
        B, C, H, Wd = (64, 3, 96, 96)
        PH, PW, D = (16, 16, 256)
        PATCH_DIM = C * PH * PW
        N_TOK = H // PH * (Wd // PW)
        key = jax.random.key(seed)
        k1, k2, k3, k4, k5 = jax.random.split(key, 5)
        x = jax.random.normal(k1, (B, C, H, Wd), dtype=jnp.float32)
        W = jax.random.normal(k2, (D, PATCH_DIM), dtype=jnp.float32) * PATCH_DIM ** (-0.5)
        b = jax.random.normal(k3, (D,), dtype=jnp.float32) * 0.02
        cls_token = jax.random.normal(k4, (1, 1, D), dtype=jnp.float32)
        pos_embedding = jax.random.normal(k5, (1, N_TOK + 1, D), dtype=jnp.float32) * 0.02
        return {'x': x, 'W': W, 'b': b, 'cls_token': cls_token, 'pos_embedding': pos_embedding}
    _L0_tok_all = _L0_tok_setup()
    _L0_tok_in = {k: v for k, v in _L0_tok_all.items() if k in ('W', 'b', 'cls_token', 'pos_embedding')}
    del _L0_tok_all

    def _L0_txt_setup():
        import jax, jax.numpy as jnp
        import numpy as np
        VOCAB, D, H = (8000, 256, 16)
        DH = D // H
        DFF = 4 * D
        EPS = 1e-05

        def layer_norm(x, g, b):
            mu = jnp.mean(x, axis=-1, keepdims=True)
            var = jnp.var(x, axis=-1, keepdims=True)
            return (x - mu) * jax.lax.rsqrt(var + EPS) * g + b

        def pos_enc(seq_len, d_model):
            pos = jnp.arange(seq_len, dtype=jnp.float32)[:, None]
            i_even = jnp.arange(0, d_model, 2, dtype=jnp.float32)[None, :]
            angle = pos / jnp.power(10000.0, 2.0 * i_even / d_model)
            pe = jnp.zeros((seq_len, d_model), dtype=jnp.float32)
            pe = pe.at[:, 0::2].set(jnp.sin(angle))
            pe = pe.at[:, 1::2].set(jnp.cos(angle))
            return pe
        key = jax.random.key(seed)
        ks = jax.random.split(key, 16)
        s = 0.02
        return {'tokens': jax.random.randint(ks[0], (4, 512), 0, VOCAB), 'emb': jax.random.normal(ks[1], (VOCAB, D), jnp.float32) * s, 'in_proj_w': jax.random.normal(ks[2], (3 * D, D), jnp.float32) * s, 'in_proj_b': jnp.zeros((3 * D,), jnp.float32), 'out_proj_w': jax.random.normal(ks[3], (D, D), jnp.float32) * s, 'out_proj_b': jnp.zeros((D,), jnp.float32), 'w1': jax.random.normal(ks[4], (DFF, D), jnp.float32) * s, 'b1': jnp.zeros((DFF,), jnp.float32), 'w2': jax.random.normal(ks[5], (D, DFF), jnp.float32) * s, 'b2': jnp.zeros((D,), jnp.float32), 'g1': jnp.ones((D,), jnp.float32), 'beta1': jnp.zeros((D,), jnp.float32), 'g2': jnp.ones((D,), jnp.float32), 'beta2': jnp.zeros((D,), jnp.float32)}
    _L0_txt_all = _L0_txt_setup()
    _L0_txt_in = {k: v for k, v in _L0_txt_all.items() if k in ('emb', 'in_proj_w', 'in_proj_b', 'out_proj_w', 'out_proj_b', 'w1', 'b1', 'w2', 'b2', 'g1', 'beta1', 'g2', 'beta2')}
    del _L0_txt_all

    def _L0_attn_setup():
        import jax, jax.numpy as jnp
        import numpy as np
        import math
        from jax import lax
        B, T, HID, H, J = (4, 512, 256, 8, 2)
        EPS = 1e-06
        LN_EPS = 1e-05

        def _alibi_slopes(n):

            def pow2(m):
                start = 2 ** (-2 ** (-(math.log2(m) - 3)))
                return [start * start ** i for i in range(m)]
            if math.log2(n).is_integer():
                return np.array(pow2(n), dtype=np.float32)
            c = 2 ** int(math.floor(math.log2(n)))
            s = pow2(c) + _alibi_slopes(2 * c).tolist()[:n - c]
            return np.array(s, dtype=np.float32)

        def _deltanet(x, Wq, Wk, Wv, Wbeta, bbeta, Wmix, bmix, Wgate, bgate, Wout, bout, ln_g, ln_b):
            b, t, hid = x.shape
            h = Wgate.shape[0]
            j = Wbeta.shape[0] // h
            d = hid // h
            r = jnp.asarray(np.exp(-_alibi_slopes(h)))[None, :, None]
            q = (jax.nn.elu(x @ Wq.T) + 1.0).reshape(b, t, h, d)
            k = (jax.nn.elu(x @ Wk.T) + 1.0).reshape(b, t, h, d)
            v = (x @ Wv.T).reshape(b, t, h, d)
            beta = (x @ Wbeta.T + bbeta).reshape(b, t, h, j)
            mix = (x @ Wmix.T + bmix).reshape(b, t, h, j)
            gate = jax.nn.sigmoid(x @ Wgate.T + bgate)

            def step(carry, inp):
                S, z = carry
                q_t, k_t, v_t, beta_t, mix_t, g_t = inp
                beta_eff = jnp.minimum(jax.nn.sigmoid(beta_t) * r, 0.9999)
                outer = jnp.einsum('bhd,bhe->bhde', k_t, v_t).astype(jnp.float32)[:, :, None]
                S = S * beta_eff[..., None, None] + g_t[:, :, None, None, None] * outer
                z = z * beta_eff[..., None] + g_t[:, :, None, None] * k_t[:, :, None, :]
                num = jnp.einsum('bhd,bhjde->bhje', q_t, S)
                denom = jnp.einsum('bhd,bhjd->bhj', q_t, z) + EPS
                w = jax.nn.softmax(mix_t, axis=-1)[..., None]
                y_t = jnp.sum(num / denom[..., None] * w, axis=2)
                return ((S, z), y_t)
            S0 = jnp.zeros((b, h, j, d, d), jnp.float32)
            z0 = jnp.zeros((b, h, j, d), jnp.float32)
            tm = lambda a: jnp.swapaxes(a, 0, 1)
            _, yT = lax.scan(step, (S0, z0), (tm(q), tm(k), tm(v), tm(beta), tm(mix), tm(gate)))
            y = jnp.swapaxes(yT, 0, 1).reshape(b, t, hid).astype(x.dtype)
            out = y @ Wout.T + bout
            hres = x + out
            mu = jnp.mean(hres, axis=-1, keepdims=True)
            var = jnp.mean(jnp.square(hres - mu), axis=-1, keepdims=True)
            return (hres - mu) / jnp.sqrt(var + LN_EPS) * ln_g + ln_b
        key = jax.random.key(seed)
        ks = jax.random.split(key, 9)
        sc = 0.02
        return {'x': jax.random.normal(ks[0], (B, T, HID), jnp.float32), 'Wq': jax.random.normal(ks[1], (HID, HID), jnp.float32) * sc, 'Wk': jax.random.normal(ks[2], (HID, HID), jnp.float32) * sc, 'Wv': jax.random.normal(ks[3], (HID, HID), jnp.float32) * sc, 'Wbeta': jax.random.normal(ks[4], (H * J, HID), jnp.float32) * sc, 'bbeta': jnp.full((H * J,), 2.1972, jnp.float32), 'Wmix': jax.random.normal(ks[5], (H * J, HID), jnp.float32) * sc, 'bmix': jnp.zeros((H * J,), jnp.float32), 'Wgate': jax.random.normal(ks[6], (H, HID), jnp.float32) * sc, 'bgate': jnp.zeros((H,), jnp.float32), 'Wout': jax.random.normal(ks[7], (HID, HID), jnp.float32) * sc, 'bout': jnp.zeros((HID,), jnp.float32), 'ln_g': jnp.ones((HID,), jnp.float32), 'ln_b': jnp.zeros((HID,), jnp.float32)}
    _L0_attn_all = _L0_attn_setup()
    _L0_attn_in = {k: v for k, v in _L0_attn_all.items() if k in ('Wq', 'Wk', 'Wv', 'Wbeta', 'bbeta', 'Wmix', 'bmix', 'Wgate', 'bgate', 'Wout', 'bout', 'ln_g', 'ln_b')}
    del _L0_attn_all

    def _L0_ffn_setup():
        import jax, jax.numpy as jnp
        import numpy as np
        EPS = 1e-05

        def _ln(x, g, b):
            mu = jnp.mean(x, axis=-1, keepdims=True)
            var = jnp.mean(jnp.square(x - mu), axis=-1, keepdims=True)
            return (x - mu) * jax.lax.rsqrt(var + EPS) * g + b

        def _forward(x, index_b, index_t, sw1, sb1, sw2, sb2, sw3, sb3, s_ln_g, s_ln_b, sg_w, sg_b, eg_w, eg_b, exp_bias, ew1, eb1, ew2, eb2, ew3, eb3, sel_ln_g, sel_ln_b):
            x1 = jnp.einsum('btd,hd->bth', x, sw1) + sb1
            x2 = jnp.einsum('btd,hd->bth', x, sw2) + sb2
            sh = _ln(jax.nn.silu(x1) * x2, s_ln_g, s_ln_b)
            shared_out = jnp.einsum('bth,dh->btd', sh, sw3) + sb3
            x_moe = x[index_b, index_t]
            shared_scores = jax.nn.sigmoid(x_moe @ sg_w.T + sg_b)
            expert_scores = jax.nn.sigmoid(x_moe @ eg_w.T + eg_b)
            top1_idx = jnp.argmax(expert_scores + exp_bias, axis=-1)
            top1_score = jnp.take_along_axis(expert_scores, top1_idx[:, None], axis=-1)
            weights = jax.nn.softmax(jnp.concatenate([shared_scores, top1_score], axis=-1), axis=-1)
            shared_w, expert_w = (weights[:, 0], weights[:, 1])
            shared_moe_out = shared_out[index_b, index_t] * shared_w[:, None]
            h1 = jnp.einsum('md,ehd->meh', x_moe, ew1) + eb1
            h2 = jnp.einsum('md,ehd->meh', x_moe, ew2) + eb2
            z = _ln(jax.nn.silu(h1) * h2, sel_ln_g, sel_ln_b)
            out_all = jnp.einsum('meh,edh->med', z, ew3) + eb3
            expert_out = jnp.take_along_axis(out_all, top1_idx[:, None, None], axis=1)[:, 0]
            expert_moe_out = expert_out * expert_w[:, None]
            final_out = shared_out.at[index_b, index_t].set(shared_moe_out + expert_moe_out)
            return final_out
        B, T, D, E, H, M = (2, 512, 256, 8, 128, 512)
        key = jax.random.key(seed)
        ks = jax.random.split(key, 24)
        s = 0.02
        inp = {}
        inp['x'] = jax.random.normal(ks[0], (B, T, D), jnp.float32)
        flat = jnp.arange(M, dtype=jnp.int32) * 2
        inp['index_b'] = flat // T
        inp['index_t'] = flat % T
        inp['sw1'] = jax.random.normal(ks[1], (H, D), jnp.float32) * s
        inp['sb1'] = jnp.zeros((H,), jnp.float32)
        inp['sw2'] = jax.random.normal(ks[2], (H, D), jnp.float32) * s
        inp['sb2'] = jnp.zeros((H,), jnp.float32)
        inp['sw3'] = jax.random.normal(ks[3], (D, H), jnp.float32) * s
        inp['sb3'] = jnp.zeros((D,), jnp.float32)
        inp['s_ln_g'] = jnp.ones((H,), jnp.float32)
        inp['s_ln_b'] = jnp.zeros((H,), jnp.float32)
        inp['sg_w'] = jax.random.normal(ks[4], (1, D), jnp.float32) * s
        inp['sg_b'] = jnp.zeros((1,), jnp.float32)
        inp['eg_w'] = jax.random.normal(ks[5], (E, D), jnp.float32) * s
        inp['eg_b'] = jnp.zeros((E,), jnp.float32)
        inp['exp_bias'] = jnp.zeros((E,), jnp.float32)
        inp['ew1'] = jax.random.normal(ks[6], (E, H, D), jnp.float32) * s
        inp['eb1'] = jnp.zeros((E, H), jnp.float32)
        inp['ew2'] = jax.random.normal(ks[7], (E, H, D), jnp.float32) * s
        inp['eb2'] = jnp.zeros((E, H), jnp.float32)
        inp['ew3'] = jax.random.normal(ks[8], (E, D, H), jnp.float32) * s
        inp['eb3'] = jnp.zeros((E, D), jnp.float32)
        inp['sel_ln_g'] = jnp.ones((H,), jnp.float32)
        inp['sel_ln_b'] = jnp.zeros((H,), jnp.float32)
        return inp
    _L0_ffn_all = _L0_ffn_setup()
    _L0_ffn_in = {k: v for k, v in _L0_ffn_all.items() if k in ('index_b', 'index_t', 'sw1', 'sb1', 'sw2', 'sb2', 'sw3', 'sb3', 's_ln_g', 's_ln_b', 'sg_w', 'sg_b', 'eg_w', 'eg_b', 'exp_bias', 'ew1', 'eb1', 'ew2', 'eb2', 'ew3', 'eb3', 'sel_ln_g', 'sel_ln_b')}
    del _L0_ffn_all

    def _L1_attn_setup():
        import jax, jax.numpy as jnp
        import numpy as np
        from jax import lax
        D_MODEL = 256
        INNER = 512
        K = 3
        B, S = (4, 512)

        def _layernorm(x, gamma, beta, eps=1e-05):
            mu = jnp.mean(x, axis=-1, keepdims=True)
            var = jnp.mean(jnp.square(x - mu), axis=-1, keepdims=True)
            return (x - mu) * lax.rsqrt(var + eps) * gamma + beta

        def _forward(x, W_in, b_in, conv_w, conv_b, Wa, ba, Wb, bb, Wc, bc, Wo, bo, gamma, beta):
            residual = x
            xn = _layernorm(x, gamma, beta)
            proj = xn @ W_in + b_in
            projected, gate = jnp.split(proj, 2, axis=-1)
            conv_in = jnp.swapaxes(projected, 1, 2)
            conv_out = lax.conv_general_dilated(conv_in, conv_w, window_strides=(1,), padding=[(K - 1, 0)], feature_group_count=INNER, dimension_numbers=('NCH', 'OIH', 'NCH'))
            conv_out = jnp.swapaxes(conv_out + conv_b[None, :, None], 1, 2)
            u = jax.nn.silu(conv_out) * jax.nn.sigmoid(gate)
            a = jax.nn.sigmoid(u @ Wa + ba)
            b = jax.nn.sigmoid(u @ Wb + bb)
            c = jnp.tanh(u @ Wc + bc)

            def step(state, abu):
                a_t, b_t, c_t, u_t = abu
                state = a_t * state + b_t * u_t
                return (state, c_t * state + u_t)
            seq = tuple((jnp.swapaxes(t, 0, 1) for t in (a, b, c, u)))
            _, y = lax.scan(step, jnp.zeros((x.shape[0], INNER), x.dtype), seq)
            y = jnp.swapaxes(y, 0, 1)
            return residual + y @ Wo + bo
        key = jax.random.key(seed)
        ks = jax.random.split(key, 8)
        s = 0.02
        return {'x': jax.random.normal(ks[0], (B, S, D_MODEL), dtype=jnp.float32), 'W_in': jax.random.normal(ks[1], (D_MODEL, 2 * INNER), dtype=jnp.float32) * s, 'b_in': jnp.zeros((2 * INNER,), jnp.float32), 'conv_w': jax.random.normal(ks[2], (INNER, 1, K), dtype=jnp.float32) * s, 'conv_b': jnp.zeros((INNER,), jnp.float32), 'Wa': jax.random.normal(ks[3], (INNER, INNER), dtype=jnp.float32) * s, 'ba': jnp.zeros((INNER,), jnp.float32), 'Wb': jax.random.normal(ks[4], (INNER, INNER), dtype=jnp.float32) * s, 'bb': jnp.zeros((INNER,), jnp.float32), 'Wc': jax.random.normal(ks[5], (INNER, INNER), dtype=jnp.float32) * s, 'bc': jnp.zeros((INNER,), jnp.float32), 'Wo': jax.random.normal(ks[6], (INNER, D_MODEL), dtype=jnp.float32) * s, 'bo': jnp.zeros((D_MODEL,), jnp.float32), 'gamma': jnp.ones((D_MODEL,), jnp.float32), 'beta': jnp.zeros((D_MODEL,), jnp.float32)}
    _L1_attn_all = _L1_attn_setup()
    _L1_attn_in = {k: v for k, v in _L1_attn_all.items() if k in ('W_in', 'b_in', 'conv_w', 'conv_b', 'Wa', 'ba', 'Wb', 'bb', 'Wc', 'bc', 'Wo', 'bo', 'gamma', 'beta')}
    del _L1_attn_all

    def _L1_ffn_setup():
        import jax, jax.numpy as jnp
        import numpy as np
        TOP_K = 2
        ROUTE_SCALE = 1.0
        EPS = 1e-20
        B, S, D = (2, 128, 256)
        E = 8
        F = 192
        FS = 192 * 1
        key = jax.random.key(seed)
        ks = jax.random.split(key, 9)
        s = 0.02
        return {'hidden_states': jax.random.normal(ks[0], (B, S, D), dtype=jnp.float32), 'W_gate_router': jax.random.normal(ks[1], (D, E), dtype=jnp.float32) * s, 'expert_bias': jnp.zeros((E,), dtype=jnp.float32), 'Wg': jax.random.normal(ks[2], (E, D, F), dtype=jnp.float32) * s, 'Wu': jax.random.normal(ks[3], (E, D, F), dtype=jnp.float32) * s, 'Wd': jax.random.normal(ks[4], (E, F, D), dtype=jnp.float32) * s, 'Wg_s': jax.random.normal(ks[5], (D, FS), dtype=jnp.float32) * s, 'Wu_s': jax.random.normal(ks[6], (D, FS), dtype=jnp.float32) * s, 'Wd_s': jax.random.normal(ks[7], (FS, D), dtype=jnp.float32) * s}
    _L1_ffn_all = _L1_ffn_setup()
    _L1_ffn_in = {k: v for k, v in _L1_ffn_all.items() if k in ('W_gate_router', 'expert_bias', 'Wg', 'Wu', 'Wd', 'Wg_s', 'Wu_s', 'Wd_s')}
    del _L1_ffn_all

    def _L2_attn_setup():
        import jax, jax.numpy as jnp
        import numpy as np
        B, T, C = (4, 512, 256)
        NQ, D = (8, C // 8)
        key = jax.random.key(seed)
        ks = jax.random.split(key, 6)
        s = 0.02
        return {'x': jax.random.normal(ks[0], (B, T, C), dtype=jnp.float32), 'Wk': jax.random.normal(ks[1], (C, D), dtype=jnp.float32) * s, 'Wv': jax.random.normal(ks[2], (C, D), dtype=jnp.float32) * s, 'Wq': jax.random.normal(ks[3], (NQ, C, D), dtype=jnp.float32) * s, 'Wp': jax.random.normal(ks[4], (NQ * D, C), dtype=jnp.float32) * s, 'bp': jnp.zeros((C,), dtype=jnp.float32)}
    _L2_attn_all = _L2_attn_setup()
    _L2_attn_in = {k: v for k, v in _L2_attn_all.items() if k in ('Wk', 'Wv', 'Wq', 'Wp', 'bp')}
    del _L2_attn_all

    def _L2_ffn_setup():
        import jax, jax.numpy as jnp
        import numpy as np
        D_MODEL = 256
        key = jax.random.key(seed)
        k_x, k_w, k_a1, k_a2 = jax.random.split(key, 4)
        x = jax.random.normal(k_x, (4, 512, D_MODEL), dtype=jnp.float32)
        weight = jax.random.normal(k_w, (D_MODEL, D_MODEL), dtype=jnp.float32) * 0.02
        aux_weight1 = jax.random.normal(k_a1, (D_MODEL, D_MODEL), dtype=jnp.float32) * 0.02
        aux_weight2 = jax.random.normal(k_a2, (D_MODEL, D_MODEL), dtype=jnp.float32) * 0.02
        bias = jnp.zeros((D_MODEL,), dtype=jnp.float32)
        return {'x': x, 'weight': weight, 'aux_weight1': aux_weight1, 'aux_weight2': aux_weight2, 'bias': bias}
    _L2_ffn_all = _L2_ffn_setup()
    _L2_ffn_in = {k: v for k, v in _L2_ffn_all.items() if k in ('weight', 'aux_weight1', 'aux_weight2', 'bias')}
    del _L2_ffn_all

    def _L3_attn_setup():
        import jax, jax.numpy as jnp
        import numpy as np
        EPS = 1e-06
        LN3 = 1.0986122886681098
        ROPE_BASE = 10000.0

        def exact_rmsnorm(x, g):
            ms = jnp.mean(jnp.square(x), axis=-1, keepdims=True)
            return x * jax.lax.rsqrt(ms + EPS) * g

        def ternary_rope(t):
            S, D = (t.shape[-2], t.shape[-1])
            half = D // 2
            inv_freq = 1.0 / ROPE_BASE ** (jnp.arange(half, dtype=jnp.float32) / half)
            ang = jnp.arange(S, dtype=jnp.float32)[:, None] * inv_freq[None, :]
            cos = jnp.round(jnp.cos(ang))
            sin = jnp.round(jnp.sin(ang))
            cos = jnp.concatenate([cos, cos], axis=-1)
            sin = jnp.concatenate([sin, sin], axis=-1)
            rot = jnp.concatenate([-t[..., half:], t[..., :half]], axis=-1)
            return t * cos + rot * sin

        def ternary_softmax(x, axis=-1):
            return jax.nn.softmax(x * LN3, axis=axis)
        key = jax.random.key(seed)
        ks = jax.random.split(key, 6)
        B, S, D = (4, 1024, 256)
        x = jax.random.normal(ks[0], (B, S, D), dtype=jnp.float32)
        g_norm = jnp.ones((D,), dtype=jnp.float32)
        w_qkv = jax.random.normal(ks[1], (D, 3 * D), dtype=jnp.float32) * 0.02
        b_qkv = jnp.zeros((3 * D,), dtype=jnp.float32)
        w_proj = jax.random.normal(ks[2], (D, D), dtype=jnp.float32) * 0.02
        b_proj = jnp.zeros((D,), dtype=jnp.float32)
        return {'x': x, 'g_norm': g_norm, 'w_qkv': w_qkv, 'b_qkv': b_qkv, 'w_proj': w_proj, 'b_proj': b_proj}
    _L3_attn_all = _L3_attn_setup()
    _L3_attn_in = {k: v for k, v in _L3_attn_all.items() if k in ('g_norm', 'w_qkv', 'b_qkv', 'w_proj', 'b_proj')}
    del _L3_attn_all

    def _L3_ffn_setup():
        import jax, jax.numpy as jnp
        import numpy as np
        D, F, E, K = (256, 688, 8, 2)
        key = jax.random.key(seed)
        k0, k1, k2, k3, k4 = jax.random.split(key, 5)
        s = 0.02
        x = jax.random.normal(k0, (2, 128, D), jnp.float32)
        Ws = jax.random.normal(k1, (D, E), jnp.float32) * s
        bs = jnp.zeros((E,), jnp.float32)
        Wg = jax.random.normal(k2, (E, D, F), jnp.float32) * s
        Wu = jax.random.normal(k3, (E, D, F), jnp.float32) * s
        Wd = jax.random.normal(k4, (E, F, D), jnp.float32) * s
        return {'x': x, 'Ws': Ws, 'bs': bs, 'Wg': Wg, 'Wu': Wu, 'Wd': Wd}
    _L3_ffn_all = _L3_ffn_setup()
    _L3_ffn_in = {k: v for k, v in _L3_ffn_all.items() if k in ('Ws', 'bs', 'Wg', 'Wu', 'Wd')}
    del _L3_ffn_all
    return {'x': x, 'x_txt': x_txt, 'L0_tok_W': _L0_tok_in['W'], 'L0_tok_b': _L0_tok_in['b'], 'L0_tok_cls_token': _L0_tok_in['cls_token'], 'L0_tok_pos_embedding': _L0_tok_in['pos_embedding'], 'L0_txt_emb': _L0_txt_in['emb'], 'L0_txt_in_proj_w': _L0_txt_in['in_proj_w'], 'L0_txt_in_proj_b': _L0_txt_in['in_proj_b'], 'L0_txt_out_proj_w': _L0_txt_in['out_proj_w'], 'L0_txt_out_proj_b': _L0_txt_in['out_proj_b'], 'L0_txt_w1': _L0_txt_in['w1'], 'L0_txt_b1': _L0_txt_in['b1'], 'L0_txt_w2': _L0_txt_in['w2'], 'L0_txt_b2': _L0_txt_in['b2'], 'L0_txt_g1': _L0_txt_in['g1'], 'L0_txt_beta1': _L0_txt_in['beta1'], 'L0_txt_g2': _L0_txt_in['g2'], 'L0_txt_beta2': _L0_txt_in['beta2'], 'L0_attn_Wq': _L0_attn_in['Wq'], 'L0_attn_Wk': _L0_attn_in['Wk'], 'L0_attn_Wv': _L0_attn_in['Wv'], 'L0_attn_Wbeta': _L0_attn_in['Wbeta'], 'L0_attn_bbeta': _L0_attn_in['bbeta'], 'L0_attn_Wmix': _L0_attn_in['Wmix'], 'L0_attn_bmix': _L0_attn_in['bmix'], 'L0_attn_Wgate': _L0_attn_in['Wgate'], 'L0_attn_bgate': _L0_attn_in['bgate'], 'L0_attn_Wout': _L0_attn_in['Wout'], 'L0_attn_bout': _L0_attn_in['bout'], 'L0_attn_ln_g': _L0_attn_in['ln_g'], 'L0_attn_ln_b': _L0_attn_in['ln_b'], 'L0_ffn_index_b': _L0_ffn_in['index_b'], 'L0_ffn_index_t': _L0_ffn_in['index_t'], 'L0_ffn_sw1': _L0_ffn_in['sw1'], 'L0_ffn_sb1': _L0_ffn_in['sb1'], 'L0_ffn_sw2': _L0_ffn_in['sw2'], 'L0_ffn_sb2': _L0_ffn_in['sb2'], 'L0_ffn_sw3': _L0_ffn_in['sw3'], 'L0_ffn_sb3': _L0_ffn_in['sb3'], 'L0_ffn_s_ln_g': _L0_ffn_in['s_ln_g'], 'L0_ffn_s_ln_b': _L0_ffn_in['s_ln_b'], 'L0_ffn_sg_w': _L0_ffn_in['sg_w'], 'L0_ffn_sg_b': _L0_ffn_in['sg_b'], 'L0_ffn_eg_w': _L0_ffn_in['eg_w'], 'L0_ffn_eg_b': _L0_ffn_in['eg_b'], 'L0_ffn_exp_bias': _L0_ffn_in['exp_bias'], 'L0_ffn_ew1': _L0_ffn_in['ew1'], 'L0_ffn_eb1': _L0_ffn_in['eb1'], 'L0_ffn_ew2': _L0_ffn_in['ew2'], 'L0_ffn_eb2': _L0_ffn_in['eb2'], 'L0_ffn_ew3': _L0_ffn_in['ew3'], 'L0_ffn_eb3': _L0_ffn_in['eb3'], 'L0_ffn_sel_ln_g': _L0_ffn_in['sel_ln_g'], 'L0_ffn_sel_ln_b': _L0_ffn_in['sel_ln_b'], 'L1_attn_W_in': _L1_attn_in['W_in'], 'L1_attn_b_in': _L1_attn_in['b_in'], 'L1_attn_conv_w': _L1_attn_in['conv_w'], 'L1_attn_conv_b': _L1_attn_in['conv_b'], 'L1_attn_Wa': _L1_attn_in['Wa'], 'L1_attn_ba': _L1_attn_in['ba'], 'L1_attn_Wb': _L1_attn_in['Wb'], 'L1_attn_bb': _L1_attn_in['bb'], 'L1_attn_Wc': _L1_attn_in['Wc'], 'L1_attn_bc': _L1_attn_in['bc'], 'L1_attn_Wo': _L1_attn_in['Wo'], 'L1_attn_bo': _L1_attn_in['bo'], 'L1_attn_gamma': _L1_attn_in['gamma'], 'L1_attn_beta': _L1_attn_in['beta'], 'L1_ffn_W_gate_router': _L1_ffn_in['W_gate_router'], 'L1_ffn_expert_bias': _L1_ffn_in['expert_bias'], 'L1_ffn_Wg': _L1_ffn_in['Wg'], 'L1_ffn_Wu': _L1_ffn_in['Wu'], 'L1_ffn_Wd': _L1_ffn_in['Wd'], 'L1_ffn_Wg_s': _L1_ffn_in['Wg_s'], 'L1_ffn_Wu_s': _L1_ffn_in['Wu_s'], 'L1_ffn_Wd_s': _L1_ffn_in['Wd_s'], 'L2_attn_Wk': _L2_attn_in['Wk'], 'L2_attn_Wv': _L2_attn_in['Wv'], 'L2_attn_Wq': _L2_attn_in['Wq'], 'L2_attn_Wp': _L2_attn_in['Wp'], 'L2_attn_bp': _L2_attn_in['bp'], 'L2_ffn_weight': _L2_ffn_in['weight'], 'L2_ffn_aux_weight1': _L2_ffn_in['aux_weight1'], 'L2_ffn_aux_weight2': _L2_ffn_in['aux_weight2'], 'L2_ffn_bias': _L2_ffn_in['bias'], 'L3_attn_g_norm': _L3_attn_in['g_norm'], 'L3_attn_w_qkv': _L3_attn_in['w_qkv'], 'L3_attn_b_qkv': _L3_attn_in['b_qkv'], 'L3_attn_w_proj': _L3_attn_in['w_proj'], 'L3_attn_b_proj': _L3_attn_in['b_proj'], 'L3_ffn_Ws': _L3_ffn_in['Ws'], 'L3_ffn_bs': _L3_ffn_in['bs'], 'L3_ffn_Wg': _L3_ffn_in['Wg'], 'L3_ffn_Wu': _L3_ffn_in['Wu'], 'L3_ffn_Wd': _L3_ffn_in['Wd']}

def reference(x, x_txt, L0_tok_W, L0_tok_b, L0_tok_cls_token, L0_tok_pos_embedding, L0_txt_emb, L0_txt_in_proj_w, L0_txt_in_proj_b, L0_txt_out_proj_w, L0_txt_out_proj_b, L0_txt_w1, L0_txt_b1, L0_txt_w2, L0_txt_b2, L0_txt_g1, L0_txt_beta1, L0_txt_g2, L0_txt_beta2, L0_attn_Wq, L0_attn_Wk, L0_attn_Wv, L0_attn_Wbeta, L0_attn_bbeta, L0_attn_Wmix, L0_attn_bmix, L0_attn_Wgate, L0_attn_bgate, L0_attn_Wout, L0_attn_bout, L0_attn_ln_g, L0_attn_ln_b, L0_ffn_index_b, L0_ffn_index_t, L0_ffn_sw1, L0_ffn_sb1, L0_ffn_sw2, L0_ffn_sb2, L0_ffn_sw3, L0_ffn_sb3, L0_ffn_s_ln_g, L0_ffn_s_ln_b, L0_ffn_sg_w, L0_ffn_sg_b, L0_ffn_eg_w, L0_ffn_eg_b, L0_ffn_exp_bias, L0_ffn_ew1, L0_ffn_eb1, L0_ffn_ew2, L0_ffn_eb2, L0_ffn_ew3, L0_ffn_eb3, L0_ffn_sel_ln_g, L0_ffn_sel_ln_b, L1_attn_W_in, L1_attn_b_in, L1_attn_conv_w, L1_attn_conv_b, L1_attn_Wa, L1_attn_ba, L1_attn_Wb, L1_attn_bb, L1_attn_Wc, L1_attn_bc, L1_attn_Wo, L1_attn_bo, L1_attn_gamma, L1_attn_beta, L1_ffn_W_gate_router, L1_ffn_expert_bias, L1_ffn_Wg, L1_ffn_Wu, L1_ffn_Wd, L1_ffn_Wg_s, L1_ffn_Wu_s, L1_ffn_Wd_s, L2_attn_Wk, L2_attn_Wv, L2_attn_Wq, L2_attn_Wp, L2_attn_bp, L2_ffn_weight, L2_ffn_aux_weight1, L2_ffn_aux_weight2, L2_ffn_bias, L3_attn_g_norm, L3_attn_w_qkv, L3_attn_b_qkv, L3_attn_w_proj, L3_attn_b_proj, L3_ffn_Ws, L3_ffn_bs, L3_ffn_Wg, L3_ffn_Wu, L3_ffn_Wd):
    import jax
    import jax.numpy as jnp

    def _L0_tok_ref(x, W, b, cls_token, pos_embedding):
        import jax, jax.numpy as jnp
        import numpy as np
        B, C, H, Wd = (64, 3, 96, 96)
        PH, PW, D = (16, 16, 256)
        PATCH_DIM = C * PH * PW
        N_TOK = H // PH * (Wd // PW)
        Bc = x.shape[0]
        nh, nw = (H // PH, Wd // PW)
        patches = x.reshape(Bc, C, nh, PH, nw, PW)
        patches = patches.transpose(0, 2, 4, 1, 3, 5).reshape(Bc, nh * nw, PATCH_DIM)
        tokens = jnp.einsum('bnp,dp->bnd', patches, W) + b
        cls = jnp.broadcast_to(cls_token, (Bc, 1, D))
        tokens = jnp.concatenate([cls, tokens], axis=1)
        return tokens + pos_embedding

    def _L0_txt_ref(tokens, emb, in_proj_w, in_proj_b, out_proj_w, out_proj_b, w1, b1, w2, b2, g1, beta1, g2, beta2):
        import jax, jax.numpy as jnp
        import numpy as np
        VOCAB, D, H = (8000, 256, 16)
        DH = D // H
        DFF = 4 * D
        EPS = 1e-05

        def layer_norm(x, g, b):
            mu = jnp.mean(x, axis=-1, keepdims=True)
            var = jnp.var(x, axis=-1, keepdims=True)
            return (x - mu) * jax.lax.rsqrt(var + EPS) * g + b

        def pos_enc(seq_len, d_model):
            pos = jnp.arange(seq_len, dtype=jnp.float32)[:, None]
            i_even = jnp.arange(0, d_model, 2, dtype=jnp.float32)[None, :]
            angle = pos / jnp.power(10000.0, 2.0 * i_even / d_model)
            pe = jnp.zeros((seq_len, d_model), dtype=jnp.float32)
            pe = pe.at[:, 0::2].set(jnp.sin(angle))
            pe = pe.at[:, 1::2].set(jnp.cos(angle))
            return pe
        B, S = tokens.shape
        x = emb[tokens] + pos_enc(S, D)[None, :, :]
        qkv = x @ in_proj_w.T + in_proj_b
        q, k, v = jnp.split(qkv, 3, axis=-1)
        q = q.reshape(B, S, H, DH)
        k = k.reshape(B, S, H, DH)
        v = v.reshape(B, S, H, DH)
        scores = jnp.einsum('bqhd,bkhd->bhqk', q, k) / jnp.sqrt(jnp.float32(DH))
        attn = jax.nn.softmax(scores, axis=-1)
        ctx = jnp.einsum('bhqk,bkhd->bqhd', attn, v).reshape(B, S, D)
        attn_out = ctx @ out_proj_w.T + out_proj_b
        h = layer_norm(x + attn_out, g1, beta1)
        ff = jax.nn.relu(h @ w1.T + b1) @ w2.T + b2
        return layer_norm(h + ff, g2, beta2)

    def _L0_attn_ref(x, Wq, Wk, Wv, Wbeta, bbeta, Wmix, bmix, Wgate, bgate, Wout, bout, ln_g, ln_b):
        import jax, jax.numpy as jnp
        import numpy as np
        import math
        from jax import lax
        B, T, HID, H, J = (4, 512, 256, 8, 2)
        EPS = 1e-06
        LN_EPS = 1e-05

        def _alibi_slopes(n):

            def pow2(m):
                start = 2 ** (-2 ** (-(math.log2(m) - 3)))
                return [start * start ** i for i in range(m)]
            if math.log2(n).is_integer():
                return np.array(pow2(n), dtype=np.float32)
            c = 2 ** int(math.floor(math.log2(n)))
            s = pow2(c) + _alibi_slopes(2 * c).tolist()[:n - c]
            return np.array(s, dtype=np.float32)

        def _deltanet(x, Wq, Wk, Wv, Wbeta, bbeta, Wmix, bmix, Wgate, bgate, Wout, bout, ln_g, ln_b):
            b, t, hid = x.shape
            h = Wgate.shape[0]
            j = Wbeta.shape[0] // h
            d = hid // h
            r = jnp.asarray(np.exp(-_alibi_slopes(h)))[None, :, None]
            q = (jax.nn.elu(x @ Wq.T) + 1.0).reshape(b, t, h, d)
            k = (jax.nn.elu(x @ Wk.T) + 1.0).reshape(b, t, h, d)
            v = (x @ Wv.T).reshape(b, t, h, d)
            beta = (x @ Wbeta.T + bbeta).reshape(b, t, h, j)
            mix = (x @ Wmix.T + bmix).reshape(b, t, h, j)
            gate = jax.nn.sigmoid(x @ Wgate.T + bgate)

            def step(carry, inp):
                S, z = carry
                q_t, k_t, v_t, beta_t, mix_t, g_t = inp
                beta_eff = jnp.minimum(jax.nn.sigmoid(beta_t) * r, 0.9999)
                outer = jnp.einsum('bhd,bhe->bhde', k_t, v_t).astype(jnp.float32)[:, :, None]
                S = S * beta_eff[..., None, None] + g_t[:, :, None, None, None] * outer
                z = z * beta_eff[..., None] + g_t[:, :, None, None] * k_t[:, :, None, :]
                num = jnp.einsum('bhd,bhjde->bhje', q_t, S)
                denom = jnp.einsum('bhd,bhjd->bhj', q_t, z) + EPS
                w = jax.nn.softmax(mix_t, axis=-1)[..., None]
                y_t = jnp.sum(num / denom[..., None] * w, axis=2)
                return ((S, z), y_t)
            S0 = jnp.zeros((b, h, j, d, d), jnp.float32)
            z0 = jnp.zeros((b, h, j, d), jnp.float32)
            tm = lambda a: jnp.swapaxes(a, 0, 1)
            _, yT = lax.scan(step, (S0, z0), (tm(q), tm(k), tm(v), tm(beta), tm(mix), tm(gate)))
            y = jnp.swapaxes(yT, 0, 1).reshape(b, t, hid).astype(x.dtype)
            out = y @ Wout.T + bout
            hres = x + out
            mu = jnp.mean(hres, axis=-1, keepdims=True)
            var = jnp.mean(jnp.square(hres - mu), axis=-1, keepdims=True)
            return (hres - mu) / jnp.sqrt(var + LN_EPS) * ln_g + ln_b
        return _deltanet(x, Wq, Wk, Wv, Wbeta, bbeta, Wmix, bmix, Wgate, bgate, Wout, bout, ln_g, ln_b)

    def _L0_ffn_ref(x, index_b, index_t, sw1, sb1, sw2, sb2, sw3, sb3, s_ln_g, s_ln_b, sg_w, sg_b, eg_w, eg_b, exp_bias, ew1, eb1, ew2, eb2, ew3, eb3, sel_ln_g, sel_ln_b):
        import jax, jax.numpy as jnp
        import numpy as np
        EPS = 1e-05

        def _ln(x, g, b):
            mu = jnp.mean(x, axis=-1, keepdims=True)
            var = jnp.mean(jnp.square(x - mu), axis=-1, keepdims=True)
            return (x - mu) * jax.lax.rsqrt(var + EPS) * g + b

        def _forward(x, index_b, index_t, sw1, sb1, sw2, sb2, sw3, sb3, s_ln_g, s_ln_b, sg_w, sg_b, eg_w, eg_b, exp_bias, ew1, eb1, ew2, eb2, ew3, eb3, sel_ln_g, sel_ln_b):
            x1 = jnp.einsum('btd,hd->bth', x, sw1) + sb1
            x2 = jnp.einsum('btd,hd->bth', x, sw2) + sb2
            sh = _ln(jax.nn.silu(x1) * x2, s_ln_g, s_ln_b)
            shared_out = jnp.einsum('bth,dh->btd', sh, sw3) + sb3
            x_moe = x[index_b, index_t]
            shared_scores = jax.nn.sigmoid(x_moe @ sg_w.T + sg_b)
            expert_scores = jax.nn.sigmoid(x_moe @ eg_w.T + eg_b)
            top1_idx = jnp.argmax(expert_scores + exp_bias, axis=-1)
            top1_score = jnp.take_along_axis(expert_scores, top1_idx[:, None], axis=-1)
            weights = jax.nn.softmax(jnp.concatenate([shared_scores, top1_score], axis=-1), axis=-1)
            shared_w, expert_w = (weights[:, 0], weights[:, 1])
            shared_moe_out = shared_out[index_b, index_t] * shared_w[:, None]
            h1 = jnp.einsum('md,ehd->meh', x_moe, ew1) + eb1
            h2 = jnp.einsum('md,ehd->meh', x_moe, ew2) + eb2
            z = _ln(jax.nn.silu(h1) * h2, sel_ln_g, sel_ln_b)
            out_all = jnp.einsum('meh,edh->med', z, ew3) + eb3
            expert_out = jnp.take_along_axis(out_all, top1_idx[:, None, None], axis=1)[:, 0]
            expert_moe_out = expert_out * expert_w[:, None]
            final_out = shared_out.at[index_b, index_t].set(shared_moe_out + expert_moe_out)
            return final_out
        return _forward(x, index_b, index_t, sw1, sb1, sw2, sb2, sw3, sb3, s_ln_g, s_ln_b, sg_w, sg_b, eg_w, eg_b, exp_bias, ew1, eb1, ew2, eb2, ew3, eb3, sel_ln_g, sel_ln_b)

    def _L1_attn_ref(x, W_in, b_in, conv_w, conv_b, Wa, ba, Wb, bb, Wc, bc, Wo, bo, gamma, beta):
        import jax, jax.numpy as jnp
        import numpy as np
        from jax import lax
        D_MODEL = 256
        INNER = 512
        K = 3
        B, S = (4, 512)

        def _layernorm(x, gamma, beta, eps=1e-05):
            mu = jnp.mean(x, axis=-1, keepdims=True)
            var = jnp.mean(jnp.square(x - mu), axis=-1, keepdims=True)
            return (x - mu) * lax.rsqrt(var + eps) * gamma + beta

        def _forward(x, W_in, b_in, conv_w, conv_b, Wa, ba, Wb, bb, Wc, bc, Wo, bo, gamma, beta):
            residual = x
            xn = _layernorm(x, gamma, beta)
            proj = xn @ W_in + b_in
            projected, gate = jnp.split(proj, 2, axis=-1)
            conv_in = jnp.swapaxes(projected, 1, 2)
            conv_out = lax.conv_general_dilated(conv_in, conv_w, window_strides=(1,), padding=[(K - 1, 0)], feature_group_count=INNER, dimension_numbers=('NCH', 'OIH', 'NCH'))
            conv_out = jnp.swapaxes(conv_out + conv_b[None, :, None], 1, 2)
            u = jax.nn.silu(conv_out) * jax.nn.sigmoid(gate)
            a = jax.nn.sigmoid(u @ Wa + ba)
            b = jax.nn.sigmoid(u @ Wb + bb)
            c = jnp.tanh(u @ Wc + bc)

            def step(state, abu):
                a_t, b_t, c_t, u_t = abu
                state = a_t * state + b_t * u_t
                return (state, c_t * state + u_t)
            seq = tuple((jnp.swapaxes(t, 0, 1) for t in (a, b, c, u)))
            _, y = lax.scan(step, jnp.zeros((x.shape[0], INNER), x.dtype), seq)
            y = jnp.swapaxes(y, 0, 1)
            return residual + y @ Wo + bo
        return _forward(x, W_in, b_in, conv_w, conv_b, Wa, ba, Wb, bb, Wc, bc, Wo, bo, gamma, beta)

    def _L1_ffn_ref(hidden_states, W_gate_router, expert_bias, Wg, Wu, Wd, Wg_s, Wu_s, Wd_s):
        import jax, jax.numpy as jnp
        import numpy as np
        TOP_K = 2
        ROUTE_SCALE = 1.0
        EPS = 1e-20
        B, S, D = (2, 128, 256)
        E = 8
        F = 192
        FS = 192 * 1
        b, s, d = hidden_states.shape
        x = hidden_states.reshape(-1, d)
        T = x.shape[0]
        logits = x @ W_gate_router
        scores = jax.nn.sigmoid(logits.astype(jnp.float32))
        _, sel = jax.lax.top_k(scores + expert_bias, TOP_K)
        top_scores = jnp.take_along_axis(scores, sel, axis=1)
        top_scores = top_scores / (top_scores.sum(-1, keepdims=True) + EPS)
        top_scores = top_scores * ROUTE_SCALE
        shared = jax.nn.silu(x @ Wg_s) * (x @ Wu_s) @ Wd_s
        tok = jnp.repeat(jnp.arange(T), TOP_K)
        exp = sel.reshape(-1)
        w = top_scores.reshape(-1)
        xr = x[tok]
        h = jax.nn.silu(jnp.einsum('nd,edf->enf', xr, Wg)) * jnp.einsum('nd,edf->enf', xr, Wu)
        out_all = jnp.einsum('enf,efd->end', h, Wd)
        routed = out_all[exp, jnp.arange(exp.shape[0])]
        routed = (routed.astype(jnp.float32) * w[:, None]).astype(hidden_states.dtype)
        out = shared.at[tok].add(routed)
        return out.reshape(b, s, d)

    def _L2_attn_ref(x, Wk, Wv, Wq, Wp, bp):
        import jax, jax.numpy as jnp
        import numpy as np
        B, T, C = (4, 512, 256)
        NQ, D = (8, C // 8)
        b, t, c = x.shape
        scale = c ** (-0.5)
        k = x @ Wk
        v = x @ Wv
        q = jnp.einsum('btc,qcd->bqtd', x, Wq)
        wei = jnp.einsum('bqtd,bsd->bqts', q, k) * scale
        causal = jnp.tril(jnp.ones((t, t), dtype=bool))
        wei = jnp.where(causal, wei, -jnp.inf)
        wei = jax.nn.softmax(wei, axis=-1)
        out = jnp.einsum('bqts,bsd->btqd', wei, v)
        out = out.reshape(b, t, -1)
        return out @ Wp + bp

    def _L2_ffn_ref(x, weight, aux_weight1, aux_weight2, bias):
        import jax, jax.numpy as jnp
        import numpy as np
        D_MODEL = 256
        h = jnp.einsum('btc,cd->btd', x, weight)
        h = jnp.einsum('btc,cd->btd', h, aux_weight1)
        h = jnp.einsum('btc,cd->btd', h, aux_weight2)
        return jnp.tanh(h + bias)

    def _L3_attn_ref(x, g_norm, w_qkv, b_qkv, w_proj, b_proj):
        import jax, jax.numpy as jnp
        import numpy as np
        EPS = 1e-06
        LN3 = 1.0986122886681098
        ROPE_BASE = 10000.0

        def exact_rmsnorm(x, g):
            ms = jnp.mean(jnp.square(x), axis=-1, keepdims=True)
            return x * jax.lax.rsqrt(ms + EPS) * g

        def ternary_rope(t):
            S, D = (t.shape[-2], t.shape[-1])
            half = D // 2
            inv_freq = 1.0 / ROPE_BASE ** (jnp.arange(half, dtype=jnp.float32) / half)
            ang = jnp.arange(S, dtype=jnp.float32)[:, None] * inv_freq[None, :]
            cos = jnp.round(jnp.cos(ang))
            sin = jnp.round(jnp.sin(ang))
            cos = jnp.concatenate([cos, cos], axis=-1)
            sin = jnp.concatenate([sin, sin], axis=-1)
            rot = jnp.concatenate([-t[..., half:], t[..., :half]], axis=-1)
            return t * cos + rot * sin

        def ternary_softmax(x, axis=-1):
            return jax.nn.softmax(x * LN3, axis=axis)
        D = x.shape[-1]
        scale = 1.0 / jnp.sqrt(jnp.float32(D))
        residual = x
        h = exact_rmsnorm(x, g_norm)
        qkv = h @ w_qkv + b_qkv
        q, k, v = jnp.split(qkv, 3, axis=-1)
        q = ternary_rope(q)
        k = ternary_rope(k)
        scores = jnp.einsum('bsd,btd->bst', q, k) * scale
        attn = ternary_softmax(scores, axis=-1)
        o = jnp.einsum('bst,btd->bsd', attn, v)
        return o @ w_proj + b_proj + residual

    def _L3_ffn_ref(x, Ws, bs, Wg, Wu, Wd):
        import jax, jax.numpy as jnp
        import numpy as np
        D, F, E, K = (256, 688, 8, 2)
        b, n, d = x.shape
        xt = x.reshape(-1, d)
        logits = xt @ Ws + bs
        topk_w, topk_idx = jax.lax.top_k(logits, K)
        topk_w = jax.nn.softmax(topk_w, axis=-1)
        combine = jnp.sum(jax.nn.one_hot(topk_idx, E, dtype=xt.dtype) * topk_w[..., None], axis=1)
        g = jnp.einsum('td,edf->tef', xt, Wg)
        u = jnp.einsum('td,edf->tef', xt, Wu)
        h = jax.nn.silu(g) * u
        y = jnp.einsum('tef,efd->ted', h, Wd)
        out = jnp.einsum('ted,te->td', y, combine)
        return out.reshape(b, n, d)
    h = _L0_tok_ref(x, L0_tok_W, L0_tok_b, L0_tok_cls_token, L0_tok_pos_embedding)
    h = jnp.concatenate([h, _L0_txt_ref(x_txt, L0_txt_emb, L0_txt_in_proj_w, L0_txt_in_proj_b, L0_txt_out_proj_w, L0_txt_out_proj_b, L0_txt_w1, L0_txt_b1, L0_txt_w2, L0_txt_b2, L0_txt_g1, L0_txt_beta1, L0_txt_g2, L0_txt_beta2)], axis=1)
    h = h + _L0_attn_ref(_layernorm(h, axis=-1), L0_attn_Wq, L0_attn_Wk, L0_attn_Wv, L0_attn_Wbeta, L0_attn_bbeta, L0_attn_Wmix, L0_attn_bmix, L0_attn_Wgate, L0_attn_bgate, L0_attn_Wout, L0_attn_bout, L0_attn_ln_g, L0_attn_ln_b)
    h = h + _L0_ffn_ref(_layernorm(h, axis=-1), L0_ffn_index_b, L0_ffn_index_t, L0_ffn_sw1, L0_ffn_sb1, L0_ffn_sw2, L0_ffn_sb2, L0_ffn_sw3, L0_ffn_sb3, L0_ffn_s_ln_g, L0_ffn_s_ln_b, L0_ffn_sg_w, L0_ffn_sg_b, L0_ffn_eg_w, L0_ffn_eg_b, L0_ffn_exp_bias, L0_ffn_ew1, L0_ffn_eb1, L0_ffn_ew2, L0_ffn_eb2, L0_ffn_ew3, L0_ffn_eb3, L0_ffn_sel_ln_g, L0_ffn_sel_ln_b)
    h = h + _L1_attn_ref(_layernorm(h, axis=-1), L1_attn_W_in, L1_attn_b_in, L1_attn_conv_w, L1_attn_conv_b, L1_attn_Wa, L1_attn_ba, L1_attn_Wb, L1_attn_bb, L1_attn_Wc, L1_attn_bc, L1_attn_Wo, L1_attn_bo, L1_attn_gamma, L1_attn_beta)
    h = h + _L1_ffn_ref(_layernorm(h, axis=-1), L1_ffn_W_gate_router, L1_ffn_expert_bias, L1_ffn_Wg, L1_ffn_Wu, L1_ffn_Wd, L1_ffn_Wg_s, L1_ffn_Wu_s, L1_ffn_Wd_s)
    h = h + _L2_attn_ref(_layernorm(h, axis=-1), L2_attn_Wk, L2_attn_Wv, L2_attn_Wq, L2_attn_Wp, L2_attn_bp)
    h = h + _L2_ffn_ref(_layernorm(h, axis=-1), L2_ffn_weight, L2_ffn_aux_weight1, L2_ffn_aux_weight2, L2_ffn_bias)
    h = h + _L3_attn_ref(_layernorm(h, axis=-1), L3_attn_g_norm, L3_attn_w_qkv, L3_attn_b_qkv, L3_attn_w_proj, L3_attn_b_proj)
    h = h + _L3_ffn_ref(_layernorm(h, axis=-1), L3_ffn_Ws, L3_ffn_bs, L3_ffn_Wg, L3_ffn_Wu, L3_ffn_Wd)
    return h

_drawn_inputs = setup_inputs


def setup_inputs(seed=0):
    import zlib

    import numpy as np

    out = dict(_drawn_inputs(seed))
    spreads = {'L0_txt_in_proj_b': (0.0, 0.1),
     'L0_txt_out_proj_b': (0.0, 0.1),
     'L0_txt_b1': (0.0, 0.1),
     'L0_txt_b2': (0.0, 0.1),
     'L0_txt_g1': (1.0, 0.2),
     'L0_txt_beta1': (0.0, 0.1),
     'L0_txt_g2': (1.0, 0.2),
     'L0_txt_beta2': (0.0, 0.1),
     'L0_attn_bbeta': (2.197200059890747, 0.6),
     'L0_attn_bmix': (0.0, 2.0),
     'L0_attn_bgate': (0.0, 2.0),
     'L0_attn_bout': (0.0, 0.1),
     'L0_attn_ln_g': (1.0, 0.2),
     'L0_attn_ln_b': (0.0, 0.1),
     'L0_ffn_sb1': (0.0, 0.288),
     'L0_ffn_sb2': (0.0, 0.1),
     'L0_ffn_sb3': (0.0, 0.1),
     'L0_ffn_s_ln_g': (1.0, 0.6),
     'L0_ffn_s_ln_b': (0.0, 0.77),
     'L0_ffn_eg_b': (0.0, 0.699),
     'L0_ffn_exp_bias': (0.0, 0.1),
     'L0_ffn_eb1': (0.0, 0.8),
     'L0_ffn_eb2': (0.0, 0.8),
     'L0_ffn_eb3': (0.0, 0.692),
     'L0_ffn_sel_ln_g': (1.0, 0.6),
     'L0_ffn_sel_ln_b': (0.0, 0.8),
     'L1_attn_b_in': (0.0, 0.8),
     'L1_attn_conv_b': (0.0, 0.8),
     'L1_attn_ba': (0.0, 0.8),
     'L1_attn_bb': (0.0, 0.8),
     'L1_attn_bc': (0.0, 0.8),
     'L1_attn_bo': (0.0, 0.1),
     'L1_attn_gamma': (1.0, 0.6),
     'L1_attn_beta': (0.0, 0.8),
     'L1_ffn_expert_bias': (0.0, 0.8),
     'L2_attn_bp': (0.0, 0.611),
     'L2_ffn_bias': (0.0, 2.0),
     'L3_attn_g_norm': (1.0, 0.6),
     'L3_attn_b_qkv': (0.0, 0.8),
     'L3_attn_b_proj': (0.0, 0.303),
     'L3_ffn_bs': (0.0, 0.8)}
    factors = {'L0_tok_b': 8.0,
     'L0_tok_pos_embedding': 8.0,
     'L0_attn_Wq': 60.621,
     'L0_attn_Wk': 43.862,
     'L0_attn_Wbeta': 8.0,
     'L0_attn_Wmix': 8.0,
     'L0_attn_Wgate': 8.0,
     'L0_ffn_sg_w': 8.0,
     'L0_ffn_eg_w': 3.347,
     'L1_attn_W_in': 8.0,
     'L1_attn_conv_w': 8.0,
     'L1_attn_Wa': 8.0,
     'L1_attn_Wb': 8.0,
     'L1_attn_Wc': 8.0,
     'L1_attn_Wo': 8.0,
     'L1_ffn_W_gate_router': 8.0,
     'L1_ffn_Wg': 8.0,
     'L1_ffn_Wu': 8.0,
     'L1_ffn_Wd': 8.0,
     'L1_ffn_Wg_s': 8.0,
     'L1_ffn_Wu_s': 8.0,
     'L1_ffn_Wd_s': 8.0,
     'L2_attn_Wk': 26.434,
     'L2_attn_Wv': 2.887,
     'L2_attn_Wq': 8.0,
     'L2_ffn_weight': 5.81,
     'L2_ffn_aux_weight1': 5.641,
     'L2_ffn_aux_weight2': 5.819,
     'L3_attn_w_qkv': 3.097,
     'L3_attn_w_proj': 2.764,
     'L3_ffn_Ws': 8.0,
     'L3_ffn_Wg': 8.0,
     'L3_ffn_Wu': 8.0,
     'L3_ffn_Wd': 8.0}
    for name, (base, spread) in spreads.items():
        noise = np.random.default_rng([zlib.crc32(name.encode()), seed]).standard_normal(out[name].shape)
        drawn = base * np.exp(spread * noise) if base else spread * noise
        out[name] = jnp.asarray(drawn.astype(out[name].dtype))
    for name, factor in factors.items():
        out[name] = (out[name] * factor).astype(out[name].dtype)
    return out
```

```python
from contextlib import ExitStack

import concourse.bass as bass
from concourse import mybir

F32 = mybir.dt.float32
F32R = mybir.dt.float32r
I32 = mybir.dt.int32
U32 = mybir.dt.uint32
ALU = mybir.AluOpType
ACT = mybir.ActivationFunctionType
AX_X = mybir.AxisListType.X

P = 128
D = 256
KD = D // P
NB = 4
S_IMG = 37
S_TXT = 512
S = S_IMG + S_TXT
NT = NB * S
CH = 6
CN = NT // CH
RT = 18
RN = NT // RT
NE = 8
VOCAB = 8000
BIG = 1.0e30


class Chain:

    def __init__(self, engine, semaphore):
        self.engine, self.semaphore = engine, semaphore
        self.base, self.n, self.turn = 0, 0, None

    def begin(self, i, per):
        self.turn, self.per, self.n = i, per, 0

    def end(self, turns):
        assert self.n == self.per, (self.n, self.per)
        self.base, self.n, self.turn = self.base + turns * self.per, 0, None

    def value(self):
        return self.base + self.n if self.turn is None else self.turn * self.per + (self.base + self.n)

    def step(self, instruction):
        self.n += 1
        instruction.then_inc(self.semaphore, 1)
        self.engine.wait_ge(self.semaphore, self.value())


class Scope:

    def __init__(self, nc, ctx, name):
        self.nc, self.ctx, self.name = nc, ctx, name

    def sb(self, name, shape, dt=F32):
        return self.ctx.enter_context(self.nc.sbuf_tensor(f"{self.name}_{name}", shape, dt))

    def ps(self, name, shape):
        return self.ctx.enter_context(self.nc.psum_tensor(f"{self.name}_{name}", shape, F32))

    def sem(self, name):
        handle = self.nc.alloc_semaphore(f"{self.name}_{name}")
        Scope.in_use.append(handle)
        return handle

    in_use = []


def clear_semaphores(nc):
    nc.clear_and_free_semaphores(Scope.in_use)
    Scope.in_use.clear()
    nc.all_engine_barrier()


def chunk(t, k, i):
    return t[:, k, bass.ds(i * CN, CN)]


def both(t, i):
    return t[:, :, bass.ds(i * CN, CN)]


def bank(ps, i, rows=P, n=CN):
    return ps[0:rows, bass.ds(i, 1), 0:n].rearrange("p a n -> p (a n)")


def bank2(ps, i, blocks, n=CN):
    return ps[:, bass.ds(i, 1), 0:n].to_broadcast([P, blocks, n])


class LayerNorm:

    def __init__(self, sc, tag, src, out, sq, rstd, avg, eps, ps, gamma=None, beta=None, rms=False,
                 chunks=CH, width=CN, final=None):
        self.n, self.w = chunks, width
        self.final = final or (lambda k, i: self.at(self.out, k, i))
        self.src, self.out, self.sq, self.rstd, self.avg, self.ps = src, out, sq, rstd, avg, ps
        self.eps, self.gamma, self.beta, self.rms = eps, gamma, beta, rms
        self.mean_ready = sc.sem(tag + "_mean_ready")
        self.centred = sc.sem(tag + "_centred")
        self.squared = sc.sem(tag + "_squared")
        self.var_ready = sc.sem(tag + "_var_ready")
        self.std_ready = sc.sem(tag + "_std_ready")
        self.rstd_ready = sc.sem(tag + "_rstd_ready")
        self.scaled = sc.sem(tag + "_scaled")
        self.normed = sc.sem(tag + "_normed")

    def at(self, t, k, i):
        return t[:, k, bass.ds(i * self.w, self.w)]

    def all(self, t, i):
        return t[:, :, bass.ds(i * self.w, self.w)]

    def tensor(self, nc, pe):
        if not self.rms:
            with nc.tensor.Fori(0, self.n) as i:
                for k in range(KD):
                    mm = nc.tensor.matmul(bank(self.ps, i, P, self.w), self.avg[:], self.at(self.src, k, i),
                                          start=(k == 0), stop=(k == KD - 1))
                mm.then_inc(self.mean_ready, 1)
        with nc.tensor.Fori(0, self.n) as i:
            pe.wait_ge(self.squared, i + 1)
            for k in range(KD):
                mm = nc.tensor.matmul(bank(self.ps, i, P, self.w), self.avg[:], self.at(self.sq, k, i),
                                      start=(k == 0), stop=(k == KD - 1))
            mm.then_inc(self.var_ready, 1)

    def scalar(self, nc, act):
        with nc.scalar.Fori(0, self.n) as i:
            if not self.rms:
                act.wait_ge(self.centred, i + 1)
            nc.scalar.activation(self.all(self.sq, i), self.all(self.src if self.rms else self.out, i),
                                 ACT.Square).then_inc(self.squared, 1)
        with nc.scalar.Fori(0, self.n) as i:
            act.wait_ge(self.var_ready, i + 1)
            nc.scalar.activation(self.rstd[:, bass.ds(i * self.w, self.w)], bank(self.ps, i, P, self.w), ACT.Sqrt,
                                 bias=self.eps).then_inc(self.std_ready, 1)

    def vector(self, nc, dve):
        if not self.rms:
            with nc.vector.Fori(0, self.n) as i:
                dve.wait_ge(self.mean_ready, i + 1)
                nc.vector.tensor_tensor(self.all(self.out, i), self.all(self.src, i), bank2(self.ps, i, KD, self.w),
                                        ALU.subtract).then_inc(self.centred, 1)
        with nc.vector.Fori(0, self.n) as i:
            r = self.rstd[:, bass.ds(i * self.w, self.w)]
            dve.wait_ge(self.std_ready, i + 1)
            nc.vector.reciprocal(r, r).then_inc(self.rstd_ready, 1)
            dve.wait_ge(self.rstd_ready, i + 1)
            rb = r.rearrange("p (a n) -> p a n", a=1).to_broadcast([P, KD, self.w])
            last = nc.vector.tensor_tensor(self.all(self.out, i), self.all(self.src if self.rms else self.out, i),
                                           rb, ALU.mult)
            if self.gamma is not None:
                last.then_inc(self.scaled, 1)
                dve.wait_ge(self.scaled, i + 1)
                for k in range(KD):
                    o, f = self.at(self.out, k, i), self.final(k, i)
                    g = self.gamma[:, k:k + 1]
                    if self.beta is None:
                        last = nc.vector.tensor_scalar(f, o, g, None, ALU.mult)
                    else:
                        last = nc.vector.tensor_scalar(f, o, g, self.beta[:, k:k + 1], ALU.mult, ALU.add)
            last.then_inc(self.normed, 1)


class Shared:

    def __init__(self, nc, ctx, dram):
        sc = Scope(nc, ctx, "g")
        self.nc, self.dram = nc, dram
        self.h = sc.sb("h", [P, KD, NT])
        self.xn = sc.sb("xn", [P, KD, NT])
        self.avg = sc.sb("avg", [P, P])
        self.ident = sc.sb("ident", [P, P])
        self.eps5 = sc.sb("eps5", [P, 1])
        self.eps6 = sc.sb("eps6", [P, 1])


def load_constants(g):
    nc = g.nc
    with ExitStack() as ctx:
        sc = Scope(nc, ctx, "cst")
        landed = sc.sem("landed")
        block = ctx.enter_context(nc.Block())

        @block.sync
        def _(sp):
            sp.dma_start(g.ident[:], g.dram["c_ident"]).then_inc(landed, 16)
            sp.wait_ge(landed, 16)

        @block.vector
        def _(dve):
            nc.vector.memset(g.avg[:], 1.0 / D)
            nc.vector.memset(g.eps5[:], 1.0e-5)
            nc.vector.memset(g.eps6[:], 1.0e-6)


def first_of_max(nc, chain, scores, top, ranked, hot, rank, top_rank):
    full = [RN, RT, NE]
    chain.step(nc.vector.tensor_reduce(top[:], scores, AX_X, ALU.max))
    tb = top[:].rearrange("p (t a) -> p t a", a=1).to_broadcast(full)
    chain.step(nc.vector.tensor_tensor(ranked[:], scores, tb, ALU.is_ge))
    rb = rank[0:RN, :].rearrange("p (a e) -> p a e", a=1).to_broadcast(full)
    chain.step(nc.vector.tensor_tensor(ranked[:], ranked[:], rb, ALU.mult))
    chain.step(nc.vector.tensor_reduce(top_rank[:], ranked[:], AX_X, ALU.max))
    kb = top_rank[:].rearrange("p (t a) -> p t a", a=1).to_broadcast(full)
    chain.step(nc.vector.tensor_tensor(hot, ranked[:], kb, ALU.is_equal))


def per_token(t, n=NE):
    return t[:].rearrange("p (t a) -> p t a", a=1).to_broadcast([RN, RT, n])


def router(g, tag, w_name, b_name, n_out, kind, x_index=None):
    nc, dram = g.nc, g.dram
    n_gate = {"L0": NE + 1, "L1": NE, "L3": NE}[kind]
    with ExitStack() as ctx:
        sc = Scope(nc, ctx, tag)
        w = sc.sb("w", [P, KD, n_out])
        bias = sc.sb("bias", [P, n_out])
        ebias = sc.sb("ebias", [P, NE])
        rank = sc.sb("rank", [P, NE])
        lg = sc.sb("lg", [RN, RT, n_out])
        score = sc.sb("score", [RN, RT, NE])
        chosen = sc.sb("chosen", [RN, RT, NE])
        ranked = sc.sb("ranked", [RN, RT, NE])
        hot1 = sc.sb("hot1", [RN, RT, NE])
        hot2 = sc.sb("hot2", [RN, RT, NE])
        gate = sc.sb("gate", [RN, RT, n_gate])
        top1 = sc.sb("top1", [RN, RT])
        top2 = sc.sb("top2", [RN, RT])
        top_rank = sc.sb("top_rank", [RN, RT])
        ex = sc.sb("ex", [RN, RT])
        den = sc.sb("den", [RN, RT])
        gate_t = sc.sb("gate_t", [n_gate, NT])
        ps = sc.ps("ps", [P, 8, 512])
        sq = sc.sb("sq", [P, KD, NT])
        rstd = sc.sb("rstd", [P, NT])
        if kind == "L0":
            idx_i = sc.sb("idx_i", [RN, 2, 512], I32)
            idx = sc.sb("idx", [RN, 2, 512])
            neg = sc.sb("neg", [RN, 2, 512])
            flat = sc.sb("flat", [RN, 512])
            same = sc.sb("same", [RN, 512])
            tok = sc.sb("tok", [RN, RT])
            member = sc.sb("member", [RN, RT])
            shared_s = sc.sb("shared_s", [RN, RT])
        landed = sc.sem("landed")
        logits = sc.sem("logits")
        act_done = sc.sem("act_done")
        act_in = sc.sem("act_in")
        dve_own = sc.sem("dve_own")
        gates = sc.sem("gates")
        turned = sc.sem("turned")
        copied = sc.sem("copied")
        stored = sc.sem("stored")
        ln = LayerNorm(sc, "ln", g.h, g.xn, sq, rstd, g.avg, g.eps5[:], ps)
        n_loads = {"L0": 7, "L1": 3, "L3": 3}[kind]
        block = ctx.enter_context(nc.Block())
        tpb = 512 // RN
        n_banks = -(-RT // tpb)

        @block.sync
        def _(sp):
            sp.dma_start(w[:], dram[w_name]).then_inc(landed, 16)
            sp.dma_start(rank[:], dram["c_rank"]).then_inc(landed, 16)
            if kind == "L1":
                sp.dma_start(ebias[:], dram["L1_ffn_expert_bias"].to_broadcast([P, NE])).then_inc(landed, 16)
            else:
                sp.dma_start(bias[:], dram[b_name].to_broadcast([P, n_out])).then_inc(landed, 16)
            if kind == "L0":
                sp.dma_start(ebias[:], dram["L0_ffn_exp_bias"].to_broadcast([P, NE])).then_inc(landed, 16)
                sp.dma_start(tok[:], dram["c_tok"]).then_inc(landed, 16)
                for n, name in enumerate(("L0_ffn_index_b", "L0_ffn_index_t")):
                    sp.dma_start(idx_i[:, n, :], dram[name].to_broadcast([RN, 512])).then_inc(landed, 16)
            sp.wait_ge(copied, n_banks)
            sp.dma_start(dram["s_gate"][0:n_gate, :], gate_t[:]).then_inc(stored, 16)
            sp.wait_ge(stored, 16)

        @block.tensor
        def _(pe):
            ln.tensor(nc, pe)
            pe.wait_ge(landed, 16 * n_loads)
            pe.wait_ge(ln.normed, CH)
            pe.wait_ge(ln.std_ready, CH)
            for t in range(RT):
                for k in range(KD):
                    mm = nc.tensor.matmul(ps[0:RN, 7, t * n_out:(t + 1) * n_out],
                                          g.xn[:, k, t * RN:(t + 1) * RN], w[:, k, :],
                                          start=(k == 0), stop=(k == KD - 1))
            mm.then_inc(logits, 1)
            pe.wait_ge(gates, 1)
            for t in range(RT):
                mm = nc.tensor.transpose(ps[0:n_gate, t // tpb, t % tpb * RN:(t % tpb + 1) * RN],
                                         gate[:, t, :], g.ident[0:RN, 0:RN])
            mm.then_inc(turned, 1)

        @block.scalar
        def _(act):
            ln.scalar(nc, act)
            if kind == "L3":
                act.wait_ge(act_in, 1)
                nc.scalar.activation(ex[:], ex[:], ACT.Exp).then_inc(act_done, 1)
            if kind == "L1":
                act.wait_ge(act_in, 1)
                nc.scalar.activation(score[:], lg[:], ACT.Sigmoid).then_inc(act_done, 1)
            if kind == "L0":
                act.wait_ge(act_in, 1)
                nc.scalar.activation(lg[:], lg[:], ACT.Sigmoid).then_inc(act_done, 1)
                act.wait_ge(act_in, 2)
                nc.scalar.activation(ex[:], ex[:], ACT.Sigmoid).then_inc(act_done, 1)

        @block.vector
        def _(dve):
            ln.vector(nc, dve)
            chain = Chain(dve, dve_own)
            v = nc.vector
            dve.wait_ge(landed, 16 * n_loads)
            if kind == "L0":
                chain.step(v.tensor_copy(idx[:], idx_i[:]))
                for n, size in enumerate((NB, S)):
                    chain.step(v.tensor_scalar(neg[:, n, :], idx[:, n, :], 0.0, float(size), ALU.is_lt, ALU.mult))
                    chain.step(v.tensor_tensor(idx[:, n, :], idx[:, n, :], neg[:, n, :], ALU.add))
                    chain.step(v.tensor_scalar(neg[:, n, :], idx[:, n, :], float(size), BIG, ALU.is_ge, ALU.mult))
                    chain.step(v.scalar_tensor_tensor(neg[:, n, :], idx[:, n, :], 0.0, neg[:, n, :], ALU.is_lt, ALU.add))
                    chain.step(v.tensor_scalar(neg[:, n, :], neg[:, n, :], BIG, None, ALU.mult))
                chain.step(v.scalar_tensor_tensor(flat[:], idx[:, 0, :], float(S), idx[:, 1, :], ALU.mult, ALU.add))
                chain.step(v.tensor_scalar(neg[:], neg[:], BIG, None, ALU.min))
                for n in range(2):
                    chain.step(v.tensor_tensor(flat[:], flat[:], neg[:, n, :], ALU.add))
                for t in range(RT):
                    chain.step(v.tensor_scalar(same[:], flat[:], tok[:, t:t + 1], None, ALU.is_equal))
                    chain.step(v.tensor_reduce(member[:, t:t + 1], same[:], AX_X, ALU.max))
            dve.wait_ge(logits, 1)
            raw = ps[0:RN, 7, 0:RT * n_out].rearrange("p (t e) -> p t e", e=n_out)
            if kind == "L1":
                v.tensor_copy(lg[:], raw).then_inc(act_in, 1)
                dve.wait_ge(act_done, 1)
                eb = ebias[0:RN, :].rearrange("p (a e) -> p a e", a=1).to_broadcast([RN, RT, NE])
                chain.step(v.tensor_tensor(chosen[:], score[:], eb, ALU.add))
            else:
                bb = bias[0:RN, :].rearrange("p (a e) -> p a e", a=1).to_broadcast([RN, RT, n_out])
                add = v.tensor_tensor(lg[:], raw, bb, ALU.add)
                if kind == "L3":
                    chain.step(add)
                else:
                    add.then_inc(act_in, 1)
                    dve.wait_ge(act_done, 1)
                    eb = ebias[0:RN, :].rearrange("p (a e) -> p a e", a=1).to_broadcast([RN, RT, NE])
                    chain.step(v.tensor_tensor(chosen[:], lg[:, :, 0:NE], eb, ALU.add))
            first_of_max(nc, chain, lg[:] if kind == "L3" else chosen[:], top1, ranked, hot1[:], rank, top_rank)
            if kind == "L0":
                chain.step(v.tensor_tensor(ranked[:], hot1[:], lg[:, :, 0:NE], ALU.mult))
                chain.step(v.tensor_reduce(top1[:], ranked[:], AX_X, ALU.add))
                v.tensor_tensor(ex[:], top1[:], lg[:, :, NE:NE + 1].rearrange("p t a -> p (t a)"),
                                ALU.subtract).then_inc(act_in, 1)
                dve.wait_ge(act_done, 2)
                chain.step(v.tensor_tensor(den[:], ex[:], member[:], ALU.mult))
                chain.step(v.tensor_tensor(gate[:, :, 0:NE], hot1[:], per_token(den), ALU.mult))
                v.tensor_scalar(gate[:, :, NE:NE + 1].rearrange("p t a -> p (t a)"), den[:], -1.0, 1.0,
                                ALU.mult, ALU.add).then_inc(gates, 1)
            else:
                src = lg if kind == "L3" else chosen
                chain.step(v.scalar_tensor_tensor(chosen[:], hot1[:], -BIG, src[:], ALU.mult, ALU.add))
                first_of_max(nc, chain, chosen[:], top2, ranked, hot2[:], rank, top_rank)
            if kind == "L3":
                v.tensor_tensor(ex[:], top2[:], top1[:], ALU.subtract).then_inc(act_in, 1)
                dve.wait_ge(act_done, 1)
                chain.step(v.tensor_scalar(den[:], ex[:], 1.0, None, ALU.add))
                chain.step(v.reciprocal(den[:], den[:]))
                chain.step(v.tensor_tensor(hot2[:], hot2[:], per_token(ex), ALU.mult))
                chain.step(v.tensor_tensor(hot1[:], hot1[:], hot2[:], ALU.add))
                v.tensor_tensor(gate[:], hot1[:], per_token(den), ALU.mult).then_inc(gates, 1)
            if kind == "L1":
                chain.step(v.tensor_tensor(hot1[:], hot1[:], hot2[:], ALU.add))
                chain.step(v.tensor_tensor(hot1[:], hot1[:], score[:], ALU.mult))
                chain.step(v.tensor_reduce(den[:], hot1[:], AX_X, ALU.add))
                chain.step(v.tensor_scalar(den[:], den[:], 1.0e-20, None, ALU.add))
                chain.step(v.reciprocal(den[:], den[:]))
                v.tensor_tensor(gate[:], hot1[:], per_token(den), ALU.mult).then_inc(gates, 1)
            dve.wait_ge(turned, 1)
            for b in range(n_banks):
                n = min(tpb, RT - b * tpb) * RN
                v.tensor_copy(gate_t[:, b * tpb * RN:b * tpb * RN + n], ps[0:n_gate, b, 0:n]).then_inc(copied, 1)


def moe(g, tag, names, F, shared_expert):
    nc, dram = g.nc, g.dram
    NF = -(-F // P)
    FO = [F * f // NF for f in range(NF + 1)]
    FT = [FO[f + 1] - FO[f] for f in range(NF)]
    wg_d, wu_d, wd_d = (dram[n] for n in names[:3])
    with ExitStack() as ctx:
        sc = Scope(nc, ctx, tag)
        wg = [sc.sb(f"wg{b}", [P, KD, F]) for b in range(2)]
        wu = [sc.sb(f"wu{b}", [P, KD, F]) for b in range(2)]
        wd = [sc.sb(f"wd{b}", [P, NF, D]) for b in range(2)]
        gate = [sc.sb(f"gate{b}", [P, NT]) for b in range(2)]
        act_g = sc.sb("act_g", [P, 2, CN])
        hid = sc.sb("hid", [P, 2, CN])
        part = sc.sb("part", [P, KD, CN])
        ps_g = [sc.ps(f"ps_g{b}", [P, 512]) for b in range(2)]
        ps_u = [sc.ps(f"ps_u{b}", [P, 512]) for b in range(2)]
        ps_y = sc.ps("ps_y", [P, KD, 512])
        w_landed = [sc.sem(f"w_landed{b}") for b in range(2)]
        g_ready = sc.sem("g_ready")
        u_ready = sc.sem("u_ready")
        silu_done = sc.sem("silu_done")
        hid_ready = sc.sem("hid_ready")
        y_ready = sc.sem("y_ready")
        y_used = sc.sem("y_used")
        h_added = sc.sem("h_added")
        n_exp = NE + (1 if shared_expert else 0)
        n_loads = 16 * (3 + NF)
        block = ctx.enter_context(nc.Block())

        def experts(engine, first, middle):
            first((0, 0, 0, 0))

            def expert(e, b, visit, nxt):
                with engine.Fori(0, CH - 1) as c:
                    middle((e, b, visit, c), (e, b, visit, c + 1))
                middle((e, b, visit, CH - 1), nxt)

            pairs = NE // 2 - 1
            with engine.Fori(0, pairs) as p:
                expert(p * 2, 0, p, (p * 2 + 1, 1, p, 0))
                expert(p * 2 + 1, 1, p, (p * 2 + 2, 0, p + 1, 0))
            for e in range(2 * pairs, n_exp):
                nxt = (e + 1, (e + 1) % 2, (e + 1) // 2, 0) if e + 1 < n_exp else None
                expert(e, e % 2, e // 2, nxt)

        def unit(at, f):
            e, _, _, c = at
            return e * (CH * NF) + c * NF + f

        def turn(at):
            e, _, _, c = at
            return e * CH + c

        def load_expert(sp, b, gs, us, ds, row):
            sp.dma_start(wg[b][:], gs).then_inc(w_landed[b], 16)
            sp.dma_start(wu[b][:], us).then_inc(w_landed[b], 16)
            for f in range(NF):
                sp.dma_start(wd[b][0:FT[f], f, :], ds[FO[f]:FO[f] + FT[f], :]).then_inc(w_landed[b], 16)
            sp.dma_start(gate[b][:], row.to_broadcast([P, NT])).then_inc(w_landed[b], 16)

        def load_routed(sp, e, b):
            load_expert(sp, b, wg_d[bass.ds(e, 1)].rearrange("a p k f -> (a p) k f"),
                        wu_d[bass.ds(e, 1)].rearrange("a p k f -> (a p) k f"),
                        wd_d[bass.ds(e, 1)].rearrange("a f d -> (a f) d"),
                        dram["s_gate"][bass.ds(e, 1), :])

        @block.sync
        def _(sp):
            for b in range(2):
                load_routed(sp, b, b)
            with nc.sync.Fori(0, NE // 2 - 1) as p:
                for b in range(2):
                    e = nc.sync.snap(p * 2 + (b + 2))
                    sp.wait_ge(y_used, p * (2 * CH) + ((b + 1) * CH + 1))
                    load_routed(sp, e, b)
            if shared_expert:
                sp.wait_ge(y_used, (NE - 1) * CH + 1)
                load_expert(sp, 0, dram[names[3]], dram[names[4]], dram[names[5]], dram["c_one_row"])

        @block.tensor
        def _(pe):
            def up(at, f, fill):
                _, b, visit, c = at
                if fill and f == 0:
                    pe.wait_ge(w_landed[b], (visit + 1) * n_loads)
                if not (isinstance(unit(at, f), int) and unit(at, f) == 0):
                    pe.wait_ge(hid_ready, unit(at, f))
                for ps, w, ready in ((ps_g, wg, g_ready), (ps_u, wu, u_ready)):
                    for k in range(KD):
                        mm = nc.tensor.matmul(ps[f % 2][0:FT[f], 0:CN], w[b][:, k, FO[f]:FO[f] + FT[f]],
                                              chunk(g.xn, k, c), start=(k == 0), stop=(k == KD - 1))
                    mm.then_inc(ready, 1)

            def down(at, f):
                b = at[1]
                if f == 0:
                    pe.wait_ge(y_used, turn(at) + 1)
                pe.wait_ge(hid_ready, unit(at, f) + 2)
                for m in range(KD):
                    mm = nc.tensor.matmul(ps_y[:, m, 0:CN], wd[b][0:FT[f], f, m * P:(m + 1) * P],
                                          hid[0:FT[f], f % 2, :], start=(f == 0), stop=(f == NF - 1))
                if f == NF - 1:
                    mm.then_inc(y_ready, 1)

            def middle(at, after):
                for f in range(NF):
                    if f + 1 < NF:
                        up(at, f + 1, False)
                    elif after is not None:
                        up(after, 0, after[1] != at[1])
                    down(at, f)

            experts(nc.tensor, lambda at: up(at, 0, True), middle)

        @block.scalar
        def _(act):
            def silu(at, f):
                act.wait_ge(g_ready, unit(at, f) + 1)
                nc.scalar.activation(act_g[0:FT[f], f % 2, :], ps_g[f % 2][0:FT[f], 0:CN],
                                     ACT.Silu).then_inc(silu_done, 1)

            def middle(at, after):
                for f in range(1, NF):
                    silu(at, f)
                if after is not None:
                    silu(after, 0)

            experts(nc.scalar, lambda at: silu(at, 0), middle)

        @block.vector
        def _(dve):
            nc.vector.memset(part[:, 0, 0:1], 0.0).then_inc(hid_ready, 1)
            nc.vector.memset(part[:, 0, 1:2], 0.0).then_inc(y_used, 1)
            nc.vector.memset(part[:, 0, 2:3], 0.0).then_inc(h_added, 1)

            def hidden(at, f):
                dve.wait_ge(silu_done, unit(at, f) + 1)
                dve.wait_ge(u_ready, unit(at, f) + 1)
                nc.vector.tensor_tensor(hid[0:FT[f], f % 2, :], act_g[0:FT[f], f % 2, :],
                                        ps_u[f % 2][0:FT[f], 0:CN], ALU.mult).then_inc(hid_ready, 1)

            def output(at, fill):
                _, b, visit, c = at
                if fill:
                    dve.wait_ge(w_landed[b], (visit + 1) * n_loads)
                dve.wait_ge(y_ready, turn(at) + 1)
                gb = gate[b][:, bass.ds(c * CN, CN)].rearrange("p (a n) -> p a n", a=1).to_broadcast([P, KD, CN])
                nc.vector.tensor_tensor(part[:], ps_y[:, :, 0:CN], gb, ALU.mult).then_inc(y_used, 1)
                dve.wait_ge(y_used, turn(at) + 2)
                dve.wait_ge(h_added, turn(at) + 1)
                nc.vector.tensor_tensor(both(g.h, c), both(g.h, c), part[:], ALU.add).then_inc(h_added, 1)

            def middle(at, after):
                for f in range(1, NF):
                    hidden(at, f)
                if after is not None:
                    hidden(after, 0)
                output(at, True)

            experts(nc.vector, lambda at: hidden(at, 0), middle)


def biased_experts(g):
    nc, dram = g.nc, g.dram
    H = P
    N = NE + 1
    with ExitStack() as ctx:
        sc = Scope(nc, ctx, "f0")
        w1 = [sc.sb(f"w1{b}", [P, KD, H]) for b in range(2)]
        w2 = [sc.sb(f"w2{b}", [P, KD, H]) for b in range(2)]
        w3 = [sc.sb(f"w3{b}", [P, D]) for b in range(2)]
        vec = [sc.sb(f"vec{b}", [P, 6]) for b in range(2)]
        gate = [sc.sb(f"gate{b}", [P, NT]) for b in range(2)]
        hid = [sc.sb(f"hid{b}", [P, NT]) for b in range(2)]
        avg_h = sc.sb("avg_h", [P, P])
        act_a = sc.sb("act_a", [P, 2, CN])
        sq = sc.sb("sq", [P, NT])
        rstd = sc.sb("rstd", [P, NT])
        z = sc.sb("z", [P, NT])
        part = sc.sb("part", [P, KD, CN])
        ps_a = [sc.ps(f"ps_a{j}", [P, 512]) for j in range(2)]
        ps_b = [sc.ps(f"ps_b{j}", [P, 512]) for j in range(2)]
        ps_m = [sc.ps(f"ps_m{j}", [P, 512]) for j in range(2)]
        ps_y = sc.ps("ps_y", [P, KD, 512])
        w_landed = [sc.sem(f"w_landed{b}") for b in range(2)]
        avg_set = sc.sem("avg_set")
        a_ready = sc.sem("a_ready")
        b_ready = sc.sem("b_ready")
        silu_done = sc.sem("silu_done")
        s_ready = sc.sem("s_ready")
        mean_ready = sc.sem("mean_ready")
        centred = sc.sem("centred")
        squared = sc.sem("squared")
        var_ready = sc.sem("var_ready")
        eps_added = sc.sem("eps_added")
        recip_done = sc.sem("recip_done")
        rstd_ready = sc.sem("rstd_ready")
        z_scaled = sc.sem("z_scaled")
        z_ready = sc.sem("z_ready")
        y_ready = sc.sem("y_ready")
        y_used = sc.sem("y_used")
        h_added = sc.sem("h_added")
        n_loads = 16 * 5
        block = ctx.enter_context(nc.Block())

        def schedule(engine, up, out, var):
            up(0, 0, 0)
            var(0, 0, 0)
            with engine.Fori(0, (N - 1) // 2) as p:
                up(p * 2 + 1, 1, p)
                out(p * 2, 0, p)
                var(p * 2 + 1, 1, p)
                up(p * 2 + 2, 0, p + 1)
                out(p * 2 + 1, 1, p)
                var(p * 2 + 2, 0, p + 1)
            out(N - 1, (N - 1) % 2, (N - 1) // 2)

        def load(sp, e, b):
            for t, name in ((w1, "f0_w1"), (w2, "f0_w2")):
                sp.dma_start(t[b][:], dram[name][bass.ds(e, 1)].rearrange("a p k f -> (a p) k f")
                             ).then_inc(w_landed[b], 16)
            for t, name in ((w3, "f0_w3"), (vec, "f0_vec")):
                sp.dma_start(t[b][:], dram[name][bass.ds(e, 1)].rearrange("a p f -> (a p) f")
                             ).then_inc(w_landed[b], 16)
            sp.dma_start(gate[b][:], dram["s_gate"][bass.ds(e, 1), :].to_broadcast([P, NT])
                         ).then_inc(w_landed[b], 16)

        @block.sync
        def _(sp):
            load(sp, 0, 0)
            load(sp, 1, 1)
            with nc.sync.Fori(0, (N - 3) // 2) as p:
                for b in range(2):
                    e = nc.sync.snap(p * 2 + (b + 2))
                    sp.wait_ge(y_used, p * (2 * CH) + ((b + 1) * CH + 1))
                    load(sp, e, b)
            sp.wait_ge(y_used, (N - 2) * CH + 1)
            load(sp, N - 1, (N - 1) % 2)

        @block.tensor
        def _(pe):
            pe.wait_ge(avg_set, 1)

            def up(e, b, visit):
                with nc.tensor.Fori(0, CH // 2) as cc:
                    pe.wait_ge(w_landed[b], (visit + 1) * n_loads)
                    for j in range(2):
                        pe.wait_ge(s_ready, e * CH + cc * 2 + (j + 1))
                        for ps, w, ready in ((ps_a, w1, a_ready), (ps_b, w2, b_ready)):
                            for k in range(KD):
                                mm = nc.tensor.matmul(ps[j][:, 0:CN], w[b][:, k, :], chunk(g.xn, k, cc * 2 + j),
                                                      start=(k == 0), stop=(k == KD - 1))
                            mm.then_inc(ready, 1)
                    for j in range(2):
                        pe.wait_ge(s_ready, e * CH + cc * 2 + (j + 3))
                        nc.tensor.matmul(ps_m[j][:, 0:CN], avg_h[:], hid[b][:, bass.ds((cc * 2 + j) * CN, CN)],
                                         start=True, stop=True).then_inc(mean_ready, 1)

            def out(e, b, visit):
                with nc.tensor.Fori(0, CH) as c:
                    pe.wait_ge(z_ready, e + 1)
                    pe.wait_ge(y_used, e * CH + c + 1)
                    for m in range(KD):
                        mm = nc.tensor.matmul(ps_y[:, m, 0:CN], w3[b][:, m * P:(m + 1) * P],
                                              z[:, bass.ds(c * CN, CN)], start=True, stop=True)
                    mm.then_inc(y_ready, 1)

            def var(e, b, visit):
                with nc.tensor.Fori(0, CH // 2) as cc:
                    pe.wait_ge(squared, (e + 1) * CH)
                    for j in range(2):
                        pe.wait_ge(eps_added, e * CH + cc * 2 + (j + 1))
                        nc.tensor.matmul(ps_m[j][:, 0:CN], avg_h[:], sq[:, bass.ds((cc * 2 + j) * CN, CN)],
                                         start=True, stop=True).then_inc(var_ready, 1)

            schedule(nc.tensor, up, out, var)

        @block.scalar
        def _(act):
            def up(e, b, visit):
                with nc.scalar.Fori(0, CH // 2) as cc:
                    act.wait_ge(w_landed[b], (visit + 1) * n_loads)
                    for j in range(2):
                        act.wait_ge(a_ready, e * CH + cc * 2 + (j + 1))
                        nc.scalar.activation(act_a[:, j, :], ps_a[j][:, 0:CN], ACT.Silu,
                                             bias=vec[b][:, 0:1]).then_inc(silu_done, 1)
                    for j in range(2):
                        act.wait_ge(centred, e * CH + cc * 2 + (j + 1))
                        at = bass.ds((cc * 2 + j) * CN, CN)
                        nc.scalar.activation(sq[:, at], hid[b][:, at], ACT.Square).then_inc(squared, 1)

            def var(e, b, visit):
                act.wait_ge(recip_done, e + 1)
                nc.scalar.activation(rstd[:], rstd[:], ACT.Sqrt).then_inc(rstd_ready, 1)

            def out(e, b, visit):
                act.wait_ge(z_scaled, e + 1)
                nc.scalar.activation(z[:], z[:], ACT.Identity, scale=vec[b][:, 2:3],
                                     bias=vec[b][:, 3:4]).then_inc(z_ready, 1)

            schedule(nc.scalar, up, out, var)

        @block.gpsimd
        def _(pool):
            def var(e, b, visit):
                pool.wait_ge(w_landed[b], (visit + 1) * n_loads)
                pool.wait_ge(rstd_ready, e + 1)
                nc.gpsimd.tensor_tensor(z[:], hid[b][:], rstd[:], ALU.mult).then_inc(z_scaled, 1)

            schedule(nc.gpsimd, lambda *a: None, lambda *a: None, var)

        @block.vector
        def _(dve):
            nc.vector.memset(part[:, 0, 0:1], 0.0).then_inc(s_ready, 2)
            nc.vector.memset(part[:, 0, 1:2], 0.0).then_inc(eps_added, 2)
            nc.vector.memset(part[:, 0, 2:3], 0.0).then_inc(y_used, 1)
            nc.vector.memset(part[:, 0, 3:4], 0.0).then_inc(h_added, 1)
            nc.vector.memset(avg_h[:], 1.0 / H).then_inc(avg_set, 1)

            def up(e, b, visit):
                with nc.vector.Fori(0, CH // 2) as cc:
                    dve.wait_ge(w_landed[b], (visit + 1) * n_loads)
                    for j in range(2):
                        dve.wait_ge(silu_done, e * CH + cc * 2 + (j + 1))
                        dve.wait_ge(b_ready, e * CH + cc * 2 + (j + 1))
                        nc.vector.scalar_tensor_tensor(hid[b][:, bass.ds((cc * 2 + j) * CN, CN)],
                                                       ps_b[j][:, 0:CN], vec[b][:, 1:2], act_a[:, j, :],
                                                       ALU.add, ALU.mult).then_inc(s_ready, 1)
                    for j in range(2):
                        dve.wait_ge(mean_ready, e * CH + cc * 2 + (j + 1))
                        at = hid[b][:, bass.ds((cc * 2 + j) * CN, CN)]
                        nc.vector.tensor_tensor(at, at, ps_m[j][:, 0:CN], ALU.subtract).then_inc(centred, 1)

            def out(e, b, visit):
                with nc.vector.Fori(0, CH) as c:
                    dve.wait_ge(y_ready, e * CH + c + 1)
                    dve.wait_ge(h_added, e * CH + c + 1)
                    for m in range(KD):
                        last = nc.vector.scalar_tensor_tensor(part[:, m, :], ps_y[:, m, 0:CN], vec[b][:, 4 + m:5 + m],
                                                              gate[b][:, bass.ds(c * CN, CN)], ALU.add, ALU.mult)
                    last.then_inc(y_used, 1)
                    dve.wait_ge(y_used, e * CH + c + 2)
                    nc.vector.tensor_tensor(both(g.h, c), both(g.h, c), part[:], ALU.add).then_inc(h_added, 1)

            def var(e, b, visit):
                with nc.vector.Fori(0, CH // 2) as cc:
                    for j in range(2):
                        dve.wait_ge(var_ready, e * CH + cc * 2 + (j + 1))
                        nc.vector.tensor_scalar(rstd[:, bass.ds((cc * 2 + j) * CN, CN)], ps_m[j][:, 0:CN],
                                                1.0e-5, None, ALU.add).then_inc(eps_added, 1)
                dve.wait_ge(eps_added, e * CH + (CH + 2))
                nc.vector.reciprocal(rstd[:], rstd[:]).then_inc(recip_done, 1)

            schedule(nc.vector, up, out, var)


def layer_norm(g, tag, src, out, gamma=None, beta=None, rms=False, loads=(), add_to=None,
               chunks=CH, width=CN, final=None):
    nc = g.nc
    with ExitStack() as ctx:
        sc = Scope(nc, ctx, tag)
        sq = sc.sb("sq", [P, KD, chunks * width])
        rstd = sc.sb("rstd", [P, chunks * width])
        ps = sc.ps("ps", [P, 8, 512])
        landed = sc.sem("landed")
        added = sc.sem("added")
        ln = LayerNorm(sc, "ln", src, out, sq, rstd, g.avg, (g.eps6 if rms else g.eps5)[:], ps, gamma, beta, rms,
                       chunks, width, final)
        block = ctx.enter_context(nc.Block())

        @block.sync
        def _(sp):
            for dst, s in loads:
                sp.dma_start(dst, s).then_inc(landed, 16)
            if loads:
                sp.wait_ge(landed, 16 * len(loads))

        @block.tensor
        def _(pe):
            ln.tensor(nc, pe)

        @block.scalar
        def _(act):
            ln.scalar(nc, act)

        @block.vector
        def _(dve):
            if loads and gamma is not None:
                dve.wait_ge(landed, 16 * len(loads))
            ln.vector(nc, dve)
            if add_to is not None:
                with nc.vector.Fori(0, CH) as i:
                    dve.wait_ge(ln.normed, i + 1)
                    nc.vector.tensor_tensor(both(add_to, i), both(add_to, i), both(out, i), ALU.add).then_inc(added, 1)


def gated_scan(g):
    nc, dram = g.nc, g.dram
    I = 512
    KI = I // P
    with ExitStack() as ctx:
        sc = Scope(nc, ctx, "s1")
        w_in = sc.sb("w_in", [P, KD, 2 * I])
        wo = sc.sb("wo", [P, KI, D])
        vec = sc.sb("vec", [P, 28])
        b_in, conv_b = vec[:, 0:8], vec[:, 8:12]
        b_abc = [vec[:, 12 + 4 * n:16 + 4 * n] for n in range(3)]
        bo, norm_g, norm_b = (sc.sb(n, [P, KD]) for n in ("bo", "norm_g", "norm_b"))
        conv_w = sc.sb("conv_w", [P, KI, 3])
        u = sc.sb("u", [P, KI, NT])
        with ExitStack() as mid:
            scm = Scope(nc, mid, "s1m")
            xg = scm.sb("xg", [P, KD, NT])
            layer_norm(g, "s1n", g.h, g.xn, loads=(
                (w_in[:], dram["L1_attn_W_in"]), (wo[:], dram["L1_attn_Wo"]), (vec[:, 0:24], dram["s1_vec"]),
                (bo[:], dram["L1_attn_bo"]), (norm_g[:], dram["L1_attn_gamma"]),
                (norm_b[:], dram["L1_attn_beta"]), (conv_w[:], dram["L1_attn_conv_w"])))
            layer_norm(g, "s1o", g.xn, xg, norm_g, norm_b)
            gated_scan_in(g, xg, w_in, b_in, conv_w, conv_b, u, KI)
        gated_scan_out(g, u, b_abc, wo, bo, KI)


def gated_scan_in(g, xg, w_in, b_in, conv_w, conv_b, u, KI):
    nc = g.nc
    with ExitStack() as ctx:
        sc = Scope(nc, ctx, "sa")
        proj = sc.sb("proj", [P, 2, NT])
        sig = sc.sb("sig", [P, 2, NT])
        ps_p = [sc.ps(f"ps_p{j}", [P, 512]) for j in range(2)]
        ps_g = [sc.ps(f"ps_g{j}", [P, 512]) for j in range(2)]
        p_ready = sc.sem("p_ready")
        g_ready = sc.sem("g_ready")
        moved = sc.sem("moved")
        own = sc.sem("own")
        conv_done = sc.sem("conv_done")
        silu_done = sc.sem("silu_done")
        u_done = sc.sem("u_done")
        block = ctx.enter_context(nc.Block())

        def by_batch(t):
            return t.rearrange("p (b s) -> p b s", s=S)

        @block.tensor
        def _(pe):
            for m in range(KI):
                with nc.tensor.Fori(0, CH // 2) as cc:
                    for j in range(2):
                        pe.wait_ge(moved, cc * 2 + (m * CH + j + 1))
                        for ps, col, ready in ((ps_p, m * P, p_ready), (ps_g, (KI + m) * P, g_ready)):
                            for k in range(KD):
                                mm = nc.tensor.matmul(ps[j][:, 0:CN], w_in[:, k, col:col + P],
                                                      chunk(xg, k, cc * 2 + j), start=(k == 0), stop=(k == KD - 1))
                            mm.then_inc(ready, 1)

        @block.scalar
        def _(act):
            def silu(m):
                act.wait_ge(conv_done, m + 1)
                nc.scalar.activation(u[:, m, :], u[:, m, :], ACT.Silu).then_inc(silu_done, 1)

            for m in range(KI):
                if m >= 2:
                    act.wait_ge(u_done, m - 1)
                with nc.scalar.Fori(0, CH // 2) as cc:
                    for j in range(2):
                        n = cc * 2 + (m * CH + j + 1)
                        at = bass.ds((cc * 2 + j) * CN, CN)
                        act.wait_ge(p_ready, n)
                        nc.scalar.activation(proj[:, m % 2, at], ps_p[j][:, 0:CN], ACT.Identity,
                                             bias=b_in[:, m:m + 1])
                        act.wait_ge(g_ready, n)
                        nc.scalar.activation(sig[:, m % 2, at], ps_g[j][:, 0:CN], ACT.Sigmoid,
                                             bias=b_in[:, KI + m:KI + m + 1]).then_inc(moved, 1)
                if m >= 1:
                    silu(m - 1)
            silu(KI - 1)

        @block.vector
        def _(dve):
            chain = Chain(dve, own)
            v = nc.vector
            v.memset(u[:, 0, 0:1], 0.0).then_inc(moved, 2)

            def product(m):
                dve.wait_ge(silu_done, m + 1)
                v.tensor_tensor(u[:, m, :], u[:, m, :], sig[:, m % 2, :], ALU.mult).then_inc(u_done, 1)

            for m in range(KI):
                dve.wait_ge(moved, (m + 1) * CH + 2)
                chain.step(v.tensor_scalar(u[:, m, :], proj[:, m % 2, :], conv_w[:, m, 2:3], conv_b[:, m:m + 1],
                                           ALU.mult, ALU.add))
                o, q = by_batch(u[:, m, :]), by_batch(proj[:, m % 2, :])
                for back in (1, 2):
                    ins = v.scalar_tensor_tensor(o[:, :, back:S], q[:, :, 0:S - back],
                                                 conv_w[:, m, 2 - back:3 - back], o[:, :, back:S],
                                                 ALU.mult, ALU.add)
                    if back == 1:
                        chain.step(ins)
                    else:
                        ins.then_inc(conv_done, 1)
                if m >= 1:
                    product(m - 1)
            product(KI - 1)


def gated_scan_out(g, u, b_abc, wo, bo, KI):
    nc, dram = g.nc, g.dram
    with ExitStack() as ctx:
        sc = Scope(nc, ctx, "sb")
        w = [sc.sb(f"w{n}", [P, KI, P]) for n in "abc"]
        w2 = [sc.sb(f"w2{n}", [P, KI, P]) for n in "abc"]
        a, b, c = (sc.sb(n, [P, NT]) for n in "abc")
        y = sc.sb("y", [P, KI, NT])
        part = sc.sb("part", [P, 2, KD, CN])
        ps = [[sc.ps(f"ps{n}{j}", [P, 512]) for j in range(2)] for n in "abc"]
        ps_o = sc.ps("ps_o", [P, KD, 512])
        w_landed = [sc.sem(f"w_landed{n}") for n in range(2)]
        abc_ready = sc.sem("abc_ready")
        moved = sc.sem("moved")
        own = sc.sem("own")
        y_done = sc.sem("y_done")
        o_ready = sc.sem("o_ready")
        o_used = sc.sem("o_used")
        h_added = sc.sem("h_added")
        block = ctx.enter_context(nc.Block())
        bufs = (w, w2)

        @block.sync
        def _(sp):
            for m in range(KI):
                if m >= 2:
                    sp.wait_ge(abc_ready, (m - 1) * CH)
                for n, name in enumerate(("L1_attn_Wa", "L1_attn_Wb", "L1_attn_Wc")):
                    sp.dma_start(bufs[m % 2][n][:], dram[name][:, :, m * P:(m + 1) * P]).then_inc(w_landed[m % 2], 16)

        @block.tensor
        def _(pe):
            for m in range(KI):
                pe.wait_ge(w_landed[m % 2], 48 * (m // 2 + 1))
                with nc.tensor.Fori(0, CH // 2) as cc:
                    for j in range(2):
                        pe.wait_ge(moved, cc * 2 + (m * CH + j + 1))
                        for n in range(3):
                            for k in range(KI):
                                mm = nc.tensor.matmul(ps[n][j][:, 0:CN], bufs[m % 2][n][:, k, :],
                                                      chunk(u, k, cc * 2 + j), start=(k == 0), stop=(k == KI - 1))
                        mm.then_inc(abc_ready, 1)
            pe.wait_ge(y_done, KI)
            with nc.tensor.Fori(0, CH) as i:
                pe.wait_ge(o_used, i + 1)
                for m in range(KD):
                    for k in range(KI):
                        mm = nc.tensor.matmul(ps_o[:, m, 0:CN], wo[:, k, m * P:(m + 1) * P], chunk(y, k, i),
                                              start=(k == 0), stop=(k == KI - 1))
                mm.then_inc(o_ready, 1)

        @block.scalar
        def _(act):
            for m in range(KI):
                if m >= 1:
                    act.wait_ge(y_done, m)
                with nc.scalar.Fori(0, CH // 2) as cc:
                    for j in range(2):
                        act.wait_ge(abc_ready, cc * 2 + (m * CH + j + 1))
                        for n, (dst, f) in enumerate(((a, ACT.Sigmoid), (b, ACT.Sigmoid), (c, ACT.Tanh))):
                            last = nc.scalar.activation(dst[:, bass.ds((cc * 2 + j) * CN, CN)], ps[n][j][:, 0:CN],
                                                        f, bias=b_abc[n][:, m:m + 1])
                        last.then_inc(moved, 1)

        @block.vector
        def _(dve):
            chain = Chain(dve, own)
            v = nc.vector
            v.memset(part[:, 0, 0, 0:1], 0.0).then_inc(moved, 2)
            v.memset(part[:, 0, 0, 1:2], 0.0).then_inc(o_used, 1)
            v.memset(part[:, 0, 0, 2:3], 0.0).then_inc(h_added, 1)
            for m in range(KI):
                dve.wait_ge(moved, (m + 1) * CH + 2)
                chain.step(v.tensor_tensor(b[:], b[:], u[:, m, :], ALU.mult))
                for s in range(NB):
                    at = slice(s * S, (s + 1) * S)
                    ins = v.tensor_tensor_scan(y[:, m, at], a[:, at], b[:, at], 0.0, ALU.mult, ALU.add)
                chain.step(ins)
                chain.step(v.tensor_tensor(y[:, m, :], y[:, m, :], c[:], ALU.mult))
                v.tensor_tensor(y[:, m, :], y[:, m, :], u[:, m, :], ALU.add).then_inc(y_done, 1)
            with nc.vector.Fori(0, CH) as i:
                dve.wait_ge(o_ready, i + 1)
                dve.wait_ge(h_added, i + 1)
                for m in range(KD):
                    last = v.scalar_tensor_tensor(part[:, 0, m, :], ps_o[:, m, 0:CN], bo[:, m:m + 1],
                                                  chunk(g.xn, m, i), ALU.add, ALU.add)
                last.then_inc(o_used, 1)
                dve.wait_ge(o_used, i + 2)
                v.tensor_tensor(both(g.h, i), both(g.h, i), part[:, 0], ALU.add).then_inc(h_added, 1)


def three_matrices(g):
    nc, dram = g.nc, g.dram
    with ExitStack() as ctx:
        sc = Scope(nc, ctx, "t2")
        w = sc.sb("w", [P, 3, KD, D])
        bias = sc.sb("bias", [P, KD])
        layer_norm(g, "t2n", g.h, g.xn, loads=[(w[:, n], dram[name]) for n, name in enumerate(
            ("L2_ffn_weight", "L2_ffn_aux_weight1", "L2_ffn_aux_weight2"))] + [(bias[:], dram["L2_ffn_bias"])])
        x1 = sc.sb("x1", [P, KD, NT])
        x2 = sc.sb("x2", [P, KD, NT])
        x3 = sc.sb("x3", [P, KD, NT])
        ps = [sc.ps(f"ps{j}", [P, KD, 512]) for j in range(2)]
        ready = sc.sem("ready")
        moved = sc.sem("moved")
        added = sc.sem("added")
        block = ctx.enter_context(nc.Block())
        src, dst = (g.xn, x1, x2), (x1, x2, x3)

        @block.tensor
        def _(pe):
            for n in range(3):
                with nc.tensor.Fori(0, CH // 2) as cc:
                    for j in range(2):
                        pe.wait_ge(moved, cc * 2 + (n * CH + j + 1))
                        for m in range(KD):
                            for k in range(KD):
                                mm = nc.tensor.matmul(ps[j][:, m, 0:CN], w[:, n, k, m * P:(m + 1) * P],
                                                      chunk(src[n], k, cc * 2 + j),
                                                      start=(k == 0), stop=(k == KD - 1))
                        mm.then_inc(ready, 1)

        @block.scalar
        def _(act):
            nc.scalar.copy(x3[:, 0, 0:1], g.ident[:, 0:1]).then_inc(moved, 2)
            for n in range(3):
                with nc.scalar.Fori(0, CH // 2) as cc:
                    for j in range(2):
                        act.wait_ge(ready, cc * 2 + (n * CH + j + 1))
                        if n < 2:
                            last = nc.scalar.copy(both(dst[n], cc * 2 + j), ps[j][:, :, 0:CN])
                        else:
                            for m in range(KD):
                                last = nc.scalar.activation(chunk(x3, m, cc * 2 + j), ps[j][:, m, 0:CN], ACT.Tanh,
                                                            bias=bias[:, m:m + 1])
                        last.then_inc(moved, 1)

        @block.vector
        def _(dve):
            with nc.vector.Fori(0, CH) as i:
                dve.wait_ge(moved, i + (2 * CH + 3))
                nc.vector.tensor_tensor(both(g.h, i), both(g.h, i), both(x3, i), ALU.add).then_inc(added, 1)


class Unit:

    def __init__(self, kind, g, tile, pair, lo, hi):
        self.kind, self.g, self.tile, self.pair, self.lo, self.hi = kind, g, tile, pair, lo, hi
        self.last = False


def attention(g, tag, src, length, heads, dh, scale, causal, k_heads, names, res, dst):
    nc, dram = g.nc, g.dram
    stripe = 2 * dh
    per = P // stripe
    pairs = per // 2
    G = heads // per
    in_tile = P // dh
    RQ, RK = heads * dh // P, max(1, k_heads * dh // P)
    tiles = [(s, min(P, length - s)) for s in range(0, length, P)]
    NTL = len(tiles)
    width = NTL * P
    even = length + length % 2
    regions = [(0, length)] if length <= 512 else [(0, 3 * P), (3 * P, length)]
    one_bank = len(regions) == 1
    shared_k = k_heads == 1
    v_cols = stripe if shared_k else heads * stripe
    b_heads = 2 if one_bank else 1
    wq_d, wk_d, wv_d, wo_d, bq_d, bk_d, bv_d, bo_d = (dram[n] for n in names)
    ROW = 96

    def cuts(lo, hi):
        return [(n, max(lo, a), min(hi, b)) for n, (a, b) in enumerate(regions) if max(lo, a) < min(hi, b)]

    def spans(lo, hi):
        return [(lo, hi)] if hi - lo <= 512 else [(a, b) for _, a, b in cuts(lo, hi)]

    def up_even(n):
        return even if n == length else n

    def maxima(gr):
        out = []
        for t, (start, rows) in enumerate(tiles):
            for pr in range(pairs):
                out += [Unit("M", gr, t, pr, lo, hi) for lo, hi in spans(0, start + rows if causal else length)]
        out[-1].last = True
        return out

    def probs(gr):
        out = []
        for t, (start, rows) in enumerate(tiles):
            for lo, hi in spans(start if causal else 0, length):
                out += [Unit("P", gr, t, pr, lo, hi) for pr in range(pairs)]
        out[-1].last = True
        return out

    def both_of(gr):
        ps, ms = probs(gr), maxima(gr + 1)
        assert len(ps) == len(ms)
        return [u for pair in zip(ps, ms) for u in pair]

    def stacks(gr):
        kinds = "B" if shared_k else "BC"
        return [Unit(k, gr, 0, h // b_heads, 0, length) for h in range(0, per, b_heads) for k in kinds]

    def turned(gr):
        return ["T%d%d" % (gr, n) for n in range(per // b_heads)]

    order = [[Unit("Q", 0, t, 0, 0, length) for t in range(RQ)] + [Unit("K", 0, t, 0, 0, length) for t in range(RK)]
             + [Unit("V", 0, t, 0, 0, v_cols) for t in range(NTL)]
             + ([Unit("C", 0, 0, 0, 0, length)] if shared_k else []) + stacks(0), maxima(0), stacks(1), *turned(0),
             both_of(0)]
    for gr in range(2, G):
        order += [stacks(gr), "S%d" % (gr - 2), *turned(gr - 1), both_of(gr - 1)]
    order += ["S%d" % (G - 2), *turned(G - 1), probs(G - 1), "S%d" % (G - 1), "O0", "O1"]
    units = [u for item in order if not isinstance(item, str) for u in item]
    for n, u in enumerate(units):
        u.n = n
        u.by_act = u.kind in "QKBCP"
        u.taken = sum(1 for w in units[:n + 1] if (w.kind in "QKBCP") == u.by_act)
    n_act = sum(u.by_act for u in units)
    nu, n_dve = len(units), len(units) - sum(u.by_act for u in units)
    for n, u in enumerate(u for u in units if u.kind == "P"):
        u.pn = n
    assert sum(u.kind == "P" for u in units) % 2 == 0
    first_b = next(u for u in units if u.kind in "BC")
    first_m = next(u for u in units if u.kind == "M")
    assert not any(u.kind == "V" for u in units[-2:]) and all(u.by_act for u in units[-2:])
    turns = [item for item in order if isinstance(item, str)]
    n_ps_t = len(turns)

    with ExitStack() as ctx:
        sc = Scope(nc, ctx, tag)
        wq = sc.sb("wq", [P, KD, RQ * P])
        wk = sc.sb("wk", [P, KD, RK * P])
        wv = sc.sb("wv", [P, KD, v_cols])
        wo = sc.sb("wo", [P, G, D])
        bq, bk, bo = sc.sb("bq", [P, RQ]), sc.sb("bk", [P, RK]), sc.sb("bo", [P, KD])
        bv = sc.sb("bv", [P, v_cols])
        ones_row = sc.sb("ones_row", [P, 1])
        swap = sc.sb("swap", [P, P])
        loads = [(wq, wq_d), (wk, wk_d), (wv, wv_d), (wo, wo_d), (bq, bq_d), (bk, bk_d), (bo, bo_d),
                 (ones_row, dram["c_ones_row"]), (swap, dram["c_swap%d" % stripe])]
        loads = [(a[:], b) for a, b in loads] + [(bv[:], bv_d.to_broadcast([P, v_cols]))]
        sel = sc.sb("sel", [P, 4, in_tile, P], F32R)
        ident_r = sc.sb("ident_r", [P, P], F32R)
        loads_r = [(sel, "c_sel%d" % dh), (ident_r, "c_ident")]
        if causal:
            mask_q = sc.sb("mask_q", [P, P], F32R)
            mask_k = sc.sb("mask_k", [P, P], F32R)
            loads_r += [(mask_q, "c_mask_q"), (mask_k, "c_mask_k")]
        xb = sc.sb("xb", [P, KD, length])
        raw = sc.sb("raw", [P, RQ + RK, width])
        hi_r = sc.sb("hi", [P, RQ + RK, width], F32R)
        lo_r = sc.sb("lo", [P, RQ + RK, width], F32R)
        q = sc.sb("q", [P, 2, per, width], F32R)
        kt = sc.sb("kt", [P, 1, 1, width] if shared_k else [P, 2, per, width], F32R)
        v = sc.sb("v", [P, NTL, v_cols])
        mx = sc.sb("mx", [P, NTL, per])
        mx2 = sc.sb("mx2", [P, 2])
        mrow = sc.sb("mrow", [P, per, NTL, P], F32R)
        pt = sc.sb("pt", [P, 2, 2, 512])
        o_sb = sc.sb("o_sb", [P, 2, length])
        rec = sc.sb("rec", [P, length])
        ctx_t = sc.sb("ctx", [P, G, length])
        ps_s = sc.ps("ps_s", [P, 2, 2, 512])
        ps_o = sc.ps("ps_o", [P, 2, 512])
        ps_t = sc.ps("ps_t", [P, 2, 512])
        landed = sc.sem("landed")
        landed_r = sc.sem("landed_r")
        xb_ready = sc.sem("xb_ready")
        xb_used = sc.sem("xb_used")
        split = sc.sem("split")
        filled = sc.sem("filled")
        act_took = sc.sem("act_took")
        dve_took = sc.sem("dve_took")
        max_done = sc.sem("max_done")
        t_ready = sc.sem("t_ready")
        t_took = sc.sem("t_took")
        o_ready = sc.sem("o_ready")
        o_took = sc.sem("o_took")
        ctx_done = sc.sem("ctx_done")
        own = sc.sem("own")
        zeroed = sc.sem("zeroed")
        block = ctx.enter_context(nc.Block())
        NR = RQ + RK

        def slot(u):
            return ps_s[:, u.n % 2]

        def heads_of(u):
            return [u.pair * 2 + i for i in range(2)]

        def k_stack(gr, h):
            return kt[:, 0, 0] if shared_k else kt[:, gr % 2, h]

        @block.sync
        def _(sp):
            for a, b in loads:
                sp.dma_start(a, b).then_inc(landed, 16)

        @block.gpsimd
        def _(pool):
            for a, b in loads_r:
                nc.gpsimd.dma_start(a[:], dram[b]).then_inc(landed_r, 16)
            pool.wait_ge(zeroed, 1)
            with nc.gpsimd.Fori(0, NB) as b:
                pool.wait_ge(xb_used, b + 1)
                nc.gpsimd.tensor_copy(xb[:], src[:, :, bass.ds(b * length, length)]).then_inc(xb_ready, 1)
                for n in range(NR):
                    pool.wait_ge(act_took, b * n_act + (n + 3))
                    nc.gpsimd.tensor_tensor(lo_r[:, n, :], raw[:, n, :], hi_r[:, n, :].bitcast(F32),
                                            ALU.subtract).then_inc(split, 1)

        @block.tensor
        def _(pe):
            pe.wait_ge(landed, 16 * len(loads))
            pe.wait_ge(landed_r, 16 * len(loads_r))
            pe.wait_ge(zeroed, 1)

            def took(u, b):
                if u.by_act:
                    pe.wait_ge(act_took, b * n_act + (u.taken + 2))
                else:
                    pe.wait_ge(dve_took, b * n_dve + u.taken)

            def fill(u, b):
                if u.n < 2:
                    pe.wait_ge(act_took, b * n_act + (u.n + 1))
                else:
                    took(units[u.n - 2], b)
                s = slot(u)
                start, rows = tiles[u.tile] if u.tile < NTL else (0, P)
                if u.kind in "QK":
                    w = wq if u.kind == "Q" else wk
                    for n, lo, hi in cuts(0, length):
                        for k in range(KD):
                            mm = nc.tensor.matmul(s[:, n, 0:hi - lo], w[:, k, u.tile * P:(u.tile + 1) * P],
                                                  xb[:, k, lo:hi], start=(k == 0), stop=(k == KD - 1))
                elif u.kind == "V":
                    for k in range(KD):
                        mm = nc.tensor.matmul(s[0:rows, 0, 0:v_cols], xb[:, k, start:start + rows], wv[:, k, :],
                                              start=(k == 0), stop=(k == KD - 1))
                elif u.kind in "BC":
                    if u is first_b:
                        pe.wait_ge(split, b * NR + NR)
                    for i in range(b_heads):
                        h = (u.g * per + u.pair * b_heads + i) if u.kind == "B" or not shared_k else 0
                        src_n = h // in_tile + (0 if u.kind == "B" else RQ)
                        for n, lo, hi in cuts(0, length):
                            o = s[:, i if one_bank else n, 0:up_even(hi) - lo]
                            for part, t in enumerate((hi_r, lo_r)):
                                mm = nc.tensor.matmul(o, sel[:, part + (0 if u.kind == "B" else 2), h % in_tile, :],
                                                      t[:, src_n, lo:up_even(hi)], start=(part == 0), stop=(part == 1))
                else:
                    if u is first_m:
                        took(units[u.n - 1], b)
                    masked = causal and u.lo <= start < u.hi
                    for i, h in enumerate(heads_of(u)):
                        qs, ks = q[:, u.g % 2, h], k_stack(u.g, h)
                        left, right = (qs, ks) if u.kind == "M" else (ks, qs)
                        mm = nc.tensor.matmul(s[:, i, 0:up_even(u.hi) - u.lo], left[:, start:start + P],
                                              right[:, u.lo:up_even(u.hi)], start=True, stop=not masked)
                        if masked:
                            m = mask_q if u.kind == "M" else mask_k
                            n = rows + rows % 2
                            mm = nc.tensor.matmul(s[:, i, start - u.lo:start - u.lo + n], ident_r[:], m[:, 0:n],
                                                  start=False, stop=True)
                mm.then_inc(filled, 1)

            def with_v(u, b):
                took(u, b)
                for n, lo, hi in cuts(u.lo, u.hi):
                    for i, h in enumerate(heads_of(u)):
                        c = 0 if shared_k else (u.g * per + h) * stripe
                        bank_n = u.g % 2 if one_bank else n
                        at = lo - regions[n][0]
                        mm = nc.tensor.matmul(ps_o[h * stripe:(h + 1) * stripe, bank_n, at:at + hi - lo],
                                              v[:, u.tile, c:c + stripe], pt[:, u.pn % 2, i, lo - u.lo:hi - u.lo],
                                              start=(u.tile == 0), stop=(u.tile == NTL - 1), skip_group_check=True)
                if u.last:
                    mm.then_inc(o_ready, 1)

            def turn(what, b, n):
                gr = int(what[1])
                if what[0] == "T":
                    pe.wait_ge(max_done, b * G + (gr + 1))
                elif what[0] == "S":
                    pe.wait_ge(o_took, b * G + (gr + 2))
                else:
                    pe.wait_ge(ctx_done, b * G + G)
                pe.wait_ge(t_took, b * n_ps_t + (n + 1))
                if what[0] == "T":
                    for i in range(b_heads):
                        h = int(what[2]) * b_heads + i
                        for t, (start, rows) in enumerate(tiles):
                            (bn, lo, hi), = cuts(start, start + rows)
                            at = lo - regions[bn][0]
                            mm = nc.tensor.matmul(ps_t[:, i if one_bank else bn, at:at + rows + rows % 2],
                                                  mrow[:, h, t, :], ident_r[:, 0:rows + rows % 2], start=True, stop=True)
                elif what[0] == "S":
                    for bn, lo, hi in cuts(0, length):
                        mm = nc.tensor.matmul(ps_t[:, bn, 0:hi - lo], swap[:], o_sb[:, gr % 2, lo:hi],
                                              start=True, stop=True)
                else:
                    for bn, lo, hi in cuts(0, length):
                        for k in range(G):
                            mm = nc.tensor.matmul(ps_t[:, bn, 0:hi - lo], wo[:, k, gr * P:(gr + 1) * P],
                                                  ctx_t[:, k, lo:hi], start=(k == 0), stop=(k == G - 1))
                mm.then_inc(t_ready, 1)

            with nc.tensor.Fori(0, NB) as b:
                pe.wait_ge(xb_ready, b + 1)
                for item in order:
                    if isinstance(item, str):
                        turn(item, b, turns.index(item))
                        continue
                    before = None
                    for u in item:
                        if u.kind == "P" and u is item[0]:
                            pe.wait_ge(t_took, b * n_ps_t + (turns.index(turned(u.g)[-1]) + 2))
                            pe.wait_ge(o_took, b * G + (u.g + 1))
                        fill(u, b)
                        if u.kind == "P":
                            if before is not None:
                                with_v(before, b)
                            before = u
                    if before is not None:
                        with_v(before, b)

        @block.scalar
        def _(act):
            act.wait_ge(landed, 16 * len(loads))
            act.wait_ge(zeroed, 1)
            nc.scalar.copy(pt[:, 0, 0, 0:1], pt[:, 0, 0, 0:1]).then_inc(act_took, 2)
            with nc.scalar.Fori(0, NB) as b:
                for u in units:
                    if not u.by_act:
                        continue
                    act.wait_ge(filled, b * nu + (u.n + 1))
                    if u.kind == "P":
                        rows, n = tiles[u.tile][1], u.hi - u.lo
                        last = nc.scalar.activation(pt[0:rows, u.pn % 2, :, 0:n], slot(u)[0:rows, :, 0:n], ACT.Exp,
                                                    scale=scale)
                    elif u.kind in "QK":
                        t, bias = (u.tile, bq) if u.kind == "Q" else (RQ + u.tile, bk)
                        for n, lo, hi in cuts(0, length):
                            for out in (raw, hi_r):
                                last = nc.scalar.activation(out[:, t, lo:hi], slot(u)[:, n, 0:hi - lo], ACT.Identity,
                                                            bias=bias[:, u.tile:u.tile + 1])
                    else:
                        for n, lo, hi in cuts(0, length):
                            if one_bank:
                                h = u.pair * b_heads
                                o, s = (q if u.kind == "B" else kt)[:, u.g % 2, h:h + 2, lo:hi], slot(u)[:, :, 0:hi]
                            else:
                                o = q[:, u.g % 2, u.pair, lo:hi] if u.kind == "B" else kt[:, 0, 0, lo:hi]
                                s = slot(u)[:, n, 0:hi - lo]
                            if u.kind == "B":
                                last = nc.scalar.copy(o, s)
                            else:
                                last = nc.scalar.activation(o, s, ACT.Identity, bias=ones_row[:])
                    last.then_inc(act_took, 1)

        @block.vector
        def _(dve):
            ve = nc.vector
            dve.wait_ge(landed, 16 * len(loads))
            ve.memset(mx2[:], 0.0).then_inc(t_took, 1)
            ve.memset(rec[:], 0.0).then_inc(o_took, 1)
            ve.memset(o_sb[:, 0, 0:1], 0.0).then_inc(xb_used, 1)
            chain = Chain(dve, own)
            for t in (mx, pt, raw):
                ve.memset(t[:], 0.0)
            for t in (q, kt, mrow, hi_r):
                ve.memset(t[:].bitcast(F32), 0.0)
            ve.memset(v[:], 0.0).then_inc(zeroed, 1)
            dve.wait_ge(zeroed, 1)

            def take(u, b):
                dve.wait_ge(filled, b * nu + (u.n + 1))
                rows = tiles[u.tile][1]
                if u.kind == "V":
                    ve.tensor_tensor(v[0:rows, u.tile, :], slot(u)[0:rows, 0, 0:v_cols], bv[0:rows, :],
                                     ALU.add).then_inc(dve_took, 1)
                    if u.tile == NTL - 1:
                        dve.wait_ge(dve_took, b * n_dve + u.taken)
                        ve.memset(mx2[:], 0.0).then_inc(xb_used, 1)
                    return
                h = u.pair * 2
                col = mx[0:rows, u.tile, h:h + 2]
                first = u.lo == 0
                out = col if first else mx2[0:rows, :]
                ve.tensor_reduce(out, slot(u)[0:rows, :, 0:u.hi - u.lo], AX_X, ALU.max).then_inc(dve_took, 1)
                if not first:
                    dve.wait_ge(dve_took, b * n_dve + u.taken)
                    chain.step(ve.tensor_tensor(col, col, mx2[0:rows, :], ALU.max))
                if u.last:
                    dve.wait_ge(dve_took, b * n_dve + u.taken)
                    m = mx[:].rearrange("p t h -> p h t")
                    hi, lo = (mrow[:, :, :, ROW + n:ROW + n + 1].rearrange("p h t a -> p h (t a)") for n in range(2))
                    chain.step(ve.tensor_scalar(hi, m, -1.0, None, ALU.mult))
                    ve.scalar_tensor_tensor(lo, m, -1.0, hi.bitcast(F32), ALU.mult, ALU.subtract).then_inc(max_done, 1)
                    dve.wait_ge(max_done, b * G + (u.g + 1))

            def turn(what, b, n):
                gr = int(what[1])
                dve.wait_ge(t_ready, b * n_ps_t + (n + 1))
                if what[0] == "T":
                    r = slice(ROW, ROW + 2)
                    for bn, lo, hi in cuts(0, length):
                        if one_bank:
                            h = int(what[2]) * b_heads
                            last = ve.tensor_copy(q[r, gr % 2, h:h + 2, lo:hi], ps_t[r, :, lo:hi])
                        else:
                            last = ve.tensor_copy(q[r, gr % 2, int(what[2]), lo:hi], ps_t[r, bn, 0:hi - lo])
                    last.then_inc(t_took, 1)
                elif what[0] == "S":
                    for bn, lo, hi in cuts(0, length):
                        last = ve.reciprocal(rec[:, lo:hi], ps_t[:, bn, 0:hi - lo])
                    last.then_inc(t_took, 1)
                    dve.wait_ge(t_took, b * n_ps_t + (n + 2))
                    ve.tensor_tensor(ctx_t[:, gr, :], o_sb[:, gr % 2, :], rec[:], ALU.mult).then_inc(ctx_done, 1)
                    dve.wait_ge(ctx_done, b * G + (gr + 1))
                else:
                    for bn, lo, hi in cuts(0, length):
                        at = bass.ds(b * length + lo, hi - lo)
                        last = ve.scalar_tensor_tensor(dst[:, gr, at], ps_t[:, bn, 0:hi - lo], bo[:, gr:gr + 1],
                                                       res[:, gr, at], ALU.add, ALU.add)
                    last.then_inc(t_took, 1)

            steps = sum(1 for u in units if u.kind == "M" and u.lo > 0) + G
            with nc.vector.Fori(0, NB) as b:
                chain.begin(b, steps)
                for item in order:
                    if isinstance(item, str):
                        turn(item, b, turns.index(item))
                        continue
                    for u in item:
                        if not u.by_act:
                            take(u, b)
                    if item[0].kind == "P":
                        gr = item[0].g
                        dve.wait_ge(o_ready, b * G + (gr + 1))
                        for n, (lo, hi) in enumerate(regions):
                            bank_n = gr % 2 if one_bank else n
                            last = ve.tensor_copy(o_sb[:, gr % 2, lo:hi], ps_o[:, bank_n, 0:hi - lo])
                        last.then_inc(o_took, 1)
                        dve.wait_ge(o_took, b * G + (gr + 2))
                chain.end(NB)


def query_attention(g):
    layer_norm(g, "q2n", g.h, g.xn)
    attention(g, "q2", g.xn, S, 8, 32, D ** -0.5, True, 1,
              ("q2_wq", "q2_wk", "q2_wv", "q2_wo", "q2_bq", "q2_bk", "q2_bv", "L2_attn_bp"), g.h, g.h)


def embed(g, xt):
    nc, dram = g.nc, g.dram
    KP = 3 * 16 * 16 // P
    N_P = NB * (S_IMG - 1)
    TT = S_TXT // P
    T = NB * TT
    with ExitStack() as ctx:
        sc = Scope(nc, ctx, "em")
        idx = sc.sb("idx", [P, T], I32)
        idx_f = sc.sb("idx_f", [P, T])
        neg = sc.sb("neg", [P, T])
        rows = sc.sb("rows", [P, T, D])
        pos = sc.sb("pos", [P, TT, D])
        patches = sc.sb("patches", [P, KP, N_P])
        w = sc.sb("w", [P, KP, D])
        vec = sc.sb("vec", [P, 2, KD])
        pos_img = sc.sb("pos_img", [P, KD, S_IMG])
        ps = sc.ps("ps", [P, 6, 512])
        ps_i = sc.ps("ps_i", [P, KD, 512])
        idx_landed = sc.sem("idx_landed")
        landed = sc.sem("landed")
        idx_ready = sc.sem("idx_ready")
        gathered = [sc.sem(f"gathered{b}") for b in range(NB)]
        placed = sc.sem("placed")
        turned = sc.sem("turned")
        copied = sc.sem("copied")
        img_ready = sc.sem("img_ready")
        img_done = sc.sem("img_done")
        own = sc.sem("own")
        block = ctx.enter_context(nc.Block())

        @block.sync
        def _(sp):
            sp.dma_start(idx[:], dram["x_txt"]).then_inc(idx_landed, 16)
            for a, b in ((pos, "c_pos_txt"), (patches, "patches"), (w, "L0_tok_W"), (vec, "tok_vec"),
                         (pos_img, "L0_tok_pos_embedding")):
                sp.dma_start(a[:], dram[b]).then_inc(landed, 16)

        @block.gpsimd
        def _(pool):
            pool.wait_ge(idx_ready, 1)
            for t in range(T):
                nc.gpsimd.indirect_dma_start(
                    rows[:, t, :], None, dram["L0_txt_emb"],
                    bass.IndirectOffsetOnAxis(ap=idx[:, t:t + 1], axis=0)).then_inc(gathered[t // TT], 16)

        @block.vector
        def _(dve):
            v = nc.vector
            chain = Chain(dve, own)
            dve.wait_ge(idx_landed, 16)
            chain.step(v.tensor_copy(idx_f[:], idx[:]))
            chain.step(v.tensor_scalar(neg[:], idx_f[:], 0.0, float(VOCAB), ALU.is_lt, ALU.mult))
            chain.step(v.tensor_tensor(idx_f[:], idx_f[:], neg[:], ALU.add))
            chain.step(v.tensor_scalar(idx_f[:], idx_f[:], 0.0, float(VOCAB - 1), ALU.max, ALU.min))
            v.tensor_copy(idx[:], idx_f[:]).then_inc(idx_ready, 1)
            dve.wait_ge(landed, 16 * 5)
            dve.wait_ge(img_ready, 1)
            img = g.h[:].rearrange("p k (b s) -> p k b s", s=S)
            for k in range(KD):
                pk = pos_img[:, k, :].rearrange("p (a s) -> p a s", a=1)
                v.scalar_tensor_tensor(img[:, k, :, 1:S_IMG],
                                       ps_i[:, k, 0:N_P].rearrange("p (b s) -> p b s", b=NB), vec[:, 0, k:k + 1],
                                       pk[:, :, 1:S_IMG].to_broadcast([P, NB, S_IMG - 1]), ALU.add, ALU.add)
                v.tensor_tensor(img[:, k, :, 0:1].rearrange("p b a -> p (b a)"),
                                vec[:, 1, k:k + 1].to_broadcast([P, NB]), pos_img[:, k, 0:1].to_broadcast([P, NB]),
                                ALU.add).then_inc(img_done, 1)
            for b in range(NB):
                dve.wait_ge(gathered[b], 16 * TT)
                r = rows[:, b * TT:(b + 1) * TT, :]
                v.tensor_tensor(r, r, pos[:], ALU.add).then_inc(placed, 1)
            for t in range(T):
                dve.wait_ge(turned, t + 1)
                v.tensor_copy(xt[:, :, t * P:(t + 1) * P],
                              ps[:, t % 6, 0:D].rearrange("p (k n) -> p k n", k=KD)).then_inc(copied, 1)

        @block.tensor
        def _(pe):
            pe.wait_ge(landed, 16 * 5)
            for m in range(KD):
                for k in range(KP):
                    mm = nc.tensor.matmul(ps_i[:, m, 0:N_P], w[:, k, m * P:(m + 1) * P], patches[:, k, :],
                                          start=(k == 0), stop=(k == KP - 1))
            mm.then_inc(img_ready, 1)
            for t in range(T):
                pe.wait_ge(placed, t // TT + 1)
                if t >= 6:
                    pe.wait_ge(copied, t - 5)
                for k in range(KD):
                    mm = nc.tensor.transpose(ps[:, t % 6, k * P:(k + 1) * P], rows[:, t, k * P:(k + 1) * P],
                                             g.ident[:])
                mm.then_inc(turned, 1)


def text_block(g):
    nc, dram = g.nc, g.dram
    NX = NB * S_TXT
    F = 4 * D
    NF = F // P
    with ExitStack() as ctx:
        sc = Scope(nc, ctx, "tx")
        xt = sc.sb("xt", [P, KD, NX])
        r1 = sc.sb("r1", [P, KD, NX])
        b1 = sc.sb("b1", [P, NF])
        vec = sc.sb("vec", [P, 5, KD])
        embed(g, xt)
        attention(g, "ta", xt, S_TXT, 16, 16, 0.25, False, 16,
                  ("ta_wq", "ta_wk", "ta_wv", "ta_wo", "ta_bq", "ta_bk", "ta_bv", "L0_txt_out_proj_b"), xt, r1)
        w1 = sc.sb("w1", [P, KD, F])
        w2 = sc.sb("w2", [P, NF, D])
        layer_norm(g, "tn", r1, xt, vec[:, 1, :], vec[:, 2, :], chunks=NB, width=S_TXT, loads=(
            (vec[:], dram["txt_vec"]), (w1[:], dram["L0_txt_w1"]), (w2[:], dram["L0_txt_w2"]),
            (b1[:], dram["L0_txt_b1"])))
        relu_ffn(g, xt, r1, w1, w2, b1, vec[:, 0, :], NF)
        layer_norm(g, "to", r1, xt, vec[:, 3, :], vec[:, 4, :], chunks=NB, width=S_TXT,
                   final=lambda k, i: g.h[:, k, bass.ds(i * S + S_IMG, S_TXT)])


def relu_ffn(g, x, out, w1, w2, b1, b2, NF):
    nc = g.nc
    with ExitStack() as ctx:
        sc = Scope(nc, ctx, "tf")
        hid = sc.sb("hid", [P, 2, S_TXT])
        ps_h = [sc.ps(f"ps_h{j}", [P, 512]) for j in range(2)]
        ps_y = sc.ps("ps_y", [P, KD, 512])
        h_ready = sc.sem("h_ready")
        hid_done = sc.sem("hid_done")
        y_ready = sc.sem("y_ready")
        y_used = sc.sem("y_used")
        block = ctx.enter_context(nc.Block())

        def at(t, k, b):
            return t[:, k, bass.ds(b * S_TXT, S_TXT)]

        @block.tensor
        def _(pe):
            def up(b, f):
                pe.wait_ge(hid_done, b * NF + (f + 1))
                for k in range(KD):
                    mm = nc.tensor.matmul(ps_h[f % 2][:], w1[:, k, f * P:(f + 1) * P], at(x, k, b),
                                          start=(k == 0), stop=(k == KD - 1))
                mm.then_inc(h_ready, 1)

            with nc.tensor.Fori(0, NB) as b:
                up(b, 0)
                for f in range(NF):
                    if f + 1 < NF:
                        up(b, f + 1)
                    if f == 0:
                        pe.wait_ge(y_used, b + 1)
                    pe.wait_ge(hid_done, b * NF + (f + 3))
                    for m in range(KD):
                        mm = nc.tensor.matmul(ps_y[:, m, :], w2[:, f, m * P:(m + 1) * P], hid[:, f % 2, :],
                                              start=(f == 0), stop=(f == NF - 1))
                mm.then_inc(y_ready, 1)

        @block.scalar
        def _(act):
            nc.scalar.copy(hid[:, 0, 0:1], g.ident[:, 0:1]).then_inc(hid_done, 2)
            with nc.scalar.Fori(0, NB) as b:
                for f in range(NF):
                    act.wait_ge(h_ready, b * NF + (f + 1))
                    nc.scalar.activation(hid[:, f % 2, :], ps_h[f % 2][:], ACT.Relu,
                                         bias=b1[:, f:f + 1]).then_inc(hid_done, 1)

        @block.vector
        def _(dve):
            nc.vector.memset(out[:, 0, 0:1], 0.0).then_inc(y_used, 1)
            dve.wait_ge(y_used, 1)
            with nc.vector.Fori(0, NB) as b:
                dve.wait_ge(y_ready, b + 1)
                for m in range(KD):
                    last = nc.vector.scalar_tensor_tensor(at(out, m, b), ps_y[:, m, :], b2[:, m:m + 1], at(x, m, b),
                                                          ALU.add, ALU.add)
                last.then_inc(y_used, 1)


def slots_schedule(units, takers):
    seen = {}
    out = []
    for u in units:
        t = takers[u[0]]
        seen[t] = seen.get(t, 0) + 1
        out.append((t, seen[t]))
    return out, seen


def full_attention(g):
    nc, dram = g.nc, g.dram
    tiles = [(s, min(P, S - s)) for s in range(0, S, P)]
    NTL = len(tiles)
    cuts = [(0, 512), (512, S)]
    scale = D ** -0.5 * 1.0986122886681098
    units = [("Q", 0), ("Q", 1), ("K", 0), ("K", 1)] + [("V", t) for t in range(NTL)] \
        + [("S", 0), ("S", 1)] + [x for t in range(2, NTL) for x in (("T", t - 2), ("S", t))] \
        + [("T", NTL - 2), ("T", NTL - 1), ("O", 0), ("O", 1), ("Y", 0), ("Y", 1)]
    takers = {"Q": "act", "K": "act", "S": "act", "T": "act", "V": "dve", "O": "dve", "Y": "dve"}
    taken, per = slots_schedule(units, takers)
    NU = len(units)
    SLOTS = 4
    pad = (-NU) % SLOTS
    with ExitStack() as ctx:
        sc = Scope(nc, ctx, "a3")
        w = sc.sb("w", [P, KD, 3 * D])
        wp = sc.sb("wp", [P, KD, D])
        vec = sc.sb("vec", [P, 4, KD])
        bv = sc.sb("bv", [P, D])
        rope = sc.sb("rope", [P, 2, S])
        x = sc.sb("x", [P, KD, NT])
        layer_norm(g, "a3n", g.h, g.xn, loads=(
            (w[:], dram["L3_attn_w_qkv"]), (wp[:], dram["L3_attn_w_proj"]), (vec[:], dram["a3_vec"]),
            (bv[:], dram["a3_bv"].to_broadcast([P, D])), (rope[:], dram["c_rope"])))
        layer_norm(g, "a3r", g.xn, x, vec[:, 0, :], None, rms=True)
        xb = sc.sb("xb", [P, KD, S])
        raw = sc.sb("raw", [P, 2, KD, S])
        rot = sc.sb("rot", [P, 2, KD, S])
        tmp = sc.sb("tmp", [P, S])
        v = sc.sb("v", [P, NTL, D])
        prob = sc.sb("prob", [P, 2, S])
        prob_t = sc.sb("prob_t", [P, NTL, S])
        small = sc.sb("small", [P, NTL, 3])
        o_sb = sc.sb("o_sb", [P, KD, S])
        ps = sc.ps("ps", [P, SLOTS, 1024])
        xb_ready = sc.sem("xb_ready")
        xb_used = sc.sem("xb_used")
        filled = sc.sem("filled")
        act_took = sc.sem("act_took")
        dve_took = sc.sem("dve_took")
        max_done = sc.sem("max_done")
        prob_done = sc.sem("prob_done")
        roped = sc.sem("roped")
        added = sc.sem("added")
        own = sc.sem("own")
        block = ctx.enter_context(nc.Block())

        def slot(n):
            return ps[:, n % SLOTS]

        @block.gpsimd
        def _(pool):
            with nc.gpsimd.Fori(0, NB) as b:
                pool.wait_ge(xb_used, b + 1)
                nc.gpsimd.tensor_copy(xb[:], x[:, :, bass.ds(b * S, S)]).then_inc(xb_ready, 1)

        def taker_wait(eng, b, n):
            who, k = taken[n]
            if who == "act":
                eng.wait_ge(act_took, b * per["act"] + k)
            else:
                eng.wait_ge(dve_took, b * per["dve"] + (k + 4))

        @block.tensor
        def _(pe):
            with nc.tensor.Fori(0, NB) as b:
                pe.wait_ge(xb_ready, b + 1)
                for n, (kind, t) in enumerate(units):
                    s = slot(n)
                    before = n - SLOTS
                    if before >= 0:
                        taker_wait(pe, b, before)
                    elif before + pad < 0:
                        pe.wait_ge(dve_took, b * per["dve"] + (4 + before + pad + 1))
                    if kind in "QK":
                        col = (0 if kind == "Q" else D) + t * P
                        for lo, hi in cuts:
                            for k in range(KD):
                                mm = nc.tensor.matmul(s[:, lo:hi], w[:, k, col:col + P], xb[:, k, lo:hi],
                                                      start=(k == 0), stop=(k == KD - 1))
                    elif kind == "V":
                        start, rows = tiles[t]
                        for k in range(KD):
                            mm = nc.tensor.matmul(s[0:rows, 0:D], xb[:, k, start:start + rows], w[:, k, 2 * D:3 * D],
                                                  start=(k == 0), stop=(k == KD - 1))
                    elif kind == "S":
                        start, rows = tiles[t]
                        if t == 0:
                            pe.wait_ge(roped, b + 1)
                        for lo, hi in cuts:
                            for k in range(KD):
                                mm = nc.tensor.matmul(s[0:rows, lo:hi], rot[:, 0, k, start:start + rows],
                                                      rot[:, 1, k, lo:hi], start=(k == 0), stop=(k == KD - 1))
                    elif kind == "T":
                        start, rows = tiles[t]
                        pe.wait_ge(prob_done, b * NTL + (t + 1))
                        for j, (js, jr) in enumerate(tiles):
                            mm = nc.tensor.transpose(s[0:jr, j * P:(j + 1) * P], prob[:, t % 2, js:js + jr],
                                                     g.ident[:])
                    elif kind == "O":
                        if t == 0:
                            taker_wait(pe, b, units.index(("T", NTL - 1)))
                        for lo, hi in cuts:
                            for j, (js, jr) in enumerate(tiles):
                                mm = nc.tensor.matmul(s[:, lo:hi], v[0:jr, j, t * P:(t + 1) * P],
                                                      prob_t[0:jr, j, lo:hi], start=(j == 0), stop=(j == NTL - 1))
                    else:
                        if t == 0:
                            taker_wait(pe, b, units.index(("O", 1)))
                        for lo, hi in cuts:
                            for k in range(KD):
                                mm = nc.tensor.matmul(s[:, lo:hi], wp[:, k, t * P:(t + 1) * P], o_sb[:, k, lo:hi],
                                                      start=(k == 0), stop=(k == KD - 1))
                    mm.then_inc(filled, 1)

        @block.scalar
        def _(act):
            with nc.scalar.Fori(0, NB) as b:
                for n, (kind, t) in enumerate(units):
                    if takers[kind] != "act":
                        continue
                    s = slot(n)
                    act.wait_ge(filled, b * NU + (n + 1))
                    if kind in "QK":
                        c = 0 if kind == "Q" else 1
                        last = nc.scalar.activation(raw[:, c, t, :], s[:, 0:S], ACT.Identity,
                                                    bias=vec[:, 1 + c, t:t + 1])
                    elif kind == "S":
                        start, rows = tiles[t]
                        act.wait_ge(max_done, b * NTL + (t + 1))
                        last = nc.scalar.activation(prob[0:rows, t % 2, :], s[0:rows, 0:S], ACT.Exp,
                                                    bias=small[0:rows, t, 0:1], scale=scale,
                                                    accum_out=small[0:rows, t, 1:2])
                    else:
                        start, rows = tiles[t]
                        full = NTL - 1
                        nc.scalar.copy(prob_t[:, 0:full, start:start + rows],
                                       s[:, 0:full * P].rearrange("p (j n) -> p j n", j=full)[:, :, 0:rows])
                        jr = tiles[full][1]
                        last = nc.scalar.copy(prob_t[0:jr, full, start:start + rows], s[0:jr, full * P:full * P + rows])
                    last.then_inc(act_took, 1)

        @block.vector
        def _(dve):
            ve = nc.vector
            ve.memset(tmp[:, 0:1], 0.0).then_inc(xb_used, 1)
            ve.memset(tmp[:, 1:2], 0.0).then_inc(dve_took, 4)
            dve.wait_ge(dve_took, 4)
            dve.wait_ge(xb_used, 1)
            chain = Chain(dve, own)
            steps = 2 * 4 + 3 * NTL
            with nc.vector.Fori(0, NB) as b:
                chain.begin(b, steps)
                for n, (kind, t) in enumerate(units):
                    s = slot(n)
                    if kind == "V":
                        rows = tiles[t][1]
                        dve.wait_ge(filled, b * NU + (n + 1))
                        ve.tensor_tensor(v[0:rows, t, :], s[0:rows, 0:D], bv[0:rows, :], ALU.add).then_inc(dve_took, 1)
                    if kind == "V" and t == NTL - 1:
                        ve.memset(small[:, 0, 2:3], 0.0).then_inc(xb_used, 1)
                        taker_wait(dve, b, units.index(("K", 1)))
                        cos, sin = rope[:, 0, :], rope[:, 1, :]
                        for c in range(2):
                            a0, a1 = raw[:, c, 0, :], raw[:, c, 1, :]
                            r0, r1 = rot[:, c, 0, :], rot[:, c, 1, :]
                            ve.tensor_tensor(r0, a0, cos, ALU.mult)
                            ve.tensor_tensor(r1, a1, cos, ALU.mult)
                            chain.step(ve.tensor_tensor(tmp[:], a1, sin, ALU.mult))
                            chain.step(ve.tensor_tensor(r0, r0, tmp[:], ALU.subtract))
                            chain.step(ve.tensor_tensor(tmp[:], a0, sin, ALU.mult))
                            ins = ve.tensor_tensor(r1, r1, tmp[:], ALU.add)
                            chain.step(ins)
                        ve.tensor_copy(tmp[:, 0:1], rope[:, 0, 0:1]).then_inc(roped, 1)
                        dve.wait_ge(roped, b + 1)
                    if kind == "S":
                        rows = tiles[t][1]
                        dve.wait_ge(filled, b * NU + (n + 1))
                        chain.step(ve.tensor_reduce(small[0:rows, t, 2:3], s[0:rows, 0:S], AX_X, ALU.max))
                        ve.tensor_scalar(small[0:rows, t, 0:1], small[0:rows, t, 2:3], -scale, None,
                                         ALU.mult).then_inc(max_done, 1)
                    if kind == "S" and t >= 1 or kind == "T" and t == NTL - 1:
                        p = t - 1 if kind == "S" else t
                        rows = tiles[p][1]
                        taker_wait(dve, b, units.index(("S", p)))
                        chain.step(ve.reciprocal(small[0:rows, p, 2:3], small[0:rows, p, 1:2]))
                        chain.step(ve.tensor_scalar(prob[0:rows, p % 2, :], prob[0:rows, p % 2, :],
                                                    small[0:rows, p, 2:3], None, ALU.mult))
                        ve.tensor_copy(tmp[:, 1:2], rope[:, 0, 0:1]).then_inc(prob_done, 1)
                        dve.wait_ge(prob_done, b * NTL + (p + 1))
                    if kind == "O":
                        dve.wait_ge(filled, b * NU + (n + 1))
                        ve.tensor_copy(o_sb[:, t, :], s[:, 0:S]).then_inc(dve_took, 1)
                    if kind == "Y":
                        at = bass.ds(b * S, S)
                        dve.wait_ge(filled, b * NU + (n + 1))
                        chain_y = ve.scalar_tensor_tensor(tmp[:], s[:, 0:S], vec[:, 3, t:t + 1], g.xn[:, t, at],
                                                          ALU.add, ALU.add)
                        chain_y.then_inc(dve_took, 1)
                        taker_wait(dve, b, n)
                        ve.tensor_tensor(g.h[:, t, at], g.h[:, t, at], tmp[:], ALU.add).then_inc(added, 1)
                        dve.wait_ge(added, b * KD + (t + 1))
                chain.end(NB)


def delta_net(g):
    nc, dram = g.nc, g.dram
    H, DH, J = 8, 32, 2
    HJ = H * J
    tiles = [(s, min(P, S - s)) for s in range(0, S, P)]
    NTL = len(tiles)
    off = [sum(S - s for s, _ in tiles[:n]) for n in range(NTL)]
    DEC = off[-1] + S - tiles[-1][0]
    VG = D + H

    def cuts(lo, hi):
        return [(max(lo, a), min(hi, b)) for a, b in ((0, 512), (512, S)) if max(lo, a) < min(hi, b)]

    units = [("q", 0), ("q", 1), ("k", 0), ("k", 1)] + [("v", t) for t in range(NTL)] \
        + [("beta", 0), ("mix", 0), ("diff", 0)] + [("a", (n, t)) for n in range(H) for t in range(NTL)] \
        + [("coef", n) for n in range(H)]
    takers = {"q": "dve", "k": "dve", "v": "dve", "beta": "act", "mix": "act", "diff": "act", "a": "act",
              "coef": "dve"}
    NU = len(units)
    assert NU % 2 == 0
    dve_n, act_n, seen_d, seen_a = [], [], 0, 0
    for kind, _ in units:
        seen_d += takers[kind] == "dve"
        seen_a += takers[kind] == "act"
        dve_n.append(seen_d)
        act_n.append(seen_a)
    ND, NA = seen_d, seen_a
    first_a = units.index(("a", (0, 0)))
    first_c = units.index(("coef", 0))
    NB_USES = HJ + 3

    with ExitStack() as ctx:
        sc = Scope(nc, ctx, "dn")
        w_qk = sc.sb("w_qk", [P, KD, 2 * D])
        w_vg = sc.sb("w_vg", [P, KD, VG])
        w_bm = sc.sb("w_bm", [P, KD, 2 * HJ])
        w_o = sc.sb("w_o", [P, H, D])
        b_gate = sc.sb("b_gate", [P, H])
        vec16 = sc.sb("vec16", [HJ, 3])
        vec = sc.sb("vec", [P, 3, KD])
        diff = sc.sb("diff", [HJ, P])
        pick = sc.sb("pick", [HJ, HJ, P])
        pick_den = sc.sb("pick_den", [P, H, HJ])
        spread = sc.sb("spread", [HJ, H, P])
        eye = sc.sb("eye", [P, S])
        hres = sc.sb("hres", [P, KD, NT])
        loads = [(w_qk, "dn_wqk"), (w_vg, "dn_wvg"), (w_bm, "dn_wbm"), (w_o, "dn_wo"), (vec16, "dn_vec16"),
                 (vec, "dn_vec"), (diff, "c_diff"), (pick, "c_pick"), (pick_den, "c_pick_den"),
                 (spread, "c_spread"), (eye, "c_eye")]
        layer_norm(g, "dnn", g.h, g.xn, loads=[(a[:], dram[n]) for a, n in loads]
                   + [(b_gate[:], dram["L0_attn_bgate"].to_broadcast([P, H]))])

        def core(ctx):
            sc = Scope(nc, ctx, "dc")
            xb = sc.sb("xb", [P, KD, S])
            qk = sc.sb("qk", [P, 4, NTL * P])
            ex = sc.sb("ex", [P, 4, S])
            gl = sc.sb("gl", [P, NTL, H])
            vr = sc.sb("vr", [P, NTL, D])
            vg = sc.sb("vg", [P, NTL, H, 2 * DH])
            beta = sc.sb("beta", [HJ, S])
            mix = sc.sb("mix", [HJ, S])
            den = sc.sb("den", [HJ, S])
            decay = sc.sb("decay", [P, J, DEC])
            a_sb = sc.sb("a_sb", [P, 2, S])
            wt = sc.sb("wt", [P, 2, J, S])
            o_sb = sc.sb("o_sb", [P, H, S])
            ps_a = sc.ps("ps_a", [P, 2, 1024])
            ps_b = sc.ps("ps_b", [P, 1024])
            ps_o = sc.ps("ps_o", [P, 1024])
            xb_ready = sc.sem("xb_ready")
            filled = sc.sem("filled")
            dve_took = sc.sem("dve_took")
            act_took = sc.sem("act_took")
            low_ready = sc.sem("low_ready")
            exp_done = sc.sem("exp_done")
            gate_in = sc.sem("gate_in")
            gate_done = sc.sem("gate_done")
            v_done = sc.sem("v_done")
            beta_done = sc.sem("beta_done")
            b_filled = sc.sem("b_filled")
            b_took = sc.sem("b_took")
            w0_done = sc.sem("w0_done")
            w1_done = sc.sem("w1_done")
            o_ready = sc.sem("o_ready")
            o_took = sc.sem("o_took")
            den_done = sc.sem("den_done")
            own = sc.sem("own")
            zeroed = sc.sem("zeroed")
            block = ctx.enter_context(nc.Block())
            UA = H * NTL

            def slot(n):
                return ps_a[:, n % 2]

            @block.gpsimd
            def _(pool):
                pool.wait_ge(zeroed, 1)
                nc.gpsimd.memset(a_sb[:, 0, 0:1], 0.0).then_inc(w1_done, 2)
                with nc.gpsimd.Fori(0, NB) as b:
                    pool.wait_ge(beta_done, b + 1)
                    nc.gpsimd.tensor_copy(xb[:], g.xn[:, :, bass.ds(b * S, S)]).then_inc(xb_ready, 1)
                    for h in range(H):
                        for t, (start, rows) in enumerate(tiles):
                            m, u = S - start, h * NTL + t
                            pool.wait_ge(act_took, b * NA + act_n[first_a + u])
                            pool.wait_ge(b_took, b * NB_USES + (h * J + 3))
                            nc.gpsimd.tensor_tensor(wt[0:rows, u % 2, 1, 0:m], a_sb[0:rows, u % 2, 0:m],
                                                    decay[0:rows, 1, off[t]:off[t] + m], ALU.mult).then_inc(w1_done, 1)

            @block.tensor
            def _(pe):
                def dve_has(n, b):
                    pe.wait_ge(dve_took, b * ND + (dve_n[n] + 2))

                def fill(n, b):
                    kind, arg = units[n]
                    s = slot(n)
                    if n >= 2:
                        if takers[units[n - 2][0]] == "dve":
                            dve_has(n - 2, b)
                        else:
                            pe.wait_ge(act_took, b * NA + act_n[n - 2])
                    else:
                        pe.wait_ge(dve_took, b * ND + (n + 1))
                    if kind in "qk":
                        col = (0 if kind == "q" else D) + arg * P
                        for lo, hi in cuts(0, S):
                            for k in range(KD):
                                mm = nc.tensor.matmul(s[:, lo:hi], w_qk[:, k, col:col + P], xb[:, k, lo:hi],
                                                      start=(k == 0), stop=(k == KD - 1))
                    elif kind == "v":
                        start, rows = tiles[arg]
                        for k in range(KD):
                            mm = nc.tensor.matmul(s[0:rows, 0:VG], xb[:, k, start:start + rows], w_vg[:, k, :],
                                                  start=(k == 0), stop=(k == KD - 1))
                    elif kind in ("beta", "mix"):
                        col = 0 if kind == "beta" else HJ
                        for lo, hi in cuts(0, S):
                            for k in range(KD):
                                mm = nc.tensor.matmul(s[0:HJ, lo:hi], w_bm[:, k, col:col + HJ], xb[:, k, lo:hi],
                                                      start=(k == 0), stop=(k == KD - 1))
                    elif kind == "diff":
                        pe.wait_ge(act_took, b * NA + act_n[n - 1])
                        for lo, hi in cuts(0, S):
                            mm = nc.tensor.matmul(s[:, lo:hi], diff[:], mix[:, lo:hi], start=True, stop=True)
                    elif kind == "a":
                        h, t = arg
                        start, rows = tiles[t]
                        r = slice(h % 4 * DH, h % 4 * DH + DH)
                        for lo, hi in cuts(0, S - start):
                            mm = nc.tensor.matmul(s[:, lo:hi], qk[r, 2 + h // 4, start:start + P],
                                                  qk[r, h // 4, start + lo:start + hi], start=True, stop=True)
                    else:
                        for lo, hi in cuts(0, S):
                            mm = nc.tensor.matmul(s[:, lo:hi], spread[:, arg, :], den[:, lo:hi], start=True, stop=True)
                    mm.then_inc(filled, 1)

                def betas(hj, b):
                    pe.wait_ge(b_took, b * NB_USES + (hj + 1))
                    for lo, hi in cuts(0, S):
                        mm = nc.tensor.matmul(ps_b[:, lo:hi], pick[:, hj, :], beta[:, lo:hi], start=True, stop=True)
                    mm.then_inc(b_filled, 1)

                def with_v(h, t, b):
                    start = tiles[t][0]
                    u = h * NTL + t
                    pe.wait_ge(w0_done, b * UA + (u + 3))
                    pe.wait_ge(w1_done, b * UA + (u + 3))
                    for j in range(J):
                        for lo, hi in cuts(start, S):
                            mm = nc.tensor.matmul(ps_o[j * 2 * DH:(j + 1) * 2 * DH, lo:hi], vg[:, t, h, :],
                                                  wt[:, u % 2, j, lo - start:hi - start], start=(t == 0),
                                                  stop=(t == NTL - 1), skip_group_check=True)
                    if t == NTL - 1:
                        mm.then_inc(o_ready, 1)

                pe.wait_ge(zeroed, 1)
                with nc.tensor.Fori(0, NB) as b:
                    pe.wait_ge(xb_ready, b + 1)
                    for n in range(first_a):
                        fill(n, b)
                    pe.wait_ge(beta_done, b + 2)
                    betas(0, b)
                    betas(1, b)
                    pe.wait_ge(v_done, b + 1)
                    for h in range(H):
                        fill(first_a + h * NTL, b)
                        for t in range(NTL):
                            if t + 1 < NTL:
                                fill(first_a + h * NTL + t + 1, b)
                            if t == 0:
                                if h >= 1:
                                    betas(h * J + 1, b)
                                pe.wait_ge(o_took, b * H + (h + 1))
                            with_v(h, t, b)
                            if t == 0 and h + 1 < H:
                                betas((h + 1) * J, b)
                    pe.wait_ge(o_took, b * H + (H + 1))
                    pe.wait_ge(b_took, b * NB_USES + (HJ + 1))
                    for lo, hi in cuts(0, S):
                        for h in range(H):
                            mm = nc.tensor.matmul(ps_b[0:HJ, lo:hi], pick_den[:, h, :], o_sb[:, h, lo:hi],
                                                  start=(h == 0), stop=(h == H - 1))
                    mm.then_inc(b_filled, 1)
                    pe.wait_ge(den_done, b + 1)
                    for h in range(H):
                        fill(first_c + h, b)
                    dve_has(NU - 1, b)
                    for m in range(KD):
                        pe.wait_ge(b_took, b * NB_USES + (HJ + 2 + m))
                        for lo, hi in cuts(0, S):
                            for h in range(H):
                                mm = nc.tensor.matmul(ps_b[:, lo:hi], w_o[:, h, m * P:(m + 1) * P], o_sb[:, h, lo:hi],
                                                      start=(h == 0), stop=(h == H - 1))
                        mm.then_inc(b_filled, 1)

            @block.scalar
            def _(act):
                with nc.scalar.Fori(0, NB) as b:
                    for n in range(4):
                        act.wait_ge(low_ready, b * 4 + (n + 1))
                        nc.scalar.activation(ex[:, n, :], ex[:, n, :], ACT.Exp).then_inc(exp_done, 1)
                    act.wait_ge(gate_in, b + 1)
                    nc.scalar.activation(gl[:], gl[:], ACT.Sigmoid).then_inc(gate_done, 1)
                    for n, (kind, arg) in enumerate(units):
                        if takers[kind] != "act":
                            continue
                        s = slot(n)
                        act.wait_ge(filled, b * NU + (n + 1))
                        if kind == "beta":
                            last = nc.scalar.activation(beta[:], s[0:HJ, 0:S], ACT.Sigmoid, bias=vec16[:, 0:1])
                        elif kind == "mix":
                            last = nc.scalar.activation(mix[:], s[0:HJ, 0:S], ACT.Identity, bias=vec16[:, 1:2])
                        elif kind == "diff":
                            last = nc.scalar.activation(mix[:], s[0:HJ, 0:S], ACT.Sigmoid)
                        else:
                            h, t = arg
                            start, rows = tiles[t]
                            u = h * NTL + t
                            act.wait_ge(w0_done, b * UA + (u + 1))
                            act.wait_ge(w1_done, b * UA + (u + 1))
                            last = nc.scalar.copy(a_sb[0:rows, u % 2, 0:S - start], s[0:rows, 0:S - start])
                        last.then_inc(act_took, 1)
                        if kind == "a" and arg[1] == NTL - 1:
                            h = arg[0]
                            act.wait_ge(o_ready, b * H + (h + 1))
                            nc.scalar.copy(o_sb[:, h, :], ps_o[:, 0:S]).then_inc(o_took, 1)

            @block.vector
            def _(dve):
                ve = nc.vector
                chain = Chain(dve, own)
                ve.memset(vg[:], 0.0).then_inc(beta_done, 1)
                ve.memset(qk[:], 0.0).then_inc(dve_took, 2)
                ve.memset(wt[:], 0.0).then_inc(b_took, 1)
                ve.memset(beta[:, 0:1], 0.0).then_inc(o_took, 1)
                ve.memset(mix[:, 0:1], 0.0).then_inc(w0_done, 2)
                ve.memset(gl[:], 0.0).then_inc(zeroed, 1)
                dve.wait_ge(zeroed, 1)

                def scan(hj, b):
                    j = hj % 2
                    dve.wait_ge(b_filled, b * NB_USES + (hj + 1))
                    for t, (start, rows) in enumerate(tiles):
                        m = S - start
                        last = ve.tensor_tensor_scan(decay[0:rows, j, off[t]:off[t] + m], ps_b[0:rows, start:S],
                                                     eye[0:rows, 0:m], 0.0, ALU.mult, ALU.add)
                    last.then_inc(b_took, 1)

                with nc.vector.Fori(0, NB) as b:
                    chain.begin(b, 1)
                    for n in range(4):
                        dve.wait_ge(filled, b * NU + (n + 1))
                        ve.tensor_scalar(ex[:, n, :], slot(n)[:, 0:S], 0.0, None, ALU.min).then_inc(low_ready, 1)
                        if n % 2 == 1:
                            for m in (n - 1, n):
                                dve.wait_ge(exp_done, b * 4 + (m + 1))
                                ve.scalar_tensor_tensor(qk[:, m, 0:S], slot(m)[:, 0:S], 0.0, ex[:, m, :], ALU.max,
                                                        ALU.add).then_inc(dve_took, 1)
                    for t, (start, rows) in enumerate(tiles):
                        s = slot(4 + t)
                        dve.wait_ge(filled, b * NU + (4 + t + 1))
                        ve.tensor_tensor(gl[0:rows, t, :], s[0:rows, D:VG], b_gate[0:rows, :], ALU.add)
                        ve.tensor_copy(vr[0:rows, t, :], s[0:rows, 0:D]).then_inc(dve_took, 1)
                    ve.tensor_copy(ex[:, 0, 0:1], eye[:, 0:1]).then_inc(gate_in, 1)
                    dve.wait_ge(act_took, b * NA + act_n[units.index(("mix", 0))])
                    ve.tensor_scalar(beta[:], beta[:], vec16[:, 2:3], 0.9999, ALU.mult, ALU.min).then_inc(beta_done, 1)
                    dve.wait_ge(gate_done, b + 1)
                    dve.wait_ge(dve_took, b * ND + (9 + 2))
                    full = NTL - 1
                    for lo, hi, rows in ((0, full, P), (full, NTL, tiles[full][1])):
                        gb = gl[0:rows, lo:hi, :].rearrange("p t (h a) -> p (t h) a", a=1).to_broadcast(
                            [rows, (hi - lo) * H, DH])
                        o = vg[0:rows, lo:hi].rearrange("p t h d -> p (t h) d")
                        ve.tensor_tensor(o[:, :, 0:DH], vr[0:rows, lo:hi, :].rearrange("p t (h d) -> p (t h) d", d=DH),
                                         gb, ALU.mult)
                        last = ve.tensor_copy(o[:, :, DH:2 * DH], gb)
                    last.then_inc(v_done, 1)
                    scan(0, b)
                    scan(1, b)
                    for h in range(H):
                        dve.wait_ge(b_took, b * NB_USES + (h * J + 3))
                        for t, (start, rows) in enumerate(tiles):
                            m, u = S - start, h * NTL + t
                            dve.wait_ge(act_took, b * NA + act_n[first_a + u])
                            ve.tensor_tensor(wt[0:rows, u % 2, 0, 0:m], a_sb[0:rows, u % 2, 0:m],
                                             decay[0:rows, 0, off[t]:off[t] + m], ALU.mult).then_inc(w0_done, 1)
                        if h + 1 < H:
                            dve.wait_ge(w0_done, b * UA + ((h + 1) * NTL + 2))
                            scan((h + 1) * J, b)
                            dve.wait_ge(w1_done, b * UA + ((h + 1) * NTL + 2))
                            scan((h + 1) * J + 1, b)
                    dve.wait_ge(b_filled, b * NB_USES + (HJ + 1))
                    ve.tensor_scalar(den[:], ps_b[0:HJ, 0:S], 1.0e-6, None, ALU.add).then_inc(b_took, 1)
                    dve.wait_ge(b_took, b * NB_USES + (HJ + 2))
                    chain.step(ve.reciprocal(den[:], den[:]))
                    ve.tensor_tensor(den[:], den[:], mix[:], ALU.mult).then_inc(den_done, 1)
                    for h in range(H):
                        dve.wait_ge(filled, b * NU + (first_c + h + 1))
                        ve.tensor_tensor(o_sb[:, h, :], o_sb[:, h, :], slot(first_c + h)[:, 0:S],
                                         ALU.mult).then_inc(dve_took, 1)
                    for m in range(KD):
                        dve.wait_ge(b_filled, b * NB_USES + (HJ + 2 + m))
                        at = bass.ds(b * S, S)
                        ve.scalar_tensor_tensor(hres[:, m, at], ps_b[:, 0:S], vec[:, 0, m:m + 1], g.xn[:, m, at],
                                                ALU.add, ALU.add).then_inc(b_took, 1)

        with ExitStack() as mid:
            core(mid)
        layer_norm(g, "dno", hres, hres, vec[:, 1, :], vec[:, 2, :], add_to=g.h)


def store_output(g, out):
    nc = g.nc
    with ExitStack() as ctx:
        sc = Scope(nc, ctx, "out")
        rows = sc.sb("rows", [RN, RT, D])
        ps = sc.ps("ps", [P, 8, 512])
        turned = sc.sem("turned")
        copied = sc.sem("copied")
        stored = sc.sem("stored")
        block = ctx.enter_context(nc.Block())
        view = out.rearrange("(t p) d -> p t d", p=RN)
        half = RT // 2

        @block.tensor
        def _(pe):
            for t in range(RT):
                if t >= 8:
                    pe.wait_ge(copied, t - 7)
                for k in range(KD):
                    mm = nc.tensor.transpose(ps[0:RN, t % 8, k * P:(k + 1) * P],
                                             g.h[:, k, t * RN:(t + 1) * RN], g.ident[:])
                mm.then_inc(turned, 1)

        @block.vector
        def _(dve):
            for t in range(RT):
                dve.wait_ge(turned, t + 1)
                nc.vector.tensor_copy(rows[:, t, :], ps[0:RN, t % 8, 0:D]).then_inc(copied, 1)

        @block.sync
        def _(sp):
            for n in range(2):
                sp.wait_ge(copied, half * (n + 1))
                sp.dma_start(view[:, half * n:half * (n + 1), :],
                             rows[:, half * n:half * (n + 1), :]).then_inc(stored, 16)
            sp.wait_ge(stored, 32)


def program(nc, dram, out):
    dram["s_gate"] = nc.dram_tensor("s_gate", (NE + 1, NT), F32).ap()
    with ExitStack() as ctx:
        Scope.in_use.clear()
        g = Shared(nc, ctx, dram)
        load_constants(g)
        text_block(g)
        clear_semaphores(nc)
        delta_net(g)
        clear_semaphores(nc)
        router(g, "r0", "f0_router_w", "f0_router_b", NE + 1, "L0")
        biased_experts(g)
        clear_semaphores(nc)
        gated_scan(g)
        clear_semaphores(nc)
        router(g, "r1", "L1_ffn_W_gate_router", None, NE, "L1")
        moe(g, "m1", ["L1_ffn_Wg", "L1_ffn_Wu", "L1_ffn_Wd", "L1_ffn_Wg_s", "L1_ffn_Wu_s", "L1_ffn_Wd_s"], 192, True)
        clear_semaphores(nc)
        query_attention(g)
        clear_semaphores(nc)
        three_matrices(g)
        clear_semaphores(nc)
        full_attention(g)
        clear_semaphores(nc)
        router(g, "r3", "L3_ffn_Ws", "L3_ffn_bs", NE, "L3")
        moe(g, "m3", ["L3_ffn_Wg", "L3_ffn_Wu", "L3_ffn_Wd"], 688, False)
        clear_semaphores(nc)
        store_output(g, out)



def _blocks(w):
    n = w.shape[-1]
    k = w.shape[-2] // P
    lead = w.shape[:-2]
    return w.reshape(*lead, k, P, n).swapaxes(-3, -2)


def _swap(np, stripe):
    half = stripe // 2
    to = np.arange(P)
    m = np.zeros((P, P), np.float32)
    m[to // stripe * stripe + half + to % half, to] = 1.0
    return m


def _stack_selection(np, dh):
    heads = P // dh
    m = np.zeros((P, 4, heads, P), np.float32)
    d = np.arange(dh)
    for h in range(heads):
        for part, places in enumerate(((0, 2), (1,), (0, 1), (2,))):
            for place in places:
                m[h * dh + d, part, h, place * dh + d] = 1.0
    return m


def _stripes(np, w, heads, dh):
    w = w.reshape(-1, heads, dh)
    return np.concatenate([w, np.zeros_like(w)], axis=2).reshape(w.shape[0], -1)


def _delta_constants(np):
    r = np.arange(16)
    diff = np.zeros((16, P), np.float32)
    diff[r, r], diff[r ^ 1, r] = 1.0, -1.0
    pick = np.zeros((16, 16, P), np.float32)
    pick[r, r] = 1.0
    pick_den = np.zeros((P, 8, 16), np.float32)
    spread = np.zeros((16, 8, P), np.float32)
    for h in range(8):
        for j in range(2):
            pick_den[64 * j + 32, h, 2 * h + j] = 1.0
            spread[2 * h + j, h, 64 * j:64 * j + 32] = 1.0
    return {"c_diff": diff, "c_pick": pick, "c_pick_den": pick_den, "c_spread": spread}


def _decay_cap(np):
    slopes = np.array([0.5 ** (n + 1) for n in range(8)], dtype=np.float32)
    return np.repeat(np.exp(-slopes), 2)[:, None]


def _constants(np):
    at = np.arange(S_TXT, dtype=np.float32)[:, None]
    even = np.arange(0, D, 2, dtype=np.float32)[None]
    angle = at / np.power(np.float32(10000.0), np.float32(2.0) * even / np.float32(D))
    pos = np.zeros((S_TXT, D), np.float32)
    pos[:, 0::2], pos[:, 1::2] = np.sin(angle), np.cos(angle)
    freq = np.float32(1.0) / np.float32(10000.0) ** (np.arange(P, dtype=np.float32) / np.float32(P))
    turn = np.arange(S, dtype=np.float32)[:, None] * freq[None]
    rope = np.stack([np.round(np.cos(turn)), np.round(np.sin(turn))]).transpose(2, 0, 1)
    tok = np.arange(NT, dtype=np.float32).reshape(RT, RN).T
    return {
        "c_ident": np.eye(P, dtype=np.float32),
        "c_rank": np.broadcast_to(np.arange(NE, 0, -1, dtype=np.float32), (P, NE)),
        "c_tok": tok,
        "c_pos_txt": pos.reshape(S_TXT // P, P, D).swapaxes(0, 1),
        "c_rope": rope,
        "c_eye": np.eye(P, S, dtype=np.float32),
        **_delta_constants(np),
        "c_one_row": np.ones((1, NT), np.float32),
        "c_ones_row": (np.arange(P)[:, None] // 2 == 48).astype(np.float32),
        "c_sel16": _stack_selection(np, 16),
        "c_sel32": _stack_selection(np, 32),
        "c_mask_q": np.triu(np.full((P, P), -BIG, np.float32), 1),
        "c_mask_k": np.tril(np.full((P, P), -BIG, np.float32), -1),
        "c_swap32": _swap(np, 32),
        "c_swap64": _swap(np, 64),
    }


def _layouts(np, x):
    a = {}
    row = lambda n: x[n].reshape(1, -1)
    col = lambda n: x[n].reshape(-1, P).T
    a["L3_ffn_Ws"] = _blocks(x["L3_ffn_Ws"])
    a["L3_ffn_bs"] = row("L3_ffn_bs")
    for n in ("L3_ffn_Wg", "L3_ffn_Wu", "L1_ffn_Wg", "L1_ffn_Wu", "L1_ffn_Wg_s", "L1_ffn_Wu_s"):
        a[n] = _blocks(x[n])
    for n in ("L3_ffn_Wd", "L1_ffn_Wd", "L1_ffn_Wd_s"):
        a[n] = x[n]
    a["L1_ffn_W_gate_router"] = _blocks(x["L1_ffn_W_gate_router"])
    a["L1_ffn_expert_bias"] = row("L1_ffn_expert_bias")
    cat = lambda e, s: np.concatenate([x["L0_ffn_" + e], x["L0_ffn_" + s][None]])
    a["f0_w1"] = _blocks(cat("ew1", "sw1").swapaxes(1, 2))
    a["f0_w2"] = _blocks(cat("ew2", "sw2").swapaxes(1, 2))
    a["f0_w3"] = cat("ew3", "sw3").swapaxes(1, 2)
    each = lambda n: np.broadcast_to(x["L0_ffn_" + n], (NE, P))
    b3 = cat("eb3", "sb3").reshape(NE + 1, KD, P)
    a["f0_vec"] = np.stack([
        cat("eb1", "sb1"), cat("eb2", "sb2"),
        np.concatenate([each("sel_ln_g"), x["L0_ffn_s_ln_g"][None]]),
        np.concatenate([each("sel_ln_b"), x["L0_ffn_s_ln_b"][None]]), b3[:, 0], b3[:, 1]], axis=-1)
    a["f0_router_w"] = _blocks(np.concatenate([x["L0_ffn_eg_w"], x["L0_ffn_sg_w"]]).T)
    a["f0_router_b"] = np.concatenate([x["L0_ffn_eg_b"], x["L0_ffn_sg_b"]])[None]
    for n in ("L0_ffn_exp_bias", "L0_ffn_index_b", "L0_ffn_index_t"):
        a[n] = row(n)
    for n in ("L1_attn_W_in", "L1_attn_Wa", "L1_attn_Wb", "L1_attn_Wc", "L1_attn_Wo",
              "L2_ffn_weight", "L2_ffn_aux_weight1", "L2_ffn_aux_weight2"):
        a[n] = _blocks(x[n])
    a["s1_vec"] = np.concatenate([col("L1_attn_" + n) for n in ("b_in", "conv_b", "ba", "bb", "bc")], axis=1)
    for n in ("L1_attn_bo", "L1_attn_gamma", "L1_attn_beta", "L2_ffn_bias"):
        a[n] = col(n)
    a["L1_attn_conv_w"] = x["L1_attn_conv_w"].reshape(-1, P, 3).swapaxes(0, 1)
    wq = x["L2_attn_Wq"].swapaxes(0, 1).reshape(D, D)
    a["q2_wq"] = _blocks(wq)
    a["q2_wk"] = _blocks(np.pad(x["L2_attn_Wk"], ((0, 0), (0, P - 32))))
    a["q2_wv"] = _blocks(_stripes(np, x["L2_attn_Wv"], 1, 32))
    a["q2_wo"] = _stripes(np, x["L2_attn_Wp"].T, 8, 32).T.reshape(-1, P, D).swapaxes(0, 1)
    a["q2_bq"] = np.zeros((P, 2), np.float32)
    a["q2_bk"] = np.zeros((P, 1), np.float32)
    a["q2_bv"] = np.repeat(np.array([[0.0, 1.0]], np.float32), 32, axis=1)
    a["L2_attn_bp"] = col("L2_attn_bp")
    p = x["x"].reshape(NB, 3, 6, 16, 6, 16).transpose(1, 3, 5, 0, 2, 4).reshape(3 * 256, -1)
    a["patches"] = _blocks(p)
    a["L0_tok_W"] = _blocks(x["L0_tok_W"].T)
    a["tok_vec"] = np.stack([col("L0_tok_b"), col("L0_tok_cls_token")], axis=1)
    a["L0_tok_pos_embedding"] = x["L0_tok_pos_embedding"][0].T.reshape(KD, P, S_IMG).swapaxes(0, 1)
    a["x_txt"] = x["x_txt"].reshape(-1, P).T
    a["L0_txt_emb"] = x["L0_txt_emb"]
    w, b = x["L0_txt_in_proj_w"].T, x["L0_txt_in_proj_b"][None]
    part = lambda t, n: t[:, n * D:(n + 1) * D]
    a["ta_wq"], a["ta_wk"] = _blocks(part(w, 0)), _blocks(part(w, 1))
    a["ta_wv"] = _blocks(_stripes(np, part(w, 2), 16, 16))
    a["ta_bq"], a["ta_bk"] = (part(b, n).reshape(-1, P).T for n in range(2))
    a["ta_bv"] = np.where(np.arange(512)[None] % 32 >= 16, np.float32(1.0), _stripes(np, part(b, 2), 16, 16))
    a["ta_wo"] = _stripes(np, x["L0_txt_out_proj_w"], 16, 16).T.reshape(-1, P, D).swapaxes(0, 1)
    a["L0_txt_out_proj_b"] = col("L0_txt_out_proj_b")
    a["L0_txt_w1"] = _blocks(x["L0_txt_w1"].T)
    a["L0_txt_w2"] = _blocks(x["L0_txt_w2"].T)
    a["L0_txt_b1"] = col("L0_txt_b1")
    a["txt_vec"] = np.stack([col("L0_txt_" + n) for n in ("b2", "g1", "beta1", "g2", "beta2")], axis=1)
    t = lambda n: x["L0_attn_" + n].T
    a["dn_wqk"] = _blocks(np.concatenate([t("Wq"), t("Wk")], axis=1))
    a["dn_wvg"] = _blocks(np.concatenate([t("Wv"), t("Wgate")], axis=1))
    a["dn_wbm"] = _blocks(np.concatenate([t("Wbeta"), t("Wmix")], axis=1))
    wo = t("Wout").reshape(8, 32, D)
    z = np.zeros_like(wo)
    a["dn_wo"] = np.concatenate([wo, z, wo, z], axis=1).swapaxes(0, 1)
    a["dn_vec16"] = np.concatenate([x["L0_attn_bbeta"][:, None], x["L0_attn_bmix"][:, None], _decay_cap(np)], axis=1)
    a["dn_vec"] = np.stack([col("L0_attn_" + n) for n in ("bout", "ln_g", "ln_b")], axis=1)
    a["L0_attn_bgate"] = row("L0_attn_bgate")
    a["L3_attn_w_qkv"] = _blocks(x["L3_attn_w_qkv"])
    a["L3_attn_w_proj"] = _blocks(x["L3_attn_w_proj"])
    qkv_b = x["L3_attn_b_qkv"].reshape(3, KD, P)
    a["a3_vec"] = np.stack([col("L3_attn_g_norm"), qkv_b[0].T, qkv_b[1].T, col("L3_attn_b_proj")], axis=1)
    a["a3_bv"] = x["L3_attn_b_qkv"][None, 2 * D:]
    return a


def kernel(**inputs):
    import numpy as np
    import concourse.bacc as bacc
    from concourse.bass_utils import run_bass_kernel_spmd

    nc = bacc.Bacc("TRN2", target_bir_lowering=False, num_devices=1)
    laid = {**_layouts(np, inputs), **_constants(np)}
    arrays, dram = {}, {}
    for name, value in laid.items():
        value = np.ascontiguousarray(value)
        arrays[f"in_{name}"] = value
        dram[name] = nc.dram_tensor(f"in_{name}", value.shape, mybir.dt.from_np(value.dtype),
                                    kind="ExternalInput").ap()
    out = nc.dram_tensor("out_0", (NT, D), F32, kind="ExternalOutput").ap()
    program(nc, dram, out)
    result = run_bass_kernel_spmd(nc, [arrays], core_ids=[0]).results[0]["out_0"]
    return result.reshape(NB, S, D)
```

```python
from contextlib import ExitStack

import concourse.bass as bass
from concourse import mybir

F32 = mybir.dt.float32
F32R = mybir.dt.float32r
I32 = mybir.dt.int32
U32 = mybir.dt.uint32
ALU = mybir.AluOpType
ACT = mybir.ActivationFunctionType
AX_X = mybir.AxisListType.X

P = 128
D = 256
KD = D // P
NB = 4
S_IMG = 37
S_TXT = 512
S = S_IMG + S_TXT
NT = NB * S
CH = 6
CN = NT // CH
RT = 18
RN = NT // RT
NE = 8
SUB = CN // RN
BLOCKS = (2 * NT + NE * (CN - 1)) // CN
N_SEL = 512
SEL_T = N_SEL // P
VOCAB = 8000
BIG = 1.0e30


class Chain:

    def __init__(self, engine, semaphore):
        self.engine, self.semaphore = engine, semaphore
        self.base, self.n, self.turn = 0, 0, None

    def begin(self, i, per):
        self.turn, self.per, self.n = i, per, 0

    def end(self, turns):
        assert self.n == self.per, (self.n, self.per)
        self.base, self.n, self.turn = self.base + turns * self.per, 0, None

    def value(self):
        return self.base + self.n if self.turn is None else self.turn * self.per + (self.base + self.n)

    def step(self, instruction):
        self.n += 1
        instruction.then_inc(self.semaphore, 1)
        self.engine.wait_ge(self.semaphore, self.value())


class Scope:

    def __init__(self, nc, ctx, name):
        self.nc, self.ctx, self.name = nc, ctx, name

    def sb(self, name, shape, dt=F32):
        return self.ctx.enter_context(self.nc.sbuf_tensor(f"{self.name}_{name}", shape, dt))

    def ps(self, name, shape):
        return self.ctx.enter_context(self.nc.psum_tensor(f"{self.name}_{name}", shape, F32))

    def sem(self, name):
        handle = self.nc.alloc_semaphore(f"{self.name}_{name}")
        Scope.in_use.append(handle)
        return handle

    in_use = []


def clear_semaphores(nc):
    nc.clear_and_free_semaphores(Scope.in_use)
    Scope.in_use.clear()
    nc.all_engine_barrier()


def chunk(t, k, i):
    return t[:, k, bass.ds(i * CN, CN)]


def both(t, i):
    return t[:, :, bass.ds(i * CN, CN)]


def bank(ps, i, rows=P, n=CN):
    return ps[0:rows, bass.ds(i, 1), 0:n].rearrange("p a n -> p (a n)")


def bank2(ps, i, blocks, n=CN):
    return ps[:, bass.ds(i, 1), 0:n].to_broadcast([P, blocks, n])


class LayerNorm:

    def __init__(self, sc, tag, src, out, sq, rstd, avg, eps, ps, gamma=None, beta=None, rms=False,
                 chunks=CH, width=CN, final=None):
        self.n, self.w = chunks, width
        self.final = final or (lambda k, i: self.at(self.out, k, i))
        self.src, self.out, self.sq, self.rstd, self.avg, self.ps = src, out, sq, rstd, avg, ps
        self.eps, self.gamma, self.beta, self.rms = eps, gamma, beta, rms
        self.mean_ready = sc.sem(tag + "_mean_ready")
        self.centred = sc.sem(tag + "_centred")
        self.squared = sc.sem(tag + "_squared")
        self.var_ready = sc.sem(tag + "_var_ready")
        self.std_ready = sc.sem(tag + "_std_ready")
        self.rstd_ready = sc.sem(tag + "_rstd_ready")
        self.scaled = sc.sem(tag + "_scaled")
        self.normed = sc.sem(tag + "_normed")

    def at(self, t, k, i):
        return t[:, k, bass.ds(i * self.w, self.w)]

    def all(self, t, i):
        return t[:, :, bass.ds(i * self.w, self.w)]

    def tensor(self, nc, pe):
        if not self.rms:
            with nc.tensor.Fori(0, self.n) as i:
                for k in range(KD):
                    mm = nc.tensor.matmul(bank(self.ps, i, P, self.w), self.avg[:], self.at(self.src, k, i),
                                          start=(k == 0), stop=(k == KD - 1))
                mm.then_inc(self.mean_ready, 1)
        with nc.tensor.Fori(0, self.n) as i:
            pe.wait_ge(self.squared, i + 1)
            for k in range(KD):
                mm = nc.tensor.matmul(bank(self.ps, i, P, self.w), self.avg[:], self.at(self.sq, k, i),
                                      start=(k == 0), stop=(k == KD - 1))
            mm.then_inc(self.var_ready, 1)

    def scalar(self, nc, act):
        with nc.scalar.Fori(0, self.n) as i:
            if not self.rms:
                act.wait_ge(self.centred, i + 1)
            nc.scalar.activation(self.all(self.sq, i), self.all(self.src if self.rms else self.out, i),
                                 ACT.Square).then_inc(self.squared, 1)
        with nc.scalar.Fori(0, self.n) as i:
            act.wait_ge(self.var_ready, i + 1)
            nc.scalar.activation(self.rstd[:, bass.ds(i * self.w, self.w)], bank(self.ps, i, P, self.w), ACT.Sqrt,
                                 bias=self.eps).then_inc(self.std_ready, 1)

    def vector(self, nc, dve):
        if not self.rms:
            with nc.vector.Fori(0, self.n) as i:
                dve.wait_ge(self.mean_ready, i + 1)
                nc.vector.tensor_tensor(self.all(self.out, i), self.all(self.src, i), bank2(self.ps, i, KD, self.w),
                                        ALU.subtract).then_inc(self.centred, 1)
        with nc.vector.Fori(0, self.n) as i:
            r = self.rstd[:, bass.ds(i * self.w, self.w)]
            dve.wait_ge(self.std_ready, i + 1)
            nc.vector.reciprocal(r, r).then_inc(self.rstd_ready, 1)
            dve.wait_ge(self.rstd_ready, i + 1)
            rb = r.rearrange("p (a n) -> p a n", a=1).to_broadcast([P, KD, self.w])
            last = nc.vector.tensor_tensor(self.all(self.out, i), self.all(self.src if self.rms else self.out, i),
                                           rb, ALU.mult)
            if self.gamma is not None:
                last.then_inc(self.scaled, 1)
                dve.wait_ge(self.scaled, i + 1)
                for k in range(KD):
                    o, f = self.at(self.out, k, i), self.final(k, i)
                    g = self.gamma[:, k:k + 1]
                    if self.beta is None:
                        last = nc.vector.tensor_scalar(f, o, g, None, ALU.mult)
                    else:
                        last = nc.vector.tensor_scalar(f, o, g, self.beta[:, k:k + 1], ALU.mult, ALU.add)
            last.then_inc(self.normed, 1)


class Shared:

    def __init__(self, nc, ctx, dram):
        sc = Scope(nc, ctx, "g")
        self.nc, self.dram = nc, dram
        self.h = sc.sb("h", [P, KD, NT])
        self.xn = sc.sb("xn", [P, KD, NT])
        self.avg = sc.sb("avg", [P, P])
        self.ident = sc.sb("ident", [P, P])
        self.eps5 = sc.sb("eps5", [P, 1])
        self.eps6 = sc.sb("eps6", [P, 1])


def load_constants(g):
    nc = g.nc
    with ExitStack() as ctx:
        sc = Scope(nc, ctx, "cst")
        landed = sc.sem("landed")
        block = ctx.enter_context(nc.Block())

        @block.sync
        def _(sp):
            sp.dma_start(g.ident[:], g.dram["c_ident"]).then_inc(landed, 16)
            sp.wait_ge(landed, 16)

        @block.vector
        def _(dve):
            nc.vector.memset(g.avg[:], 1.0 / D)
            nc.vector.memset(g.eps5[:], 1.0e-5)
            nc.vector.memset(g.eps6[:], 1.0e-6)


def first_of_max(nc, chain, scores, top, ranked, hot, rank, top_rank, full=(RN, RT, NE)):
    full = list(full)
    chain.step(nc.vector.tensor_reduce(top[:], scores, AX_X, ALU.max))
    tb = top[:].rearrange("p (t a) -> p t a", a=1).to_broadcast(full)
    chain.step(nc.vector.tensor_tensor(ranked[:], scores, tb, ALU.is_ge))
    rb = rank[0:full[0], :].rearrange("p (a e) -> p a e", a=1).to_broadcast(full)
    chain.step(nc.vector.tensor_tensor(ranked[:], ranked[:], rb, ALU.mult))
    chain.step(nc.vector.tensor_reduce(top_rank[:], ranked[:], AX_X, ALU.max))
    kb = top_rank[:].rearrange("p (t a) -> p t a", a=1).to_broadcast(full)
    chain.step(nc.vector.tensor_tensor(hot, ranked[:], kb, ALU.is_equal))


def prefix_sum(nc, chain, out, values, keep):
    chain.step(nc.vector.tensor_tensor_scan(out, keep, values, 0.0, ALU.mult, ALU.add))


class Routes:

    def __init__(self, sc):
        self.pos = sc.sb("pos", [RN, 2, RT], I32)
        self.gate = sc.sb("gate", [RN, 2, RT])
        self.w_row = sc.sb("w_row", [P, BLOCKS], I32)
        self.token = sc.sb("token", [RN, BLOCKS * SUB], I32)


def router(g, tag, w_name, b_name, kind, routes):
    nc, dram = g.nc, g.dram
    with ExitStack() as ctx:
        sc = Scope(nc, ctx, tag)
        w = sc.sb("w", [P, KD, NE])
        bias = sc.sb("bias", [P, NE])
        ebias = sc.sb("ebias", [P, NE])
        rank = sc.sb("rank", [P, NE])
        lg = sc.sb("lg", [RN, RT, NE])
        score = sc.sb("score", [RN, RT, NE])
        chosen = sc.sb("chosen", [RN, RT, NE])
        ranked = sc.sb("ranked", [RN, RT, NE])
        hot1 = sc.sb("hot1", [RN, RT, NE])
        hot2 = sc.sb("hot2", [RN, RT, NE])
        count = sc.sb("count", [P, NE, RT])
        upto = sc.sb("upto", [P, NE, RT])
        keep = sc.sb("keep", [P, NE, RT])
        ones = sc.sb("ones", [P, NE])
        lower = sc.sb("lower", [P, P])
        all_ones = sc.sb("all_ones", [P, P])
        over = sc.sb("over", [P, NE, CH])
        steps = sc.sb("steps", [P, BLOCKS])
        lane = sc.sb("lane", [P, 1])
        blocks = sc.sb("blocks", [P, NE])
        upto_b = sc.sb("upto_b", [P, NE])
        reached = sc.sb("reached", [P, BLOCKS, NE])
        expert = sc.sb("expert", [P, BLOCKS])
        place = sc.sb("place", [RN, RT, NE])
        pos_f = sc.sb("pos_f", [RN, RT])
        tok = sc.sb("tok", [RN, RT])
        zero = sc.sb("zero", [BLOCKS * SUB, RN])
        slot_t = sc.sb("slot_t", [BLOCKS * SUB, RN])
        rows = sc.sb("rows", [RN, RT, D])
        sel_ready = sc.sem("sel_ready")
        counted = sc.sem("counted")
        placed = sc.sem("placed")
        zeroed = sc.sem("zeroed")
        cleared = sc.sem("cleared")
        scattered = sc.sem("scattered")
        listed = sc.sem("listed")
        rows_turned = sc.sem("rows_turned")
        rows_copied = sc.sem("rows_copied")
        top1 = sc.sb("top1", [RN, RT])
        top2 = sc.sb("top2", [RN, RT])
        top_rank = sc.sb("top_rank", [RN, RT])
        ex = sc.sb("ex", [RN, RT])
        den = sc.sb("den", [RN, RT])
        ps = sc.ps("ps", [P, 8, 512])
        sq = sc.sb("sq", [P, KD, NT])
        rstd = sc.sb("rstd", [P, NT])
        landed = sc.sem("landed")
        logits = sc.sem("logits")
        act_done = sc.sem("act_done")
        act_in = sc.sem("act_in")
        dve_own = sc.sem("dve_own")
        turned = sc.sem("turned")
        stored = sc.sem("stored")
        ln = LayerNorm(sc, "ln", g.h, g.xn, sq, rstd, g.avg, g.eps5[:], ps)
        n_loads = 8
        block = ctx.enter_context(nc.Block())

        @block.sync
        def _(sp):
            sp.dma_start(w[:], dram[w_name]).then_inc(landed, 16)
            sp.dma_start(rank[:], dram["c_rank"]).then_inc(landed, 16)
            if kind == "L1":
                sp.dma_start(ebias[:], dram["L1_ffn_expert_bias"].to_broadcast([P, NE])).then_inc(landed, 16)
            else:
                sp.dma_start(bias[:], dram[b_name].to_broadcast([P, NE])).then_inc(landed, 16)
            for a, name in ((keep, "c_keep"), (lower, "c_lower"), (steps, "c_steps"), (lane, "c_lane"),
                            (tok, "c_tok")):
                sp.dma_start(a[:], dram[name]).then_inc(landed, 16)
            sp.wait_ge(zeroed, 1)
            sp.dma_start(dram["s_slot"].rearrange("(c p) a -> c (p a)", p=RN), zero[:]).then_inc(cleared, 16)
            view = dram["s_rows"].rearrange("(t p) d -> p t d", p=RN)
            half = RT // 2
            for n in range(2):
                sp.wait_ge(rows_copied, half * (n + 1))
                sp.dma_start(view[:, half * n:half * (n + 1), :],
                             rows[:, half * n:half * (n + 1), :]).then_inc(stored, 16)
            sp.wait_ge(scattered, 16 * 2 * RT)
            sp.dma_start(slot_t[:], dram["s_slot"].rearrange("(c p) a -> c (p a)", p=RN)).then_inc(listed, 16)
            sp.wait_ge(stored, 32)

        @block.tensor
        def _(pe):
            ln.tensor(nc, pe)
            pe.wait_ge(landed, 16 * n_loads)
            pe.wait_ge(ln.normed, CH)
            pe.wait_ge(ln.std_ready, CH)
            for t in range(RT):
                for k in range(KD):
                    mm = nc.tensor.matmul(ps[0:RN, 7, t * NE:(t + 1) * NE],
                                          g.xn[:, k, t * RN:(t + 1) * RN], w[:, k, :],
                                          start=(k == 0), stop=(k == KD - 1))
            mm.then_inc(logits, 1)
            for t in range(RT):
                if t >= 3:
                    pe.wait_ge(rows_copied, t - 2)
                for k in range(KD):
                    mm = nc.tensor.transpose(ps[0:RN, t % 3, k * P:(k + 1) * P],
                                             g.xn[:, k, t * RN:(t + 1) * RN], g.ident[:])
                mm.then_inc(rows_turned, 1)
            pe.wait_ge(sel_ready, 1)
            chosen_all = chosen[:].rearrange("p t e -> p (t e)")
            nc.tensor.matmul(ps[0:RN, 4, 0:RT * NE], lower[0:RN, 0:RN], chosen_all, start=True, stop=True)
            nc.tensor.matmul(ps[:, 5, 0:RT * NE], all_ones[0:RN, :], chosen_all,
                             start=True, stop=True).then_inc(counted, 1)
            pe.wait_ge(listed, 16)
            nc.tensor.transpose(ps[0:RN, 6, 0:BLOCKS * SUB], slot_t[:],
                                g.ident[0:BLOCKS * SUB, 0:BLOCKS * SUB]).then_inc(turned, 1)

        @block.scalar
        def _(act):
            ln.scalar(nc, act)
            for t in range(RT):
                act.wait_ge(rows_turned, t + 1)
                nc.scalar.copy(rows[:, t, :], ps[0:RN, t % 3, 0:D]).then_inc(rows_copied, 1)
            if kind == "L3":
                act.wait_ge(act_in, 1)
                nc.scalar.activation(ex[:], ex[:], ACT.Exp).then_inc(act_done, 1)
            if kind == "L1":
                act.wait_ge(act_in, 1)
                nc.scalar.activation(score[:], lg[:], ACT.Sigmoid).then_inc(act_done, 1)

        @block.gpsimd
        def _(pool):
            pool.wait_ge(cleared, 16)
            pool.wait_ge(landed, 16 * n_loads)
            pool.wait_ge(placed, 2)
            for t in range(RT):
                for n in range(2):
                    nc.gpsimd.indirect_dma_start(
                        dram["s_slot"], bass.IndirectOffsetOnAxis(ap=routes.pos[:, n, t:t + 1], axis=0),
                        tok[:, t:t + 1], None).then_inc(scattered, 16)

        @block.vector
        def _(dve):
            v = nc.vector
            v.memset(ones[:], 1.0)
            v.memset(all_ones[:], 1.0)
            v.memset(zero[:], 0.0).then_inc(zeroed, 1)
            dve.wait_ge(zeroed, 1)
            ln.vector(nc, dve)
            chain = Chain(dve, dve_own)
            dve.wait_ge(landed, 16 * n_loads)
            dve.wait_ge(logits, 1)
            raw = ps[0:RN, 7, 0:RT * NE].rearrange("p (t e) -> p t e", e=NE)
            if kind == "L1":
                v.tensor_copy(lg[:], raw).then_inc(act_in, 1)
                dve.wait_ge(act_done, 1)
                eb = ebias[0:RN, :].rearrange("p (a e) -> p a e", a=1).to_broadcast([RN, RT, NE])
                chain.step(v.tensor_tensor(chosen[:], score[:], eb, ALU.add))
            else:
                bb = bias[0:RN, :].rearrange("p (a e) -> p a e", a=1).to_broadcast([RN, RT, NE])
                chain.step(v.tensor_tensor(lg[:], raw, bb, ALU.add))
            first_of_max(nc, chain, lg[:] if kind == "L3" else chosen[:], top1, ranked, hot1[:], rank, top_rank)
            src = lg if kind == "L3" else chosen
            chain.step(v.scalar_tensor_tensor(chosen[:], hot1[:], -BIG, src[:], ALU.mult, ALU.add))
            first_of_max(nc, chain, chosen[:], top2, ranked, hot2[:], rank, top_rank)
            chain.step(v.tensor_tensor(chosen[:], hot1[:], hot2[:], ALU.add))
            v.tensor_copy(den[:], top1[:]).then_inc(sel_ready, 1)
            dve.wait_ge(sel_ready, 1)
            gate1, gate2 = routes.gate[:, 0, :], routes.gate[:, 1, :]
            if kind == "L3":
                v.tensor_tensor(ex[:], top2[:], top1[:], ALU.subtract).then_inc(act_in, 1)
                dve.wait_ge(act_done, 1)
                chain.step(v.tensor_scalar(den[:], ex[:], 1.0, None, ALU.add))
                chain.step(v.reciprocal(gate1, den[:]))
                chain.step(v.tensor_tensor(gate2, ex[:], gate1, ALU.mult))
            if kind == "L1":
                for hot, top in ((hot1, top1), (hot2, top2)):
                    chain.step(v.tensor_tensor(ranked[:], hot[:], score[:], ALU.mult))
                    chain.step(v.tensor_reduce(top[:], ranked[:], AX_X, ALU.add))
                chain.step(v.tensor_tensor(den[:], top1[:], top2[:], ALU.add))
                chain.step(v.tensor_scalar(den[:], den[:], 1.0e-20, None, ALU.add))
                chain.step(v.reciprocal(den[:], den[:]))
                chain.step(v.tensor_tensor(gate1, top1[:], den[:], ALU.mult))
                chain.step(v.tensor_tensor(gate2, top2[:], den[:], ALU.mult))
            dve.wait_ge(counted, 1)
            by_expert = ps[:, 5, 0:RT * NE].rearrange("p (t e) -> p e t", e=NE)
            chain.step(v.tensor_copy(count[:], by_expert))
            flat = lambda t: t[:].rearrange("p e t -> p (e t)")
            prefix_sum(nc, chain, flat(upto), flat(count), flat(keep))
            total = upto[:, :, RT - 1:RT]
            over_at = steps[:, 0:CH].rearrange("p (a n) -> p a n", a=1).to_broadcast([P, NE, CH])
            chain.step(v.tensor_scalar(over[:], over_at, float(CN), None, ALU.mult))
            chain.step(v.tensor_tensor(over[:], total.to_broadcast([P, NE, CH]), over[:], ALU.is_gt))
            chain.step(v.tensor_reduce(blocks[:], over[:], AX_X, ALU.add))
            prefix_sum(nc, chain, upto_b[:], blocks[:], ones[:])
            chain.step(v.tensor_tensor(upto_b[:], upto_b[:], blocks[:], ALU.subtract))
            full = [P, BLOCKS, NE]
            fb = upto_b[:].rearrange("p (a e) -> p a e", a=1).to_broadcast(full)
            jb = steps[:].rearrange("p (j a) -> p j a", a=1).to_broadcast(full)
            chain.step(v.tensor_tensor(reached[:], fb, jb, ALU.is_le))
            chain.step(v.tensor_reduce(expert[:], reached[:], AX_X, ALU.add))
            chain.step(v.tensor_scalar(expert[:], expert[:], float(P), lane[:, 0:1], ALU.mult, ALU.add))
            chain.step(v.tensor_copy(routes.w_row[:], expert[:]))
            chain.step(v.tensor_tensor(upto[:], upto[:], count[:], ALU.subtract))
            chain.step(v.tensor_scalar(upto_b[:], upto_b[:], float(CN), None, ALU.mult))
            first = upto_b[0:RN, :].rearrange("p (a e) -> p a e", a=1).to_broadcast([RN, RT, NE])
            chain.step(v.tensor_tensor(place[:], ps[0:RN, 4, 0:RT * NE].rearrange("p (t e) -> p t e", e=NE),
                                       first, ALU.add))
            chain.step(v.tensor_tensor(place[:], place[:], upto[0:RN].rearrange("p e t -> p t e"), ALU.add))
            for n, hot in enumerate((hot1, hot2)):
                chain.step(v.tensor_tensor(ranked[:], place[:], hot[:], ALU.mult))
                chain.step(v.tensor_reduce(pos_f[:], ranked[:], AX_X, ALU.add))
                v.tensor_copy(routes.pos[:, n, :], pos_f[:]).then_inc(placed, 1)
                dve.wait_ge(placed, n + 1)
            dve.wait_ge(turned, 1)
            chain.step(v.tensor_copy(routes.token[:], ps[0:RN, 6, 0:BLOCKS * SUB]))


def routed_experts(g, tag, w_name, F, routes):
    nc, dram = g.nc, g.dram
    NF, FO, FT = hidden_tiles(F)
    W = 2 * KD * F + NF * D
    with ExitStack() as ctx:
        sc = Scope(nc, ctx, tag)
        w = [sc.sb(f"w{b}", [P, W]) for b in range(2)]
        rows = [sc.sb(f"rows{b}", [RN, SUB, D]) for b in range(2)]
        x = [sc.sb(f"x{b}", [P, KD, CN]) for b in range(2)]
        act_g = sc.sb("act_g", [P, 2, CN])
        hid = sc.sb("hid", [P, 2, CN])
        y = [sc.sb(f"y{b}", [RN, SUB, D]) for b in range(2)]
        ps_x = sc.ps("ps_x", [P, 512])
        ps_g = [sc.ps(f"ps_g{b}", [P, 512]) for b in range(2)]
        ps_u = [sc.ps(f"ps_u{b}", [P, 512]) for b in range(2)]
        ps_y = sc.ps("ps_y", [P, SUB, 512])
        w_landed = [sc.sem(f"w_landed{b}") for b in range(2)]
        rows_landed = [sc.sem(f"rows_landed{b}") for b in range(2)]
        turned = sc.sem("turned")
        x_ready = sc.sem("x_ready")
        g_ready = sc.sem("g_ready")
        u_ready = sc.sem("u_ready")
        silu_done = sc.sem("silu_done")
        hid_ready = sc.sem("hid_ready")
        y_ready = sc.sem("y_ready")
        y_copied = sc.sem("y_copied")
        y_stored = [sc.sem(f"y_stored{b}") for b in range(2)]
        block = ctx.enter_context(nc.Block())

        def weight(b, which, k, f):
            at = (which * KD + k) * F + FO[f]
            return w[b][:, at:at + FT[f]]

        def down_weight(b, f):
            at = 2 * KD * F + f * D
            return w[b][0:FT[f], at:at + D]

        def blocks(engine, first, middle):
            first()
            with engine.Fori(0, (BLOCKS - 1) // 2) as p:
                for b in range(2):
                    middle(p * 2 + b, b, p, False)
            for j in range((BLOCKS - 1) // 2 * 2, BLOCKS):
                middle(j, j % 2, j // 2, j == BLOCKS - 1)

        @block.gpsimd
        def _(pool):
            for j in range(BLOCKS):
                b = j % 2
                if j >= 2:
                    pool.wait_ge(turned, (j - 1) * KD)
                for s in range(SUB):
                    nc.gpsimd.indirect_dma_start(rows[b][:, s, :], None, dram["s_rows"], bass.IndirectOffsetOnAxis(
                        ap=routes.token[:, j * SUB + s:j * SUB + s + 1], axis=0)).then_inc(rows_landed[b], 16)
                if j >= 2:
                    pool.wait_ge(y_copied, j + 1)
                nc.gpsimd.indirect_dma_start(w[b][:], None, dram[w_name], bass.IndirectOffsetOnAxis(
                    ap=routes.w_row[:, j:j + 1], axis=0)).then_inc(w_landed[b], 16)

        @block.sync
        def _(sp):
            for j in range(BLOCKS):
                sp.wait_ge(y_copied, j + 3)
                sp.dma_start(dram["s_y"][j * CN:(j + 1) * CN, :].rearrange("(s p) d -> p s d", p=RN),
                             y[j % 2][:]).then_inc(y_stored[j % 2], 16)
            for b in range(2):
                sp.wait_ge(y_stored[b], 16 * ((BLOCKS + 1 - b) // 2 + 1))

        @block.tensor
        def _(pe):
            def turn(j, b, visit, k):
                pe.wait_ge(rows_landed[b], (visit + 1) * (16 * SUB))
                pe.wait_ge(x_ready, j * KD + (k + 1))
                for s in range(SUB):
                    mm = nc.tensor.transpose(ps_x[:, s * RN:(s + 1) * RN], rows[b][:, s, k * P:(k + 1) * P],
                                             g.ident[0:RN, 0:RN])
                mm.then_inc(turned, 1)

            def up(j, b, visit, f):
                if f == 0:
                    pe.wait_ge(w_landed[b], (visit + 1) * 16)
                    pe.wait_ge(x_ready, j * KD + (KD + 1))
                if not (isinstance(j, int) and j * NF + f == 0):
                    pe.wait_ge(hid_ready, j * NF + f)
                for which, ps, ready in ((0, ps_g, g_ready), (1, ps_u, u_ready)):
                    for k in range(KD):
                        mm = nc.tensor.matmul(ps[f % 2][0:FT[f], 0:CN], weight(b, which, k, f), x[b][:, k, :],
                                              start=(k == 0), stop=(k == KD - 1))
                    mm.then_inc(ready, 1)

            def down(j, b, f):
                if f == 0:
                    pe.wait_ge(y_copied, j + 2)
                pe.wait_ge(hid_ready, j * NF + (f + 2))
                for s in range(SUB):
                    mm = nc.tensor.matmul(ps_y[0:RN, s, 0:D], hid[0:FT[f], f % 2, s * RN:(s + 1) * RN],
                                          down_weight(b, f), start=(f == 0), stop=(f == NF - 1))
                if f == NF - 1:
                    mm.then_inc(y_ready, 1)

            def first():
                for k in range(KD):
                    turn(0, 0, 0, k)
                up(0, 0, 0, 0)

            def middle(j, b, visit, last):
                nxt = (j + 1, 1 - b, visit + b)
                for f in range(NF):
                    if not last and f < KD:
                        turn(*nxt, f)
                    if f + 1 < NF:
                        up(j, b, visit, f + 1)
                    elif not last:
                        up(*nxt, 0)
                    down(j, b, f)

            blocks(nc.tensor, first, middle)

        @block.scalar
        def _(act):
            nc.scalar.copy(act_g[:, 0, 0:1], g.ident[:, 0:1]).then_inc(x_ready, 1)
            act.wait_ge(x_ready, 1)

            def copy(j, b, visit, k):
                act.wait_ge(turned, j * KD + (k + 1))
                nc.scalar.copy(x[b][:, k, :], ps_x[:, 0:CN]).then_inc(x_ready, 1)

            def silu(j, f):
                act.wait_ge(g_ready, j * NF + (f + 1))
                nc.scalar.activation(act_g[0:FT[f], f % 2, :], ps_g[f % 2][0:FT[f], 0:CN],
                                     ACT.Silu).then_inc(silu_done, 1)

            def first():
                for k in range(KD):
                    copy(0, 0, 0, k)
                silu(0, 0)

            def middle(j, b, visit, last):
                for f in range(NF):
                    if not last and f < KD:
                        copy(j + 1, 1 - b, visit + b, f)
                    if f + 1 < NF:
                        silu(j, f + 1)
                    elif not last:
                        silu(j + 1, 0)

            blocks(nc.scalar, first, middle)

        @block.vector
        def _(dve):
            nc.vector.memset(hid[:, 0, 0:1], 0.0).then_inc(hid_ready, 1)
            dve.wait_ge(hid_ready, 1)
            for b in range(2):
                nc.vector.memset(y[b][:, 0, 0:1], 0.0).then_inc(y_stored[b], 16)
                dve.wait_ge(y_stored[b], 16)
            nc.vector.memset(y[0][:, 0, 0:1], 0.0).then_inc(y_copied, 2)
            dve.wait_ge(y_copied, 2)

            def hidden(j, f):
                dve.wait_ge(silu_done, j * NF + (f + 1))
                dve.wait_ge(u_ready, j * NF + (f + 1))
                nc.vector.tensor_tensor(hid[0:FT[f], f % 2, :], act_g[0:FT[f], f % 2, :],
                                        ps_u[f % 2][0:FT[f], 0:CN], ALU.mult).then_inc(hid_ready, 1)

            def middle(j, b, visit, last):
                for f in range(1, NF):
                    hidden(j, f)
                if not last:
                    hidden(j + 1, 0)
                dve.wait_ge(y_ready, j + 1)
                dve.wait_ge(y_stored[b], (visit + 1) * 16)
                nc.vector.tensor_copy(y[b][:], ps_y[0:RN, :, 0:D]).then_inc(y_copied, 1)

            blocks(nc.vector, lambda: hidden(0, 0), middle)


def add_rows(g, tag, routes):
    nc, dram = g.nc, g.dram
    TB = 512 // RN
    with ExitStack() as ctx:
        sc = Scope(nc, ctx, tag)
        y = sc.sb("y", [RN, 2, RT, D])
        ps = sc.ps("ps", [P, 8, 512])
        landed = [[sc.sem(f"landed{n}_{i}") for i in range(-(-RT // TB))] for n in range(2)]
        weighed = sc.sem("weighed")
        summed = sc.sem("summed")
        turned = sc.sem("turned")
        added = sc.sem("added")
        block = ctx.enter_context(nc.Block())
        groups = [(t, min(t + TB, RT)) for t in range(0, RT, TB)]

        @block.gpsimd
        def _(pool):
            for t in range(RT):
                for n in range(2):
                    nc.gpsimd.indirect_dma_start(
                        y[:, n, t, :], None, dram["s_y"],
                        bass.IndirectOffsetOnAxis(ap=routes.pos[:, n, t:t + 1], axis=0)).then_inc(landed[n][t // TB], 16)

        @block.scalar
        def _(act):
            for i, (lo, hi) in enumerate(groups):
                act.wait_ge(landed[0][i], 16 * (hi - lo))
                for t in range(lo, hi):
                    nc.scalar.activation(y[:, 0, t, :], y[:, 0, t, :], ACT.Copy,
                                         scale=routes.gate[:, 0, t:t + 1]).then_inc(weighed, 1)

        @block.tensor
        def _(pe):
            for i, (lo, hi) in enumerate(groups):
                if i >= 4:
                    pe.wait_ge(added, (i - 3) * KD)
                for t in range(lo, hi):
                    pe.wait_ge(summed, t + 1)
                    for k in range(KD):
                        mm = nc.tensor.transpose(ps[:, i % 4 * KD + k, (t - lo) * RN:(t - lo + 1) * RN],
                                                 y[:, 1, t, k * P:(k + 1) * P], g.ident[0:RN, 0:RN])
                mm.then_inc(turned, 1)

        @block.vector
        def _(dve):
            def add(i):
                lo, hi = groups[i]
                dve.wait_ge(turned, i + 1)
                for k in range(KD):
                    o = g.h[:, k, lo * RN:hi * RN]
                    nc.vector.tensor_tensor(o, o, ps[:, i % 4 * KD + k, 0:(hi - lo) * RN], ALU.add).then_inc(added, 1)

            for i, (lo, hi) in enumerate(groups):
                dve.wait_ge(landed[1][i], 16 * (hi - lo))
                for t in range(lo, hi):
                    dve.wait_ge(weighed, t + 1)
                    nc.vector.scalar_tensor_tensor(y[:, 1, t, :], y[:, 1, t, :], routes.gate[:, 1, t:t + 1],
                                                   y[:, 0, t, :], ALU.mult, ALU.add).then_inc(summed, 1)
                if i > 0:
                    add(i - 1)
            add(len(groups) - 1)


def mixture(g, tag, w_name, F, kind, w_router, b_router, shared=None):
    with ExitStack() as ctx:
        routes = Routes(Scope(g.nc, ctx, tag + "r"))
        router(g, tag + "s", w_router, b_router, kind, routes)
        if shared is not None:
            dense_expert(g, tag + "d", shared, F)
        routed_experts(g, tag + "e", w_name, F, routes)
        add_rows(g, tag + "a", routes)


def hidden_tiles(F):
    n = -(-F // P)
    starts = [F * f // n for f in range(n + 1)]
    return n, starts[:n], [starts[f + 1] - starts[f] for f in range(n)]


def dense_expert(g, tag, names, F):
    nc, dram = g.nc, g.dram
    NF, FO, FT = hidden_tiles(F)
    with ExitStack() as ctx:
        sc = Scope(nc, ctx, tag)
        wg = sc.sb("wg", [P, KD, F])
        wu = sc.sb("wu", [P, KD, F])
        wd = sc.sb("wd", [P, NF, D])
        act_g = sc.sb("act_g", [P, 2, CN])
        hid = sc.sb("hid", [P, 2, CN])
        ps_g = [sc.ps(f"ps_g{b}", [P, 512]) for b in range(2)]
        ps_u = [sc.ps(f"ps_u{b}", [P, 512]) for b in range(2)]
        ps_y = sc.ps("ps_y", [P, KD, 512])
        w_landed = sc.sem("w_landed")
        g_ready = sc.sem("g_ready")
        u_ready = sc.sem("u_ready")
        silu_done = sc.sem("silu_done")
        hid_ready = sc.sem("hid_ready")
        y_ready = sc.sem("y_ready")
        y_added = sc.sem("y_added")
        block = ctx.enter_context(nc.Block())
        units = [(c, f) for c in range(CH) for f in range(NF)]

        @block.sync
        def _(sp):
            sp.dma_start(wg[:], dram[names[0]]).then_inc(w_landed, 16)
            sp.dma_start(wu[:], dram[names[1]]).then_inc(w_landed, 16)
            for f in range(NF):
                sp.dma_start(wd[0:FT[f], f, :], dram[names[2]][FO[f]:FO[f] + FT[f], :]).then_inc(w_landed, 16)

        @block.tensor
        def _(pe):
            def up(q):
                c, f = units[q]
                if q >= 2:
                    pe.wait_ge(hid_ready, q - 1)
                for ps, w, ready in ((ps_g, wg, g_ready), (ps_u, wu, u_ready)):
                    for k in range(KD):
                        mm = nc.tensor.matmul(ps[q % 2][0:FT[f], 0:CN], w[:, k, FO[f]:FO[f] + FT[f]],
                                              g.xn[:, k, c * CN:(c + 1) * CN], start=(k == 0), stop=(k == KD - 1))
                    mm.then_inc(ready, 1)

            pe.wait_ge(w_landed, 16 * (2 + NF))
            up(0)
            for q, (c, f) in enumerate(units):
                if q + 1 < len(units):
                    up(q + 1)
                if f == 0 and c > 0:
                    pe.wait_ge(y_added, c)
                pe.wait_ge(hid_ready, q + 1)
                for m in range(KD):
                    mm = nc.tensor.matmul(ps_y[:, m, 0:CN], wd[0:FT[f], f, m * P:(m + 1) * P],
                                          hid[0:FT[f], q % 2, :], start=(f == 0), stop=(f == NF - 1))
                if f == NF - 1:
                    mm.then_inc(y_ready, 1)

        @block.scalar
        def _(act):
            for q, (c, f) in enumerate(units):
                act.wait_ge(g_ready, q + 1)
                if q >= 2:
                    act.wait_ge(hid_ready, q - 1)
                nc.scalar.activation(act_g[0:FT[f], q % 2, :], ps_g[q % 2][0:FT[f], 0:CN],
                                     ACT.Silu).then_inc(silu_done, 1)

        @block.vector
        def _(dve):
            def hidden(q):
                f = units[q][1]
                dve.wait_ge(silu_done, q + 1)
                dve.wait_ge(u_ready, q + 1)
                nc.vector.tensor_tensor(hid[0:FT[f], q % 2, :], act_g[0:FT[f], q % 2, :],
                                        ps_u[q % 2][0:FT[f], 0:CN], ALU.mult).then_inc(hid_ready, 1)

            hidden(0)
            for q, (c, f) in enumerate(units):
                if q + 1 < len(units):
                    hidden(q + 1)
                if f == NF - 1:
                    dve.wait_ge(y_ready, c + 1)
                    at = slice(c * CN, (c + 1) * CN)
                    nc.vector.tensor_tensor(g.h[:, :, at], g.h[:, :, at], ps_y[:, :, 0:CN], ALU.add).then_inc(y_added, 1)


def biased_experts(g, tag, x, out_t, first_e, N, chunks, width, gated):
    nc, dram = g.nc, g.dram
    H = P
    CH, CN, NT = chunks, width, chunks * width

    def chunk(t, k, i):
        return t[:, k, bass.ds(i * CN, CN)]

    def both(t, i):
        return t[:, :, bass.ds(i * CN, CN)]

    with ExitStack() as ctx:
        sc = Scope(nc, ctx, tag)
        w1 = [sc.sb(f"w1{b}", [P, KD, H]) for b in range(2)]
        w2 = [sc.sb(f"w2{b}", [P, KD, H]) for b in range(2)]
        w3 = [sc.sb(f"w3{b}", [P, D]) for b in range(2)]
        vec = [sc.sb(f"vec{b}", [P, 6]) for b in range(2)]
        gate = [sc.sb(f"gate{b}", [P, NT]) for b in range(2)]
        hid = [sc.sb(f"hid{b}", [P, NT]) for b in range(2)]
        avg_h = sc.sb("avg_h", [P, P])
        act_a = sc.sb("act_a", [P, 2, CN])
        sq = sc.sb("sq", [P, NT])
        rstd = sc.sb("rstd", [P, NT])
        z = sc.sb("z", [P, NT])
        part = sc.sb("part", [P, KD, CN])
        ps_a = [sc.ps(f"ps_a{j}", [P, 512]) for j in range(2)]
        ps_b = [sc.ps(f"ps_b{j}", [P, 512]) for j in range(2)]
        ps_m = [sc.ps(f"ps_m{j}", [P, 512]) for j in range(2)]
        ps_y = sc.ps("ps_y", [P, KD, 512])
        w_landed = [sc.sem(f"w_landed{b}") for b in range(2)]
        avg_set = sc.sem("avg_set")
        a_ready = sc.sem("a_ready")
        b_ready = sc.sem("b_ready")
        silu_done = sc.sem("silu_done")
        s_ready = sc.sem("s_ready")
        mean_ready = sc.sem("mean_ready")
        centred = sc.sem("centred")
        squared = sc.sem("squared")
        var_ready = sc.sem("var_ready")
        eps_added = sc.sem("eps_added")
        recip_done = sc.sem("recip_done")
        rstd_ready = sc.sem("rstd_ready")
        z_scaled = sc.sem("z_scaled")
        z_ready = sc.sem("z_ready")
        y_ready = sc.sem("y_ready")
        y_used = sc.sem("y_used")
        h_added = sc.sem("h_added")
        n_loads = 16 * (5 if gated else 4)
        block = ctx.enter_context(nc.Block())

        def schedule(engine, up, out, var):
            up(0, 0, 0)
            var(0, 0, 0)
            if N == 1:
                out(0, 0, 0)
                return
            with engine.Fori(0, (N - 1) // 2) as p:
                up(p * 2 + 1, 1, p)
                out(p * 2, 0, p)
                var(p * 2 + 1, 1, p)
                up(p * 2 + 2, 0, p + 1)
                out(p * 2 + 1, 1, p)
                var(p * 2 + 2, 0, p + 1)
            out(N - 1, (N - 1) % 2, (N - 1) // 2)

        def load(sp, n, b):
            e = n + first_e
            for t, name in ((w1, "f0_w1"), (w2, "f0_w2")):
                sp.dma_start(t[b][:], dram[name][bass.ds(e, 1)].rearrange("a p k f -> (a p) k f")
                             ).then_inc(w_landed[b], 16)
            for t, name in ((w3, "f0_w3"), (vec, "f0_vec")):
                sp.dma_start(t[b][:], dram[name][bass.ds(e, 1)].rearrange("a p f -> (a p) f")
                             ).then_inc(w_landed[b], 16)
            if gated:
                sp.dma_start(gate[b][:], dram["s_gate"][bass.ds(e, 1), :].to_broadcast([P, NT])
                             ).then_inc(w_landed[b], 16)

        @block.sync
        def _(sp):
            load(sp, 0, 0)
            if N == 1:
                return
            load(sp, 1, 1)
            with nc.sync.Fori(0, (N - 3) // 2) as p:
                for b in range(2):
                    n = nc.sync.snap(p * 2 + (b + 2))
                    sp.wait_ge(y_used, p * (2 * CH) + ((b + 1) * CH + 1))
                    load(sp, n, b)
            sp.wait_ge(y_used, (N - 2) * CH + 1)
            load(sp, N - 1, (N - 1) % 2)

        @block.tensor
        def _(pe):
            pe.wait_ge(avg_set, 1)

            def up(e, b, visit):
                with nc.tensor.Fori(0, CH // 2) as cc:
                    pe.wait_ge(w_landed[b], (visit + 1) * n_loads)
                    for j in range(2):
                        pe.wait_ge(s_ready, e * CH + cc * 2 + (j + 1))
                        for ps, w, ready in ((ps_a, w1, a_ready), (ps_b, w2, b_ready)):
                            for k in range(KD):
                                mm = nc.tensor.matmul(ps[j][:, 0:CN], w[b][:, k, :], chunk(x, k, cc * 2 + j),
                                                      start=(k == 0), stop=(k == KD - 1))
                            mm.then_inc(ready, 1)
                    for j in range(2):
                        pe.wait_ge(s_ready, e * CH + cc * 2 + (j + 3))
                        nc.tensor.matmul(ps_m[j][:, 0:CN], avg_h[:], hid[b][:, bass.ds((cc * 2 + j) * CN, CN)],
                                         start=True, stop=True).then_inc(mean_ready, 1)

            def out(e, b, visit):
                with nc.tensor.Fori(0, CH) as c:
                    pe.wait_ge(z_ready, e + 1)
                    pe.wait_ge(y_used, e * CH + c + 1)
                    for m in range(KD):
                        mm = nc.tensor.matmul(ps_y[:, m, 0:CN], w3[b][:, m * P:(m + 1) * P],
                                              z[:, bass.ds(c * CN, CN)], start=True, stop=True)
                    mm.then_inc(y_ready, 1)

            def var(e, b, visit):
                with nc.tensor.Fori(0, CH // 2) as cc:
                    pe.wait_ge(squared, (e + 1) * CH)
                    for j in range(2):
                        pe.wait_ge(eps_added, e * CH + cc * 2 + (j + 1))
                        nc.tensor.matmul(ps_m[j][:, 0:CN], avg_h[:], sq[:, bass.ds((cc * 2 + j) * CN, CN)],
                                         start=True, stop=True).then_inc(var_ready, 1)

            schedule(nc.tensor, up, out, var)

        @block.scalar
        def _(act):
            def up(e, b, visit):
                with nc.scalar.Fori(0, CH // 2) as cc:
                    act.wait_ge(w_landed[b], (visit + 1) * n_loads)
                    for j in range(2):
                        act.wait_ge(a_ready, e * CH + cc * 2 + (j + 1))
                        nc.scalar.activation(act_a[:, j, :], ps_a[j][:, 0:CN], ACT.Silu,
                                             bias=vec[b][:, 0:1]).then_inc(silu_done, 1)
                    for j in range(2):
                        act.wait_ge(centred, e * CH + cc * 2 + (j + 1))
                        at = bass.ds((cc * 2 + j) * CN, CN)
                        nc.scalar.activation(sq[:, at], hid[b][:, at], ACT.Square).then_inc(squared, 1)

            def var(e, b, visit):
                act.wait_ge(recip_done, e + 1)
                nc.scalar.activation(rstd[:], rstd[:], ACT.Sqrt).then_inc(rstd_ready, 1)

            def out(e, b, visit):
                act.wait_ge(z_scaled, e + 1)
                nc.scalar.activation(z[:], z[:], ACT.Identity, scale=vec[b][:, 2:3],
                                     bias=vec[b][:, 3:4]).then_inc(z_ready, 1)

            schedule(nc.scalar, up, out, var)

        @block.gpsimd
        def _(pool):
            def var(e, b, visit):
                pool.wait_ge(w_landed[b], (visit + 1) * n_loads)
                pool.wait_ge(rstd_ready, e + 1)
                nc.gpsimd.tensor_tensor(z[:], hid[b][:], rstd[:], ALU.mult).then_inc(z_scaled, 1)

            schedule(nc.gpsimd, lambda *a: None, lambda *a: None, var)

        @block.vector
        def _(dve):
            nc.vector.memset(part[:, 0, 0:1], 0.0).then_inc(s_ready, 2)
            nc.vector.memset(part[:, 0, 1:2], 0.0).then_inc(eps_added, 2)
            nc.vector.memset(part[:, 0, 2:3], 0.0).then_inc(y_used, 1)
            nc.vector.memset(part[:, 0, 3:4], 0.0).then_inc(h_added, 1)
            nc.vector.memset(avg_h[:], 1.0 / H).then_inc(avg_set, 1)

            def up(e, b, visit):
                with nc.vector.Fori(0, CH // 2) as cc:
                    dve.wait_ge(w_landed[b], (visit + 1) * n_loads)
                    for j in range(2):
                        dve.wait_ge(silu_done, e * CH + cc * 2 + (j + 1))
                        dve.wait_ge(b_ready, e * CH + cc * 2 + (j + 1))
                        nc.vector.scalar_tensor_tensor(hid[b][:, bass.ds((cc * 2 + j) * CN, CN)],
                                                       ps_b[j][:, 0:CN], vec[b][:, 1:2], act_a[:, j, :],
                                                       ALU.add, ALU.mult).then_inc(s_ready, 1)
                    for j in range(2):
                        dve.wait_ge(mean_ready, e * CH + cc * 2 + (j + 1))
                        at = hid[b][:, bass.ds((cc * 2 + j) * CN, CN)]
                        nc.vector.tensor_tensor(at, at, ps_m[j][:, 0:CN], ALU.subtract).then_inc(centred, 1)

            def out(e, b, visit):
                with nc.vector.Fori(0, CH) as c:
                    dve.wait_ge(y_ready, e * CH + c + 1)
                    dve.wait_ge(h_added, e * CH + c + 1)
                    for m in range(KD):
                        p, bias = ps_y[:, m, 0:CN], vec[b][:, 4 + m:5 + m]
                        if gated:
                            last = nc.vector.scalar_tensor_tensor(part[:, m, :], p, bias,
                                                                  gate[b][:, bass.ds(c * CN, CN)], ALU.add, ALU.mult)
                        else:
                            last = nc.vector.tensor_scalar(part[:, m, :], p, bias, None, ALU.add)
                    last.then_inc(y_used, 1)
                    dve.wait_ge(y_used, e * CH + c + 2)
                    nc.vector.tensor_tensor(both(out_t, c), both(out_t, c), part[:], ALU.add).then_inc(h_added, 1)

            def var(e, b, visit):
                with nc.vector.Fori(0, CH // 2) as cc:
                    for j in range(2):
                        dve.wait_ge(var_ready, e * CH + cc * 2 + (j + 1))
                        nc.vector.tensor_scalar(rstd[:, bass.ds((cc * 2 + j) * CN, CN)], ps_m[j][:, 0:CN],
                                                1.0e-5, None, ALU.add).then_inc(eps_added, 1)
                dve.wait_ge(eps_added, e * CH + (CH + 2))
                nc.vector.reciprocal(rstd[:], rstd[:]).then_inc(recip_done, 1)

            schedule(nc.vector, up, out, var)


def selected_ffn(g):
    with ExitStack() as ctx:
        sc = Scope(g.nc, ctx, "f0")
        xs = sc.sb("xs", [P, KD, N_SEL])
        ys = sc.sb("ys", [P, KD, N_SEL])
        row = sc.sb("row", [P, SEL_T], I32)
        select(g, xs, ys, row)
        biased_experts(g, "f0e", xs, ys, 0, NE + 1, 2, N_SEL // 2, True)
        scatter_rows(g, ys, row)
    biased_experts(g, "f0s", g.xn, g.h, NE, 1, CH, CN, False)
    add_extra(g)


def select(g, xs, ys, row):
    nc, dram = g.nc, g.dram
    with ExitStack() as ctx:
        sc = Scope(nc, ctx, "f0r")
        w = sc.sb("w", [P, KD, NE + 1])
        bias = sc.sb("bias", [P, NE + 1])
        ebias = sc.sb("ebias", [P, NE])
        rank = sc.sb("rank", [P, NE])
        idx_i = sc.sb("idx_i", [P, 2, SEL_T], I32)
        idx = sc.sb("idx", [P, 2, SEL_T])
        bad = sc.sb("bad", [P, 2, SEL_T])
        neg = sc.sb("neg", [P, 2, SEL_T])
        flat = sc.sb("flat", [P, SEL_T])
        target = sc.sb("target", [P, SEL_T])
        source = sc.sb("source", [P, SEL_T], I32)
        rows = sc.sb("rows", [RN, RT, D])
        picked = sc.sb("picked", [P, SEL_T, D])
        lg = sc.sb("lg", [P, SEL_T, NE + 1])
        chosen = sc.sb("chosen", [P, SEL_T, NE])
        ranked = sc.sb("ranked", [P, SEL_T, NE])
        hot = sc.sb("hot", [P, SEL_T, NE])
        gate = sc.sb("gate", [P, SEL_T, NE + 1])
        top = sc.sb("top", [P, SEL_T])
        top_rank = sc.sb("top_rank", [P, SEL_T])
        ex = sc.sb("ex", [P, SEL_T])
        gate_t = sc.sb("gate_t", [NE + 1, N_SEL])
        zero = sc.sb("zero", [RN, RT, D])
        sq = sc.sb("sq", [P, KD, NT])
        rstd = sc.sb("rstd", [P, NT])
        ps = sc.ps("ps", [P, 8, 512])
        landed = sc.sem("landed")
        zeroed = sc.sem("zeroed")
        stored = sc.sem("stored")
        rows_turned = sc.sem("rows_turned")
        rows_copied = sc.sem("rows_copied")
        source_ready = sc.sem("source_ready")
        gathered = [sc.sem(f"gathered{t}") for t in range(SEL_T)]
        x_turned = sc.sem("x_turned")
        x_copied = sc.sem("x_copied")
        logits = sc.sem("logits")
        act_in = sc.sem("act_in")
        act_done = sc.sem("act_done")
        gates = sc.sem("gates")
        gates_turned = sc.sem("gates_turned")
        copied = sc.sem("copied")
        gates_stored = sc.sem("gates_stored")
        own = sc.sem("own")
        ln = LayerNorm(sc, "ln", g.h, g.xn, sq, rstd, g.avg, g.eps5[:], ps)
        block = ctx.enter_context(nc.Block())
        half = RT // 2
        loads = [(idx_i[:], dram["f0_index"]), (w[:], dram["f0_router_w"]),
                 (bias[:], dram["f0_router_b"].to_broadcast([P, NE + 1])),
                 (ebias[:], dram["L0_ffn_exp_bias"].to_broadcast([P, NE])), (rank[:], dram["c_rank"])]

        @block.sync
        def _(sp):
            for a, b in loads:
                sp.dma_start(a, b).then_inc(landed, 16)
            sp.wait_ge(zeroed, 1)
            sp.dma_start(dram["s_extra"][0:NT, :].rearrange("(t p) d -> p t d", p=RN), zero[:]).then_inc(stored, 16)
            view = dram["s_rows"].rearrange("(t p) d -> p t d", p=RN)
            for n in range(2):
                sp.wait_ge(rows_copied, half * (n + 1))
                sp.dma_start(view[:, half * n:half * (n + 1), :],
                             rows[:, half * n:half * (n + 1), :]).then_inc(stored, 16)
            sp.wait_ge(copied, 1)
            sp.dma_start(dram["s_gate"], gate_t[:]).then_inc(gates_stored, 16)
            sp.wait_ge(gates_stored, 16)

        @block.tensor
        def _(pe):
            ln.tensor(nc, pe)
            pe.wait_ge(ln.normed, CH)
            pe.wait_ge(ln.std_ready, CH)
            for t in range(RT):
                if t >= 3:
                    pe.wait_ge(rows_copied, t - 2)
                for k in range(KD):
                    mm = nc.tensor.transpose(ps[0:RN, t % 3, k * P:(k + 1) * P],
                                             g.xn[:, k, t * RN:(t + 1) * RN], g.ident[:])
                mm.then_inc(rows_turned, 1)
            for t in range(SEL_T):
                pe.wait_ge(gathered[t], 16)
                for k in range(KD):
                    mm = nc.tensor.transpose(ps[:, 3 + k, t * P:(t + 1) * P], picked[:, t, k * P:(k + 1) * P],
                                             g.ident[:])
            mm.then_inc(x_turned, 1)
            pe.wait_ge(landed, 16 * len(loads))
            pe.wait_ge(x_copied, KD)
            for t in range(SEL_T):
                for k in range(KD):
                    mm = nc.tensor.matmul(ps[:, 5, t * (NE + 1):(t + 1) * (NE + 1)], xs[:, k, t * P:(t + 1) * P],
                                          w[:, k, :], start=(k == 0), stop=(k == KD - 1))
            mm.then_inc(logits, 1)
            pe.wait_ge(gates, 1)
            for t in range(SEL_T):
                mm = nc.tensor.transpose(ps[0:NE + 1, 6, t * P:(t + 1) * P], gate[:, t, :], g.ident[:])
            mm.then_inc(gates_turned, 1)

        @block.scalar
        def _(act):
            ln.scalar(nc, act)
            for t in range(RT):
                act.wait_ge(rows_turned, t + 1)
                nc.scalar.copy(rows[:, t, :], ps[0:RN, t % 3, 0:D]).then_inc(rows_copied, 1)
            act.wait_ge(act_in, 1)
            nc.scalar.activation(lg[:], lg[:], ACT.Sigmoid).then_inc(act_done, 1)
            act.wait_ge(act_in, 2)
            nc.scalar.activation(ex[:], ex[:], ACT.Sigmoid).then_inc(act_done, 1)

        @block.gpsimd
        def _(pool):
            nc.gpsimd.memset(zero[:], 0.0).then_inc(zeroed, 1)
            nc.gpsimd.memset(ys[:], 0.0)
            pool.wait_ge(source_ready, 1)
            pool.wait_ge(stored, 16 * 3)
            for t in range(SEL_T):
                nc.gpsimd.indirect_dma_start(picked[:, t, :], None, dram["s_rows"], bass.IndirectOffsetOnAxis(
                    ap=source[:, t:t + 1], axis=0)).then_inc(gathered[t], 16)

        @block.vector
        def _(dve):
            v = nc.vector
            ln.vector(nc, dve)
            chain = Chain(dve, own)
            dve.wait_ge(landed, 16 * len(loads))
            chain.step(v.tensor_copy(idx[:], idx_i[:]))
            for n, size in enumerate((NB, S)):
                i, b = idx[:, n, :], bad[:, n, :]
                chain.step(v.tensor_scalar(neg[:, n, :], i, 0.0, float(size), ALU.is_lt, ALU.mult))
                chain.step(v.tensor_tensor(i, i, neg[:, n, :], ALU.add))
                chain.step(v.tensor_scalar(b, i, float(size), None, ALU.is_ge))
                chain.step(v.scalar_tensor_tensor(b, i, 0.0, b, ALU.is_lt, ALU.add))
                chain.step(v.tensor_scalar(i, i, 0.0, float(size - 1), ALU.max, ALU.min))
            chain.step(v.scalar_tensor_tensor(flat[:], idx[:, 0, :], float(S), idx[:, 1, :], ALU.mult, ALU.add))
            v.tensor_copy(source[:], flat[:]).then_inc(source_ready, 1)
            chain.step(v.tensor_tensor(target[:], bad[:, 0, :], bad[:, 1, :], ALU.add))
            chain.step(v.tensor_scalar(target[:], target[:], float(NT), None, ALU.mult))
            chain.step(v.tensor_tensor(target[:], target[:], flat[:], ALU.add))
            chain.step(v.tensor_scalar(target[:], target[:], float(NT), None, ALU.min))
            chain.step(v.tensor_copy(row[:], target[:]))
            dve.wait_ge(x_turned, 1)
            for k in range(KD):
                v.tensor_copy(xs[:, k, :], ps[:, 3 + k, :]).then_inc(x_copied, 1)
            dve.wait_ge(logits, 1)
            full = [P, SEL_T, NE]
            bb = bias[:].rearrange("p (a e) -> p a e", a=1).to_broadcast([P, SEL_T, NE + 1])
            v.tensor_tensor(lg[:], ps[:, 5, 0:SEL_T * (NE + 1)].rearrange("p (t e) -> p t e", t=SEL_T), bb,
                            ALU.add).then_inc(act_in, 1)
            dve.wait_ge(act_done, 1)
            eb = ebias[:].rearrange("p (a e) -> p a e", a=1).to_broadcast(full)
            chain.step(v.tensor_tensor(chosen[:], lg[:, :, 0:NE], eb, ALU.add))
            first_of_max(nc, chain, chosen[:], top, ranked, hot[:], rank, top_rank, full)
            chain.step(v.tensor_tensor(ranked[:], hot[:], lg[:, :, 0:NE], ALU.mult))
            chain.step(v.tensor_reduce(top[:], ranked[:], AX_X, ALU.add))
            v.tensor_tensor(ex[:], top[:], lg[:, :, NE:NE + 1].rearrange("p t a -> p (t a)"),
                            ALU.subtract).then_inc(act_in, 1)
            dve.wait_ge(act_done, 2)
            exb = ex[:].rearrange("p (t a) -> p t a", a=1).to_broadcast(full)
            chain.step(v.tensor_tensor(gate[:, :, 0:NE], hot[:], exb, ALU.mult))
            v.tensor_scalar(gate[:, :, NE:NE + 1].rearrange("p t a -> p (t a)"), ex[:], -1.0, None,
                            ALU.mult).then_inc(gates, 1)
            dve.wait_ge(gates_turned, 1)
            v.tensor_copy(gate_t[:], ps[0:NE + 1, 6, :]).then_inc(copied, 1)


def scatter_rows(g, ys, row):
    nc, dram = g.nc, g.dram
    with ExitStack() as ctx:
        sc = Scope(nc, ctx, "f0w")
        rows = sc.sb("rows", [P, SEL_T, D])
        ps = sc.ps("ps", [P, SEL_T, 512])
        turned = sc.sem("turned")
        copied = sc.sem("copied")
        stored = sc.sem("stored")
        block = ctx.enter_context(nc.Block())

        @block.tensor
        def _(pe):
            for t in range(SEL_T):
                for k in range(KD):
                    mm = nc.tensor.transpose(ps[:, t, k * P:(k + 1) * P], ys[:, k, t * P:(t + 1) * P], g.ident[:])
                mm.then_inc(turned, 1)

        @block.vector
        def _(dve):
            for t in range(SEL_T):
                dve.wait_ge(turned, t + 1)
                nc.vector.tensor_copy(rows[:, t, :], ps[:, t, 0:D]).then_inc(copied, 1)

        @block.gpsimd
        def _(pool):
            for t in range(SEL_T):
                pool.wait_ge(copied, t + 1)
                nc.gpsimd.indirect_dma_start(dram["s_extra"], bass.IndirectOffsetOnAxis(ap=row[:, t:t + 1], axis=0),
                                             rows[:, t, :], None).then_inc(stored, 16)
            pool.wait_ge(stored, 16 * SEL_T)


def add_extra(g):
    nc, dram = g.nc, g.dram
    TB = 512 // RN
    groups = [(t, min(t + TB, RT)) for t in range(0, RT, TB)]
    with ExitStack() as ctx:
        sc = Scope(nc, ctx, "f0x")
        rows = sc.sb("rows", [RN, RT, D])
        ps = sc.ps("ps", [P, 8, 512])
        landed = sc.sem("landed")
        turned = sc.sem("turned")
        added = sc.sem("added")
        block = ctx.enter_context(nc.Block())

        @block.sync
        def _(sp):
            sp.dma_start(rows[:], dram["s_extra"][0:NT, :].rearrange("(t p) d -> p t d", p=RN)).then_inc(landed, 16)

        @block.tensor
        def _(pe):
            pe.wait_ge(landed, 16)
            for i, (lo, hi) in enumerate(groups):
                if i >= 4:
                    pe.wait_ge(added, (i - 3) * KD)
                for t in range(lo, hi):
                    for k in range(KD):
                        mm = nc.tensor.transpose(ps[:, i % 4 * KD + k, (t - lo) * RN:(t - lo + 1) * RN],
                                                 rows[:, t, k * P:(k + 1) * P], g.ident[0:RN, 0:RN])
                mm.then_inc(turned, 1)

        @block.vector
        def _(dve):
            for i, (lo, hi) in enumerate(groups):
                dve.wait_ge(turned, i + 1)
                for k in range(KD):
                    o = g.h[:, k, lo * RN:hi * RN]
                    nc.vector.tensor_tensor(o, o, ps[:, i % 4 * KD + k, 0:(hi - lo) * RN], ALU.add).then_inc(added, 1)


def layer_norm(g, tag, src, out, gamma=None, beta=None, rms=False, loads=(), add_to=None,
               chunks=CH, width=CN, final=None):
    nc = g.nc
    with ExitStack() as ctx:
        sc = Scope(nc, ctx, tag)
        sq = sc.sb("sq", [P, KD, chunks * width])
        rstd = sc.sb("rstd", [P, chunks * width])
        ps = sc.ps("ps", [P, 8, 512])
        landed = sc.sem("landed")
        added = sc.sem("added")
        ln = LayerNorm(sc, "ln", src, out, sq, rstd, g.avg, (g.eps6 if rms else g.eps5)[:], ps, gamma, beta, rms,
                       chunks, width, final)
        block = ctx.enter_context(nc.Block())

        @block.sync
        def _(sp):
            for dst, s in loads:
                sp.dma_start(dst, s).then_inc(landed, 16)
            if loads:
                sp.wait_ge(landed, 16 * len(loads))

        @block.tensor
        def _(pe):
            ln.tensor(nc, pe)

        @block.scalar
        def _(act):
            ln.scalar(nc, act)

        @block.vector
        def _(dve):
            if loads and gamma is not None:
                dve.wait_ge(landed, 16 * len(loads))
            ln.vector(nc, dve)
            if add_to is not None:
                with nc.vector.Fori(0, CH) as i:
                    dve.wait_ge(ln.normed, i + 1)
                    nc.vector.tensor_tensor(both(add_to, i), both(add_to, i), both(out, i), ALU.add).then_inc(added, 1)


def gated_scan(g):
    nc, dram = g.nc, g.dram
    I = 512
    KI = I // P
    with ExitStack() as ctx:
        sc = Scope(nc, ctx, "s1")
        w_in = sc.sb("w_in", [P, KD, 2 * I])
        wo = sc.sb("wo", [P, KI, D])
        vec = sc.sb("vec", [P, 28])
        b_in, conv_b = vec[:, 0:8], vec[:, 8:12]
        b_abc = [vec[:, 12 + 4 * n:16 + 4 * n] for n in range(3)]
        bo, norm_g, norm_b = (sc.sb(n, [P, KD]) for n in ("bo", "norm_g", "norm_b"))
        conv_w = sc.sb("conv_w", [P, KI, 3])
        u = sc.sb("u", [P, KI, NT])
        with ExitStack() as mid:
            scm = Scope(nc, mid, "s1m")
            xg = scm.sb("xg", [P, KD, NT])
            layer_norm(g, "s1n", g.h, g.xn, loads=(
                (w_in[:], dram["L1_attn_W_in"]), (wo[:], dram["L1_attn_Wo"]), (vec[:, 0:24], dram["s1_vec"]),
                (bo[:], dram["L1_attn_bo"]), (norm_g[:], dram["L1_attn_gamma"]),
                (norm_b[:], dram["L1_attn_beta"]), (conv_w[:], dram["L1_attn_conv_w"])))
            layer_norm(g, "s1o", g.xn, xg, norm_g, norm_b)
            gated_scan_in(g, xg, w_in, b_in, conv_w, conv_b, u, KI)
        gated_scan_out(g, u, b_abc, wo, bo, KI)


def gated_scan_in(g, xg, w_in, b_in, conv_w, conv_b, u, KI):
    nc = g.nc
    with ExitStack() as ctx:
        sc = Scope(nc, ctx, "sa")
        proj = sc.sb("proj", [P, 2, NT])
        sig = sc.sb("sig", [P, 2, NT])
        ps_p = [sc.ps(f"ps_p{j}", [P, 512]) for j in range(2)]
        ps_g = [sc.ps(f"ps_g{j}", [P, 512]) for j in range(2)]
        p_ready = sc.sem("p_ready")
        g_ready = sc.sem("g_ready")
        moved = sc.sem("moved")
        own = sc.sem("own")
        conv_done = sc.sem("conv_done")
        silu_done = sc.sem("silu_done")
        u_done = sc.sem("u_done")
        block = ctx.enter_context(nc.Block())

        def by_batch(t):
            return t.rearrange("p (b s) -> p b s", s=S)

        @block.tensor
        def _(pe):
            for m in range(KI):
                with nc.tensor.Fori(0, CH // 2) as cc:
                    for j in range(2):
                        pe.wait_ge(moved, cc * 2 + (m * CH + j + 1))
                        for ps, col, ready in ((ps_p, m * P, p_ready), (ps_g, (KI + m) * P, g_ready)):
                            for k in range(KD):
                                mm = nc.tensor.matmul(ps[j][:, 0:CN], w_in[:, k, col:col + P],
                                                      chunk(xg, k, cc * 2 + j), start=(k == 0), stop=(k == KD - 1))
                            mm.then_inc(ready, 1)

        @block.scalar
        def _(act):
            def silu(m):
                act.wait_ge(conv_done, m + 1)
                nc.scalar.activation(u[:, m, :], u[:, m, :], ACT.Silu).then_inc(silu_done, 1)

            for m in range(KI):
                if m >= 2:
                    act.wait_ge(u_done, m - 1)
                with nc.scalar.Fori(0, CH // 2) as cc:
                    for j in range(2):
                        n = cc * 2 + (m * CH + j + 1)
                        at = bass.ds((cc * 2 + j) * CN, CN)
                        act.wait_ge(p_ready, n)
                        nc.scalar.activation(proj[:, m % 2, at], ps_p[j][:, 0:CN], ACT.Identity,
                                             bias=b_in[:, m:m + 1])
                        act.wait_ge(g_ready, n)
                        nc.scalar.activation(sig[:, m % 2, at], ps_g[j][:, 0:CN], ACT.Sigmoid,
                                             bias=b_in[:, KI + m:KI + m + 1]).then_inc(moved, 1)
                if m >= 1:
                    silu(m - 1)
            silu(KI - 1)

        @block.vector
        def _(dve):
            chain = Chain(dve, own)
            v = nc.vector
            v.memset(u[:, 0, 0:1], 0.0).then_inc(moved, 2)

            def product(m):
                dve.wait_ge(silu_done, m + 1)
                v.tensor_tensor(u[:, m, :], u[:, m, :], sig[:, m % 2, :], ALU.mult).then_inc(u_done, 1)

            for m in range(KI):
                dve.wait_ge(moved, (m + 1) * CH + 2)
                chain.step(v.tensor_scalar(u[:, m, :], proj[:, m % 2, :], conv_w[:, m, 2:3], conv_b[:, m:m + 1],
                                           ALU.mult, ALU.add))
                o, q = by_batch(u[:, m, :]), by_batch(proj[:, m % 2, :])
                for back in (1, 2):
                    ins = v.scalar_tensor_tensor(o[:, :, back:S], q[:, :, 0:S - back],
                                                 conv_w[:, m, 2 - back:3 - back], o[:, :, back:S],
                                                 ALU.mult, ALU.add)
                    if back == 1:
                        chain.step(ins)
                    else:
                        ins.then_inc(conv_done, 1)
                if m >= 1:
                    product(m - 1)
            product(KI - 1)


def gated_scan_out(g, u, b_abc, wo, bo, KI):
    nc, dram = g.nc, g.dram
    with ExitStack() as ctx:
        sc = Scope(nc, ctx, "sb")
        w = [sc.sb(f"w{n}", [P, KI, P]) for n in "abc"]
        w2 = [sc.sb(f"w2{n}", [P, KI, P]) for n in "abc"]
        a, b, c = (sc.sb(n, [P, NT]) for n in "abc")
        y = sc.sb("y", [P, KI, NT])
        part = sc.sb("part", [P, 2, KD, CN])
        ps = [[sc.ps(f"ps{n}{j}", [P, 512]) for j in range(2)] for n in "abc"]
        ps_o = sc.ps("ps_o", [P, KD, 512])
        w_landed = [sc.sem(f"w_landed{n}") for n in range(2)]
        abc_ready = sc.sem("abc_ready")
        moved = sc.sem("moved")
        own = sc.sem("own")
        y_done = sc.sem("y_done")
        o_ready = sc.sem("o_ready")
        o_used = sc.sem("o_used")
        h_added = sc.sem("h_added")
        block = ctx.enter_context(nc.Block())
        bufs = (w, w2)

        @block.sync
        def _(sp):
            for m in range(KI):
                if m >= 2:
                    sp.wait_ge(abc_ready, (m - 1) * CH)
                for n, name in enumerate(("L1_attn_Wa", "L1_attn_Wb", "L1_attn_Wc")):
                    sp.dma_start(bufs[m % 2][n][:], dram[name][:, :, m * P:(m + 1) * P]).then_inc(w_landed[m % 2], 16)

        @block.tensor
        def _(pe):
            for m in range(KI):
                pe.wait_ge(w_landed[m % 2], 48 * (m // 2 + 1))
                with nc.tensor.Fori(0, CH // 2) as cc:
                    for j in range(2):
                        pe.wait_ge(moved, cc * 2 + (m * CH + j + 1))
                        for n in range(3):
                            for k in range(KI):
                                mm = nc.tensor.matmul(ps[n][j][:, 0:CN], bufs[m % 2][n][:, k, :],
                                                      chunk(u, k, cc * 2 + j), start=(k == 0), stop=(k == KI - 1))
                        mm.then_inc(abc_ready, 1)
            pe.wait_ge(y_done, KI)
            with nc.tensor.Fori(0, CH) as i:
                pe.wait_ge(o_used, i + 1)
                for m in range(KD):
                    for k in range(KI):
                        mm = nc.tensor.matmul(ps_o[:, m, 0:CN], wo[:, k, m * P:(m + 1) * P], chunk(y, k, i),
                                              start=(k == 0), stop=(k == KI - 1))
                mm.then_inc(o_ready, 1)

        @block.scalar
        def _(act):
            for m in range(KI):
                if m >= 1:
                    act.wait_ge(y_done, m)
                with nc.scalar.Fori(0, CH // 2) as cc:
                    for j in range(2):
                        act.wait_ge(abc_ready, cc * 2 + (m * CH + j + 1))
                        for n, (dst, f) in enumerate(((a, ACT.Sigmoid), (b, ACT.Sigmoid), (c, ACT.Tanh))):
                            last = nc.scalar.activation(dst[:, bass.ds((cc * 2 + j) * CN, CN)], ps[n][j][:, 0:CN],
                                                        f, bias=b_abc[n][:, m:m + 1])
                        last.then_inc(moved, 1)

        @block.vector
        def _(dve):
            chain = Chain(dve, own)
            v = nc.vector
            v.memset(part[:, 0, 0, 0:1], 0.0).then_inc(moved, 2)
            v.memset(part[:, 0, 0, 1:2], 0.0).then_inc(o_used, 1)
            v.memset(part[:, 0, 0, 2:3], 0.0).then_inc(h_added, 1)
            for m in range(KI):
                dve.wait_ge(moved, (m + 1) * CH + 2)
                chain.step(v.tensor_tensor(b[:], b[:], u[:, m, :], ALU.mult))
                for s in range(NB):
                    at = slice(s * S, (s + 1) * S)
                    ins = v.tensor_tensor_scan(y[:, m, at], a[:, at], b[:, at], 0.0, ALU.mult, ALU.add)
                chain.step(ins)
                chain.step(v.tensor_tensor(y[:, m, :], y[:, m, :], c[:], ALU.mult))
                v.tensor_tensor(y[:, m, :], y[:, m, :], u[:, m, :], ALU.add).then_inc(y_done, 1)
            with nc.vector.Fori(0, CH) as i:
                dve.wait_ge(o_ready, i + 1)
                dve.wait_ge(h_added, i + 1)
                for m in range(KD):
                    last = v.scalar_tensor_tensor(part[:, 0, m, :], ps_o[:, m, 0:CN], bo[:, m:m + 1],
                                                  chunk(g.xn, m, i), ALU.add, ALU.add)
                last.then_inc(o_used, 1)
                dve.wait_ge(o_used, i + 2)
                v.tensor_tensor(both(g.h, i), both(g.h, i), part[:, 0], ALU.add).then_inc(h_added, 1)


def three_matrices(g):
    nc, dram = g.nc, g.dram
    with ExitStack() as ctx:
        sc = Scope(nc, ctx, "t2")
        w = sc.sb("w", [P, 3, KD, D])
        bias = sc.sb("bias", [P, KD])
        layer_norm(g, "t2n", g.h, g.xn, loads=[(w[:, n], dram[name]) for n, name in enumerate(
            ("L2_ffn_weight", "L2_ffn_aux_weight1", "L2_ffn_aux_weight2"))] + [(bias[:], dram["L2_ffn_bias"])])
        x1 = sc.sb("x1", [P, KD, NT])
        x2 = sc.sb("x2", [P, KD, NT])
        x3 = sc.sb("x3", [P, KD, NT])
        ps = [sc.ps(f"ps{j}", [P, KD, 512]) for j in range(2)]
        ready = sc.sem("ready")
        moved = sc.sem("moved")
        added = sc.sem("added")
        block = ctx.enter_context(nc.Block())
        src, dst = (g.xn, x1, x2), (x1, x2, x3)

        @block.tensor
        def _(pe):
            for n in range(3):
                with nc.tensor.Fori(0, CH // 2) as cc:
                    for j in range(2):
                        pe.wait_ge(moved, cc * 2 + (n * CH + j + 1))
                        for m in range(KD):
                            for k in range(KD):
                                mm = nc.tensor.matmul(ps[j][:, m, 0:CN], w[:, n, k, m * P:(m + 1) * P],
                                                      chunk(src[n], k, cc * 2 + j),
                                                      start=(k == 0), stop=(k == KD - 1))
                        mm.then_inc(ready, 1)

        @block.scalar
        def _(act):
            nc.scalar.copy(x3[:, 0, 0:1], g.ident[:, 0:1]).then_inc(moved, 2)
            for n in range(3):
                with nc.scalar.Fori(0, CH // 2) as cc:
                    for j in range(2):
                        act.wait_ge(ready, cc * 2 + (n * CH + j + 1))
                        if n < 2:
                            last = nc.scalar.copy(both(dst[n], cc * 2 + j), ps[j][:, :, 0:CN])
                        else:
                            for m in range(KD):
                                last = nc.scalar.activation(chunk(x3, m, cc * 2 + j), ps[j][:, m, 0:CN], ACT.Tanh,
                                                            bias=bias[:, m:m + 1])
                        last.then_inc(moved, 1)

        @block.vector
        def _(dve):
            with nc.vector.Fori(0, CH) as i:
                dve.wait_ge(moved, i + (2 * CH + 3))
                nc.vector.tensor_tensor(both(g.h, i), both(g.h, i), both(x3, i), ALU.add).then_inc(added, 1)


class Unit:

    def __init__(self, kind, g, tile, pair, lo, hi):
        self.kind, self.g, self.tile, self.pair, self.lo, self.hi = kind, g, tile, pair, lo, hi
        self.last = False


def attention(g, tag, src, length, heads, dh, scale, causal, k_heads, names, res, dst):
    nc, dram = g.nc, g.dram
    stripe = 2 * dh
    per = P // stripe
    pairs = per // 2
    G = heads // per
    in_tile = P // dh
    RQ, RK = heads * dh // P, max(1, k_heads * dh // P)
    tiles = [(s, min(P, length - s)) for s in range(0, length, P)]
    NTL = len(tiles)
    width = NTL * P
    even = length + length % 2
    regions = [(0, length)] if length <= 512 else [(0, 3 * P), (3 * P, length)]
    one_bank = len(regions) == 1
    shared_k = k_heads == 1
    v_cols = stripe if shared_k else heads * stripe
    b_heads = 2 if one_bank else 1
    wq_d, wk_d, wv_d, wo_d, bq_d, bk_d, bv_d, bo_d = (dram[n] for n in names)
    ROW = 96

    def cuts(lo, hi):
        return [(n, max(lo, a), min(hi, b)) for n, (a, b) in enumerate(regions) if max(lo, a) < min(hi, b)]

    def spans(lo, hi):
        return [(lo, hi)] if hi - lo <= 512 else [(a, b) for _, a, b in cuts(lo, hi)]

    def up_even(n):
        return even if n == length else n

    def maxima(gr):
        out = []
        for t, (start, rows) in enumerate(tiles):
            for pr in range(pairs):
                out += [Unit("M", gr, t, pr, lo, hi) for lo, hi in spans(0, start + rows if causal else length)]
        out[-1].last = True
        return out

    def probs(gr):
        out = []
        for t, (start, rows) in enumerate(tiles):
            for lo, hi in spans(start if causal else 0, length):
                out += [Unit("P", gr, t, pr, lo, hi) for pr in range(pairs)]
        out[-1].last = True
        return out

    def both_of(gr):
        ps, ms = probs(gr), maxima(gr + 1)
        assert len(ps) == len(ms)
        return [u for pair in zip(ps, ms) for u in pair]

    def stacks(gr):
        kinds = "B" if shared_k else "BC"
        return [Unit(k, gr, 0, h // b_heads, 0, length) for h in range(0, per, b_heads) for k in kinds]

    def turned(gr):
        return ["T%d%d" % (gr, n) for n in range(per // b_heads)]

    order = [[Unit("Q", 0, t, 0, 0, length) for t in range(RQ)] + [Unit("K", 0, t, 0, 0, length) for t in range(RK)]
             + [Unit("V", 0, t, 0, 0, v_cols) for t in range(NTL)]
             + ([Unit("C", 0, 0, 0, 0, length)] if shared_k else []) + stacks(0), maxima(0), stacks(1), *turned(0),
             both_of(0)]
    for gr in range(2, G):
        order += [stacks(gr), "S%d" % (gr - 2), *turned(gr - 1), both_of(gr - 1)]
    order += ["S%d" % (G - 2), *turned(G - 1), probs(G - 1), "S%d" % (G - 1), "O0", "O1"]
    units = [u for item in order if not isinstance(item, str) for u in item]
    for n, u in enumerate(units):
        u.n = n
        u.by_act = u.kind in "QKBCP"
        u.taken = sum(1 for w in units[:n + 1] if (w.kind in "QKBCP") == u.by_act)
    n_act = sum(u.by_act for u in units)
    nu, n_dve = len(units), len(units) - sum(u.by_act for u in units)
    for n, u in enumerate(u for u in units if u.kind == "P"):
        u.pn = n
    assert sum(u.kind == "P" for u in units) % 2 == 0
    first_b = next(u for u in units if u.kind in "BC")
    first_m = next(u for u in units if u.kind == "M")
    assert not any(u.kind == "V" for u in units[-2:]) and all(u.by_act for u in units[-2:])
    turns = [item for item in order if isinstance(item, str)]
    n_ps_t = len(turns)

    with ExitStack() as ctx:
        sc = Scope(nc, ctx, tag)
        wq = sc.sb("wq", [P, KD, RQ * P])
        wk = sc.sb("wk", [P, KD, RK * P])
        wv = sc.sb("wv", [P, KD, v_cols])
        wo = sc.sb("wo", [P, G, D])
        bq, bk, bo = sc.sb("bq", [P, RQ]), sc.sb("bk", [P, RK]), sc.sb("bo", [P, KD])
        bv = sc.sb("bv", [P, v_cols])
        ones_row = sc.sb("ones_row", [P, 1])
        swap = sc.sb("swap", [P, P])
        loads = [(wq, wq_d), (wk, wk_d), (wv, wv_d), (wo, wo_d), (bq, bq_d), (bk, bk_d), (bo, bo_d),
                 (ones_row, dram["c_ones_row"]), (swap, dram["c_swap%d" % stripe])]
        loads = [(a[:], b) for a, b in loads] + [(bv[:], bv_d.to_broadcast([P, v_cols]))]
        sel = sc.sb("sel", [P, 4, in_tile, P], F32R)
        ident_r = sc.sb("ident_r", [P, P], F32R)
        loads_r = [(sel, "c_sel%d" % dh), (ident_r, "c_ident")]
        if causal:
            mask_q = sc.sb("mask_q", [P, P], F32R)
            mask_k = sc.sb("mask_k", [P, P], F32R)
            loads_r += [(mask_q, "c_mask_q"), (mask_k, "c_mask_k")]
        xb = sc.sb("xb", [P, KD, length])
        raw = sc.sb("raw", [P, RQ + RK, width])
        hi_r = sc.sb("hi", [P, RQ + RK, width], F32R)
        lo_r = sc.sb("lo", [P, RQ + RK, width], F32R)
        q = sc.sb("q", [P, 2, per, width], F32R)
        kt = sc.sb("kt", [P, 1, 1, width] if shared_k else [P, 2, per, width], F32R)
        v = sc.sb("v", [P, NTL, v_cols])
        mx = sc.sb("mx", [P, NTL, per])
        mx2 = sc.sb("mx2", [P, 2])
        mrow = sc.sb("mrow", [P, per, NTL, P], F32R)
        pt = sc.sb("pt", [P, 2, 2, 512])
        o_sb = sc.sb("o_sb", [P, 2, length])
        rec = sc.sb("rec", [P, length])
        ctx_t = sc.sb("ctx", [P, G, length])
        ps_s = sc.ps("ps_s", [P, 2, 2, 512])
        ps_o = sc.ps("ps_o", [P, 2, 512])
        ps_t = sc.ps("ps_t", [P, 2, 512])
        landed = sc.sem("landed")
        landed_r = sc.sem("landed_r")
        xb_ready = sc.sem("xb_ready")
        xb_used = sc.sem("xb_used")
        split = sc.sem("split")
        filled = sc.sem("filled")
        act_took = sc.sem("act_took")
        dve_took = sc.sem("dve_took")
        max_done = sc.sem("max_done")
        t_ready = sc.sem("t_ready")
        t_took = sc.sem("t_took")
        o_ready = sc.sem("o_ready")
        o_took = sc.sem("o_took")
        ctx_done = sc.sem("ctx_done")
        own = sc.sem("own")
        zeroed = sc.sem("zeroed")
        block = ctx.enter_context(nc.Block())
        NR = RQ + RK

        def slot(u):
            return ps_s[:, u.n % 2]

        def heads_of(u):
            return [u.pair * 2 + i for i in range(2)]

        def k_stack(gr, h):
            return kt[:, 0, 0] if shared_k else kt[:, gr % 2, h]

        @block.sync
        def _(sp):
            for a, b in loads:
                sp.dma_start(a, b).then_inc(landed, 16)

        @block.gpsimd
        def _(pool):
            for a, b in loads_r:
                nc.gpsimd.dma_start(a[:], dram[b]).then_inc(landed_r, 16)
            pool.wait_ge(zeroed, 1)
            with nc.gpsimd.Fori(0, NB) as b:
                pool.wait_ge(xb_used, b + 1)
                nc.gpsimd.tensor_copy(xb[:], src[:, :, bass.ds(b * length, length)]).then_inc(xb_ready, 1)
                for n in range(NR):
                    pool.wait_ge(act_took, b * n_act + (n + 3))
                    nc.gpsimd.tensor_tensor(lo_r[:, n, :], raw[:, n, :], hi_r[:, n, :].bitcast(F32),
                                            ALU.subtract).then_inc(split, 1)

        @block.tensor
        def _(pe):
            pe.wait_ge(landed, 16 * len(loads))
            pe.wait_ge(landed_r, 16 * len(loads_r))
            pe.wait_ge(zeroed, 1)

            def took(u, b):
                if u.by_act:
                    pe.wait_ge(act_took, b * n_act + (u.taken + 2))
                else:
                    pe.wait_ge(dve_took, b * n_dve + u.taken)

            def fill(u, b):
                if u.n < 2:
                    pe.wait_ge(act_took, b * n_act + (u.n + 1))
                else:
                    took(units[u.n - 2], b)
                s = slot(u)
                start, rows = tiles[u.tile] if u.tile < NTL else (0, P)
                if u.kind in "QK":
                    w = wq if u.kind == "Q" else wk
                    for n, lo, hi in cuts(0, length):
                        for k in range(KD):
                            mm = nc.tensor.matmul(s[:, n, 0:hi - lo], w[:, k, u.tile * P:(u.tile + 1) * P],
                                                  xb[:, k, lo:hi], start=(k == 0), stop=(k == KD - 1))
                elif u.kind == "V":
                    for k in range(KD):
                        mm = nc.tensor.matmul(s[0:rows, 0, 0:v_cols], xb[:, k, start:start + rows], wv[:, k, :],
                                              start=(k == 0), stop=(k == KD - 1))
                elif u.kind in "BC":
                    if u is first_b:
                        pe.wait_ge(split, b * NR + NR)
                    for i in range(b_heads):
                        h = (u.g * per + u.pair * b_heads + i) if u.kind == "B" or not shared_k else 0
                        src_n = h // in_tile + (0 if u.kind == "B" else RQ)
                        for n, lo, hi in cuts(0, length):
                            o = s[:, i if one_bank else n, 0:up_even(hi) - lo]
                            for part, t in enumerate((hi_r, lo_r)):
                                mm = nc.tensor.matmul(o, sel[:, part + (0 if u.kind == "B" else 2), h % in_tile, :],
                                                      t[:, src_n, lo:up_even(hi)], start=(part == 0), stop=(part == 1))
                else:
                    if u is first_m:
                        took(units[u.n - 1], b)
                    masked = causal and u.lo <= start < u.hi
                    for i, h in enumerate(heads_of(u)):
                        qs, ks = q[:, u.g % 2, h], k_stack(u.g, h)
                        left, right = (qs, ks) if u.kind == "M" else (ks, qs)
                        mm = nc.tensor.matmul(s[:, i, 0:up_even(u.hi) - u.lo], left[:, start:start + P],
                                              right[:, u.lo:up_even(u.hi)], start=True, stop=not masked)
                        if masked:
                            m = mask_q if u.kind == "M" else mask_k
                            n = rows + rows % 2
                            mm = nc.tensor.matmul(s[:, i, start - u.lo:start - u.lo + n], ident_r[:], m[:, 0:n],
                                                  start=False, stop=True)
                mm.then_inc(filled, 1)

            def with_v(u, b):
                took(u, b)
                for n, lo, hi in cuts(u.lo, u.hi):
                    for i, h in enumerate(heads_of(u)):
                        c = 0 if shared_k else (u.g * per + h) * stripe
                        bank_n = u.g % 2 if one_bank else n
                        at = lo - regions[n][0]
                        mm = nc.tensor.matmul(ps_o[h * stripe:(h + 1) * stripe, bank_n, at:at + hi - lo],
                                              v[:, u.tile, c:c + stripe], pt[:, u.pn % 2, i, lo - u.lo:hi - u.lo],
                                              start=(u.tile == 0), stop=(u.tile == NTL - 1), skip_group_check=True)
                if u.last:
                    mm.then_inc(o_ready, 1)

            def turn(what, b, n):
                gr = int(what[1])
                if what[0] == "T":
                    pe.wait_ge(max_done, b * G + (gr + 1))
                elif what[0] == "S":
                    pe.wait_ge(o_took, b * G + (gr + 2))
                else:
                    pe.wait_ge(ctx_done, b * G + G)
                pe.wait_ge(t_took, b * n_ps_t + (n + 1))
                if what[0] == "T":
                    for i in range(b_heads):
                        h = int(what[2]) * b_heads + i
                        for t, (start, rows) in enumerate(tiles):
                            (bn, lo, hi), = cuts(start, start + rows)
                            at = lo - regions[bn][0]
                            mm = nc.tensor.matmul(ps_t[:, i if one_bank else bn, at:at + rows + rows % 2],
                                                  mrow[:, h, t, :], ident_r[:, 0:rows + rows % 2], start=True, stop=True)
                elif what[0] == "S":
                    for bn, lo, hi in cuts(0, length):
                        mm = nc.tensor.matmul(ps_t[:, bn, 0:hi - lo], swap[:], o_sb[:, gr % 2, lo:hi],
                                              start=True, stop=True)
                else:
                    for bn, lo, hi in cuts(0, length):
                        for k in range(G):
                            mm = nc.tensor.matmul(ps_t[:, bn, 0:hi - lo], wo[:, k, gr * P:(gr + 1) * P],
                                                  ctx_t[:, k, lo:hi], start=(k == 0), stop=(k == G - 1))
                mm.then_inc(t_ready, 1)

            with nc.tensor.Fori(0, NB) as b:
                pe.wait_ge(xb_ready, b + 1)
                for item in order:
                    if isinstance(item, str):
                        turn(item, b, turns.index(item))
                        continue
                    before = None
                    for u in item:
                        if u.kind == "P" and u is item[0]:
                            pe.wait_ge(t_took, b * n_ps_t + (turns.index(turned(u.g)[-1]) + 2))
                            pe.wait_ge(o_took, b * G + (u.g + 1))
                        fill(u, b)
                        if u.kind == "P":
                            if before is not None:
                                with_v(before, b)
                            before = u
                    if before is not None:
                        with_v(before, b)

        @block.scalar
        def _(act):
            act.wait_ge(landed, 16 * len(loads))
            act.wait_ge(zeroed, 1)
            nc.scalar.copy(pt[:, 0, 0, 0:1], pt[:, 0, 0, 0:1]).then_inc(act_took, 2)
            with nc.scalar.Fori(0, NB) as b:
                for u in units:
                    if not u.by_act:
                        continue
                    act.wait_ge(filled, b * nu + (u.n + 1))
                    if u.kind == "P":
                        rows, n = tiles[u.tile][1], u.hi - u.lo
                        last = nc.scalar.activation(pt[0:rows, u.pn % 2, :, 0:n], slot(u)[0:rows, :, 0:n], ACT.Exp,
                                                    scale=scale)
                    elif u.kind in "QK":
                        t, bias = (u.tile, bq) if u.kind == "Q" else (RQ + u.tile, bk)
                        for n, lo, hi in cuts(0, length):
                            for out in (raw, hi_r):
                                last = nc.scalar.activation(out[:, t, lo:hi], slot(u)[:, n, 0:hi - lo], ACT.Identity,
                                                            bias=bias[:, u.tile:u.tile + 1])
                    else:
                        for n, lo, hi in cuts(0, length):
                            if one_bank:
                                h = u.pair * b_heads
                                o, s = (q if u.kind == "B" else kt)[:, u.g % 2, h:h + 2, lo:hi], slot(u)[:, :, 0:hi]
                            else:
                                o = q[:, u.g % 2, u.pair, lo:hi] if u.kind == "B" else kt[:, 0, 0, lo:hi]
                                s = slot(u)[:, n, 0:hi - lo]
                            if u.kind == "B":
                                last = nc.scalar.copy(o, s)
                            else:
                                last = nc.scalar.activation(o, s, ACT.Identity, bias=ones_row[:])
                    last.then_inc(act_took, 1)

        @block.vector
        def _(dve):
            ve = nc.vector
            dve.wait_ge(landed, 16 * len(loads))
            ve.memset(mx2[:], 0.0).then_inc(t_took, 1)
            ve.memset(rec[:], 0.0).then_inc(o_took, 1)
            ve.memset(o_sb[:, 0, 0:1], 0.0).then_inc(xb_used, 1)
            chain = Chain(dve, own)
            for t in (mx, pt, raw):
                ve.memset(t[:], 0.0)
            for t in (q, kt, mrow, hi_r):
                ve.memset(t[:].bitcast(F32), 0.0)
            ve.memset(v[:], 0.0).then_inc(zeroed, 1)
            dve.wait_ge(zeroed, 1)

            def take(u, b):
                dve.wait_ge(filled, b * nu + (u.n + 1))
                rows = tiles[u.tile][1]
                if u.kind == "V":
                    ve.tensor_tensor(v[0:rows, u.tile, :], slot(u)[0:rows, 0, 0:v_cols], bv[0:rows, :],
                                     ALU.add).then_inc(dve_took, 1)
                    if u.tile == NTL - 1:
                        dve.wait_ge(dve_took, b * n_dve + u.taken)
                        ve.memset(mx2[:], 0.0).then_inc(xb_used, 1)
                    return
                h = u.pair * 2
                col = mx[0:rows, u.tile, h:h + 2]
                first = u.lo == 0
                out = col if first else mx2[0:rows, :]
                ve.tensor_reduce(out, slot(u)[0:rows, :, 0:u.hi - u.lo], AX_X, ALU.max).then_inc(dve_took, 1)
                if not first:
                    dve.wait_ge(dve_took, b * n_dve + u.taken)
                    chain.step(ve.tensor_tensor(col, col, mx2[0:rows, :], ALU.max))
                if u.last:
                    dve.wait_ge(dve_took, b * n_dve + u.taken)
                    m = mx[:].rearrange("p t h -> p h t")
                    hi, lo = (mrow[:, :, :, ROW + n:ROW + n + 1].rearrange("p h t a -> p h (t a)") for n in range(2))
                    chain.step(ve.tensor_scalar(hi, m, -1.0, None, ALU.mult))
                    ve.scalar_tensor_tensor(lo, m, -1.0, hi.bitcast(F32), ALU.mult, ALU.subtract).then_inc(max_done, 1)
                    dve.wait_ge(max_done, b * G + (u.g + 1))

            def turn(what, b, n):
                gr = int(what[1])
                dve.wait_ge(t_ready, b * n_ps_t + (n + 1))
                if what[0] == "T":
                    r = slice(ROW, ROW + 2)
                    for bn, lo, hi in cuts(0, length):
                        if one_bank:
                            h = int(what[2]) * b_heads
                            last = ve.tensor_copy(q[r, gr % 2, h:h + 2, lo:hi], ps_t[r, :, lo:hi])
                        else:
                            last = ve.tensor_copy(q[r, gr % 2, int(what[2]), lo:hi], ps_t[r, bn, 0:hi - lo])
                    last.then_inc(t_took, 1)
                elif what[0] == "S":
                    for bn, lo, hi in cuts(0, length):
                        last = ve.reciprocal(rec[:, lo:hi], ps_t[:, bn, 0:hi - lo])
                    last.then_inc(t_took, 1)
                    dve.wait_ge(t_took, b * n_ps_t + (n + 2))
                    ve.tensor_tensor(ctx_t[:, gr, :], o_sb[:, gr % 2, :], rec[:], ALU.mult).then_inc(ctx_done, 1)
                    dve.wait_ge(ctx_done, b * G + (gr + 1))
                else:
                    for bn, lo, hi in cuts(0, length):
                        at = bass.ds(b * length + lo, hi - lo)
                        last = ve.scalar_tensor_tensor(dst[:, gr, at], ps_t[:, bn, 0:hi - lo], bo[:, gr:gr + 1],
                                                       res[:, gr, at], ALU.add, ALU.add)
                    last.then_inc(t_took, 1)

            steps = sum(1 for u in units if u.kind == "M" and u.lo > 0) + G
            with nc.vector.Fori(0, NB) as b:
                chain.begin(b, steps)
                for item in order:
                    if isinstance(item, str):
                        turn(item, b, turns.index(item))
                        continue
                    for u in item:
                        if not u.by_act:
                            take(u, b)
                    if item[0].kind == "P":
                        gr = item[0].g
                        dve.wait_ge(o_ready, b * G + (gr + 1))
                        for n, (lo, hi) in enumerate(regions):
                            bank_n = gr % 2 if one_bank else n
                            last = ve.tensor_copy(o_sb[:, gr % 2, lo:hi], ps_o[:, bank_n, 0:hi - lo])
                        last.then_inc(o_took, 1)
                        dve.wait_ge(o_took, b * G + (gr + 2))
                chain.end(NB)


def query_attention(g):
    layer_norm(g, "q2n", g.h, g.xn)
    attention(g, "q2", g.xn, S, 8, 32, D ** -0.5, True, 1,
              ("q2_wq", "q2_wk", "q2_wv", "q2_wo", "q2_bq", "q2_bk", "q2_bv", "L2_attn_bp"), g.h, g.h)


def embed(g, xt):
    nc, dram = g.nc, g.dram
    KP = 3 * 16 * 16 // P
    N_P = NB * (S_IMG - 1)
    TT = S_TXT // P
    T = NB * TT
    with ExitStack() as ctx:
        sc = Scope(nc, ctx, "em")
        idx = sc.sb("idx", [P, T], I32)
        idx_f = sc.sb("idx_f", [P, T])
        neg = sc.sb("neg", [P, T])
        rows = sc.sb("rows", [P, T, D])
        pos = sc.sb("pos", [P, TT, D])
        patches = sc.sb("patches", [P, KP, N_P])
        w = sc.sb("w", [P, KP, D])
        vec = sc.sb("vec", [P, 2, KD])
        pos_img = sc.sb("pos_img", [P, KD, S_IMG])
        ps = sc.ps("ps", [P, 6, 512])
        ps_i = sc.ps("ps_i", [P, KD, 512])
        idx_landed = sc.sem("idx_landed")
        landed = sc.sem("landed")
        idx_ready = sc.sem("idx_ready")
        gathered = [sc.sem(f"gathered{b}") for b in range(NB)]
        placed = sc.sem("placed")
        turned = sc.sem("turned")
        copied = sc.sem("copied")
        img_ready = sc.sem("img_ready")
        img_done = sc.sem("img_done")
        own = sc.sem("own")
        block = ctx.enter_context(nc.Block())

        @block.sync
        def _(sp):
            sp.dma_start(idx[:], dram["x_txt"]).then_inc(idx_landed, 16)
            for a, b in ((pos, "c_pos_txt"), (patches, "patches"), (w, "L0_tok_W"), (vec, "tok_vec"),
                         (pos_img, "L0_tok_pos_embedding")):
                sp.dma_start(a[:], dram[b]).then_inc(landed, 16)

        @block.gpsimd
        def _(pool):
            pool.wait_ge(idx_ready, 1)
            for t in range(T):
                nc.gpsimd.indirect_dma_start(
                    rows[:, t, :], None, dram["L0_txt_emb"],
                    bass.IndirectOffsetOnAxis(ap=idx[:, t:t + 1], axis=0)).then_inc(gathered[t // TT], 16)

        @block.vector
        def _(dve):
            v = nc.vector
            chain = Chain(dve, own)
            dve.wait_ge(idx_landed, 16)
            chain.step(v.tensor_copy(idx_f[:], idx[:]))
            chain.step(v.tensor_scalar(neg[:], idx_f[:], 0.0, float(VOCAB), ALU.is_lt, ALU.mult))
            chain.step(v.tensor_tensor(idx_f[:], idx_f[:], neg[:], ALU.add))
            chain.step(v.tensor_scalar(idx_f[:], idx_f[:], 0.0, float(VOCAB - 1), ALU.max, ALU.min))
            v.tensor_copy(idx[:], idx_f[:]).then_inc(idx_ready, 1)
            dve.wait_ge(landed, 16 * 5)
            dve.wait_ge(img_ready, 1)
            img = g.h[:].rearrange("p k (b s) -> p k b s", s=S)
            for k in range(KD):
                pk = pos_img[:, k, :].rearrange("p (a s) -> p a s", a=1)
                v.scalar_tensor_tensor(img[:, k, :, 1:S_IMG],
                                       ps_i[:, k, 0:N_P].rearrange("p (b s) -> p b s", b=NB), vec[:, 0, k:k + 1],
                                       pk[:, :, 1:S_IMG].to_broadcast([P, NB, S_IMG - 1]), ALU.add, ALU.add)
                v.tensor_tensor(img[:, k, :, 0:1].rearrange("p b a -> p (b a)"),
                                vec[:, 1, k:k + 1].to_broadcast([P, NB]), pos_img[:, k, 0:1].to_broadcast([P, NB]),
                                ALU.add).then_inc(img_done, 1)
            for b in range(NB):
                dve.wait_ge(gathered[b], 16 * TT)
                r = rows[:, b * TT:(b + 1) * TT, :]
                v.tensor_tensor(r, r, pos[:], ALU.add).then_inc(placed, 1)
            for t in range(T):
                dve.wait_ge(turned, t + 1)
                v.tensor_copy(xt[:, :, t * P:(t + 1) * P],
                              ps[:, t % 6, 0:D].rearrange("p (k n) -> p k n", k=KD)).then_inc(copied, 1)

        @block.tensor
        def _(pe):
            pe.wait_ge(landed, 16 * 5)
            for m in range(KD):
                for k in range(KP):
                    mm = nc.tensor.matmul(ps_i[:, m, 0:N_P], w[:, k, m * P:(m + 1) * P], patches[:, k, :],
                                          start=(k == 0), stop=(k == KP - 1))
            mm.then_inc(img_ready, 1)
            for t in range(T):
                pe.wait_ge(placed, t // TT + 1)
                if t >= 6:
                    pe.wait_ge(copied, t - 5)
                for k in range(KD):
                    mm = nc.tensor.transpose(ps[:, t % 6, k * P:(k + 1) * P], rows[:, t, k * P:(k + 1) * P],
                                             g.ident[:])
                mm.then_inc(turned, 1)


def text_block(g):
    nc, dram = g.nc, g.dram
    NX = NB * S_TXT
    F = 4 * D
    NF = F // P
    with ExitStack() as ctx:
        sc = Scope(nc, ctx, "tx")
        xt = sc.sb("xt", [P, KD, NX])
        r1 = sc.sb("r1", [P, KD, NX])
        b1 = sc.sb("b1", [P, NF])
        vec = sc.sb("vec", [P, 5, KD])
        embed(g, xt)
        attention(g, "ta", xt, S_TXT, 16, 16, 0.25, False, 16,
                  ("ta_wq", "ta_wk", "ta_wv", "ta_wo", "ta_bq", "ta_bk", "ta_bv", "L0_txt_out_proj_b"), xt, r1)
        w1 = sc.sb("w1", [P, KD, F])
        w2 = sc.sb("w2", [P, NF, D])
        layer_norm(g, "tn", r1, xt, vec[:, 1, :], vec[:, 2, :], chunks=NB, width=S_TXT, loads=(
            (vec[:], dram["txt_vec"]), (w1[:], dram["L0_txt_w1"]), (w2[:], dram["L0_txt_w2"]),
            (b1[:], dram["L0_txt_b1"])))
        relu_ffn(g, xt, r1, w1, w2, b1, vec[:, 0, :], NF)
        layer_norm(g, "to", r1, xt, vec[:, 3, :], vec[:, 4, :], chunks=NB, width=S_TXT,
                   final=lambda k, i: g.h[:, k, bass.ds(i * S + S_IMG, S_TXT)])


def relu_ffn(g, x, out, w1, w2, b1, b2, NF):
    nc = g.nc
    with ExitStack() as ctx:
        sc = Scope(nc, ctx, "tf")
        hid = sc.sb("hid", [P, 2, S_TXT])
        ps_h = [sc.ps(f"ps_h{j}", [P, 512]) for j in range(2)]
        ps_y = sc.ps("ps_y", [P, KD, 512])
        h_ready = sc.sem("h_ready")
        hid_done = sc.sem("hid_done")
        y_ready = sc.sem("y_ready")
        y_used = sc.sem("y_used")
        block = ctx.enter_context(nc.Block())

        def at(t, k, b):
            return t[:, k, bass.ds(b * S_TXT, S_TXT)]

        @block.tensor
        def _(pe):
            def up(b, f):
                pe.wait_ge(hid_done, b * NF + (f + 1))
                for k in range(KD):
                    mm = nc.tensor.matmul(ps_h[f % 2][:], w1[:, k, f * P:(f + 1) * P], at(x, k, b),
                                          start=(k == 0), stop=(k == KD - 1))
                mm.then_inc(h_ready, 1)

            with nc.tensor.Fori(0, NB) as b:
                up(b, 0)
                for f in range(NF):
                    if f + 1 < NF:
                        up(b, f + 1)
                    if f == 0:
                        pe.wait_ge(y_used, b + 1)
                    pe.wait_ge(hid_done, b * NF + (f + 3))
                    for m in range(KD):
                        mm = nc.tensor.matmul(ps_y[:, m, :], w2[:, f, m * P:(m + 1) * P], hid[:, f % 2, :],
                                              start=(f == 0), stop=(f == NF - 1))
                mm.then_inc(y_ready, 1)

        @block.scalar
        def _(act):
            nc.scalar.copy(hid[:, 0, 0:1], g.ident[:, 0:1]).then_inc(hid_done, 2)
            with nc.scalar.Fori(0, NB) as b:
                for f in range(NF):
                    act.wait_ge(h_ready, b * NF + (f + 1))
                    nc.scalar.activation(hid[:, f % 2, :], ps_h[f % 2][:], ACT.Relu,
                                         bias=b1[:, f:f + 1]).then_inc(hid_done, 1)

        @block.vector
        def _(dve):
            nc.vector.memset(out[:, 0, 0:1], 0.0).then_inc(y_used, 1)
            dve.wait_ge(y_used, 1)
            with nc.vector.Fori(0, NB) as b:
                dve.wait_ge(y_ready, b + 1)
                for m in range(KD):
                    last = nc.vector.scalar_tensor_tensor(at(out, m, b), ps_y[:, m, :], b2[:, m:m + 1], at(x, m, b),
                                                          ALU.add, ALU.add)
                last.then_inc(y_used, 1)


def slots_schedule(units, takers):
    seen = {}
    out = []
    for u in units:
        t = takers[u[0]]
        seen[t] = seen.get(t, 0) + 1
        out.append((t, seen[t]))
    return out, seen


def full_attention(g):
    nc, dram = g.nc, g.dram
    tiles = [(s, min(P, S - s)) for s in range(0, S, P)]
    NTL = len(tiles)
    cuts = [(0, 512), (512, S)]
    scale = D ** -0.5 * 1.0986122886681098
    units = [("Q", 0), ("Q", 1), ("K", 0), ("K", 1)] + [("V", t) for t in range(NTL)] \
        + [("S", 0), ("S", 1)] + [x for t in range(2, NTL) for x in (("T", t - 2), ("S", t))] \
        + [("T", NTL - 2), ("T", NTL - 1), ("O", 0), ("O", 1), ("Y", 0), ("Y", 1)]
    takers = {"Q": "act", "K": "act", "S": "act", "T": "act", "V": "dve", "O": "dve", "Y": "dve"}
    taken, per = slots_schedule(units, takers)
    NU = len(units)
    SLOTS = 4
    pad = (-NU) % SLOTS
    with ExitStack() as ctx:
        sc = Scope(nc, ctx, "a3")
        w = sc.sb("w", [P, KD, 3 * D])
        wp = sc.sb("wp", [P, KD, D])
        vec = sc.sb("vec", [P, 4, KD])
        bv = sc.sb("bv", [P, D])
        rope = sc.sb("rope", [P, 2, S])
        x = sc.sb("x", [P, KD, NT])
        layer_norm(g, "a3n", g.h, g.xn, loads=(
            (w[:], dram["L3_attn_w_qkv"]), (wp[:], dram["L3_attn_w_proj"]), (vec[:], dram["a3_vec"]),
            (bv[:], dram["a3_bv"].to_broadcast([P, D])), (rope[:], dram["c_rope"])))
        layer_norm(g, "a3r", g.xn, x, vec[:, 0, :], None, rms=True)
        xb = sc.sb("xb", [P, KD, S])
        raw = sc.sb("raw", [P, 2, KD, S])
        rot = sc.sb("rot", [P, 2, KD, S])
        tmp = sc.sb("tmp", [P, S])
        v = sc.sb("v", [P, NTL, D])
        prob = sc.sb("prob", [P, 2, S])
        prob_t = sc.sb("prob_t", [P, NTL, S])
        small = sc.sb("small", [P, NTL, 3])
        o_sb = sc.sb("o_sb", [P, KD, S])
        ps = sc.ps("ps", [P, SLOTS, 1024])
        xb_ready = sc.sem("xb_ready")
        xb_used = sc.sem("xb_used")
        filled = sc.sem("filled")
        act_took = sc.sem("act_took")
        dve_took = sc.sem("dve_took")
        max_done = sc.sem("max_done")
        prob_done = sc.sem("prob_done")
        roped = sc.sem("roped")
        added = sc.sem("added")
        own = sc.sem("own")
        block = ctx.enter_context(nc.Block())

        def slot(n):
            return ps[:, n % SLOTS]

        @block.gpsimd
        def _(pool):
            with nc.gpsimd.Fori(0, NB) as b:
                pool.wait_ge(xb_used, b + 1)
                nc.gpsimd.tensor_copy(xb[:], x[:, :, bass.ds(b * S, S)]).then_inc(xb_ready, 1)

        def taker_wait(eng, b, n):
            who, k = taken[n]
            if who == "act":
                eng.wait_ge(act_took, b * per["act"] + k)
            else:
                eng.wait_ge(dve_took, b * per["dve"] + (k + 4))

        @block.tensor
        def _(pe):
            with nc.tensor.Fori(0, NB) as b:
                pe.wait_ge(xb_ready, b + 1)
                for n, (kind, t) in enumerate(units):
                    s = slot(n)
                    before = n - SLOTS
                    if before >= 0:
                        taker_wait(pe, b, before)
                    elif before + pad < 0:
                        pe.wait_ge(dve_took, b * per["dve"] + (4 + before + pad + 1))
                    if kind in "QK":
                        col = (0 if kind == "Q" else D) + t * P
                        for lo, hi in cuts:
                            for k in range(KD):
                                mm = nc.tensor.matmul(s[:, lo:hi], w[:, k, col:col + P], xb[:, k, lo:hi],
                                                      start=(k == 0), stop=(k == KD - 1))
                    elif kind == "V":
                        start, rows = tiles[t]
                        for k in range(KD):
                            mm = nc.tensor.matmul(s[0:rows, 0:D], xb[:, k, start:start + rows], w[:, k, 2 * D:3 * D],
                                                  start=(k == 0), stop=(k == KD - 1))
                    elif kind == "S":
                        start, rows = tiles[t]
                        if t == 0:
                            pe.wait_ge(roped, b + 1)
                        for lo, hi in cuts:
                            for k in range(KD):
                                mm = nc.tensor.matmul(s[0:rows, lo:hi], rot[:, 0, k, start:start + rows],
                                                      rot[:, 1, k, lo:hi], start=(k == 0), stop=(k == KD - 1))
                    elif kind == "T":
                        start, rows = tiles[t]
                        pe.wait_ge(prob_done, b * NTL + (t + 1))
                        for j, (js, jr) in enumerate(tiles):
                            mm = nc.tensor.transpose(s[0:jr, j * P:(j + 1) * P], prob[:, t % 2, js:js + jr],
                                                     g.ident[:])
                    elif kind == "O":
                        if t == 0:
                            taker_wait(pe, b, units.index(("T", NTL - 1)))
                        for lo, hi in cuts:
                            for j, (js, jr) in enumerate(tiles):
                                mm = nc.tensor.matmul(s[:, lo:hi], v[0:jr, j, t * P:(t + 1) * P],
                                                      prob_t[0:jr, j, lo:hi], start=(j == 0), stop=(j == NTL - 1))
                    else:
                        if t == 0:
                            taker_wait(pe, b, units.index(("O", 1)))
                        for lo, hi in cuts:
                            for k in range(KD):
                                mm = nc.tensor.matmul(s[:, lo:hi], wp[:, k, t * P:(t + 1) * P], o_sb[:, k, lo:hi],
                                                      start=(k == 0), stop=(k == KD - 1))
                    mm.then_inc(filled, 1)

        @block.scalar
        def _(act):
            with nc.scalar.Fori(0, NB) as b:
                for n, (kind, t) in enumerate(units):
                    if takers[kind] != "act":
                        continue
                    s = slot(n)
                    act.wait_ge(filled, b * NU + (n + 1))
                    if kind in "QK":
                        c = 0 if kind == "Q" else 1
                        last = nc.scalar.activation(raw[:, c, t, :], s[:, 0:S], ACT.Identity,
                                                    bias=vec[:, 1 + c, t:t + 1])
                    elif kind == "S":
                        start, rows = tiles[t]
                        act.wait_ge(max_done, b * NTL + (t + 1))
                        last = nc.scalar.activation(prob[0:rows, t % 2, :], s[0:rows, 0:S], ACT.Exp,
                                                    bias=small[0:rows, t, 0:1], scale=scale,
                                                    accum_out=small[0:rows, t, 1:2])
                    else:
                        start, rows = tiles[t]
                        full = NTL - 1
                        nc.scalar.copy(prob_t[:, 0:full, start:start + rows],
                                       s[:, 0:full * P].rearrange("p (j n) -> p j n", j=full)[:, :, 0:rows])
                        jr = tiles[full][1]
                        last = nc.scalar.copy(prob_t[0:jr, full, start:start + rows], s[0:jr, full * P:full * P + rows])
                    last.then_inc(act_took, 1)

        @block.vector
        def _(dve):
            ve = nc.vector
            ve.memset(tmp[:, 0:1], 0.0).then_inc(xb_used, 1)
            ve.memset(tmp[:, 1:2], 0.0).then_inc(dve_took, 4)
            dve.wait_ge(dve_took, 4)
            dve.wait_ge(xb_used, 1)
            chain = Chain(dve, own)
            steps = 2 * 4 + 3 * NTL
            with nc.vector.Fori(0, NB) as b:
                chain.begin(b, steps)
                for n, (kind, t) in enumerate(units):
                    s = slot(n)
                    if kind == "V":
                        rows = tiles[t][1]
                        dve.wait_ge(filled, b * NU + (n + 1))
                        ve.tensor_tensor(v[0:rows, t, :], s[0:rows, 0:D], bv[0:rows, :], ALU.add).then_inc(dve_took, 1)
                    if kind == "V" and t == NTL - 1:
                        ve.memset(small[:, 0, 2:3], 0.0).then_inc(xb_used, 1)
                        taker_wait(dve, b, units.index(("K", 1)))
                        cos, sin = rope[:, 0, :], rope[:, 1, :]
                        for c in range(2):
                            a0, a1 = raw[:, c, 0, :], raw[:, c, 1, :]
                            r0, r1 = rot[:, c, 0, :], rot[:, c, 1, :]
                            ve.tensor_tensor(r0, a0, cos, ALU.mult)
                            ve.tensor_tensor(r1, a1, cos, ALU.mult)
                            chain.step(ve.tensor_tensor(tmp[:], a1, sin, ALU.mult))
                            chain.step(ve.tensor_tensor(r0, r0, tmp[:], ALU.subtract))
                            chain.step(ve.tensor_tensor(tmp[:], a0, sin, ALU.mult))
                            ins = ve.tensor_tensor(r1, r1, tmp[:], ALU.add)
                            chain.step(ins)
                        ve.tensor_copy(tmp[:, 0:1], rope[:, 0, 0:1]).then_inc(roped, 1)
                        dve.wait_ge(roped, b + 1)
                    if kind == "S":
                        rows = tiles[t][1]
                        dve.wait_ge(filled, b * NU + (n + 1))
                        chain.step(ve.tensor_reduce(small[0:rows, t, 2:3], s[0:rows, 0:S], AX_X, ALU.max))
                        ve.tensor_scalar(small[0:rows, t, 0:1], small[0:rows, t, 2:3], -scale, None,
                                         ALU.mult).then_inc(max_done, 1)
                    if kind == "S" and t >= 1 or kind == "T" and t == NTL - 1:
                        p = t - 1 if kind == "S" else t
                        rows = tiles[p][1]
                        taker_wait(dve, b, units.index(("S", p)))
                        chain.step(ve.reciprocal(small[0:rows, p, 2:3], small[0:rows, p, 1:2]))
                        chain.step(ve.tensor_scalar(prob[0:rows, p % 2, :], prob[0:rows, p % 2, :],
                                                    small[0:rows, p, 2:3], None, ALU.mult))
                        ve.tensor_copy(tmp[:, 1:2], rope[:, 0, 0:1]).then_inc(prob_done, 1)
                        dve.wait_ge(prob_done, b * NTL + (p + 1))
                    if kind == "O":
                        dve.wait_ge(filled, b * NU + (n + 1))
                        ve.tensor_copy(o_sb[:, t, :], s[:, 0:S]).then_inc(dve_took, 1)
                    if kind == "Y":
                        at = bass.ds(b * S, S)
                        dve.wait_ge(filled, b * NU + (n + 1))
                        chain_y = ve.scalar_tensor_tensor(tmp[:], s[:, 0:S], vec[:, 3, t:t + 1], g.xn[:, t, at],
                                                          ALU.add, ALU.add)
                        chain_y.then_inc(dve_took, 1)
                        taker_wait(dve, b, n)
                        ve.tensor_tensor(g.h[:, t, at], g.h[:, t, at], tmp[:], ALU.add).then_inc(added, 1)
                        dve.wait_ge(added, b * KD + (t + 1))
                chain.end(NB)


def delta_net(g):
    nc, dram = g.nc, g.dram
    H, DH, J = 8, 32, 2
    HJ = H * J
    tiles = [(s, min(P, S - s)) for s in range(0, S, P)]
    NTL = len(tiles)
    off = [sum(S - s for s, _ in tiles[:n]) for n in range(NTL)]
    DEC = off[-1] + S - tiles[-1][0]
    VG = D + H

    def cuts(lo, hi):
        return [(max(lo, a), min(hi, b)) for a, b in ((0, 512), (512, S)) if max(lo, a) < min(hi, b)]

    units = [("q", 0), ("q", 1), ("k", 0), ("k", 1)] + [("v", t) for t in range(NTL)] \
        + [("beta", 0), ("mix", 0), ("diff", 0)] + [("a", (n, t)) for n in range(H) for t in range(NTL)] \
        + [("coef", n) for n in range(H)]
    takers = {"q": "dve", "k": "dve", "v": "dve", "beta": "act", "mix": "act", "diff": "act", "a": "act",
              "coef": "dve"}
    NU = len(units)
    assert NU % 2 == 0
    dve_n, act_n, seen_d, seen_a = [], [], 0, 0
    for kind, _ in units:
        seen_d += takers[kind] == "dve"
        seen_a += takers[kind] == "act"
        dve_n.append(seen_d)
        act_n.append(seen_a)
    ND, NA = seen_d, seen_a
    first_a = units.index(("a", (0, 0)))
    first_c = units.index(("coef", 0))
    NB_USES = HJ + 3

    with ExitStack() as ctx:
        sc = Scope(nc, ctx, "dn")
        w_qk = sc.sb("w_qk", [P, KD, 2 * D])
        w_vg = sc.sb("w_vg", [P, KD, VG])
        w_bm = sc.sb("w_bm", [P, KD, 2 * HJ])
        w_o = sc.sb("w_o", [P, H, D])
        b_gate = sc.sb("b_gate", [P, H])
        vec16 = sc.sb("vec16", [HJ, 3])
        vec = sc.sb("vec", [P, 3, KD])
        diff = sc.sb("diff", [HJ, P])
        pick = sc.sb("pick", [HJ, HJ, P])
        pick_den = sc.sb("pick_den", [P, H, HJ])
        spread = sc.sb("spread", [HJ, H, P])
        eye = sc.sb("eye", [P, S])
        hres = sc.sb("hres", [P, KD, NT])
        loads = [(w_qk, "dn_wqk"), (w_vg, "dn_wvg"), (w_bm, "dn_wbm"), (w_o, "dn_wo"), (vec16, "dn_vec16"),
                 (vec, "dn_vec"), (diff, "c_diff"), (pick, "c_pick"), (pick_den, "c_pick_den"),
                 (spread, "c_spread"), (eye, "c_eye")]
        layer_norm(g, "dnn", g.h, g.xn, loads=[(a[:], dram[n]) for a, n in loads]
                   + [(b_gate[:], dram["L0_attn_bgate"].to_broadcast([P, H]))])

        def core(ctx):
            sc = Scope(nc, ctx, "dc")
            xb = sc.sb("xb", [P, KD, S])
            qk = sc.sb("qk", [P, 4, NTL * P])
            ex = sc.sb("ex", [P, 4, S])
            gl = sc.sb("gl", [P, NTL, H])
            vr = sc.sb("vr", [P, NTL, D])
            vg = sc.sb("vg", [P, NTL, H, 2 * DH])
            beta = sc.sb("beta", [HJ, S])
            mix = sc.sb("mix", [HJ, S])
            den = sc.sb("den", [HJ, S])
            decay = sc.sb("decay", [P, J, DEC])
            a_sb = sc.sb("a_sb", [P, 2, S])
            wt = sc.sb("wt", [P, 2, J, S])
            o_sb = sc.sb("o_sb", [P, H, S])
            ps_a = sc.ps("ps_a", [P, 2, 1024])
            ps_b = sc.ps("ps_b", [P, 1024])
            ps_o = sc.ps("ps_o", [P, 1024])
            xb_ready = sc.sem("xb_ready")
            filled = sc.sem("filled")
            dve_took = sc.sem("dve_took")
            act_took = sc.sem("act_took")
            low_ready = sc.sem("low_ready")
            exp_done = sc.sem("exp_done")
            gate_in = sc.sem("gate_in")
            gate_done = sc.sem("gate_done")
            v_done = sc.sem("v_done")
            beta_done = sc.sem("beta_done")
            b_filled = sc.sem("b_filled")
            b_took = sc.sem("b_took")
            w0_done = sc.sem("w0_done")
            w1_done = sc.sem("w1_done")
            o_ready = sc.sem("o_ready")
            o_took = sc.sem("o_took")
            den_done = sc.sem("den_done")
            own = sc.sem("own")
            zeroed = sc.sem("zeroed")
            block = ctx.enter_context(nc.Block())
            UA = H * NTL

            def slot(n):
                return ps_a[:, n % 2]

            @block.gpsimd
            def _(pool):
                pool.wait_ge(zeroed, 1)
                nc.gpsimd.memset(a_sb[:, 0, 0:1], 0.0).then_inc(w1_done, 2)
                with nc.gpsimd.Fori(0, NB) as b:
                    pool.wait_ge(beta_done, b + 1)
                    nc.gpsimd.tensor_copy(xb[:], g.xn[:, :, bass.ds(b * S, S)]).then_inc(xb_ready, 1)
                    for h in range(H):
                        for t, (start, rows) in enumerate(tiles):
                            m, u = S - start, h * NTL + t
                            pool.wait_ge(act_took, b * NA + act_n[first_a + u])
                            pool.wait_ge(b_took, b * NB_USES + (h * J + 3))
                            nc.gpsimd.tensor_tensor(wt[0:rows, u % 2, 1, 0:m], a_sb[0:rows, u % 2, 0:m],
                                                    decay[0:rows, 1, off[t]:off[t] + m], ALU.mult).then_inc(w1_done, 1)

            @block.tensor
            def _(pe):
                def dve_has(n, b):
                    pe.wait_ge(dve_took, b * ND + (dve_n[n] + 2))

                def fill(n, b):
                    kind, arg = units[n]
                    s = slot(n)
                    if n >= 2:
                        if takers[units[n - 2][0]] == "dve":
                            dve_has(n - 2, b)
                        else:
                            pe.wait_ge(act_took, b * NA + act_n[n - 2])
                    else:
                        pe.wait_ge(dve_took, b * ND + (n + 1))
                    if kind in "qk":
                        col = (0 if kind == "q" else D) + arg * P
                        for lo, hi in cuts(0, S):
                            for k in range(KD):
                                mm = nc.tensor.matmul(s[:, lo:hi], w_qk[:, k, col:col + P], xb[:, k, lo:hi],
                                                      start=(k == 0), stop=(k == KD - 1))
                    elif kind == "v":
                        start, rows = tiles[arg]
                        for k in range(KD):
                            mm = nc.tensor.matmul(s[0:rows, 0:VG], xb[:, k, start:start + rows], w_vg[:, k, :],
                                                  start=(k == 0), stop=(k == KD - 1))
                    elif kind in ("beta", "mix"):
                        col = 0 if kind == "beta" else HJ
                        for lo, hi in cuts(0, S):
                            for k in range(KD):
                                mm = nc.tensor.matmul(s[0:HJ, lo:hi], w_bm[:, k, col:col + HJ], xb[:, k, lo:hi],
                                                      start=(k == 0), stop=(k == KD - 1))
                    elif kind == "diff":
                        pe.wait_ge(act_took, b * NA + act_n[n - 1])
                        for lo, hi in cuts(0, S):
                            mm = nc.tensor.matmul(s[:, lo:hi], diff[:], mix[:, lo:hi], start=True, stop=True)
                    elif kind == "a":
                        h, t = arg
                        start, rows = tiles[t]
                        r = slice(h % 4 * DH, h % 4 * DH + DH)
                        for lo, hi in cuts(0, S - start):
                            mm = nc.tensor.matmul(s[:, lo:hi], qk[r, 2 + h // 4, start:start + P],
                                                  qk[r, h // 4, start + lo:start + hi], start=True, stop=True)
                    else:
                        for lo, hi in cuts(0, S):
                            mm = nc.tensor.matmul(s[:, lo:hi], spread[:, arg, :], den[:, lo:hi], start=True, stop=True)
                    mm.then_inc(filled, 1)

                def betas(hj, b):
                    pe.wait_ge(b_took, b * NB_USES + (hj + 1))
                    for lo, hi in cuts(0, S):
                        mm = nc.tensor.matmul(ps_b[:, lo:hi], pick[:, hj, :], beta[:, lo:hi], start=True, stop=True)
                    mm.then_inc(b_filled, 1)

                def with_v(h, t, b):
                    start = tiles[t][0]
                    u = h * NTL + t
                    pe.wait_ge(w0_done, b * UA + (u + 3))
                    pe.wait_ge(w1_done, b * UA + (u + 3))
                    for j in range(J):
                        for lo, hi in cuts(start, S):
                            mm = nc.tensor.matmul(ps_o[j * 2 * DH:(j + 1) * 2 * DH, lo:hi], vg[:, t, h, :],
                                                  wt[:, u % 2, j, lo - start:hi - start], start=(t == 0),
                                                  stop=(t == NTL - 1), skip_group_check=True)
                    if t == NTL - 1:
                        mm.then_inc(o_ready, 1)

                pe.wait_ge(zeroed, 1)
                with nc.tensor.Fori(0, NB) as b:
                    pe.wait_ge(xb_ready, b + 1)
                    for n in range(first_a):
                        fill(n, b)
                    pe.wait_ge(beta_done, b + 2)
                    betas(0, b)
                    betas(1, b)
                    pe.wait_ge(v_done, b + 1)
                    for h in range(H):
                        fill(first_a + h * NTL, b)
                        for t in range(NTL):
                            if t + 1 < NTL:
                                fill(first_a + h * NTL + t + 1, b)
                            if t == 0:
                                if h >= 1:
                                    betas(h * J + 1, b)
                                pe.wait_ge(o_took, b * H + (h + 1))
                            with_v(h, t, b)
                            if t == 0 and h + 1 < H:
                                betas((h + 1) * J, b)
                    pe.wait_ge(o_took, b * H + (H + 1))
                    pe.wait_ge(b_took, b * NB_USES + (HJ + 1))
                    for lo, hi in cuts(0, S):
                        for h in range(H):
                            mm = nc.tensor.matmul(ps_b[0:HJ, lo:hi], pick_den[:, h, :], o_sb[:, h, lo:hi],
                                                  start=(h == 0), stop=(h == H - 1))
                    mm.then_inc(b_filled, 1)
                    pe.wait_ge(den_done, b + 1)
                    for h in range(H):
                        fill(first_c + h, b)
                    dve_has(NU - 1, b)
                    for m in range(KD):
                        pe.wait_ge(b_took, b * NB_USES + (HJ + 2 + m))
                        for lo, hi in cuts(0, S):
                            for h in range(H):
                                mm = nc.tensor.matmul(ps_b[:, lo:hi], w_o[:, h, m * P:(m + 1) * P], o_sb[:, h, lo:hi],
                                                      start=(h == 0), stop=(h == H - 1))
                        mm.then_inc(b_filled, 1)

            @block.scalar
            def _(act):
                with nc.scalar.Fori(0, NB) as b:
                    for n in range(4):
                        act.wait_ge(low_ready, b * 4 + (n + 1))
                        nc.scalar.activation(ex[:, n, :], ex[:, n, :], ACT.Exp).then_inc(exp_done, 1)
                    act.wait_ge(gate_in, b + 1)
                    nc.scalar.activation(gl[:], gl[:], ACT.Sigmoid).then_inc(gate_done, 1)
                    for n, (kind, arg) in enumerate(units):
                        if takers[kind] != "act":
                            continue
                        s = slot(n)
                        act.wait_ge(filled, b * NU + (n + 1))
                        if kind == "beta":
                            last = nc.scalar.activation(beta[:], s[0:HJ, 0:S], ACT.Sigmoid, bias=vec16[:, 0:1])
                        elif kind == "mix":
                            last = nc.scalar.activation(mix[:], s[0:HJ, 0:S], ACT.Identity, bias=vec16[:, 1:2])
                        elif kind == "diff":
                            last = nc.scalar.activation(mix[:], s[0:HJ, 0:S], ACT.Sigmoid)
                        else:
                            h, t = arg
                            start, rows = tiles[t]
                            u = h * NTL + t
                            act.wait_ge(w0_done, b * UA + (u + 1))
                            act.wait_ge(w1_done, b * UA + (u + 1))
                            last = nc.scalar.copy(a_sb[0:rows, u % 2, 0:S - start], s[0:rows, 0:S - start])
                        last.then_inc(act_took, 1)
                        if kind == "a" and arg[1] == NTL - 1:
                            h = arg[0]
                            act.wait_ge(o_ready, b * H + (h + 1))
                            nc.scalar.copy(o_sb[:, h, :], ps_o[:, 0:S]).then_inc(o_took, 1)

            @block.vector
            def _(dve):
                ve = nc.vector
                chain = Chain(dve, own)
                ve.memset(vg[:], 0.0).then_inc(beta_done, 1)
                ve.memset(qk[:], 0.0).then_inc(dve_took, 2)
                ve.memset(wt[:], 0.0).then_inc(b_took, 1)
                ve.memset(beta[:, 0:1], 0.0).then_inc(o_took, 1)
                ve.memset(mix[:, 0:1], 0.0).then_inc(w0_done, 2)
                ve.memset(gl[:], 0.0).then_inc(zeroed, 1)
                dve.wait_ge(zeroed, 1)

                def scan(hj, b):
                    j = hj % 2
                    dve.wait_ge(b_filled, b * NB_USES + (hj + 1))
                    for t, (start, rows) in enumerate(tiles):
                        m = S - start
                        last = ve.tensor_tensor_scan(decay[0:rows, j, off[t]:off[t] + m], ps_b[0:rows, start:S],
                                                     eye[0:rows, 0:m], 0.0, ALU.mult, ALU.add)
                    last.then_inc(b_took, 1)

                with nc.vector.Fori(0, NB) as b:
                    chain.begin(b, 1)
                    for n in range(4):
                        dve.wait_ge(filled, b * NU + (n + 1))
                        ve.tensor_scalar(ex[:, n, :], slot(n)[:, 0:S], 0.0, None, ALU.min).then_inc(low_ready, 1)
                        if n % 2 == 1:
                            for m in (n - 1, n):
                                dve.wait_ge(exp_done, b * 4 + (m + 1))
                                ve.scalar_tensor_tensor(qk[:, m, 0:S], slot(m)[:, 0:S], 0.0, ex[:, m, :], ALU.max,
                                                        ALU.add).then_inc(dve_took, 1)
                    for t, (start, rows) in enumerate(tiles):
                        s = slot(4 + t)
                        dve.wait_ge(filled, b * NU + (4 + t + 1))
                        ve.tensor_tensor(gl[0:rows, t, :], s[0:rows, D:VG], b_gate[0:rows, :], ALU.add)
                        ve.tensor_copy(vr[0:rows, t, :], s[0:rows, 0:D]).then_inc(dve_took, 1)
                    ve.tensor_copy(ex[:, 0, 0:1], eye[:, 0:1]).then_inc(gate_in, 1)
                    dve.wait_ge(act_took, b * NA + act_n[units.index(("mix", 0))])
                    ve.tensor_scalar(beta[:], beta[:], vec16[:, 2:3], 0.9999, ALU.mult, ALU.min).then_inc(beta_done, 1)
                    dve.wait_ge(gate_done, b + 1)
                    dve.wait_ge(dve_took, b * ND + (9 + 2))
                    full = NTL - 1
                    for lo, hi, rows in ((0, full, P), (full, NTL, tiles[full][1])):
                        gb = gl[0:rows, lo:hi, :].rearrange("p t (h a) -> p (t h) a", a=1).to_broadcast(
                            [rows, (hi - lo) * H, DH])
                        o = vg[0:rows, lo:hi].rearrange("p t h d -> p (t h) d")
                        ve.tensor_tensor(o[:, :, 0:DH], vr[0:rows, lo:hi, :].rearrange("p t (h d) -> p (t h) d", d=DH),
                                         gb, ALU.mult)
                        last = ve.tensor_copy(o[:, :, DH:2 * DH], gb)
                    last.then_inc(v_done, 1)
                    scan(0, b)
                    scan(1, b)
                    for h in range(H):
                        dve.wait_ge(b_took, b * NB_USES + (h * J + 3))
                        for t, (start, rows) in enumerate(tiles):
                            m, u = S - start, h * NTL + t
                            dve.wait_ge(act_took, b * NA + act_n[first_a + u])
                            ve.tensor_tensor(wt[0:rows, u % 2, 0, 0:m], a_sb[0:rows, u % 2, 0:m],
                                             decay[0:rows, 0, off[t]:off[t] + m], ALU.mult).then_inc(w0_done, 1)
                        if h + 1 < H:
                            dve.wait_ge(w0_done, b * UA + ((h + 1) * NTL + 2))
                            scan((h + 1) * J, b)
                            dve.wait_ge(w1_done, b * UA + ((h + 1) * NTL + 2))
                            scan((h + 1) * J + 1, b)
                    dve.wait_ge(b_filled, b * NB_USES + (HJ + 1))
                    ve.tensor_scalar(den[:], ps_b[0:HJ, 0:S], 1.0e-6, None, ALU.add).then_inc(b_took, 1)
                    dve.wait_ge(b_took, b * NB_USES + (HJ + 2))
                    chain.step(ve.reciprocal(den[:], den[:]))
                    ve.tensor_tensor(den[:], den[:], mix[:], ALU.mult).then_inc(den_done, 1)
                    for h in range(H):
                        dve.wait_ge(filled, b * NU + (first_c + h + 1))
                        ve.tensor_tensor(o_sb[:, h, :], o_sb[:, h, :], slot(first_c + h)[:, 0:S],
                                         ALU.mult).then_inc(dve_took, 1)
                    for m in range(KD):
                        dve.wait_ge(b_filled, b * NB_USES + (HJ + 2 + m))
                        at = bass.ds(b * S, S)
                        ve.scalar_tensor_tensor(hres[:, m, at], ps_b[:, 0:S], vec[:, 0, m:m + 1], g.xn[:, m, at],
                                                ALU.add, ALU.add).then_inc(b_took, 1)

        with ExitStack() as mid:
            core(mid)
        layer_norm(g, "dno", hres, hres, vec[:, 1, :], vec[:, 2, :], add_to=g.h)


def store_output(g, out):
    nc = g.nc
    with ExitStack() as ctx:
        sc = Scope(nc, ctx, "out")
        rows = sc.sb("rows", [RN, RT, D])
        ps = sc.ps("ps", [P, 8, 512])
        turned = sc.sem("turned")
        copied = sc.sem("copied")
        stored = sc.sem("stored")
        block = ctx.enter_context(nc.Block())
        view = out.rearrange("(t p) d -> p t d", p=RN)
        half = RT // 2

        @block.tensor
        def _(pe):
            for t in range(RT):
                if t >= 8:
                    pe.wait_ge(copied, t - 7)
                for k in range(KD):
                    mm = nc.tensor.transpose(ps[0:RN, t % 8, k * P:(k + 1) * P],
                                             g.h[:, k, t * RN:(t + 1) * RN], g.ident[:])
                mm.then_inc(turned, 1)

        @block.vector
        def _(dve):
            for t in range(RT):
                dve.wait_ge(turned, t + 1)
                nc.vector.tensor_copy(rows[:, t, :], ps[0:RN, t % 8, 0:D]).then_inc(copied, 1)

        @block.sync
        def _(sp):
            for n in range(2):
                sp.wait_ge(copied, half * (n + 1))
                sp.dma_start(view[:, half * n:half * (n + 1), :],
                             rows[:, half * n:half * (n + 1), :]).then_inc(stored, 16)
            sp.wait_ge(stored, 32)


def program(nc, dram, out):
    dram["s_gate"] = nc.dram_tensor("s_gate", (NE + 1, N_SEL), F32).ap()
    dram["s_rows"] = nc.dram_tensor("s_rows", (NT, D), F32).ap()
    dram["s_slot"] = nc.dram_tensor("s_slot", (BLOCKS * CN, 1), F32).ap()
    dram["s_extra"] = nc.dram_tensor("s_extra", (NT + 1, D), F32).ap()
    dram["s_y"] = nc.dram_tensor("s_y", (BLOCKS * CN, D), F32).ap()
    with ExitStack() as ctx:
        Scope.in_use.clear()
        g = Shared(nc, ctx, dram)
        load_constants(g)
        text_block(g)
        clear_semaphores(nc)
        delta_net(g)
        clear_semaphores(nc)
        selected_ffn(g)
        clear_semaphores(nc)
        gated_scan(g)
        clear_semaphores(nc)
        mixture(g, "m1", "m1_w", 192, "L1", "L1_ffn_W_gate_router", None,
                ("L1_ffn_Wg_s", "L1_ffn_Wu_s", "L1_ffn_Wd_s"))
        clear_semaphores(nc)
        query_attention(g)
        clear_semaphores(nc)
        three_matrices(g)
        clear_semaphores(nc)
        full_attention(g)
        clear_semaphores(nc)
        mixture(g, "m3", "m3_w", 688, "L3", "L3_ffn_Ws", "L3_ffn_bs")
        clear_semaphores(nc)
        store_output(g, out)



def _blocks(w):
    n = w.shape[-1]
    k = w.shape[-2] // P
    lead = w.shape[:-2]
    return w.reshape(*lead, k, P, n).swapaxes(-3, -2)


def _swap(np, stripe):
    half = stripe // 2
    to = np.arange(P)
    m = np.zeros((P, P), np.float32)
    m[to // stripe * stripe + half + to % half, to] = 1.0
    return m


def _stack_selection(np, dh):
    heads = P // dh
    m = np.zeros((P, 4, heads, P), np.float32)
    d = np.arange(dh)
    for h in range(heads):
        for part, places in enumerate(((0, 2), (1,), (0, 1), (2,))):
            for place in places:
                m[h * dh + d, part, h, place * dh + d] = 1.0
    return m


def _stripes(np, w, heads, dh):
    w = w.reshape(-1, heads, dh)
    return np.concatenate([w, np.zeros_like(w)], axis=2).reshape(w.shape[0], -1)


def _delta_constants(np):
    r = np.arange(16)
    diff = np.zeros((16, P), np.float32)
    diff[r, r], diff[r ^ 1, r] = 1.0, -1.0
    pick = np.zeros((16, 16, P), np.float32)
    pick[r, r] = 1.0
    pick_den = np.zeros((P, 8, 16), np.float32)
    spread = np.zeros((16, 8, P), np.float32)
    for h in range(8):
        for j in range(2):
            pick_den[64 * j + 32, h, 2 * h + j] = 1.0
            spread[2 * h + j, h, 64 * j:64 * j + 32] = 1.0
    return {"c_diff": diff, "c_pick": pick, "c_pick_den": pick_den, "c_spread": spread}


def _decay_cap(np):
    slopes = np.array([0.5 ** (n + 1) for n in range(8)], dtype=np.float32)
    return np.repeat(np.exp(-slopes), 2)[:, None]


def _expert_rows(np, wg, wu, wd):
    e, f, _ = wd.shape
    n, starts, widths = hidden_tiles(f)
    down = np.zeros((e, P, n, D), wd.dtype)
    for i in range(n):
        down[:, :widths[i], i] = wd[:, starts[i]:starts[i] + widths[i]]
    parts = [_blocks(wg), _blocks(wu), down]
    return np.concatenate([p.reshape(e * P, -1) for p in parts], axis=1)


def _constants(np):
    at = np.arange(S_TXT, dtype=np.float32)[:, None]
    even = np.arange(0, D, 2, dtype=np.float32)[None]
    angle = at / np.power(np.float32(10000.0), np.float32(2.0) * even / np.float32(D))
    pos = np.zeros((S_TXT, D), np.float32)
    pos[:, 0::2], pos[:, 1::2] = np.sin(angle), np.cos(angle)
    freq = np.float32(1.0) / np.float32(10000.0) ** (np.arange(P, dtype=np.float32) / np.float32(P))
    turn = np.arange(S, dtype=np.float32)[:, None] * freq[None]
    rope = np.stack([np.round(np.cos(turn)), np.round(np.sin(turn))]).transpose(2, 0, 1)
    tok = np.arange(NT, dtype=np.float32).reshape(RT, RN).T
    return {
        "c_ident": np.eye(P, dtype=np.float32),
        "c_rank": np.broadcast_to(np.arange(NE, 0, -1, dtype=np.float32), (P, NE)),
        "c_tok": tok,
        "c_keep": np.broadcast_to(np.arange(RT) > 0, (P, NE, RT)).astype(np.float32),
        "c_lower": np.triu(np.ones((P, P), np.float32), 1),
        "c_steps": np.broadcast_to(np.arange(BLOCKS, dtype=np.float32), (P, BLOCKS)),
        "c_lane": np.arange(P, dtype=np.float32)[:, None] - P,
        "c_pos_txt": pos.reshape(S_TXT // P, P, D).swapaxes(0, 1),
        "c_rope": rope,
        "c_eye": np.eye(P, S, dtype=np.float32),
        **_delta_constants(np),
        "c_ones_row": (np.arange(P)[:, None] // 2 == 48).astype(np.float32),
        "c_sel16": _stack_selection(np, 16),
        "c_sel32": _stack_selection(np, 32),
        "c_mask_q": np.triu(np.full((P, P), -BIG, np.float32), 1),
        "c_mask_k": np.tril(np.full((P, P), -BIG, np.float32), -1),
        "c_swap32": _swap(np, 32),
        "c_swap64": _swap(np, 64),
    }


def _layouts(np, x):
    a = {}
    row = lambda n: x[n].reshape(1, -1)
    col = lambda n: x[n].reshape(-1, P).T
    a["L3_ffn_Ws"] = _blocks(x["L3_ffn_Ws"])
    a["L3_ffn_bs"] = row("L3_ffn_bs")
    for n in ("L1", "L3"):
        a[f"m{n[1]}_w"] = _expert_rows(np, *(x[f"{n}_ffn_W{m}"] for m in "gud"))
    for n in ("L1_ffn_Wg_s", "L1_ffn_Wu_s"):
        a[n] = _blocks(x[n])
    a["L1_ffn_Wd_s"] = x["L1_ffn_Wd_s"]
    a["L1_ffn_W_gate_router"] = _blocks(x["L1_ffn_W_gate_router"])
    a["L1_ffn_expert_bias"] = row("L1_ffn_expert_bias")
    cat = lambda e, s: np.concatenate([x["L0_ffn_" + e], x["L0_ffn_" + s][None]])
    a["f0_w1"] = _blocks(cat("ew1", "sw1").swapaxes(1, 2))
    a["f0_w2"] = _blocks(cat("ew2", "sw2").swapaxes(1, 2))
    a["f0_w3"] = cat("ew3", "sw3").swapaxes(1, 2)
    each = lambda n: np.broadcast_to(x["L0_ffn_" + n], (NE, P))
    b3 = cat("eb3", "sb3").reshape(NE + 1, KD, P)
    a["f0_vec"] = np.stack([
        cat("eb1", "sb1"), cat("eb2", "sb2"),
        np.concatenate([each("sel_ln_g"), x["L0_ffn_s_ln_g"][None]]),
        np.concatenate([each("sel_ln_b"), x["L0_ffn_s_ln_b"][None]]), b3[:, 0], b3[:, 1]], axis=-1)
    a["f0_router_w"] = _blocks(np.concatenate([x["L0_ffn_eg_w"], x["L0_ffn_sg_w"]]).T)
    a["f0_router_b"] = np.concatenate([x["L0_ffn_eg_b"], x["L0_ffn_sg_b"]])[None]
    a["L0_ffn_exp_bias"] = row("L0_ffn_exp_bias")
    a["f0_index"] = np.stack([x["L0_ffn_index_" + n].reshape(SEL_T, P).T for n in "bt"], axis=1)
    for n in ("L1_attn_W_in", "L1_attn_Wa", "L1_attn_Wb", "L1_attn_Wc", "L1_attn_Wo",
              "L2_ffn_weight", "L2_ffn_aux_weight1", "L2_ffn_aux_weight2"):
        a[n] = _blocks(x[n])
    a["s1_vec"] = np.concatenate([col("L1_attn_" + n) for n in ("b_in", "conv_b", "ba", "bb", "bc")], axis=1)
    for n in ("L1_attn_bo", "L1_attn_gamma", "L1_attn_beta", "L2_ffn_bias"):
        a[n] = col(n)
    a["L1_attn_conv_w"] = x["L1_attn_conv_w"].reshape(-1, P, 3).swapaxes(0, 1)
    wq = x["L2_attn_Wq"].swapaxes(0, 1).reshape(D, D)
    a["q2_wq"] = _blocks(wq)
    a["q2_wk"] = _blocks(np.pad(x["L2_attn_Wk"], ((0, 0), (0, P - 32))))
    a["q2_wv"] = _blocks(_stripes(np, x["L2_attn_Wv"], 1, 32))
    a["q2_wo"] = _stripes(np, x["L2_attn_Wp"].T, 8, 32).T.reshape(-1, P, D).swapaxes(0, 1)
    a["q2_bq"] = np.zeros((P, 2), np.float32)
    a["q2_bk"] = np.zeros((P, 1), np.float32)
    a["q2_bv"] = np.repeat(np.array([[0.0, 1.0]], np.float32), 32, axis=1)
    a["L2_attn_bp"] = col("L2_attn_bp")
    p = x["x"].reshape(NB, 3, 6, 16, 6, 16).transpose(1, 3, 5, 0, 2, 4).reshape(3 * 256, -1)
    a["patches"] = _blocks(p)
    a["L0_tok_W"] = _blocks(x["L0_tok_W"].T)
    a["tok_vec"] = np.stack([col("L0_tok_b"), col("L0_tok_cls_token")], axis=1)
    a["L0_tok_pos_embedding"] = x["L0_tok_pos_embedding"][0].T.reshape(KD, P, S_IMG).swapaxes(0, 1)
    a["x_txt"] = x["x_txt"].reshape(-1, P).T
    a["L0_txt_emb"] = x["L0_txt_emb"]
    w, b = x["L0_txt_in_proj_w"].T, x["L0_txt_in_proj_b"][None]
    part = lambda t, n: t[:, n * D:(n + 1) * D]
    a["ta_wq"], a["ta_wk"] = _blocks(part(w, 0)), _blocks(part(w, 1))
    a["ta_wv"] = _blocks(_stripes(np, part(w, 2), 16, 16))
    a["ta_bq"], a["ta_bk"] = (part(b, n).reshape(-1, P).T for n in range(2))
    a["ta_bv"] = np.where(np.arange(512)[None] % 32 >= 16, np.float32(1.0), _stripes(np, part(b, 2), 16, 16))
    a["ta_wo"] = _stripes(np, x["L0_txt_out_proj_w"], 16, 16).T.reshape(-1, P, D).swapaxes(0, 1)
    a["L0_txt_out_proj_b"] = col("L0_txt_out_proj_b")
    a["L0_txt_w1"] = _blocks(x["L0_txt_w1"].T)
    a["L0_txt_w2"] = _blocks(x["L0_txt_w2"].T)
    a["L0_txt_b1"] = col("L0_txt_b1")
    a["txt_vec"] = np.stack([col("L0_txt_" + n) for n in ("b2", "g1", "beta1", "g2", "beta2")], axis=1)
    t = lambda n: x["L0_attn_" + n].T
    a["dn_wqk"] = _blocks(np.concatenate([t("Wq"), t("Wk")], axis=1))
    a["dn_wvg"] = _blocks(np.concatenate([t("Wv"), t("Wgate")], axis=1))
    a["dn_wbm"] = _blocks(np.concatenate([t("Wbeta"), t("Wmix")], axis=1))
    wo = t("Wout").reshape(8, 32, D)
    z = np.zeros_like(wo)
    a["dn_wo"] = np.concatenate([wo, z, wo, z], axis=1).swapaxes(0, 1)
    a["dn_vec16"] = np.concatenate([x["L0_attn_bbeta"][:, None], x["L0_attn_bmix"][:, None], _decay_cap(np)], axis=1)
    a["dn_vec"] = np.stack([col("L0_attn_" + n) for n in ("bout", "ln_g", "ln_b")], axis=1)
    a["L0_attn_bgate"] = row("L0_attn_bgate")
    a["L3_attn_w_qkv"] = _blocks(x["L3_attn_w_qkv"])
    a["L3_attn_w_proj"] = _blocks(x["L3_attn_w_proj"])
    qkv_b = x["L3_attn_b_qkv"].reshape(3, KD, P)
    a["a3_vec"] = np.stack([col("L3_attn_g_norm"), qkv_b[0].T, qkv_b[1].T, col("L3_attn_b_proj")], axis=1)
    a["a3_bv"] = x["L3_attn_b_qkv"][None, 2 * D:]
    return a


def kernel(**inputs):
    import numpy as np
    import concourse.bacc as bacc
    from concourse.bass_utils import run_bass_kernel_spmd

    nc = bacc.Bacc("TRN2", target_bir_lowering=False, num_devices=1)
    laid = {**_layouts(np, inputs), **_constants(np)}
    arrays, dram = {}, {}
    for name, value in laid.items():
        value = np.ascontiguousarray(value)
        arrays[f"in_{name}"] = value
        dram[name] = nc.dram_tensor(f"in_{name}", value.shape, mybir.dt.from_np(value.dtype),
                                    kind="ExternalInput").ap()
    out = nc.dram_tensor("out_0", (NT, D), F32, kind="ExternalOutput").ap()
    program(nc, dram, out)
    result = run_bass_kernel_spmd(nc, [arrays], core_ids=[0]).results[0]["out_0"]
    return result.reshape(NB, S, D)
```

```python
from contextlib import ExitStack

import concourse.bass as bass
from concourse import mybir

F32 = mybir.dt.float32
F32R = mybir.dt.float32r
I32 = mybir.dt.int32
ALU = mybir.AluOpType
ACT = mybir.ActivationFunctionType
AX_X = mybir.AxisListType.X

P = 128
D = 256
KD = D // P
NB = 4
S_IMG = 37
S_TXT = 512
S = S_IMG + S_TXT
NT = NB * S
CH = 6
CN = NT // CH
RT = 18
RN = NT // RT
NE = 8
SUB = CN // RN
BLOCKS = (2 * NT + NE * (CN - 1)) // CN
SLOT_TILES = BLOCKS * SUB
N_SEL = 512
SEL_T = N_SEL // P
VOCAB = 8000
BIG = 1.0e30


class Chain:

    def __init__(self, engine, semaphore):
        self.engine, self.semaphore = engine, semaphore
        self.base, self.n, self.turn = 0, 0, None

    def begin(self, i, per):
        self.turn, self.per, self.n = i, per, 0

    def end(self, turns):
        assert self.n == self.per, (self.n, self.per)
        self.base, self.n, self.turn = self.base + turns * self.per, 0, None

    def value(self):
        return self.base + self.n if self.turn is None else self.turn * self.per + (self.base + self.n)

    def step(self, instruction):
        self.n += 1
        instruction.then_inc(self.semaphore, 1)
        self.engine.wait_ge(self.semaphore, self.value())


class Scope:

    def __init__(self, nc, ctx, name):
        self.nc, self.ctx, self.name = nc, ctx, name

    def sb(self, name, shape, dt=F32):
        return self.ctx.enter_context(self.nc.sbuf_tensor(f"{self.name}_{name}", shape, dt))

    def ps(self, name, shape):
        return self.ctx.enter_context(self.nc.psum_tensor(f"{self.name}_{name}", shape, F32))

    def sem(self, name):
        handle = self.nc.alloc_semaphore(f"{self.name}_{name}")
        Scope.in_use.append(handle)
        return handle

    in_use = []


def clear_semaphores(nc):
    nc.clear_and_free_semaphores(Scope.in_use)
    Scope.in_use.clear()
    nc.all_engine_barrier()


def chunk(t, k, i):
    return t[:, k, bass.ds(i * CN, CN)]


def both(t, i):
    return t[:, :, bass.ds(i * CN, CN)]


def bank(ps, i, rows=P, n=CN):
    return ps[0:rows, bass.ds(i, 1), 0:n].rearrange("p a n -> p (a n)")


def bank2(ps, i, blocks, n=CN):
    return ps[:, bass.ds(i, 1), 0:n].to_broadcast([P, blocks, n])


class LayerNorm:

    def __init__(self, sc, tag, src, out, avg, ident, eps, ps, gamma=None, beta=None, rms=False,
                 chunks=CH, width=CN, final=None):
        self.n, self.w = chunks, width
        self.tile = RN if width == CN else P
        self.tiles = width // self.tile
        self.final = final or (lambda k, i: self.at(self.out, k, i))
        self.src, self.out, self.avg, self.ident, self.ps = src, out, avg, ident, ps
        self.eps, self.gamma, self.beta, self.rms = eps, gamma, beta, rms
        self.sq = sc.sb(tag + "_sq", [P, KD, chunks * width])
        self.rstd = sc.sb(tag + "_rstd", [P, chunks, self.tiles])
        self.mean_ready = sc.sem(tag + "_mean_ready")
        self.centred = sc.sem(tag + "_centred")
        self.squared = sc.sem(tag + "_squared")
        self.sq_summed = sc.sem(tag + "_sq_summed")
        self.var_ready = sc.sem(tag + "_var_ready")
        self.std_ready = sc.sem(tag + "_std_ready")
        self.rstd_ready = sc.sem(tag + "_rstd_ready")
        self.spread = sc.sem(tag + "_spread")
        self.scaled = sc.sem(tag + "_scaled")
        self.normed = sc.sem(tag + "_normed")

    def at(self, t, k, i):
        return t[:, k, bass.ds(i * self.w, self.w)]

    def of_chunk(self, i):
        return self.rstd[0:self.tile, bass.ds(i, 1), :].rearrange("p a t -> p (a t)")

    def all(self, t, i):
        return t[:, :, bass.ds(i * self.w, self.w)]

    def tensor(self, nc, pe):
        if not self.rms:
            with nc.tensor.Fori(0, self.n) as i:
                for k in range(KD):
                    mm = nc.tensor.matmul(bank(self.ps, i, P, self.w), self.avg[:], self.at(self.src, k, i),
                                          start=(k == 0), stop=(k == KD - 1))
                mm.then_inc(self.mean_ready, 1)
        def variance(i):
            pe.wait_ge(self.sq_summed, i + 1)
            if i >= 2:
                pe.wait_ge(self.std_ready, i - 1)
            for t in range(self.tiles):
                at = i * self.w + t * self.tile
                mm = nc.tensor.matmul(self.ps[0:self.tile, 6 + i % 2, t:t + 1], self.sq[:, 0, at:at + self.tile],
                                      self.avg[:, 0:1], start=True, stop=True)
            mm.then_inc(self.var_ready, 1)

        variance(0)
        variance(1)
        for i in range(self.n):
            if i + 2 < self.n:
                variance(i + 2)
            pe.wait_ge(self.rstd_ready, i + 1)
            for t in range(self.tiles):
                one = self.rstd[0:self.tile, i, t:t + 1].to_broadcast([self.tile, P])
                mm = nc.tensor.matmul(self.ps[:, i, t * self.tile:(t + 1) * self.tile], one,
                                      self.ident[0:self.tile, 0:self.tile], start=True, stop=True)
            mm.then_inc(self.spread, 1)

    def gpsimd(self, nc, pool):
        with nc.gpsimd.Fori(0, self.n) as i:
            pool.wait_ge(self.squared, i + 1)
            nc.gpsimd.tensor_tensor(self.at(self.sq, 0, i), self.at(self.sq, 0, i), self.at(self.sq, 1, i),
                                    ALU.add).then_inc(self.sq_summed, 1)

    def scalar(self, nc, act):
        for i in range(self.n):
            if not self.rms:
                act.wait_ge(self.centred, i + 1)
            nc.scalar.activation(self.all(self.sq, i), self.all(self.src if self.rms else self.out, i),
                                 ACT.Square).then_inc(self.squared, 1)
        for i in range(self.n):
            act.wait_ge(self.var_ready, i + 1)
            nc.scalar.activation(self.of_chunk(i), self.ps[0:self.tile, 6 + i % 2, 0:self.tiles], ACT.Sqrt,
                                 bias=self.eps[0:self.tile]).then_inc(self.std_ready, 1)

    def vector(self, nc, dve):
        if not self.rms:
            with nc.vector.Fori(0, self.n) as i:
                dve.wait_ge(self.mean_ready, i + 1)
                nc.vector.tensor_tensor(self.all(self.out, i), self.all(self.src, i), bank2(self.ps, i, KD, self.w),
                                        ALU.subtract).then_inc(self.centred, 1)

        def invert(i):
            dve.wait_ge(self.std_ready, i + 1)
            r = self.of_chunk(i)
            nc.vector.reciprocal(r, r).then_inc(self.rstd_ready, 1)

        def scale(i):
            dve.wait_ge(self.spread, i + 1)
            last = nc.vector.tensor_tensor(self.all(self.out, i), self.all(self.src if self.rms else self.out, i),
                                           bank2(self.ps, i, KD, self.w), ALU.mult)
            if self.gamma is not None:
                last.then_inc(self.scaled, 1)
                dve.wait_ge(self.scaled, i + 1)
                for k in range(KD):
                    o, f = self.at(self.out, k, i), self.final(k, i)
                    g = self.gamma[:, k:k + 1]
                    if self.beta is None:
                        last = nc.vector.tensor_scalar(f, o, g, None, ALU.mult)
                    else:
                        last = nc.vector.tensor_scalar(f, o, g, self.beta[:, k:k + 1], ALU.mult, ALU.add)
            last.then_inc(self.normed, 1)

        invert(0)
        with nc.vector.Fori(0, self.n - 1) as i:
            invert(i + 1)
            scale(i)
        scale(self.n - 1)


class Shared:

    def __init__(self, nc, ctx, dram):
        sc = Scope(nc, ctx, "g")
        self.nc, self.dram = nc, dram
        self.h = sc.sb("h", [P, KD, NT])
        self.xn = sc.sb("xn", [P, KD, NT])
        self.avg = sc.sb("avg", [P, P])
        self.ident = sc.sb("ident", [P, P])
        self.eps5 = sc.sb("eps5", [P, 1])
        self.eps6 = sc.sb("eps6", [P, 1])


def load_constants(g):
    nc = g.nc
    with ExitStack() as ctx:
        sc = Scope(nc, ctx, "cst")
        landed = sc.sem("landed")
        block = ctx.enter_context(nc.Block())

        @block.sync
        def _(sp):
            sp.dma_start(g.ident[:], g.dram["c_ident"]).then_inc(landed, 16)
            sp.wait_ge(landed, 16)

        @block.vector
        def _(dve):
            nc.vector.memset(g.avg[:], 1.0 / D)
            nc.vector.memset(g.eps5[:], 1.0e-5)
            nc.vector.memset(g.eps6[:], 1.0e-6)


def first_of_max(nc, chain, scores, top, ranked, hot, rank, top_rank, full=(RN, RT, NE)):
    full = list(full)
    chain.step(nc.vector.tensor_reduce(top[:], scores, AX_X, ALU.max))
    tb = top[:].rearrange("p (t a) -> p t a", a=1).to_broadcast(full)
    chain.step(nc.vector.tensor_tensor(ranked[:], scores, tb, ALU.is_ge))
    rb = rank[0:full[0], :].rearrange("p (a e) -> p a e", a=1).to_broadcast(full)
    chain.step(nc.vector.tensor_tensor(ranked[:], ranked[:], rb, ALU.mult))
    chain.step(nc.vector.tensor_reduce(top_rank[:], ranked[:], AX_X, ALU.max))
    kb = top_rank[:].rearrange("p (t a) -> p t a", a=1).to_broadcast(full)
    chain.step(nc.vector.tensor_tensor(hot, ranked[:], kb, ALU.is_equal))


def prefix_sum(nc, chain, out, values, keep):
    chain.step(nc.vector.tensor_tensor_scan(out, keep, values, 0.0, ALU.mult, ALU.add))


class Routes:

    def __init__(self, sc):
        self.pos = sc.sb("pos", [RN, 2, RT], I32)
        self.gate = sc.sb("gate", [RN, 2, RT])
        self.w_row = sc.sb("w_row", [P, BLOCKS], I32)
        self.token = sc.sb("token", [RN, SLOT_TILES], I32)


def router(g, tag, w_name, b_name, kind, routes):
    nc, dram = g.nc, g.dram
    with ExitStack() as ctx:
        sc = Scope(nc, ctx, tag)
        w = sc.sb("w", [P, KD, NE])
        bias = sc.sb("bias", [P, NE])
        ebias = sc.sb("ebias", [P, NE])
        rank = sc.sb("rank", [P, NE])
        lg = sc.sb("lg", [RN, RT, NE])
        score = sc.sb("score", [RN, RT, NE])
        chosen = sc.sb("chosen", [RN, RT, NE])
        ranked = sc.sb("ranked", [RN, RT, NE])
        hot1 = sc.sb("hot1", [RN, RT, NE])
        hot2 = sc.sb("hot2", [RN, RT, NE])
        count = sc.sb("count", [P, NE, RT])
        upto = sc.sb("upto", [P, NE, RT])
        keep = sc.sb("keep", [P, NE, RT])
        ones = sc.sb("ones", [P, NE])
        lower = sc.sb("lower", [P, P])
        all_ones = sc.sb("all_ones", [P, P])
        over = sc.sb("over", [P, NE, CH])
        steps = sc.sb("steps", [P, BLOCKS])
        lane = sc.sb("lane", [P, 1])
        blocks = sc.sb("blocks", [P, NE])
        upto_b = sc.sb("upto_b", [P, NE])
        reached = sc.sb("reached", [P, BLOCKS, NE])
        expert = sc.sb("expert", [P, BLOCKS])
        place = sc.sb("place", [RN, RT, NE])
        pos_f = sc.sb("pos_f", [RN, 2 * RT])
        from_tile = sc.sb("from_tile", [RN, 2 * RT, SLOT_TILES + 1])
        in_tile = sc.sb("in_tile", [RN, 2 * RT, SLOT_TILES])
        tile_at = sc.sb("tile_at", [P, SLOT_TILES + 1])
        in_lane = sc.sb("in_lane", [RN, 2 * RT, RN])
        lanes = sc.sb("lanes", [P, RN])
        low = sc.sb("low", [RN, 2 * RT])
        tok = sc.sb("tok", [RN, RT])
        rows = sc.sb("rows", [RN, RT, D])
        sel_ready = sc.sem("sel_ready")
        counted = sc.sem("counted")
        placed = sc.sem("placed")
        rows_turned = sc.sem("rows_turned")
        rows_copied = sc.sem("rows_copied")
        top1 = sc.sb("top1", [RN, RT])
        top2 = sc.sb("top2", [RN, RT])
        top_rank = sc.sb("top_rank", [RN, RT])
        ex = sc.sb("ex", [RN, RT])
        den = sc.sb("den", [RN, RT])
        ps = sc.ps("ps", [P, 8, 512])
        landed = sc.sem("landed")
        logits = sc.sem("logits")
        act_done = sc.sem("act_done")
        act_in = sc.sem("act_in")
        dve_own = sc.sem("dve_own")
        turned = sc.sem("turned")
        stored = sc.sem("stored")
        ln = LayerNorm(sc, "ln", g.h, g.xn, g.avg, g.ident, g.eps5, ps)
        n_loads = 10
        block = ctx.enter_context(nc.Block())

        @block.sync
        def _(sp):
            sp.dma_start(w[:], dram[w_name]).then_inc(landed, 16)
            sp.dma_start(rank[:], dram["c_rank"]).then_inc(landed, 16)
            if kind == "L1":
                sp.dma_start(ebias[:], dram["L1_ffn_expert_bias"].to_broadcast([P, NE])).then_inc(landed, 16)
            else:
                sp.dma_start(bias[:], dram[b_name].to_broadcast([P, NE])).then_inc(landed, 16)
            for a, name in ((keep, "c_keep"), (lower, "c_lower"), (steps, "c_steps"), (lane, "c_lane"),
                            (tok, "c_tok"), (tile_at, "c_tile_at"), (lanes, "c_lanes")):
                sp.dma_start(a[:], dram[name]).then_inc(landed, 16)
            view = dram["s_rows"].rearrange("(t p) d -> p t d", p=RN)
            half = RT // 2
            for n in range(2):
                sp.wait_ge(rows_copied, half * (n + 1))
                sp.dma_start(view[:, half * n:half * (n + 1), :],
                             rows[:, half * n:half * (n + 1), :]).then_inc(stored, 16)
            sp.wait_ge(stored, 32)

        @block.tensor
        def _(pe):
            ln.tensor(nc, pe)
            pe.wait_ge(landed, 16 * n_loads)
            pe.wait_ge(ln.normed, CH)
            pe.wait_ge(ln.std_ready, CH)
            for t in range(RT):
                for k in range(KD):
                    mm = nc.tensor.matmul(ps[0:RN, 7, t * NE:(t + 1) * NE],
                                          g.xn[:, k, t * RN:(t + 1) * RN], w[:, k, :],
                                          start=(k == 0), stop=(k == KD - 1))
            mm.then_inc(logits, 1)
            for t in range(RT):
                if t >= 3:
                    pe.wait_ge(rows_copied, t - 2)
                for k in range(KD):
                    mm = nc.tensor.transpose(ps[0:RN, t % 3, k * P:(k + 1) * P],
                                             g.xn[:, k, t * RN:(t + 1) * RN], g.ident[:])
                mm.then_inc(rows_turned, 1)
            pe.wait_ge(sel_ready, 1)
            chosen_all = chosen[:].rearrange("p t e -> p (t e)")
            nc.tensor.matmul(ps[0:RN, 4, 0:RT * NE], lower[0:RN, 0:RN], chosen_all, start=True, stop=True)
            nc.tensor.matmul(ps[:, 5, 0:RT * NE], all_ones[0:RN, :], chosen_all,
                             start=True, stop=True).then_inc(counted, 1)
            for n in range(2 * RT):
                pe.wait_ge(placed, 2 if n < RT else 3)
                mm = nc.tensor.matmul(ps[0:RN, 6, 0:SLOT_TILES], in_lane[:, n, :], in_tile[:, n, :], start=(n == 0),
                                      stop=(n == 2 * RT - 1))
            mm.then_inc(turned, 1)

        @block.gpsimd
        def _(pool):
            ln.gpsimd(nc, pool)

        @block.scalar
        def _(act):
            ln.scalar(nc, act)
            for t in range(RT):
                act.wait_ge(rows_turned, t + 1)
                nc.scalar.copy(rows[:, t, :], ps[0:RN, t % 3, 0:D]).then_inc(rows_copied, 1)
            if kind == "L3":
                act.wait_ge(act_in, 1)
                nc.scalar.activation(ex[:], ex[:], ACT.Exp).then_inc(act_done, 1)
            if kind == "L1":
                act.wait_ge(act_in, 1)
                nc.scalar.activation(score[:], lg[:], ACT.Sigmoid).then_inc(act_done, 1)

        @block.vector
        def _(dve):
            v = nc.vector
            v.memset(ones[:], 1.0)
            v.memset(all_ones[:], 1.0)
            ln.vector(nc, dve)
            chain = Chain(dve, dve_own)
            dve.wait_ge(landed, 16 * n_loads)
            dve.wait_ge(logits, 1)
            raw = ps[0:RN, 7, 0:RT * NE].rearrange("p (t e) -> p t e", e=NE)
            if kind == "L1":
                v.tensor_copy(lg[:], raw).then_inc(act_in, 1)
                dve.wait_ge(act_done, 1)
                eb = ebias[0:RN, :].rearrange("p (a e) -> p a e", a=1).to_broadcast([RN, RT, NE])
                chain.step(v.tensor_tensor(chosen[:], score[:], eb, ALU.add))
            else:
                bb = bias[0:RN, :].rearrange("p (a e) -> p a e", a=1).to_broadcast([RN, RT, NE])
                chain.step(v.tensor_tensor(lg[:], raw, bb, ALU.add))
            first_of_max(nc, chain, lg[:] if kind == "L3" else chosen[:], top1, ranked, hot1[:], rank, top_rank)
            src = lg if kind == "L3" else chosen
            chain.step(v.scalar_tensor_tensor(chosen[:], hot1[:], -BIG, src[:], ALU.mult, ALU.add))
            first_of_max(nc, chain, chosen[:], top2, ranked, hot2[:], rank, top_rank)
            chain.step(v.tensor_tensor(chosen[:], hot1[:], hot2[:], ALU.add))
            v.tensor_copy(den[:], top1[:]).then_inc(sel_ready, 1)
            dve.wait_ge(sel_ready, 1)
            gate1, gate2 = routes.gate[:, 0, :], routes.gate[:, 1, :]
            if kind == "L3":
                v.tensor_tensor(ex[:], top2[:], top1[:], ALU.subtract).then_inc(act_in, 1)
                dve.wait_ge(act_done, 1)
                chain.step(v.tensor_scalar(den[:], ex[:], 1.0, None, ALU.add))
                chain.step(v.reciprocal(gate1, den[:]))
                chain.step(v.tensor_tensor(gate2, ex[:], gate1, ALU.mult))
            if kind == "L1":
                for hot, top in ((hot1, top1), (hot2, top2)):
                    chain.step(v.tensor_tensor(ranked[:], hot[:], score[:], ALU.mult))
                    chain.step(v.tensor_reduce(top[:], ranked[:], AX_X, ALU.add))
                chain.step(v.tensor_tensor(den[:], top1[:], top2[:], ALU.add))
                chain.step(v.tensor_scalar(den[:], den[:], 1.0e-20, None, ALU.add))
                chain.step(v.reciprocal(den[:], den[:]))
                chain.step(v.tensor_tensor(gate1, top1[:], den[:], ALU.mult))
                chain.step(v.tensor_tensor(gate2, top2[:], den[:], ALU.mult))
            dve.wait_ge(counted, 1)
            by_expert = ps[:, 5, 0:RT * NE].rearrange("p (t e) -> p e t", e=NE)
            chain.step(v.tensor_copy(count[:], by_expert))
            flat = lambda t: t[:].rearrange("p e t -> p (e t)")
            prefix_sum(nc, chain, flat(upto), flat(count), flat(keep))
            total = upto[:, :, RT - 1:RT]
            over_at = steps[:, 0:CH].rearrange("p (a n) -> p a n", a=1).to_broadcast([P, NE, CH])
            chain.step(v.tensor_scalar(over[:], over_at, float(CN), None, ALU.mult))
            chain.step(v.tensor_tensor(over[:], total.to_broadcast([P, NE, CH]), over[:], ALU.is_gt))
            chain.step(v.tensor_reduce(blocks[:], over[:], AX_X, ALU.add))
            prefix_sum(nc, chain, upto_b[:], blocks[:], ones[:])
            chain.step(v.tensor_tensor(upto_b[:], upto_b[:], blocks[:], ALU.subtract))
            full = [P, BLOCKS, NE]
            fb = upto_b[:].rearrange("p (a e) -> p a e", a=1).to_broadcast(full)
            jb = steps[:].rearrange("p (j a) -> p j a", a=1).to_broadcast(full)
            chain.step(v.tensor_tensor(reached[:], fb, jb, ALU.is_le))
            chain.step(v.tensor_reduce(expert[:], reached[:], AX_X, ALU.add))
            chain.step(v.tensor_scalar(expert[:], expert[:], float(P), lane[:, 0:1], ALU.mult, ALU.add))
            chain.step(v.tensor_copy(routes.w_row[:], expert[:]))
            chain.step(v.tensor_tensor(upto[:], upto[:], count[:], ALU.subtract))
            chain.step(v.tensor_scalar(upto_b[:], upto_b[:], float(CN), None, ALU.mult))
            first = upto_b[0:RN, :].rearrange("p (a e) -> p a e", a=1).to_broadcast([RN, RT, NE])
            chain.step(v.tensor_tensor(place[:], ps[0:RN, 4, 0:RT * NE].rearrange("p (t e) -> p t e", e=NE),
                                       first, ALU.add))
            chain.step(v.tensor_tensor(place[:], place[:], upto[0:RN].rearrange("p e t -> p t e"), ALU.add))
            for n, hot in enumerate((hot1, hot2)):
                chain.step(v.tensor_tensor(ranked[:], place[:], hot[:], ALU.mult))
                chain.step(v.tensor_reduce(pos_f[:, n * RT:(n + 1) * RT], ranked[:], AX_X, ALU.add))
            v.tensor_copy(routes.pos[:].rearrange("p n t -> p (n t)"), pos_f[:]).then_inc(placed, 1)
            N, M = 2 * RT, SLOT_TILES
            each = lambda t, m: t[:].rearrange("p (n a) -> p n a", a=1).to_broadcast([RN, N, m])
            along = lambda t, m: t[0:RN, :].rearrange("p (a m) -> p a m", a=1).to_broadcast([RN, N, m])
            chain.step(v.tensor_tensor(from_tile[:], each(pos_f, M + 1), along(tile_at, M + 1), ALU.is_ge))
            chain.step(v.tensor_reduce(low[:], from_tile[:], AX_X, ALU.add))
            chain.step(v.tensor_scalar(low[:], low[:], -1.0, float(-RN), ALU.add, ALU.mult))
            chain.step(v.tensor_tensor(low[:], low[:], pos_f[:], ALU.add))
            chain.step(v.tensor_tensor(in_tile[:], from_tile[:, :, 0:M], from_tile[:, :, 1:M + 1], ALU.subtract))
            for n in range(2):
                half = slice(n * RT, (n + 1) * RT)
                number = tok[:].rearrange("p (t a) -> p t a", a=1).to_broadcast([RN, RT, M])
                v.tensor_tensor(in_tile[:, half, :], in_tile[:, half, :], number, ALU.mult)
                v.tensor_tensor(in_lane[:, half, :], along(lanes, RN)[:, half, :], each(low, RN)[:, half, :],
                                ALU.is_equal).then_inc(placed, 1)
            dve.wait_ge(turned, 1)
            chain.step(v.tensor_copy(routes.token[:], ps[0:RN, 6, 0:M]))


def routed_experts(g, tag, w_name, F, routes):
    nc, dram = g.nc, g.dram
    NF, FO, FT = hidden_tiles(F)
    W = 2 * KD * F + NF * D
    with ExitStack() as ctx:
        sc = Scope(nc, ctx, tag)
        w = [sc.sb(f"w{b}", [P, W]) for b in range(2)]
        rows = [sc.sb(f"rows{b}", [RN, SUB, D]) for b in range(2)]
        x = [sc.sb(f"x{b}", [P, KD, CN]) for b in range(2)]
        act_g = sc.sb("act_g", [P, 2, CN])
        hid = sc.sb("hid", [P, 2, CN])
        y = [sc.sb(f"y{b}", [RN, SUB, D]) for b in range(2)]
        ps_x = sc.ps("ps_x", [P, 512])
        ps_g = [sc.ps(f"ps_g{b}", [P, 512]) for b in range(2)]
        ps_u = [sc.ps(f"ps_u{b}", [P, 512]) for b in range(2)]
        ps_y = sc.ps("ps_y", [P, SUB, 512])
        w_landed = [sc.sem(f"w_landed{b}") for b in range(2)]
        rows_landed = [sc.sem(f"rows_landed{b}") for b in range(2)]
        turned = sc.sem("turned")
        x_ready = sc.sem("x_ready")
        g_ready = sc.sem("g_ready")
        u_ready = sc.sem("u_ready")
        silu_done = sc.sem("silu_done")
        hid_ready = sc.sem("hid_ready")
        y_ready = sc.sem("y_ready")
        y_copied = sc.sem("y_copied")
        y_stored = [sc.sem(f"y_stored{b}") for b in range(2)]
        block = ctx.enter_context(nc.Block())

        def weight(b, which, k, f):
            at = (which * KD + k) * F + FO[f]
            return w[b][:, at:at + FT[f]]

        def down_weight(b, f):
            at = 2 * KD * F + f * D
            return w[b][0:FT[f], at:at + D]

        def blocks(engine, first, middle):
            first()
            with engine.Fori(0, (BLOCKS - 1) // 2) as p:
                for b in range(2):
                    middle(p * 2 + b, b, p, False)
            for j in range((BLOCKS - 1) // 2 * 2, BLOCKS):
                middle(j, j % 2, j // 2, j == BLOCKS - 1)

        @block.gpsimd
        def _(pool):
            for j in range(BLOCKS):
                b = j % 2
                if j >= 2:
                    pool.wait_ge(turned, (j - 1) * KD)
                for s in range(SUB):
                    nc.gpsimd.indirect_dma_start(rows[b][:, s, :], None, dram["s_rows"], bass.IndirectOffsetOnAxis(
                        ap=routes.token[:, j * SUB + s:j * SUB + s + 1], axis=0)).then_inc(rows_landed[b], 16)
                if j >= 2:
                    pool.wait_ge(y_copied, j + 1)
                nc.gpsimd.indirect_dma_start(w[b][:], None, dram[w_name], bass.IndirectOffsetOnAxis(
                    ap=routes.w_row[:, j:j + 1], axis=0)).then_inc(w_landed[b], 16)

        @block.sync
        def _(sp):
            for j in range(BLOCKS):
                sp.wait_ge(y_copied, j + 3)
                sp.dma_start(dram["s_y"][j * CN:(j + 1) * CN, :].rearrange("(s p) d -> p s d", p=RN),
                             y[j % 2][:]).then_inc(y_stored[j % 2], 16)
            for b in range(2):
                sp.wait_ge(y_stored[b], 16 * ((BLOCKS + 1 - b) // 2 + 1))

        @block.tensor
        def _(pe):
            def turn(j, b, visit, k):
                pe.wait_ge(rows_landed[b], (visit + 1) * (16 * SUB))
                pe.wait_ge(x_ready, j * KD + (k + 1))
                for s in range(SUB):
                    mm = nc.tensor.transpose(ps_x[:, s * RN:(s + 1) * RN], rows[b][:, s, k * P:(k + 1) * P],
                                             g.ident[0:RN, 0:RN])
                mm.then_inc(turned, 1)

            def up(j, b, visit, f):
                if f == 0:
                    pe.wait_ge(w_landed[b], (visit + 1) * 16)
                    pe.wait_ge(x_ready, j * KD + (KD + 1))
                if not (isinstance(j, int) and j * NF + f == 0):
                    pe.wait_ge(hid_ready, j * NF + f)
                for which, ps, ready in ((0, ps_g, g_ready), (1, ps_u, u_ready)):
                    for k in range(KD):
                        mm = nc.tensor.matmul(ps[f % 2][0:FT[f], 0:CN], weight(b, which, k, f), x[b][:, k, :],
                                              start=(k == 0), stop=(k == KD - 1))
                    mm.then_inc(ready, 1)

            def down(j, b, f):
                if f == 0:
                    pe.wait_ge(y_copied, j + 2)
                pe.wait_ge(hid_ready, j * NF + (f + 2))
                for s in range(SUB):
                    mm = nc.tensor.matmul(ps_y[0:RN, s, 0:D], hid[0:FT[f], f % 2, s * RN:(s + 1) * RN],
                                          down_weight(b, f), start=(f == 0), stop=(f == NF - 1))
                if f == NF - 1:
                    mm.then_inc(y_ready, 1)

            def first():
                for k in range(KD):
                    turn(0, 0, 0, k)
                up(0, 0, 0, 0)

            def middle(j, b, visit, last):
                nxt = (j + 1, 1 - b, visit + b)
                for f in range(NF):
                    if not last and f < KD:
                        turn(*nxt, f)
                    if f + 1 < NF:
                        up(j, b, visit, f + 1)
                    elif not last:
                        up(*nxt, 0)
                    down(j, b, f)

            blocks(nc.tensor, first, middle)

        @block.scalar
        def _(act):
            nc.scalar.copy(act_g[:, 0, 0:1], g.ident[:, 0:1]).then_inc(x_ready, 1)
            act.wait_ge(x_ready, 1)

            def copy(j, b, visit, k):
                act.wait_ge(turned, j * KD + (k + 1))
                nc.scalar.copy(x[b][:, k, :], ps_x[:, 0:CN]).then_inc(x_ready, 1)

            def silu(j, f):
                act.wait_ge(g_ready, j * NF + (f + 1))
                nc.scalar.activation(act_g[0:FT[f], f % 2, :], ps_g[f % 2][0:FT[f], 0:CN],
                                     ACT.Silu).then_inc(silu_done, 1)

            def first():
                for k in range(KD):
                    copy(0, 0, 0, k)
                silu(0, 0)

            def middle(j, b, visit, last):
                for f in range(NF):
                    if not last and f < KD:
                        copy(j + 1, 1 - b, visit + b, f)
                    if f + 1 < NF:
                        silu(j, f + 1)
                    elif not last:
                        silu(j + 1, 0)

            blocks(nc.scalar, first, middle)

        @block.vector
        def _(dve):
            nc.vector.memset(hid[:, 0, 0:1], 0.0).then_inc(hid_ready, 1)
            dve.wait_ge(hid_ready, 1)
            for b in range(2):
                nc.vector.memset(y[b][:, 0, 0:1], 0.0).then_inc(y_stored[b], 16)
                dve.wait_ge(y_stored[b], 16)
            nc.vector.memset(y[0][:, 0, 0:1], 0.0).then_inc(y_copied, 2)
            dve.wait_ge(y_copied, 2)

            def hidden(j, f):
                dve.wait_ge(silu_done, j * NF + (f + 1))
                dve.wait_ge(u_ready, j * NF + (f + 1))
                nc.vector.tensor_tensor(hid[0:FT[f], f % 2, :], act_g[0:FT[f], f % 2, :],
                                        ps_u[f % 2][0:FT[f], 0:CN], ALU.mult).then_inc(hid_ready, 1)

            def middle(j, b, visit, last):
                for f in range(1, NF):
                    hidden(j, f)
                if not last:
                    hidden(j + 1, 0)
                dve.wait_ge(y_ready, j + 1)
                dve.wait_ge(y_stored[b], (visit + 1) * 16)
                nc.vector.tensor_copy(y[b][:], ps_y[0:RN, :, 0:D]).then_inc(y_copied, 1)

            blocks(nc.vector, lambda: hidden(0, 0), middle)


class DenseExpert:

    def __init__(self, g, sc, names, F):
        self.g, self.names = g, names
        self.NF, self.FO, self.FT = hidden_tiles(F)
        self.wg = sc.sb("wg", [P, KD, F])
        self.wu = sc.sb("wu", [P, KD, F])
        self.wd = sc.sb("wd", [P, self.NF, D])
        self.act_g = sc.sb("act_g", [P, 2, CN])
        self.hid = sc.sb("hid", [P, 2, CN])
        self.ps_g = [sc.ps(f"ps_g{b}", [P, 512]) for b in range(2)]
        self.ps_u = [sc.ps(f"ps_u{b}", [P, 512]) for b in range(2)]
        self.ps_y = sc.ps("ps_y", [P, KD, 512])
        self.w_landed = sc.sem("w_landed")
        self.g_ready = sc.sem("g_ready")
        self.u_ready = sc.sem("u_ready")
        self.silu_done = sc.sem("silu_done")
        self.hid_ready = sc.sem("hid_ready")
        self.y_ready = sc.sem("y_ready")
        self.y_added = sc.sem("y_added")
        self.units = [(c, f) for c in range(CH) for f in range(self.NF)]

    def sync(self, nc, sp):
        dram = self.g.dram
        sp.dma_start(self.wg[:], dram[self.names[0]]).then_inc(self.w_landed, 16)
        sp.dma_start(self.wu[:], dram[self.names[1]]).then_inc(self.w_landed, 16)
        for f in range(self.NF):
            sp.dma_start(self.wd[0:self.FT[f], f, :],
                         dram[self.names[2]][self.FO[f]:self.FO[f] + self.FT[f], :]).then_inc(self.w_landed, 16)

    def tensor(self, nc, pe):
        units, FO, FT = self.units, self.FO, self.FT

        def up(q):
            c, f = units[q]
            if q >= 2:
                pe.wait_ge(self.hid_ready, q - 1)
            for ps, w, ready in ((self.ps_g, self.wg, self.g_ready), (self.ps_u, self.wu, self.u_ready)):
                for k in range(KD):
                    mm = nc.tensor.matmul(ps[q % 2][0:FT[f], 0:CN], w[:, k, FO[f]:FO[f] + FT[f]],
                                          self.g.xn[:, k, c * CN:(c + 1) * CN], start=(k == 0), stop=(k == KD - 1))
                mm.then_inc(ready, 1)

        pe.wait_ge(self.w_landed, 16 * (2 + self.NF))
        up(0)
        for q, (c, f) in enumerate(units):
            if q + 1 < len(units):
                up(q + 1)
            if f == 0 and c > 0:
                pe.wait_ge(self.y_added, c)
            pe.wait_ge(self.hid_ready, q + 1)
            for m in range(KD):
                mm = nc.tensor.matmul(self.ps_y[:, m, 0:CN], self.wd[0:FT[f], f, m * P:(m + 1) * P],
                                      self.hid[0:FT[f], q % 2, :], start=(f == 0), stop=(f == self.NF - 1))
            if f == self.NF - 1:
                mm.then_inc(self.y_ready, 1)

    def scalar(self, nc, act):
        for q, (c, f) in enumerate(self.units):
            act.wait_ge(self.g_ready, q + 1)
            if q >= 2:
                act.wait_ge(self.hid_ready, q - 1)
            nc.scalar.activation(self.act_g[0:self.FT[f], q % 2, :], self.ps_g[q % 2][0:self.FT[f], 0:CN],
                                 ACT.Silu).then_inc(self.silu_done, 1)

    def vector(self, nc, dve):
        def hidden(q):
            n = self.FT[self.units[q][1]]
            dve.wait_ge(self.silu_done, q + 1)
            dve.wait_ge(self.u_ready, q + 1)
            nc.vector.tensor_tensor(self.hid[0:n, q % 2, :], self.act_g[0:n, q % 2, :], self.ps_u[q % 2][0:n, 0:CN],
                                    ALU.mult).then_inc(self.hid_ready, 1)

        hidden(0)
        for q, (c, f) in enumerate(self.units):
            if q + 1 < len(self.units):
                hidden(q + 1)
            if f == self.NF - 1:
                dve.wait_ge(self.y_ready, c + 1)
                at = self.g.h[:, :, c * CN:(c + 1) * CN]
                nc.vector.tensor_tensor(at, at, self.ps_y[:, :, 0:CN], ALU.add).then_inc(self.y_added, 1)


class ChoiceRows:

    def __init__(self, g, sc, routes):
        self.g, self.routes = g, routes
        self.first = sc.sb("first", [RN, RT, D])
        self.y = sc.sb("y", [RN, RT, D])
        self.groups = [(t, min(t + 4, RT)) for t in range(0, RT, 4)]
        self.landed = [[sc.sem(f"landed{n}_{i}") for i in range(len(self.groups))] for n in range(2)]
        self.weighed = sc.sem("weighed")
        self.summed = sc.sem("summed")

    def gather(self, nc):
        for t in range(RT):
            for n, out in enumerate((self.first, self.y)):
                nc.gpsimd.indirect_dma_start(
                    out[:, t, :], None, self.g.dram["s_y"], bass.IndirectOffsetOnAxis(
                        ap=self.routes.pos[:, n, t:t + 1], axis=0)).then_inc(self.landed[n][t // 4], 16)

    def weigh(self, nc, act):
        for i, (lo, hi) in enumerate(self.groups):
            act.wait_ge(self.landed[0][i], 16 * (hi - lo))
            for t in range(lo, hi):
                nc.scalar.activation(self.first[:, t, :], self.first[:, t, :], ACT.Copy,
                                     scale=self.routes.gate[:, 0, t:t + 1]).then_inc(self.weighed, 1)

    def add(self, nc, dve, i):
        lo, hi = self.groups[i]
        dve.wait_ge(self.landed[1][i], 16 * (hi - lo))
        for t in range(lo, hi):
            dve.wait_ge(self.weighed, t + 1)
            nc.vector.scalar_tensor_tensor(self.y[:, t, :], self.y[:, t, :], self.routes.gate[:, 1, t:t + 1],
                                           self.first[:, t, :], ALU.mult, ALU.add).then_inc(self.summed, 1)


def add_choices(g, tag, routes, shared, F):
    nc = g.nc
    with ExitStack() as ctx:
        sc = Scope(nc, ctx, tag)
        dense = DenseExpert(g, sc, shared, F)
        rows = ChoiceRows(g, sc, routes)
        ps = sc.ps("ps", [P, KD, 512])
        turned = sc.sem("turned")
        added = sc.sem("added")
        block = ctx.enter_context(nc.Block())

        @block.sync
        def _(sp):
            dense.sync(nc, sp)

        @block.gpsimd
        def _(pool):
            rows.gather(nc)

        @block.scalar
        def _(act):
            dense.scalar(nc, act)
            rows.weigh(nc, act)

        @block.tensor
        def _(pe):
            dense.tensor(nc, pe)
            for i, (lo, hi) in enumerate(rows.groups):
                if i >= 1:
                    pe.wait_ge(added, i * KD)
                for t in range(lo, hi):
                    pe.wait_ge(rows.summed, t + 1)
                    for k in range(KD):
                        mm = nc.tensor.transpose(ps[:, k, (t - lo) * RN:(t - lo + 1) * RN],
                                                 rows.y[:, t, k * P:(k + 1) * P], g.ident[0:RN, 0:RN])
                mm.then_inc(turned, 1)

        @block.vector
        def _(dve):
            dense.vector(nc, dve)
            dve.wait_ge(dense.y_added, CH)

            def to_h(i):
                lo, hi = rows.groups[i]
                dve.wait_ge(turned, i + 1)
                for k in range(KD):
                    o = g.h[:, k, lo * RN:hi * RN]
                    nc.vector.tensor_tensor(o, o, ps[:, k, 0:(hi - lo) * RN], ALU.add).then_inc(added, 1)

            for i in range(len(rows.groups)):
                rows.add(nc, dve, i)
                if i > 0:
                    to_h(i - 1)
            to_h(len(rows.groups) - 1)


def store_sum(g, tag, routes, out):
    nc = g.nc
    with ExitStack() as ctx:
        sc = Scope(nc, ctx, tag)
        rows = ChoiceRows(g, sc, routes)
        total = sc.sb("total", [RN, RT, D])
        ps = sc.ps("ps", [P, 8, 512])
        turned = sc.sem("turned")
        added = sc.sem("added")
        stored = sc.sem("stored")
        block = ctx.enter_context(nc.Block())
        view = out.rearrange("(t p) d -> p t d", p=RN)

        @block.gpsimd
        def _(pool):
            rows.gather(nc)

        @block.scalar
        def _(act):
            rows.weigh(nc, act)

        @block.tensor
        def _(pe):
            for t in range(RT):
                if t >= 8:
                    pe.wait_ge(added, t - 7)
                for k in range(KD):
                    mm = nc.tensor.transpose(ps[0:RN, t % 8, k * P:(k + 1) * P], g.h[:, k, t * RN:(t + 1) * RN],
                                             g.ident[:])
                mm.then_inc(turned, 1)

        @block.vector
        def _(dve):
            for i, (lo, hi) in enumerate(rows.groups):
                rows.add(nc, dve, i)
                for t in range(lo, hi):
                    dve.wait_ge(rows.summed, t + 1)
                    dve.wait_ge(turned, t + 1)
                    nc.vector.tensor_tensor(total[:, t, :], rows.y[:, t, :], ps[0:RN, t % 8, 0:D],
                                            ALU.add).then_inc(added, 1)

        @block.sync
        def _(sp):
            for lo, hi in rows.groups:
                sp.wait_ge(added, hi)
                sp.dma_start(view[:, lo:hi, :], total[:, lo:hi, :]).then_inc(stored, 16)
            sp.wait_ge(stored, 16 * len(rows.groups))


def mixture(g, tag, w_name, F, kind, w_router, b_router, finish):
    with ExitStack() as ctx:
        routes = Routes(Scope(g.nc, ctx, tag + "r"))
        router(g, tag + "s", w_router, b_router, kind, routes)
        routed_experts(g, tag + "e", w_name, F, routes)
        finish(tag + "a", routes)


def hidden_tiles(F):
    n = -(-F // P)
    starts = [F * f // n for f in range(n + 1)]
    return n, starts[:n], [starts[f + 1] - starts[f] for f in range(n)]


def biased_experts(g, tag, x, out_t, first_e, N, chunks, width, gated):
    nc, dram = g.nc, g.dram
    H = P
    CH, CN, NT = chunks, width, chunks * width

    def chunk(t, k, i):
        return t[:, k, bass.ds(i * CN, CN)]

    def both(t, i):
        return t[:, :, bass.ds(i * CN, CN)]

    with ExitStack() as ctx:
        sc = Scope(nc, ctx, tag)
        w1 = [sc.sb(f"w1{b}", [P, KD, H]) for b in range(2)]
        w2 = [sc.sb(f"w2{b}", [P, KD, H]) for b in range(2)]
        w3 = [sc.sb(f"w3{b}", [P, D]) for b in range(2)]
        vec = [sc.sb(f"vec{b}", [P, 6]) for b in range(2)]
        gate = [sc.sb(f"gate{b}", [P, NT]) for b in range(2)]
        hid = [sc.sb(f"hid{b}", [P, NT]) for b in range(2)]
        avg_h = sc.sb("avg_h", [P, P])
        act_a = sc.sb("act_a", [P, 2, CN])
        sq = sc.sb("sq", [P, NT])
        rstd = sc.sb("rstd", [P, NT])
        z = sc.sb("z", [P, NT])
        part = sc.sb("part", [P, KD, CN])
        ps_a = [sc.ps(f"ps_a{j}", [P, 512]) for j in range(2)]
        ps_b = [sc.ps(f"ps_b{j}", [P, 512]) for j in range(2)]
        ps_m = [sc.ps(f"ps_m{j}", [P, 512]) for j in range(2)]
        ps_y = sc.ps("ps_y", [P, KD, 512])
        w_landed = [sc.sem(f"w_landed{b}") for b in range(2)]
        avg_set = sc.sem("avg_set")
        a_ready = sc.sem("a_ready")
        b_ready = sc.sem("b_ready")
        silu_done = sc.sem("silu_done")
        s_ready = sc.sem("s_ready")
        mean_ready = sc.sem("mean_ready")
        centred = sc.sem("centred")
        squared = sc.sem("squared")
        var_ready = sc.sem("var_ready")
        eps_added = sc.sem("eps_added")
        recip_done = sc.sem("recip_done")
        rstd_ready = sc.sem("rstd_ready")
        z_scaled = sc.sem("z_scaled")
        z_ready = sc.sem("z_ready")
        y_ready = sc.sem("y_ready")
        y_used = sc.sem("y_used")
        h_added = sc.sem("h_added")
        n_loads = 16 * (5 if gated else 4)
        block = ctx.enter_context(nc.Block())

        def schedule(engine, up, out, var):
            up(0, 0, 0)
            var(0, 0, 0)
            if N == 1:
                out(0, 0, 0)
                return
            with engine.Fori(0, (N - 1) // 2) as p:
                up(p * 2 + 1, 1, p)
                out(p * 2, 0, p)
                var(p * 2 + 1, 1, p)
                up(p * 2 + 2, 0, p + 1)
                out(p * 2 + 1, 1, p)
                var(p * 2 + 2, 0, p + 1)
            out(N - 1, (N - 1) % 2, (N - 1) // 2)

        def load(sp, n, b):
            e = n + first_e
            for t, name in ((w1, "f0_w1"), (w2, "f0_w2")):
                sp.dma_start(t[b][:], dram[name][bass.ds(e, 1)].rearrange("a p k f -> (a p) k f")
                             ).then_inc(w_landed[b], 16)
            for t, name in ((w3, "f0_w3"), (vec, "f0_vec")):
                sp.dma_start(t[b][:], dram[name][bass.ds(e, 1)].rearrange("a p f -> (a p) f")
                             ).then_inc(w_landed[b], 16)
            if gated:
                sp.dma_start(gate[b][:], dram["s_gate"][bass.ds(e, 1), :].to_broadcast([P, NT])
                             ).then_inc(w_landed[b], 16)

        @block.sync
        def _(sp):
            load(sp, 0, 0)
            if N == 1:
                return
            load(sp, 1, 1)
            with nc.sync.Fori(0, (N - 3) // 2) as p:
                for b in range(2):
                    n = nc.sync.snap(p * 2 + (b + 2))
                    sp.wait_ge(y_used, p * (2 * CH) + ((b + 1) * CH + 1))
                    load(sp, n, b)
            sp.wait_ge(y_used, (N - 2) * CH + 1)
            load(sp, N - 1, (N - 1) % 2)

        @block.tensor
        def _(pe):
            pe.wait_ge(avg_set, 1)

            def up(e, b, visit):
                with nc.tensor.Fori(0, CH // 2) as cc:
                    pe.wait_ge(w_landed[b], (visit + 1) * n_loads)
                    for j in range(2):
                        pe.wait_ge(s_ready, e * CH + cc * 2 + (j + 1))
                        for ps, w, ready in ((ps_a, w1, a_ready), (ps_b, w2, b_ready)):
                            for k in range(KD):
                                mm = nc.tensor.matmul(ps[j][:, 0:CN], w[b][:, k, :], chunk(x, k, cc * 2 + j),
                                                      start=(k == 0), stop=(k == KD - 1))
                            mm.then_inc(ready, 1)
                    for j in range(2):
                        pe.wait_ge(s_ready, e * CH + cc * 2 + (j + 3))
                        nc.tensor.matmul(ps_m[j][:, 0:CN], avg_h[:], hid[b][:, bass.ds((cc * 2 + j) * CN, CN)],
                                         start=True, stop=True).then_inc(mean_ready, 1)

            def out(e, b, visit):
                with nc.tensor.Fori(0, CH) as c:
                    pe.wait_ge(z_ready, e + 1)
                    pe.wait_ge(y_used, e * CH + c + 1)
                    for m in range(KD):
                        mm = nc.tensor.matmul(ps_y[:, m, 0:CN], w3[b][:, m * P:(m + 1) * P],
                                              z[:, bass.ds(c * CN, CN)], start=True, stop=True)
                    mm.then_inc(y_ready, 1)

            def var(e, b, visit):
                with nc.tensor.Fori(0, CH // 2) as cc:
                    pe.wait_ge(squared, (e + 1) * CH)
                    for j in range(2):
                        pe.wait_ge(eps_added, e * CH + cc * 2 + (j + 1))
                        nc.tensor.matmul(ps_m[j][:, 0:CN], avg_h[:], sq[:, bass.ds((cc * 2 + j) * CN, CN)],
                                         start=True, stop=True).then_inc(var_ready, 1)

            schedule(nc.tensor, up, out, var)

        @block.scalar
        def _(act):
            def up(e, b, visit):
                with nc.scalar.Fori(0, CH // 2) as cc:
                    act.wait_ge(w_landed[b], (visit + 1) * n_loads)
                    for j in range(2):
                        act.wait_ge(a_ready, e * CH + cc * 2 + (j + 1))
                        nc.scalar.activation(act_a[:, j, :], ps_a[j][:, 0:CN], ACT.Silu,
                                             bias=vec[b][:, 0:1]).then_inc(silu_done, 1)
                    for j in range(2):
                        act.wait_ge(centred, e * CH + cc * 2 + (j + 1))
                        at = bass.ds((cc * 2 + j) * CN, CN)
                        nc.scalar.activation(sq[:, at], hid[b][:, at], ACT.Square).then_inc(squared, 1)

            def var(e, b, visit):
                act.wait_ge(recip_done, e + 1)
                nc.scalar.activation(rstd[:], rstd[:], ACT.Sqrt).then_inc(rstd_ready, 1)

            def out(e, b, visit):
                act.wait_ge(z_scaled, e + 1)
                nc.scalar.activation(z[:], z[:], ACT.Identity, scale=vec[b][:, 2:3],
                                     bias=vec[b][:, 3:4]).then_inc(z_ready, 1)

            schedule(nc.scalar, up, out, var)

        @block.gpsimd
        def _(pool):
            def var(e, b, visit):
                pool.wait_ge(w_landed[b], (visit + 1) * n_loads)
                pool.wait_ge(rstd_ready, e + 1)
                nc.gpsimd.tensor_tensor(z[:], hid[b][:], rstd[:], ALU.mult).then_inc(z_scaled, 1)

            schedule(nc.gpsimd, lambda *a: None, lambda *a: None, var)

        @block.vector
        def _(dve):
            nc.vector.memset(part[:, 0, 0:1], 0.0).then_inc(s_ready, 2)
            nc.vector.memset(part[:, 0, 1:2], 0.0).then_inc(eps_added, 2)
            nc.vector.memset(part[:, 0, 2:3], 0.0).then_inc(y_used, 1)
            nc.vector.memset(part[:, 0, 3:4], 0.0).then_inc(h_added, 1)
            nc.vector.memset(avg_h[:], 1.0 / H).then_inc(avg_set, 1)

            def up(e, b, visit):
                with nc.vector.Fori(0, CH // 2) as cc:
                    dve.wait_ge(w_landed[b], (visit + 1) * n_loads)
                    for j in range(2):
                        dve.wait_ge(silu_done, e * CH + cc * 2 + (j + 1))
                        dve.wait_ge(b_ready, e * CH + cc * 2 + (j + 1))
                        nc.vector.scalar_tensor_tensor(hid[b][:, bass.ds((cc * 2 + j) * CN, CN)],
                                                       ps_b[j][:, 0:CN], vec[b][:, 1:2], act_a[:, j, :],
                                                       ALU.add, ALU.mult).then_inc(s_ready, 1)
                    for j in range(2):
                        dve.wait_ge(mean_ready, e * CH + cc * 2 + (j + 1))
                        at = hid[b][:, bass.ds((cc * 2 + j) * CN, CN)]
                        nc.vector.tensor_tensor(at, at, ps_m[j][:, 0:CN], ALU.subtract).then_inc(centred, 1)

            def out(e, b, visit):
                with nc.vector.Fori(0, CH) as c:
                    dve.wait_ge(y_ready, e * CH + c + 1)
                    dve.wait_ge(h_added, e * CH + c + 1)
                    for m in range(KD):
                        p, bias = ps_y[:, m, 0:CN], vec[b][:, 4 + m:5 + m]
                        if gated:
                            last = nc.vector.scalar_tensor_tensor(part[:, m, :], p, bias,
                                                                  gate[b][:, bass.ds(c * CN, CN)], ALU.add, ALU.mult)
                        else:
                            last = nc.vector.tensor_scalar(part[:, m, :], p, bias, None, ALU.add)
                    last.then_inc(y_used, 1)
                    dve.wait_ge(y_used, e * CH + c + 2)
                    nc.vector.tensor_tensor(both(out_t, c), both(out_t, c), part[:], ALU.add).then_inc(h_added, 1)

            def var(e, b, visit):
                with nc.vector.Fori(0, CH // 2) as cc:
                    for j in range(2):
                        dve.wait_ge(var_ready, e * CH + cc * 2 + (j + 1))
                        nc.vector.tensor_scalar(rstd[:, bass.ds((cc * 2 + j) * CN, CN)], ps_m[j][:, 0:CN],
                                                1.0e-5, None, ALU.add).then_inc(eps_added, 1)
                dve.wait_ge(eps_added, e * CH + (CH + 2))
                nc.vector.reciprocal(rstd[:], rstd[:]).then_inc(recip_done, 1)

            schedule(nc.vector, up, out, var)


def selected_ffn(g):
    with ExitStack() as ctx:
        sc = Scope(g.nc, ctx, "f0")
        xs = sc.sb("xs", [P, KD, N_SEL])
        ys = sc.sb("ys", [P, KD, N_SEL])
        row = sc.sb("row", [P, SEL_T], I32)
        select(g, xs, ys, row)
        biased_experts(g, "f0e", xs, ys, 0, NE + 1, 2, N_SEL // 2, True)
        scatter_rows(g, ys, row)
    biased_experts(g, "f0s", g.xn, g.h, NE, 1, CH, CN, False)
    add_extra(g)


def select(g, xs, ys, row):
    nc, dram = g.nc, g.dram
    with ExitStack() as ctx:
        sc = Scope(nc, ctx, "f0r")
        w = sc.sb("w", [P, KD, NE + 1])
        bias = sc.sb("bias", [P, NE + 1])
        ebias = sc.sb("ebias", [P, NE])
        rank = sc.sb("rank", [P, NE])
        idx_i = sc.sb("idx_i", [P, 2, SEL_T], I32)
        idx = sc.sb("idx", [P, 2, SEL_T])
        bad = sc.sb("bad", [P, 2, SEL_T])
        neg = sc.sb("neg", [P, 2, SEL_T])
        flat = sc.sb("flat", [P, SEL_T])
        target = sc.sb("target", [P, SEL_T])
        spare = sc.sb("spare", [P, SEL_T])
        source = sc.sb("source", [P, SEL_T], I32)
        rows = sc.sb("rows", [RN, RT, D])
        picked = sc.sb("picked", [P, SEL_T, D])
        lg = sc.sb("lg", [P, SEL_T, NE + 1])
        chosen = sc.sb("chosen", [P, SEL_T, NE])
        ranked = sc.sb("ranked", [P, SEL_T, NE])
        hot = sc.sb("hot", [P, SEL_T, NE])
        gate = sc.sb("gate", [P, SEL_T, NE + 1])
        top = sc.sb("top", [P, SEL_T])
        top_rank = sc.sb("top_rank", [P, SEL_T])
        ex = sc.sb("ex", [P, SEL_T])
        gate_t = sc.sb("gate_t", [NE + 1, N_SEL])
        zero = sc.sb("zero", [RN, RT, D])
        ps = sc.ps("ps", [P, 8, 512])
        landed = sc.sem("landed")
        zeroed = sc.sem("zeroed")
        stored = sc.sem("stored")
        rows_turned = sc.sem("rows_turned")
        rows_copied = sc.sem("rows_copied")
        source_ready = sc.sem("source_ready")
        gathered = [sc.sem(f"gathered{t}") for t in range(SEL_T)]
        x_turned = sc.sem("x_turned")
        x_copied = sc.sem("x_copied")
        logits = sc.sem("logits")
        act_in = sc.sem("act_in")
        act_done = sc.sem("act_done")
        gates = sc.sem("gates")
        gates_turned = sc.sem("gates_turned")
        copied = sc.sem("copied")
        gates_stored = sc.sem("gates_stored")
        own = sc.sem("own")
        ln = LayerNorm(sc, "ln", g.h, g.xn, g.avg, g.ident, g.eps5, ps)
        block = ctx.enter_context(nc.Block())
        half = RT // 2
        loads = [(idx_i[:], dram["f0_index"]), (w[:], dram["f0_router_w"]),
                 (bias[:], dram["f0_router_b"].to_broadcast([P, NE + 1])),
                 (ebias[:], dram["L0_ffn_exp_bias"].to_broadcast([P, NE])), (rank[:], dram["c_rank"]),
                 (spare[:], dram["c_spare"])]

        @block.sync
        def _(sp):
            for a, b in loads:
                sp.dma_start(a, b).then_inc(landed, 16)
            sp.wait_ge(zeroed, 1)
            sp.dma_start(dram["s_extra"][0:NT, :].rearrange("(t p) d -> p t d", p=RN), zero[:]).then_inc(stored, 16)
            view = dram["s_rows"].rearrange("(t p) d -> p t d", p=RN)
            for n in range(2):
                sp.wait_ge(rows_copied, half * (n + 1))
                sp.dma_start(view[:, half * n:half * (n + 1), :],
                             rows[:, half * n:half * (n + 1), :]).then_inc(stored, 16)
            sp.wait_ge(copied, 1)
            sp.dma_start(dram["s_gate"], gate_t[:]).then_inc(gates_stored, 16)
            sp.wait_ge(gates_stored, 16)

        @block.tensor
        def _(pe):
            ln.tensor(nc, pe)
            pe.wait_ge(ln.normed, CH)
            pe.wait_ge(ln.std_ready, CH)
            for t in range(RT):
                if t >= 3:
                    pe.wait_ge(rows_copied, t - 2)
                for k in range(KD):
                    mm = nc.tensor.transpose(ps[0:RN, t % 3, k * P:(k + 1) * P],
                                             g.xn[:, k, t * RN:(t + 1) * RN], g.ident[:])
                mm.then_inc(rows_turned, 1)
            for t in range(SEL_T):
                pe.wait_ge(gathered[t], 16)
                for k in range(KD):
                    mm = nc.tensor.transpose(ps[:, 3 + k, t * P:(t + 1) * P], picked[:, t, k * P:(k + 1) * P],
                                             g.ident[:])
            mm.then_inc(x_turned, 1)
            pe.wait_ge(landed, 16 * len(loads))
            pe.wait_ge(x_copied, KD)
            for t in range(SEL_T):
                for k in range(KD):
                    mm = nc.tensor.matmul(ps[:, 5, t * (NE + 1):(t + 1) * (NE + 1)], xs[:, k, t * P:(t + 1) * P],
                                          w[:, k, :], start=(k == 0), stop=(k == KD - 1))
            mm.then_inc(logits, 1)
            pe.wait_ge(gates, 1)
            for t in range(SEL_T):
                mm = nc.tensor.transpose(ps[0:NE + 1, 6, t * P:(t + 1) * P], gate[:, t, :], g.ident[:])
            mm.then_inc(gates_turned, 1)

        @block.scalar
        def _(act):
            ln.scalar(nc, act)
            for t in range(RT):
                act.wait_ge(rows_turned, t + 1)
                nc.scalar.copy(rows[:, t, :], ps[0:RN, t % 3, 0:D]).then_inc(rows_copied, 1)
            act.wait_ge(act_in, 1)
            nc.scalar.activation(lg[:], lg[:], ACT.Sigmoid).then_inc(act_done, 1)
            act.wait_ge(act_in, 2)
            nc.scalar.activation(ex[:], ex[:], ACT.Sigmoid).then_inc(act_done, 1)

        @block.gpsimd
        def _(pool):
            ln.gpsimd(nc, pool)
            nc.gpsimd.memset(zero[:], 0.0).then_inc(zeroed, 1)
            nc.gpsimd.memset(ys[:], 0.0)
            pool.wait_ge(source_ready, 1)
            pool.wait_ge(stored, 16 * 3)
            for t in range(SEL_T):
                nc.gpsimd.indirect_dma_start(picked[:, t, :], None, dram["s_rows"], bass.IndirectOffsetOnAxis(
                    ap=source[:, t:t + 1], axis=0)).then_inc(gathered[t], 16)

        @block.vector
        def _(dve):
            v = nc.vector
            ln.vector(nc, dve)
            chain = Chain(dve, own)
            dve.wait_ge(landed, 16 * len(loads))
            chain.step(v.tensor_copy(idx[:], idx_i[:]))
            for n, size in enumerate((NB, S)):
                i, b = idx[:, n, :], bad[:, n, :]
                chain.step(v.tensor_scalar(neg[:, n, :], i, 0.0, float(size), ALU.is_lt, ALU.mult))
                chain.step(v.tensor_tensor(i, i, neg[:, n, :], ALU.add))
                chain.step(v.tensor_scalar(b, i, float(size), None, ALU.is_ge))
                chain.step(v.scalar_tensor_tensor(b, i, 0.0, b, ALU.is_lt, ALU.add))
                chain.step(v.tensor_scalar(i, i, 0.0, float(size - 1), ALU.max, ALU.min))
            chain.step(v.scalar_tensor_tensor(flat[:], idx[:, 0, :], float(S), idx[:, 1, :], ALU.mult, ALU.add))
            v.tensor_copy(source[:], flat[:]).then_inc(source_ready, 1)
            chain.step(v.tensor_tensor(target[:], bad[:, 0, :], bad[:, 1, :], ALU.add))
            chain.step(v.tensor_scalar(target[:], target[:], 1.0, None, ALU.min))
            chain.step(v.tensor_tensor(spare[:], spare[:], flat[:], ALU.subtract))
            chain.step(v.tensor_tensor(target[:], target[:], spare[:], ALU.mult))
            chain.step(v.tensor_tensor(target[:], target[:], flat[:], ALU.add))
            chain.step(v.tensor_copy(row[:], target[:]))
            dve.wait_ge(x_turned, 1)
            for k in range(KD):
                v.tensor_copy(xs[:, k, :], ps[:, 3 + k, :]).then_inc(x_copied, 1)
            dve.wait_ge(logits, 1)
            full = [P, SEL_T, NE]
            bb = bias[:].rearrange("p (a e) -> p a e", a=1).to_broadcast([P, SEL_T, NE + 1])
            v.tensor_tensor(lg[:], ps[:, 5, 0:SEL_T * (NE + 1)].rearrange("p (t e) -> p t e", t=SEL_T), bb,
                            ALU.add).then_inc(act_in, 1)
            dve.wait_ge(act_done, 1)
            eb = ebias[:].rearrange("p (a e) -> p a e", a=1).to_broadcast(full)
            chain.step(v.tensor_tensor(chosen[:], lg[:, :, 0:NE], eb, ALU.add))
            first_of_max(nc, chain, chosen[:], top, ranked, hot[:], rank, top_rank, full)
            chain.step(v.tensor_tensor(ranked[:], hot[:], lg[:, :, 0:NE], ALU.mult))
            chain.step(v.tensor_reduce(top[:], ranked[:], AX_X, ALU.add))
            v.tensor_tensor(ex[:], top[:], lg[:, :, NE:NE + 1].rearrange("p t a -> p (t a)"),
                            ALU.subtract).then_inc(act_in, 1)
            dve.wait_ge(act_done, 2)
            exb = ex[:].rearrange("p (t a) -> p t a", a=1).to_broadcast(full)
            chain.step(v.tensor_tensor(gate[:, :, 0:NE], hot[:], exb, ALU.mult))
            v.tensor_scalar(gate[:, :, NE:NE + 1].rearrange("p t a -> p (t a)"), ex[:], -1.0, None,
                            ALU.mult).then_inc(gates, 1)
            dve.wait_ge(gates_turned, 1)
            v.tensor_copy(gate_t[:], ps[0:NE + 1, 6, :]).then_inc(copied, 1)


def scatter_rows(g, ys, row):
    nc, dram = g.nc, g.dram
    with ExitStack() as ctx:
        sc = Scope(nc, ctx, "f0w")
        rows = sc.sb("rows", [P, SEL_T, D])
        ps = sc.ps("ps", [P, SEL_T, 512])
        turned = sc.sem("turned")
        copied = sc.sem("copied")
        stored = sc.sem("stored")
        block = ctx.enter_context(nc.Block())

        @block.tensor
        def _(pe):
            for t in range(SEL_T):
                for k in range(KD):
                    mm = nc.tensor.transpose(ps[:, t, k * P:(k + 1) * P], ys[:, k, t * P:(t + 1) * P], g.ident[:])
                mm.then_inc(turned, 1)

        @block.vector
        def _(dve):
            for t in range(SEL_T):
                dve.wait_ge(turned, t + 1)
                nc.vector.tensor_copy(rows[:, t, :], ps[:, t, 0:D]).then_inc(copied, 1)

        @block.gpsimd
        def _(pool):
            for t in range(SEL_T):
                pool.wait_ge(copied, t + 1)
                nc.gpsimd.indirect_dma_start(dram["s_extra"], bass.IndirectOffsetOnAxis(ap=row[:, t:t + 1], axis=0),
                                             rows[:, t, :], None).then_inc(stored, 16)
            pool.wait_ge(stored, 16 * SEL_T)


def add_extra(g):
    nc, dram = g.nc, g.dram
    TB = 512 // RN
    groups = [(t, min(t + TB, RT)) for t in range(0, RT, TB)]
    with ExitStack() as ctx:
        sc = Scope(nc, ctx, "f0x")
        rows = sc.sb("rows", [RN, RT, D])
        ps = sc.ps("ps", [P, 8, 512])
        landed = sc.sem("landed")
        turned = sc.sem("turned")
        added = sc.sem("added")
        block = ctx.enter_context(nc.Block())

        @block.sync
        def _(sp):
            sp.dma_start(rows[:], dram["s_extra"][0:NT, :].rearrange("(t p) d -> p t d", p=RN)).then_inc(landed, 16)

        @block.tensor
        def _(pe):
            pe.wait_ge(landed, 16)
            for i, (lo, hi) in enumerate(groups):
                if i >= 4:
                    pe.wait_ge(added, (i - 3) * KD)
                for t in range(lo, hi):
                    for k in range(KD):
                        mm = nc.tensor.transpose(ps[:, i % 4 * KD + k, (t - lo) * RN:(t - lo + 1) * RN],
                                                 rows[:, t, k * P:(k + 1) * P], g.ident[0:RN, 0:RN])
                mm.then_inc(turned, 1)

        @block.vector
        def _(dve):
            for i, (lo, hi) in enumerate(groups):
                dve.wait_ge(turned, i + 1)
                for k in range(KD):
                    o = g.h[:, k, lo * RN:hi * RN]
                    nc.vector.tensor_tensor(o, o, ps[:, i % 4 * KD + k, 0:(hi - lo) * RN], ALU.add).then_inc(added, 1)


def layer_norm(g, tag, src, out, gamma=None, beta=None, rms=False, loads=(), add_to=None,
               chunks=CH, width=CN, final=None):
    nc = g.nc
    with ExitStack() as ctx:
        sc = Scope(nc, ctx, tag)
        ps = sc.ps("ps", [P, 8, 512])
        landed = sc.sem("landed")
        added = sc.sem("added")
        ln = LayerNorm(sc, "ln", src, out, g.avg, g.ident, g.eps6 if rms else g.eps5, ps, gamma, beta, rms, chunks,
                       width, final)
        block = ctx.enter_context(nc.Block())

        @block.sync
        def _(sp):
            for dst, s in loads:
                sp.dma_start(dst, s).then_inc(landed, 16)
            if loads:
                sp.wait_ge(landed, 16 * len(loads))

        @block.tensor
        def _(pe):
            ln.tensor(nc, pe)

        @block.gpsimd
        def _(pool):
            ln.gpsimd(nc, pool)

        @block.scalar
        def _(act):
            ln.scalar(nc, act)

        @block.vector
        def _(dve):
            if loads and gamma is not None:
                dve.wait_ge(landed, 16 * len(loads))
            ln.vector(nc, dve)
            if add_to is not None:
                with nc.vector.Fori(0, CH) as i:
                    dve.wait_ge(ln.normed, i + 1)
                    nc.vector.tensor_tensor(both(add_to, i), both(add_to, i), both(out, i), ALU.add).then_inc(added, 1)


def gated_scan(g):
    nc, dram = g.nc, g.dram
    I = 512
    KI = I // P
    with ExitStack() as ctx:
        sc = Scope(nc, ctx, "s1")
        w_in = sc.sb("w_in", [P, KD, 2 * I])
        wo = sc.sb("wo", [P, KI, D])
        vec = sc.sb("vec", [P, 28])
        b_in, conv_b = vec[:, 0:8], vec[:, 8:12]
        b_abc = [vec[:, 12 + 4 * n:16 + 4 * n] for n in range(3)]
        bo, norm_g, norm_b = (sc.sb(n, [P, KD]) for n in ("bo", "norm_g", "norm_b"))
        conv_w = sc.sb("conv_w", [P, KI, 3])
        u = sc.sb("u", [P, KI, NT])
        with ExitStack() as mid:
            scm = Scope(nc, mid, "s1m")
            xg = scm.sb("xg", [P, KD, NT])
            layer_norm(g, "s1n", g.h, g.xn, loads=(
                (w_in[:], dram["L1_attn_W_in"]), (wo[:], dram["L1_attn_Wo"]), (vec[:, 0:24], dram["s1_vec"]),
                (bo[:], dram["L1_attn_bo"]), (norm_g[:], dram["L1_attn_gamma"]),
                (norm_b[:], dram["L1_attn_beta"]), (conv_w[:], dram["L1_attn_conv_w"])))
            layer_norm(g, "s1o", g.xn, xg, norm_g, norm_b)
            gated_scan_in(g, xg, w_in, b_in, conv_w, conv_b, u, KI)
        gated_scan_out(g, u, b_abc, wo, bo, KI)


def gated_scan_in(g, xg, w_in, b_in, conv_w, conv_b, u, KI):
    nc = g.nc
    with ExitStack() as ctx:
        sc = Scope(nc, ctx, "sa")
        proj = sc.sb("proj", [P, 3, NT])
        sig = sc.sb("sig", [P, 3, NT])
        ps_p = [sc.ps(f"ps_p{j}", [P, 512]) for j in range(2)]
        ps_g = [sc.ps(f"ps_g{j}", [P, 512]) for j in range(2)]
        p_ready = sc.sem("p_ready")
        g_ready = sc.sem("g_ready")
        moved = sc.sem("moved")
        own = sc.sem("own")
        conv_done = sc.sem("conv_done")
        silu_done = sc.sem("silu_done")
        u_done = sc.sem("u_done")
        block = ctx.enter_context(nc.Block())

        def by_batch(t):
            return t.rearrange("p (b s) -> p b s", s=S)

        @block.tensor
        def _(pe):
            for m in range(KI):
                with nc.tensor.Fori(0, CH // 2) as cc:
                    for j in range(2):
                        pe.wait_ge(moved, cc * 2 + (m * CH + j + 1))
                        for ps, col, ready in ((ps_p, m * P, p_ready), (ps_g, (KI + m) * P, g_ready)):
                            for k in range(KD):
                                mm = nc.tensor.matmul(ps[j][:, 0:CN], w_in[:, k, col:col + P],
                                                      chunk(xg, k, cc * 2 + j), start=(k == 0), stop=(k == KD - 1))
                            mm.then_inc(ready, 1)

        @block.scalar
        def _(act):
            def silu(m):
                act.wait_ge(conv_done, m + 1)
                nc.scalar.activation(u[:, m, :], u[:, m, :], ACT.Silu).then_inc(silu_done, 1)

            for m in range(KI):
                if m >= 3:
                    act.wait_ge(u_done, m - 2)
                with nc.scalar.Fori(0, CH // 2) as cc:
                    for j in range(2):
                        n = cc * 2 + (m * CH + j + 1)
                        at = bass.ds((cc * 2 + j) * CN, CN)
                        act.wait_ge(p_ready, n)
                        nc.scalar.activation(proj[:, m % 3, at], ps_p[j][:, 0:CN], ACT.Identity,
                                             bias=b_in[:, m:m + 1])
                        act.wait_ge(g_ready, n)
                        nc.scalar.activation(sig[:, m % 3, at], ps_g[j][:, 0:CN], ACT.Sigmoid,
                                             bias=b_in[:, KI + m:KI + m + 1]).then_inc(moved, 1)
                if m >= 1:
                    silu(m - 1)
            silu(KI - 1)

        @block.vector
        def _(dve):
            chain = Chain(dve, own)
            v = nc.vector
            v.memset(u[:, 0, 0:1], 0.0).then_inc(moved, 2)

            def product(m):
                dve.wait_ge(silu_done, m + 1)
                v.tensor_tensor(u[:, m, :], u[:, m, :], sig[:, m % 3, :], ALU.mult).then_inc(u_done, 1)

            for m in range(KI):
                dve.wait_ge(moved, (m + 1) * CH + 2)
                chain.step(v.tensor_scalar(u[:, m, :], proj[:, m % 3, :], conv_w[:, m, 2:3], conv_b[:, m:m + 1],
                                           ALU.mult, ALU.add))
                o, q = by_batch(u[:, m, :]), by_batch(proj[:, m % 3, :])
                for back in (1, 2):
                    ins = v.scalar_tensor_tensor(o[:, :, back:S], q[:, :, 0:S - back],
                                                 conv_w[:, m, 2 - back:3 - back], o[:, :, back:S],
                                                 ALU.mult, ALU.add)
                    if back == 1:
                        chain.step(ins)
                    else:
                        ins.then_inc(conv_done, 1)
                if m >= 1:
                    product(m - 1)
            product(KI - 1)


def gated_scan_out(g, u, b_abc, wo, bo, KI):
    nc, dram = g.nc, g.dram
    with ExitStack() as ctx:
        sc = Scope(nc, ctx, "sb")
        w = [sc.sb(f"w{n}", [P, KI, P]) for n in "abc"]
        w2 = [sc.sb(f"w2{n}", [P, KI, P]) for n in "abc"]
        a, b, c = (sc.sb(n, [P, NT]) for n in "abc")
        y = sc.sb("y", [P, KI, NT])
        part = sc.sb("part", [P, KD, CN])
        ps = [[sc.ps(f"ps{n}{j}", [P, 512]) for j in range(2)] for n in "abc"]
        ps_o = sc.ps("ps_o", [P, KD, 512])
        w_landed = [sc.sem(f"w_landed{n}") for n in range(2)]
        abc_ready = sc.sem("abc_ready")
        moved = sc.sem("moved")
        own = sc.sem("own")
        y_done = sc.sem("y_done")
        o_ready = sc.sem("o_ready")
        o_used = sc.sem("o_used")
        h_added = sc.sem("h_added")
        block = ctx.enter_context(nc.Block())
        bufs = (w, w2)

        def out_bank(j, m):
            return ps_o[:, m, 0:CN] if j == 0 else ps[0][m][:, 0:CN]

        @block.sync
        def _(sp):
            for m in range(KI):
                if m >= 2:
                    sp.wait_ge(abc_ready, (m - 1) * CH)
                for n, name in enumerate(("L1_attn_Wa", "L1_attn_Wb", "L1_attn_Wc")):
                    sp.dma_start(bufs[m % 2][n][:], dram[name][:, :, m * P:(m + 1) * P]).then_inc(w_landed[m % 2], 16)

        @block.tensor
        def _(pe):
            for m in range(KI):
                pe.wait_ge(w_landed[m % 2], 48 * (m // 2 + 1))
                with nc.tensor.Fori(0, CH // 2) as cc:
                    for j in range(2):
                        pe.wait_ge(moved, cc * 2 + (m * CH + j + 1))
                        for n in range(3):
                            for k in range(KI):
                                mm = nc.tensor.matmul(ps[n][j][:, 0:CN], bufs[m % 2][n][:, k, :],
                                                      chunk(u, k, cc * 2 + j), start=(k == 0), stop=(k == KI - 1))
                        mm.then_inc(abc_ready, 1)
            pe.wait_ge(y_done, KI)
            with nc.tensor.Fori(0, CH // 2) as cc:
                for j in range(2):
                    pe.wait_ge(o_used, cc * 2 + (j + 1))
                    for m in range(KD):
                        for k in range(KI):
                            mm = nc.tensor.matmul(out_bank(j, m), wo[:, k, m * P:(m + 1) * P], chunk(y, k, cc * 2 + j),
                                                  start=(k == 0), stop=(k == KI - 1))
                    mm.then_inc(o_ready, 1)

        @block.scalar
        def _(act):
            for m in range(KI):
                if m >= 1:
                    act.wait_ge(y_done, m)
                with nc.scalar.Fori(0, CH // 2) as cc:
                    for j in range(2):
                        act.wait_ge(abc_ready, cc * 2 + (m * CH + j + 1))
                        for n, (dst, f) in enumerate(((a, ACT.Sigmoid), (b, ACT.Sigmoid), (c, ACT.Tanh))):
                            last = nc.scalar.activation(dst[:, bass.ds((cc * 2 + j) * CN, CN)], ps[n][j][:, 0:CN],
                                                        f, bias=b_abc[n][:, m:m + 1])
                        last.then_inc(moved, 1)

        @block.vector
        def _(dve):
            chain = Chain(dve, own)
            v = nc.vector
            v.memset(part[:, 0, 0:1], 0.0).then_inc(moved, 2)
            v.memset(part[:, 0, 1:2], 0.0).then_inc(o_used, 2)
            v.memset(part[:, 0, 2:3], 0.0).then_inc(h_added, 1)
            for m in range(KI):
                dve.wait_ge(moved, (m + 1) * CH + 2)
                chain.step(v.tensor_tensor(b[:], b[:], u[:, m, :], ALU.mult))
                for s in range(NB):
                    at = slice(s * S, (s + 1) * S)
                    ins = v.tensor_tensor_scan(y[:, m, at], a[:, at], b[:, at], 0.0, ALU.mult, ALU.add)
                chain.step(ins)
                chain.step(v.tensor_tensor(y[:, m, :], y[:, m, :], c[:], ALU.mult))
                v.tensor_tensor(y[:, m, :], y[:, m, :], u[:, m, :], ALU.add).then_inc(y_done, 1)
            with nc.vector.Fori(0, CH // 2) as cc:
                for j in range(2):
                    i = cc * 2 + j
                    dve.wait_ge(o_ready, cc * 2 + (j + 1))
                    dve.wait_ge(h_added, cc * 2 + (j + 1))
                    for m in range(KD):
                        last = v.scalar_tensor_tensor(part[:, m, :], out_bank(j, m), bo[:, m:m + 1],
                                                      chunk(g.xn, m, i), ALU.add, ALU.add)
                    last.then_inc(o_used, 1)
                    dve.wait_ge(o_used, cc * 2 + (j + 3))
                    v.tensor_tensor(both(g.h, i), both(g.h, i), part[:], ALU.add).then_inc(h_added, 1)


def three_matrices(g):
    nc, dram = g.nc, g.dram
    with ExitStack() as ctx:
        sc = Scope(nc, ctx, "t2")
        w = sc.sb("w", [P, 3, KD, D])
        bias = sc.sb("bias", [P, KD])
        layer_norm(g, "t2n", g.h, g.xn, loads=[(w[:, n], dram[name]) for n, name in enumerate(
            ("L2_ffn_weight", "L2_ffn_aux_weight1", "L2_ffn_aux_weight2"))] + [(bias[:], dram["L2_ffn_bias"])])
        x1 = sc.sb("x1", [P, KD, NT])
        x2 = sc.sb("x2", [P, KD, NT])
        x3 = sc.sb("x3", [P, KD, NT])
        ps = [sc.ps(f"ps{j}", [P, KD, 512]) for j in range(2)]
        ready = sc.sem("ready")
        moved = sc.sem("moved")
        added = sc.sem("added")
        block = ctx.enter_context(nc.Block())
        src, dst = (g.xn, x1, x2), (x1, x2, x3)

        @block.tensor
        def _(pe):
            for n in range(3):
                with nc.tensor.Fori(0, CH // 2) as cc:
                    for j in range(2):
                        pe.wait_ge(moved, cc * 2 + (n * CH + j + 1))
                        for m in range(KD):
                            for k in range(KD):
                                mm = nc.tensor.matmul(ps[j][:, m, 0:CN], w[:, n, k, m * P:(m + 1) * P],
                                                      chunk(src[n], k, cc * 2 + j),
                                                      start=(k == 0), stop=(k == KD - 1))
                        mm.then_inc(ready, 1)

        @block.scalar
        def _(act):
            nc.scalar.copy(x3[:, 0, 0:1], g.ident[:, 0:1]).then_inc(moved, 2)
            for n in range(3):
                with nc.scalar.Fori(0, CH // 2) as cc:
                    for j in range(2):
                        act.wait_ge(ready, cc * 2 + (n * CH + j + 1))
                        if n < 2:
                            last = nc.scalar.copy(both(dst[n], cc * 2 + j), ps[j][:, :, 0:CN])
                        else:
                            for m in range(KD):
                                last = nc.scalar.activation(chunk(x3, m, cc * 2 + j), ps[j][:, m, 0:CN], ACT.Tanh,
                                                            bias=bias[:, m:m + 1])
                        last.then_inc(moved, 1)

        @block.vector
        def _(dve):
            with nc.vector.Fori(0, CH) as i:
                dve.wait_ge(moved, i + (2 * CH + 3))
                nc.vector.tensor_tensor(both(g.h, i), both(g.h, i), both(x3, i), ALU.add).then_inc(added, 1)


class Unit:

    def __init__(self, kind, g, tile, pair, lo, hi):
        self.kind, self.g, self.tile, self.pair, self.lo, self.hi = kind, g, tile, pair, lo, hi
        self.last = False


def attention(g, tag, src, length, heads, dh, scale, causal, k_heads, names, res, dst):
    nc, dram = g.nc, g.dram
    stripe = 2 * dh
    per = P // stripe
    pairs = per // 2
    G = heads // per
    in_tile = P // dh
    RQ, RK = heads * dh // P, max(1, k_heads * dh // P)
    tiles = [(s, min(P, length - s)) for s in range(0, length, P)]
    NTL = len(tiles)
    width = NTL * P
    even = length + length % 2
    regions = [(0, length)] if length <= 512 else [(0, 3 * P), (3 * P, length)]
    one_bank = len(regions) == 1
    shared_k = k_heads == 1
    v_cols = stripe if shared_k else heads * stripe
    o_banks = 2 if one_bank else 1
    b_heads = 2 if one_bank else 1
    wq_d, wk_d, wv_d, wo_d, bq_d, bk_d, bv_d, bo_d = (dram[n] for n in names)
    ROW = 96

    def cuts(lo, hi):
        return [(n, max(lo, a), min(hi, b)) for n, (a, b) in enumerate(regions) if max(lo, a) < min(hi, b)]

    def spans(lo, hi):
        return [(lo, hi)] if hi - lo <= 512 else [(a, b) for _, a, b in cuts(lo, hi)]

    def up_even(n):
        return even if n == length else n

    def maxima(gr):
        out = []
        for t, (start, rows) in enumerate(tiles):
            for pr in range(pairs):
                out += [Unit("M", gr, t, pr, lo, hi) for lo, hi in spans(0, start + rows if causal else length)]
        out[-1].last = True
        return out

    def probs(gr):
        out = []
        for t, (start, rows) in enumerate(tiles):
            for lo, hi in spans(start if causal else 0, length):
                out += [Unit("P", gr, t, pr, lo, hi) for pr in range(pairs)]
        out[-1].last = True
        return out

    def both_of(gr):
        ps, ms = probs(gr), maxima(gr + 1)
        n = -(-len(ms) // 2)
        first = [u for i in range(n) for u in ps[i:i + 1] + ms[2 * i:2 * i + 2]]
        later = [*turned(gr + 1), *(["S%d" % (gr - 1)] if gr > 0 else [])]
        out = [first + ps[n:n + 1]]
        for i, what in enumerate(later):
            out += [what] + ([[ps[n + 1 + i]]] if n + 1 + i < len(ps) else [])
        rest = ps[n + 1 + len(later):]
        return out + ([rest] if rest else [])

    def stacks(gr):
        kinds = "B" if shared_k else "BC"
        return [Unit(k, gr, 0, h // b_heads, 0, length) for h in range(0, per, b_heads) for k in kinds]

    def turned(gr):
        return ["T%d%d" % (gr, n) for n in range(per // b_heads)]

    order = [[Unit("Q", 0, t, 0, 0, length) for t in range(RQ)] + [Unit("K", 0, t, 0, 0, length) for t in range(RK)]
             + [Unit("V", 0, t, 0, 0, v_cols) for t in range(NTL)]
             + ([Unit("C", 0, 0, 0, 0, length)] if shared_k else []) + stacks(0), maxima(0), stacks(1), *turned(0)]
    for gr in range(G - 1):
        order += [*both_of(gr)] + ([stacks(gr + 2)] if gr + 2 < G else [])
    order += ["S%d" % (G - 2), probs(G - 1), "S%d" % (G - 1), "O0", "O1"]
    units = [u for item in order if not isinstance(item, str) for u in item]
    for n, u in enumerate(units):
        u.n = n
        u.by_act = u.kind in "QKBCP"
        u.taken = sum(1 for w in units[:n + 1] if (w.kind in "QKBCP") == u.by_act)
    n_act = sum(u.by_act for u in units)
    nu, n_dve = len(units), len(units) - sum(u.by_act for u in units)
    for n, u in enumerate(u for u in units if u.kind == "P"):
        u.pn = n
    assert sum(u.kind == "P" for u in units) % 2 == 0
    first_b = next(u for u in units if u.kind in "BC")
    firsts = [next(u for u in units if u.kind == "P" and u.g == gr) for gr in range(G)]
    first_m = next(u for u in units if u.kind == "M")
    assert not any(u.kind == "V" for u in units[-2:]) and all(u.by_act for u in units[-2:])
    turns = [item for item in order if isinstance(item, str)]
    n_ps_t = len(turns)

    with ExitStack() as ctx:
        sc = Scope(nc, ctx, tag)
        wq = sc.sb("wq", [P, KD, RQ * P])
        wk = sc.sb("wk", [P, KD, RK * P])
        wv = sc.sb("wv", [P, KD, v_cols])
        wo = sc.sb("wo", [P, G, D])
        bq, bk, bo = sc.sb("bq", [P, RQ]), sc.sb("bk", [P, RK]), sc.sb("bo", [P, KD])
        bv = sc.sb("bv", [P, v_cols])
        ones_row = sc.sb("ones_row", [P, 1])
        swap = sc.sb("swap", [P, P])
        loads = [(wq, wq_d), (wk, wk_d), (wv, wv_d), (wo, wo_d), (bq, bq_d), (bk, bk_d), (bo, bo_d),
                 (ones_row, dram["c_ones_row"]), (swap, dram["c_swap%d" % stripe])]
        loads = [(a[:], b) for a, b in loads] + [(bv[:], bv_d.to_broadcast([P, v_cols]))]
        sel = sc.sb("sel", [P, 4, in_tile, P], F32R)
        ident_r = sc.sb("ident_r", [P, P], F32R)
        loads_r = [(sel, "c_sel%d" % dh), (ident_r, "c_ident")]
        if causal:
            mask_q = sc.sb("mask_q", [P, P], F32R)
            mask_k = sc.sb("mask_k", [P, P], F32R)
            loads_r += [(mask_q, "c_mask_q"), (mask_k, "c_mask_k")]
        xb = sc.sb("xb", [P, KD, length])
        raw = sc.sb("raw", [P, RQ + RK, width])
        hi_r = sc.sb("hi", [P, RQ + RK, width], F32R)
        lo_r = sc.sb("lo", [P, RQ + RK, width], F32R)
        q = sc.sb("q", [P, 2, per, width], F32R)
        kt = sc.sb("kt", [P, 1, 1, width] if shared_k else [P, 2, per, width], F32R)
        v = sc.sb("v", [P, NTL, v_cols])
        mx = sc.sb("mx", [P, NTL, per])
        mx2 = sc.sb("mx2", [P, 2])
        mrow = sc.sb("mrow", [P, per, NTL, P], F32R)
        pt = sc.sb("pt", [P, 2, 2, 512])
        o_sb = sc.sb("o_sb", [P, 2, length])
        rec = sc.sb("rec", [P, length])
        ctx_t = sc.sb("ctx", [P, G, length])
        ps_s = sc.ps("ps_s", [P, 2, 2, 512])
        ps_o = sc.ps("ps_o", [P, 2, 512])
        ps_t = sc.ps("ps_t", [P, 2, 512])
        landed = sc.sem("landed")
        landed_r = sc.sem("landed_r")
        xb_ready = sc.sem("xb_ready")
        xb_used = sc.sem("xb_used")
        split = sc.sem("split")
        filled = sc.sem("filled")
        act_took = sc.sem("act_took")
        dve_took = sc.sem("dve_took")
        max_done = sc.sem("max_done")
        t_ready = sc.sem("t_ready")
        t_took = sc.sem("t_took")
        o_ready = sc.sem("o_ready")
        o_took = sc.sem("o_took")
        ctx_done = sc.sem("ctx_done")
        own = sc.sem("own")
        zeroed = sc.sem("zeroed")
        block = ctx.enter_context(nc.Block())
        NR = RQ + RK

        def slot(u):
            return ps_s[:, u.n % 2]

        def heads_of(u):
            return [u.pair * 2 + i for i in range(2)]

        def k_stack(gr, h):
            return kt[:, 0, 0] if shared_k else kt[:, gr % 2, h]

        @block.sync
        def _(sp):
            for a, b in loads:
                sp.dma_start(a, b).then_inc(landed, 16)

        @block.gpsimd
        def _(pool):
            for a, b in loads_r:
                nc.gpsimd.dma_start(a[:], dram[b]).then_inc(landed_r, 16)
            pool.wait_ge(zeroed, 1)
            with nc.gpsimd.Fori(0, NB) as b:
                pool.wait_ge(xb_used, b + 1)
                nc.gpsimd.tensor_copy(xb[:], src[:, :, bass.ds(b * length, length)]).then_inc(xb_ready, 1)
                for n in range(NR):
                    pool.wait_ge(act_took, b * n_act + (n + 3))
                    nc.gpsimd.tensor_tensor(lo_r[:, n, :], raw[:, n, :], hi_r[:, n, :].bitcast(F32),
                                            ALU.subtract).then_inc(split, 1)

        @block.tensor
        def _(pe):
            pe.wait_ge(landed, 16 * len(loads))
            pe.wait_ge(landed_r, 16 * len(loads_r))
            pe.wait_ge(zeroed, 1)

            def took(u, b):
                if u.by_act:
                    pe.wait_ge(act_took, b * n_act + (u.taken + 2))
                else:
                    pe.wait_ge(dve_took, b * n_dve + u.taken)

            def fill(u, b):
                if u.n < 2:
                    pe.wait_ge(act_took, b * n_act + (u.n + 1))
                else:
                    took(units[u.n - 2], b)
                s = slot(u)
                start, rows = tiles[u.tile] if u.tile < NTL else (0, P)
                if u.kind in "QK":
                    w = wq if u.kind == "Q" else wk
                    for n, lo, hi in cuts(0, length):
                        for k in range(KD):
                            mm = nc.tensor.matmul(s[:, n, 0:hi - lo], w[:, k, u.tile * P:(u.tile + 1) * P],
                                                  xb[:, k, lo:hi], start=(k == 0), stop=(k == KD - 1))
                elif u.kind == "V":
                    for k in range(KD):
                        mm = nc.tensor.matmul(s[0:rows, 0, 0:v_cols], xb[:, k, start:start + rows], wv[:, k, :],
                                              start=(k == 0), stop=(k == KD - 1))
                elif u.kind in "BC":
                    if u is first_b:
                        pe.wait_ge(split, b * NR + NR)
                    for i in range(b_heads):
                        h = (u.g * per + u.pair * b_heads + i) if u.kind == "B" or not shared_k else 0
                        src_n = h // in_tile + (0 if u.kind == "B" else RQ)
                        for n, lo, hi in cuts(0, length):
                            o = s[:, i if one_bank else n, 0:up_even(hi) - lo]
                            for part, t in enumerate((hi_r, lo_r)):
                                mm = nc.tensor.matmul(o, sel[:, part + (0 if u.kind == "B" else 2), h % in_tile, :],
                                                      t[:, src_n, lo:up_even(hi)], start=(part == 0), stop=(part == 1))
                else:
                    if u is first_m:
                        took(units[u.n - 1], b)
                    masked = causal and u.lo <= start < u.hi
                    for i, h in enumerate(heads_of(u)):
                        qs, ks = q[:, u.g % 2, h], k_stack(u.g, h)
                        left, right = (qs, ks) if u.kind == "M" else (ks, qs)
                        mm = nc.tensor.matmul(s[:, i, 0:up_even(u.hi) - u.lo], left[:, start:start + P],
                                              right[:, u.lo:up_even(u.hi)], start=True, stop=not masked)
                        if masked:
                            m = mask_q if u.kind == "M" else mask_k
                            n = rows + rows % 2
                            mm = nc.tensor.matmul(s[:, i, start - u.lo:start - u.lo + n], ident_r[:], m[:, 0:n],
                                                  start=False, stop=True)
                mm.then_inc(filled, 1)

            def with_v(u, b):
                took(u, b)
                for n, lo, hi in cuts(u.lo, u.hi):
                    for i, h in enumerate(heads_of(u)):
                        c = 0 if shared_k else (u.g * per + h) * stripe
                        bank_n = u.g % 2 if one_bank else n
                        at = lo - regions[n][0]
                        mm = nc.tensor.matmul(ps_o[h * stripe:(h + 1) * stripe, bank_n, at:at + hi - lo],
                                              v[:, u.tile, c:c + stripe], pt[:, u.pn % 2, i, lo - u.lo:hi - u.lo],
                                              start=(u.tile == 0), stop=(u.tile == NTL - 1), skip_group_check=True)
                if u.last:
                    mm.then_inc(o_ready, 1)

            def turn(what, b, n):
                gr = int(what[1])
                if what[0] == "T":
                    pe.wait_ge(max_done, b * G + (gr + 1))
                elif what[0] == "S":
                    pe.wait_ge(o_took, b * G + (gr + 1 + o_banks))
                else:
                    pe.wait_ge(ctx_done, b * G + G)
                pe.wait_ge(t_took, b * n_ps_t + (n + 1))
                if what[0] == "T":
                    for i in range(b_heads):
                        h = int(what[2]) * b_heads + i
                        for t, (start, rows) in enumerate(tiles):
                            (bn, lo, hi), = cuts(start, start + rows)
                            at = lo - regions[bn][0]
                            mm = nc.tensor.matmul(ps_t[:, i if one_bank else bn, at:at + rows + rows % 2],
                                                  mrow[:, h, t, :], ident_r[:, 0:rows + rows % 2], start=True, stop=True)
                elif what[0] == "S":
                    for bn, lo, hi in cuts(0, length):
                        mm = nc.tensor.matmul(ps_t[:, bn, 0:hi - lo], swap[:], o_sb[:, gr % 2, lo:hi],
                                              start=True, stop=True)
                else:
                    for bn, lo, hi in cuts(0, length):
                        for k in range(G):
                            mm = nc.tensor.matmul(ps_t[:, bn, 0:hi - lo], wo[:, k, gr * P:(gr + 1) * P],
                                                  ctx_t[:, k, lo:hi], start=(k == 0), stop=(k == G - 1))
                mm.then_inc(t_ready, 1)

            with nc.tensor.Fori(0, NB) as b:
                pe.wait_ge(xb_ready, b + 1)
                before = None
                for item in order:
                    if isinstance(item, str):
                        turn(item, b, turns.index(item))
                        continue
                    for u in item:
                        if u.kind == "P" and u is firsts[u.g]:
                            pe.wait_ge(t_took, b * n_ps_t + (turns.index(turned(u.g)[-1]) + 2))
                            pe.wait_ge(o_took, b * G + (u.g + 1))
                        fill(u, b)
                        if u.kind == "P":
                            if before is not None:
                                with_v(before, b)
                            before = u
                            if u.last:
                                with_v(u, b)
                                before = None

        @block.scalar
        def _(act):
            act.wait_ge(landed, 16 * len(loads))
            act.wait_ge(zeroed, 1)
            nc.scalar.copy(pt[:, 0, 0, 0:1], pt[:, 0, 0, 0:1]).then_inc(act_took, 2)
            with nc.scalar.Fori(0, NB) as b:
                for u in units:
                    if not u.by_act:
                        continue
                    act.wait_ge(filled, b * nu + (u.n + 1))
                    if u.kind == "P":
                        rows, n = tiles[u.tile][1], u.hi - u.lo
                        last = nc.scalar.activation(pt[0:rows, u.pn % 2, :, 0:n], slot(u)[0:rows, :, 0:n], ACT.Exp,
                                                    scale=scale)
                    elif u.kind in "QK":
                        t, bias = (u.tile, bq) if u.kind == "Q" else (RQ + u.tile, bk)
                        for n, lo, hi in cuts(0, length):
                            for out in (raw, hi_r):
                                last = nc.scalar.activation(out[:, t, lo:hi], slot(u)[:, n, 0:hi - lo], ACT.Identity,
                                                            bias=bias[:, u.tile:u.tile + 1])
                    else:
                        for n, lo, hi in cuts(0, length):
                            if one_bank:
                                h = u.pair * b_heads
                                o, s = (q if u.kind == "B" else kt)[:, u.g % 2, h:h + 2, lo:hi], slot(u)[:, :, 0:hi]
                            else:
                                o = q[:, u.g % 2, u.pair, lo:hi] if u.kind == "B" else kt[:, 0, 0, lo:hi]
                                s = slot(u)[:, n, 0:hi - lo]
                            if u.kind == "B":
                                last = nc.scalar.copy(o, s)
                            else:
                                last = nc.scalar.activation(o, s, ACT.Identity, bias=ones_row[:])
                    last.then_inc(act_took, 1)

        @block.vector
        def _(dve):
            ve = nc.vector
            dve.wait_ge(landed, 16 * len(loads))
            ve.memset(mx2[:], 0.0).then_inc(t_took, 1)
            ve.memset(rec[:], 0.0).then_inc(o_took, o_banks)
            ve.memset(o_sb[:, 0, 0:1], 0.0).then_inc(xb_used, 1)
            chain = Chain(dve, own)
            for t in (mx, pt, raw):
                ve.memset(t[:], 0.0)
            for t in (q, kt, mrow, hi_r):
                ve.memset(t[:].bitcast(F32), 0.0)
            ve.memset(v[:], 0.0).then_inc(zeroed, 1)
            dve.wait_ge(zeroed, 1)

            def take(u, b):
                dve.wait_ge(filled, b * nu + (u.n + 1))
                rows = tiles[u.tile][1]
                if u.kind == "V":
                    ve.tensor_tensor(v[0:rows, u.tile, :], slot(u)[0:rows, 0, 0:v_cols], bv[0:rows, :],
                                     ALU.add).then_inc(dve_took, 1)
                    if u.tile == NTL - 1:
                        dve.wait_ge(dve_took, b * n_dve + u.taken)
                        ve.memset(mx2[:], 0.0).then_inc(xb_used, 1)
                    return
                h = u.pair * 2
                col = mx[0:rows, u.tile, h:h + 2]
                first = u.lo == 0
                out = col if first else mx2[0:rows, :]
                ve.tensor_reduce(out, slot(u)[0:rows, :, 0:u.hi - u.lo], AX_X, ALU.max).then_inc(dve_took, 1)
                if not first:
                    dve.wait_ge(dve_took, b * n_dve + u.taken)
                    chain.step(ve.tensor_tensor(col, col, mx2[0:rows, :], ALU.max))
                if u.last:
                    dve.wait_ge(dve_took, b * n_dve + u.taken)
                    m = mx[:].rearrange("p t h -> p h t")
                    hi, lo = (mrow[:, :, :, ROW + n:ROW + n + 1].rearrange("p h t a -> p h (t a)") for n in range(2))
                    chain.step(ve.tensor_scalar(hi, m, -1.0, None, ALU.mult))
                    ve.scalar_tensor_tensor(lo, m, -1.0, hi.bitcast(F32), ALU.mult, ALU.subtract).then_inc(max_done, 1)
                    dve.wait_ge(max_done, b * G + (u.g + 1))

            def turn(what, b, n):
                gr = int(what[1])
                dve.wait_ge(t_ready, b * n_ps_t + (n + 1))
                if what[0] == "T":
                    r = slice(ROW, ROW + 2)
                    for bn, lo, hi in cuts(0, length):
                        if one_bank:
                            h = int(what[2]) * b_heads
                            last = ve.tensor_copy(q[r, gr % 2, h:h + 2, lo:hi], ps_t[r, :, lo:hi])
                        else:
                            last = ve.tensor_copy(q[r, gr % 2, int(what[2]), lo:hi], ps_t[r, bn, 0:hi - lo])
                    last.then_inc(t_took, 1)
                elif what[0] == "S":
                    for bn, lo, hi in cuts(0, length):
                        last = ve.reciprocal(rec[:, lo:hi], ps_t[:, bn, 0:hi - lo])
                    last.then_inc(t_took, 1)
                    dve.wait_ge(t_took, b * n_ps_t + (n + 2))
                    ve.tensor_tensor(ctx_t[:, gr, :], o_sb[:, gr % 2, :], rec[:], ALU.mult).then_inc(ctx_done, 1)
                    dve.wait_ge(ctx_done, b * G + (gr + 1))
                else:
                    for bn, lo, hi in cuts(0, length):
                        at = bass.ds(b * length + lo, hi - lo)
                        last = ve.scalar_tensor_tensor(dst[:, gr, at], ps_t[:, bn, 0:hi - lo], bo[:, gr:gr + 1],
                                                       res[:, gr, at], ALU.add, ALU.add)
                    last.then_inc(t_took, 1)

            steps = sum(1 for u in units if u.kind == "M" and u.lo > 0) + G
            with nc.vector.Fori(0, NB) as b:
                chain.begin(b, steps)
                for item in order:
                    if isinstance(item, str):
                        turn(item, b, turns.index(item))
                        continue
                    for u in item:
                        if not u.by_act:
                            take(u, b)
                    if any(u.kind == "P" and u.last for u in item):
                        gr = item[0].g
                        dve.wait_ge(o_ready, b * G + (gr + 1))
                        for n, (lo, hi) in enumerate(regions):
                            bank_n = gr % 2 if one_bank else n
                            last = ve.tensor_copy(o_sb[:, gr % 2, lo:hi], ps_o[:, bank_n, 0:hi - lo])
                        last.then_inc(o_took, 1)
                        dve.wait_ge(o_took, b * G + (gr + 1 + o_banks))
                chain.end(NB)


def query_attention(g):
    layer_norm(g, "q2n", g.h, g.xn)
    attention(g, "q2", g.xn, S, 8, 32, D ** -0.5, True, 1,
              ("q2_wq", "q2_wk", "q2_wv", "q2_wo", "q2_bq", "q2_bk", "q2_bv", "L2_attn_bp"), g.h, g.h)


def embed(g, xt):
    nc, dram = g.nc, g.dram
    KP = 3 * 16 * 16 // P
    N_P = NB * (S_IMG - 1)
    TT = S_TXT // P
    T = NB * TT
    with ExitStack() as ctx:
        sc = Scope(nc, ctx, "em")
        idx = sc.sb("idx", [P, T], I32)
        idx_f = sc.sb("idx_f", [P, T])
        neg = sc.sb("neg", [P, T])
        rows = sc.sb("rows", [P, T, D])
        pos = sc.sb("pos", [P, TT, D])
        patches = sc.sb("patches", [P, KP, N_P])
        w = sc.sb("w", [P, KP, D])
        vec = sc.sb("vec", [P, 2, KD])
        pos_img = sc.sb("pos_img", [P, KD, S_IMG])
        ps = sc.ps("ps", [P, 6, 512])
        ps_i = sc.ps("ps_i", [P, KD, 512])
        idx_landed = sc.sem("idx_landed")
        landed = sc.sem("landed")
        idx_ready = sc.sem("idx_ready")
        gathered = [sc.sem(f"gathered{b}") for b in range(NB)]
        placed = sc.sem("placed")
        turned = sc.sem("turned")
        copied = sc.sem("copied")
        img_ready = sc.sem("img_ready")
        img_done = sc.sem("img_done")
        own = sc.sem("own")
        block = ctx.enter_context(nc.Block())

        @block.sync
        def _(sp):
            sp.dma_start(idx[:], dram["x_txt"]).then_inc(idx_landed, 16)
            for a, b in ((pos, "c_pos_txt"), (patches, "patches"), (w, "L0_tok_W"), (vec, "tok_vec"),
                         (pos_img, "L0_tok_pos_embedding")):
                sp.dma_start(a[:], dram[b]).then_inc(landed, 16)

        @block.gpsimd
        def _(pool):
            pool.wait_ge(idx_ready, 1)
            for t in range(T):
                nc.gpsimd.indirect_dma_start(
                    rows[:, t, :], None, dram["L0_txt_emb"],
                    bass.IndirectOffsetOnAxis(ap=idx[:, t:t + 1], axis=0)).then_inc(gathered[t // TT], 16)

        @block.vector
        def _(dve):
            v = nc.vector
            chain = Chain(dve, own)
            dve.wait_ge(idx_landed, 16)
            chain.step(v.tensor_copy(idx_f[:], idx[:]))
            chain.step(v.tensor_scalar(neg[:], idx_f[:], 0.0, float(VOCAB), ALU.is_lt, ALU.mult))
            chain.step(v.tensor_tensor(idx_f[:], idx_f[:], neg[:], ALU.add))
            chain.step(v.tensor_scalar(idx_f[:], idx_f[:], 0.0, float(VOCAB - 1), ALU.max, ALU.min))
            v.tensor_copy(idx[:], idx_f[:]).then_inc(idx_ready, 1)
            dve.wait_ge(landed, 16 * 5)
            dve.wait_ge(img_ready, 1)
            img = g.h[:].rearrange("p k (b s) -> p k b s", s=S)
            for k in range(KD):
                pk = pos_img[:, k, :].rearrange("p (a s) -> p a s", a=1)
                v.scalar_tensor_tensor(img[:, k, :, 1:S_IMG],
                                       ps_i[:, k, 0:N_P].rearrange("p (b s) -> p b s", b=NB), vec[:, 0, k:k + 1],
                                       pk[:, :, 1:S_IMG].to_broadcast([P, NB, S_IMG - 1]), ALU.add, ALU.add)
                v.tensor_tensor(img[:, k, :, 0:1].rearrange("p b a -> p (b a)"),
                                vec[:, 1, k:k + 1].to_broadcast([P, NB]), pos_img[:, k, 0:1].to_broadcast([P, NB]),
                                ALU.add).then_inc(img_done, 1)
            for b in range(NB):
                dve.wait_ge(gathered[b], 16 * TT)
                r = rows[:, b * TT:(b + 1) * TT, :]
                v.tensor_tensor(r, r, pos[:], ALU.add).then_inc(placed, 1)
            for t in range(T):
                dve.wait_ge(turned, t + 1)
                v.tensor_copy(xt[:, :, t * P:(t + 1) * P],
                              ps[:, t % 6, 0:D].rearrange("p (k n) -> p k n", k=KD)).then_inc(copied, 1)

        @block.tensor
        def _(pe):
            pe.wait_ge(landed, 16 * 5)
            for m in range(KD):
                for k in range(KP):
                    mm = nc.tensor.matmul(ps_i[:, m, 0:N_P], w[:, k, m * P:(m + 1) * P], patches[:, k, :],
                                          start=(k == 0), stop=(k == KP - 1))
            mm.then_inc(img_ready, 1)
            for t in range(T):
                pe.wait_ge(placed, t // TT + 1)
                if t >= 6:
                    pe.wait_ge(copied, t - 5)
                for k in range(KD):
                    mm = nc.tensor.transpose(ps[:, t % 6, k * P:(k + 1) * P], rows[:, t, k * P:(k + 1) * P],
                                             g.ident[:])
                mm.then_inc(turned, 1)


def text_block(g):
    nc, dram = g.nc, g.dram
    NX = NB * S_TXT
    F = 4 * D
    NF = F // P
    with ExitStack() as ctx:
        sc = Scope(nc, ctx, "tx")
        xt = sc.sb("xt", [P, KD, NX])
        r1 = sc.sb("r1", [P, KD, NX])
        b1 = sc.sb("b1", [P, NF])
        vec = sc.sb("vec", [P, 5, KD])
        embed(g, xt)
        attention(g, "ta", xt, S_TXT, 16, 16, 0.25, False, 16,
                  ("ta_wq", "ta_wk", "ta_wv", "ta_wo", "ta_bq", "ta_bk", "ta_bv", "L0_txt_out_proj_b"), xt, r1)
        w1 = sc.sb("w1", [P, KD, F])
        w2 = sc.sb("w2", [P, NF, D])
        layer_norm(g, "tn", r1, xt, vec[:, 1, :], vec[:, 2, :], chunks=NB, width=S_TXT, loads=(
            (vec[:], dram["txt_vec"]), (w1[:], dram["L0_txt_w1"]), (w2[:], dram["L0_txt_w2"]),
            (b1[:], dram["L0_txt_b1"])))
        relu_ffn(g, xt, r1, w1, w2, b1, vec[:, 0, :], NF)
        layer_norm(g, "to", r1, xt, vec[:, 3, :], vec[:, 4, :], chunks=NB, width=S_TXT,
                   final=lambda k, i: g.h[:, k, bass.ds(i * S + S_IMG, S_TXT)])


def relu_ffn(g, x, out, w1, w2, b1, b2, NF):
    nc = g.nc
    with ExitStack() as ctx:
        sc = Scope(nc, ctx, "tf")
        hid = sc.sb("hid", [P, 2, S_TXT])
        ps_h = [sc.ps(f"ps_h{j}", [P, 512]) for j in range(2)]
        ps_y = sc.ps("ps_y", [P, KD, 512])
        h_ready = sc.sem("h_ready")
        hid_done = sc.sem("hid_done")
        y_ready = sc.sem("y_ready")
        y_used = sc.sem("y_used")
        block = ctx.enter_context(nc.Block())

        def at(t, k, b):
            return t[:, k, bass.ds(b * S_TXT, S_TXT)]

        @block.tensor
        def _(pe):
            def up(b, f):
                pe.wait_ge(hid_done, b * NF + (f + 1))
                for k in range(KD):
                    mm = nc.tensor.matmul(ps_h[f % 2][:], w1[:, k, f * P:(f + 1) * P], at(x, k, b),
                                          start=(k == 0), stop=(k == KD - 1))
                mm.then_inc(h_ready, 1)

            with nc.tensor.Fori(0, NB) as b:
                up(b, 0)
                for f in range(NF):
                    if f + 1 < NF:
                        up(b, f + 1)
                    if f == 0:
                        pe.wait_ge(y_used, b + 1)
                    pe.wait_ge(hid_done, b * NF + (f + 3))
                    for m in range(KD):
                        mm = nc.tensor.matmul(ps_y[:, m, :], w2[:, f, m * P:(m + 1) * P], hid[:, f % 2, :],
                                              start=(f == 0), stop=(f == NF - 1))
                mm.then_inc(y_ready, 1)

        @block.scalar
        def _(act):
            nc.scalar.copy(hid[:, 0, 0:1], g.ident[:, 0:1]).then_inc(hid_done, 2)
            with nc.scalar.Fori(0, NB) as b:
                for f in range(NF):
                    act.wait_ge(h_ready, b * NF + (f + 1))
                    nc.scalar.activation(hid[:, f % 2, :], ps_h[f % 2][:], ACT.Relu,
                                         bias=b1[:, f:f + 1]).then_inc(hid_done, 1)

        @block.vector
        def _(dve):
            nc.vector.memset(out[:, 0, 0:1], 0.0).then_inc(y_used, 1)
            dve.wait_ge(y_used, 1)
            with nc.vector.Fori(0, NB) as b:
                dve.wait_ge(y_ready, b + 1)
                for m in range(KD):
                    last = nc.vector.scalar_tensor_tensor(at(out, m, b), ps_y[:, m, :], b2[:, m:m + 1], at(x, m, b),
                                                          ALU.add, ALU.add)
                last.then_inc(y_used, 1)


def slots_schedule(units, takers):
    seen = {}
    out = []
    for u in units:
        t = takers[u[0]]
        seen[t] = seen.get(t, 0) + 1
        out.append((t, seen[t]))
    return out, seen


def full_attention(g):
    nc, dram = g.nc, g.dram
    tiles = [(s, min(P, S - s)) for s in range(0, S, P)]
    NTL = len(tiles)
    cuts = [(0, 512), (512, S)]
    scale = D ** -0.5 * 1.0986122886681098
    units = [("Q", 0), ("Q", 1), ("K", 0), ("K", 1)] + [("V", t) for t in range(NTL)] \
        + [("S", 0), ("S", 1)] + [x for t in range(2, NTL) for x in (("T", t - 2), ("S", t))] \
        + [("T", NTL - 2), ("T", NTL - 1), ("O", 0), ("O", 1), ("Y", 0), ("Y", 1)]
    takers = {"Q": "act", "K": "act", "S": "act", "T": "act", "V": "dve", "O": "dve", "Y": "dve"}
    taken, per = slots_schedule(units, takers)
    NU = len(units)
    SLOTS = 4
    pad = (-NU) % SLOTS
    with ExitStack() as ctx:
        sc = Scope(nc, ctx, "a3")
        w = sc.sb("w", [P, KD, 3 * D])
        wp = sc.sb("wp", [P, KD, D])
        vec = sc.sb("vec", [P, 4, KD])
        bv = sc.sb("bv", [P, D])
        rope = sc.sb("rope", [P, 2, S])
        x = sc.sb("x", [P, KD, NT])
        layer_norm(g, "a3n", g.h, g.xn, loads=(
            (w[:], dram["L3_attn_w_qkv"]), (wp[:], dram["L3_attn_w_proj"]), (vec[:], dram["a3_vec"]),
            (bv[:], dram["a3_bv"].to_broadcast([P, D])), (rope[:], dram["c_rope"])))
        layer_norm(g, "a3r", g.xn, x, vec[:, 0, :], None, rms=True)
        xb = sc.sb("xb", [P, KD, S])
        raw = sc.sb("raw", [P, 2, KD, S])
        rot = sc.sb("rot", [P, 2, KD, S])
        tmp = sc.sb("tmp", [P, S])
        v = sc.sb("v", [P, NTL, D])
        prob = sc.sb("prob", [P, 2, S])
        prob_t = sc.sb("prob_t", [P, NTL, S])
        small = sc.sb("small", [P, NTL, 3])
        o_sb = sc.sb("o_sb", [P, KD, S])
        ps = sc.ps("ps", [P, SLOTS, 1024])
        xb_ready = sc.sem("xb_ready")
        xb_used = sc.sem("xb_used")
        filled = sc.sem("filled")
        act_took = sc.sem("act_took")
        dve_took = sc.sem("dve_took")
        max_done = sc.sem("max_done")
        prob_done = sc.sem("prob_done")
        roped = sc.sem("roped")
        added = sc.sem("added")
        own = sc.sem("own")
        block = ctx.enter_context(nc.Block())

        def slot(n):
            return ps[:, n % SLOTS]

        @block.gpsimd
        def _(pool):
            with nc.gpsimd.Fori(0, NB) as b:
                pool.wait_ge(xb_used, b + 1)
                nc.gpsimd.tensor_copy(xb[:], x[:, :, bass.ds(b * S, S)]).then_inc(xb_ready, 1)

        def taker_wait(eng, b, n):
            who, k = taken[n]
            if who == "act":
                eng.wait_ge(act_took, b * per["act"] + k)
            else:
                eng.wait_ge(dve_took, b * per["dve"] + (k + 4))

        @block.tensor
        def _(pe):
            with nc.tensor.Fori(0, NB) as b:
                pe.wait_ge(xb_ready, b + 1)
                for n, (kind, t) in enumerate(units):
                    s = slot(n)
                    before = n - SLOTS
                    if before >= 0:
                        taker_wait(pe, b, before)
                    elif before + pad < 0:
                        pe.wait_ge(dve_took, b * per["dve"] + (4 + before + pad + 1))
                    if kind in "QK":
                        col = (0 if kind == "Q" else D) + t * P
                        for lo, hi in cuts:
                            for k in range(KD):
                                mm = nc.tensor.matmul(s[:, lo:hi], w[:, k, col:col + P], xb[:, k, lo:hi],
                                                      start=(k == 0), stop=(k == KD - 1))
                    elif kind == "V":
                        start, rows = tiles[t]
                        for k in range(KD):
                            mm = nc.tensor.matmul(s[0:rows, 0:D], xb[:, k, start:start + rows], w[:, k, 2 * D:3 * D],
                                                  start=(k == 0), stop=(k == KD - 1))
                    elif kind == "S":
                        start, rows = tiles[t]
                        if t == 0:
                            pe.wait_ge(roped, b + 1)
                        for lo, hi in cuts:
                            for k in range(KD):
                                mm = nc.tensor.matmul(s[0:rows, lo:hi], rot[:, 0, k, start:start + rows],
                                                      rot[:, 1, k, lo:hi], start=(k == 0), stop=(k == KD - 1))
                    elif kind == "T":
                        start, rows = tiles[t]
                        pe.wait_ge(prob_done, b * NTL + (t + 1))
                        for j, (js, jr) in enumerate(tiles):
                            mm = nc.tensor.transpose(s[0:jr, j * P:(j + 1) * P], prob[:, t % 2, js:js + jr],
                                                     g.ident[:])
                    elif kind == "O":
                        if t == 0:
                            taker_wait(pe, b, units.index(("T", NTL - 1)))
                        for lo, hi in cuts:
                            for j, (js, jr) in enumerate(tiles):
                                mm = nc.tensor.matmul(s[:, lo:hi], v[0:jr, j, t * P:(t + 1) * P],
                                                      prob_t[0:jr, j, lo:hi], start=(j == 0), stop=(j == NTL - 1))
                    else:
                        if t == 0:
                            taker_wait(pe, b, units.index(("O", 1)))
                        for lo, hi in cuts:
                            for k in range(KD):
                                mm = nc.tensor.matmul(s[:, lo:hi], wp[:, k, t * P:(t + 1) * P], o_sb[:, k, lo:hi],
                                                      start=(k == 0), stop=(k == KD - 1))
                    mm.then_inc(filled, 1)

        @block.scalar
        def _(act):
            with nc.scalar.Fori(0, NB) as b:
                for n, (kind, t) in enumerate(units):
                    if takers[kind] != "act":
                        continue
                    s = slot(n)
                    act.wait_ge(filled, b * NU + (n + 1))
                    if kind in "QK":
                        c = 0 if kind == "Q" else 1
                        last = nc.scalar.activation(raw[:, c, t, :], s[:, 0:S], ACT.Identity,
                                                    bias=vec[:, 1 + c, t:t + 1])
                    elif kind == "S":
                        start, rows = tiles[t]
                        act.wait_ge(max_done, b * NTL + (t + 1))
                        last = nc.scalar.activation(prob[0:rows, t % 2, :], s[0:rows, 0:S], ACT.Exp,
                                                    bias=small[0:rows, t, 0:1], scale=scale,
                                                    accum_out=small[0:rows, t, 1:2])
                    else:
                        start, rows = tiles[t]
                        full = NTL - 1
                        nc.scalar.copy(prob_t[:, 0:full, start:start + rows],
                                       s[:, 0:full * P].rearrange("p (j n) -> p j n", j=full)[:, :, 0:rows])
                        jr = tiles[full][1]
                        last = nc.scalar.copy(prob_t[0:jr, full, start:start + rows], s[0:jr, full * P:full * P + rows])
                    last.then_inc(act_took, 1)

        @block.vector
        def _(dve):
            ve = nc.vector
            ve.memset(tmp[:, 0:1], 0.0).then_inc(xb_used, 1)
            ve.memset(tmp[:, 1:2], 0.0).then_inc(dve_took, 4)
            dve.wait_ge(dve_took, 4)
            dve.wait_ge(xb_used, 1)
            chain = Chain(dve, own)
            steps = 2 * 4 + 3 * NTL
            with nc.vector.Fori(0, NB) as b:
                chain.begin(b, steps)
                cos, sin = rope[:, 0, :], rope[:, 1, :]
                for c, name in enumerate("QK"):
                    taker_wait(dve, b, units.index((name, 1)))
                    a0, a1 = raw[:, c, 0, :], raw[:, c, 1, :]
                    r0, r1 = rot[:, c, 0, :], rot[:, c, 1, :]
                    ve.tensor_tensor(r0, a0, cos, ALU.mult)
                    ve.tensor_tensor(r1, a1, cos, ALU.mult)
                    chain.step(ve.tensor_tensor(tmp[:], a1, sin, ALU.mult))
                    chain.step(ve.tensor_tensor(r0, r0, tmp[:], ALU.subtract))
                    chain.step(ve.tensor_tensor(tmp[:], a0, sin, ALU.mult))
                    chain.step(ve.tensor_tensor(r1, r1, tmp[:], ALU.add))
                ve.tensor_copy(tmp[:, 0:1], rope[:, 0, 0:1]).then_inc(roped, 1)
                dve.wait_ge(roped, b + 1)
                for n, (kind, t) in enumerate(units):
                    s = slot(n)
                    if kind == "V":
                        rows = tiles[t][1]
                        dve.wait_ge(filled, b * NU + (n + 1))
                        ve.tensor_tensor(v[0:rows, t, :], s[0:rows, 0:D], bv[0:rows, :], ALU.add).then_inc(dve_took, 1)
                    if kind == "V" and t == NTL - 1:
                        ve.memset(small[:, 0, 2:3], 0.0).then_inc(xb_used, 1)
                        dve.wait_ge(xb_used, b + 2)
                    if kind == "S":
                        rows = tiles[t][1]
                        dve.wait_ge(filled, b * NU + (n + 1))
                        chain.step(ve.tensor_reduce(small[0:rows, t, 2:3], s[0:rows, 0:S], AX_X, ALU.max))
                        ve.tensor_scalar(small[0:rows, t, 0:1], small[0:rows, t, 2:3], -scale, None,
                                         ALU.mult).then_inc(max_done, 1)
                    if kind == "S" and t >= 1 or kind == "T" and t == NTL - 1:
                        p = t - 1 if kind == "S" else t
                        rows = tiles[p][1]
                        taker_wait(dve, b, units.index(("S", p)))
                        chain.step(ve.reciprocal(small[0:rows, p, 2:3], small[0:rows, p, 1:2]))
                        chain.step(ve.tensor_scalar(prob[0:rows, p % 2, :], prob[0:rows, p % 2, :],
                                                    small[0:rows, p, 2:3], None, ALU.mult))
                        ve.tensor_copy(tmp[:, 1:2], rope[:, 0, 0:1]).then_inc(prob_done, 1)
                        dve.wait_ge(prob_done, b * NTL + (p + 1))
                    if kind == "O":
                        dve.wait_ge(filled, b * NU + (n + 1))
                        ve.tensor_copy(o_sb[:, t, :], s[:, 0:S]).then_inc(dve_took, 1)
                    if kind == "Y":
                        at = bass.ds(b * S, S)
                        dve.wait_ge(filled, b * NU + (n + 1))
                        chain_y = ve.scalar_tensor_tensor(tmp[:], s[:, 0:S], vec[:, 3, t:t + 1], g.xn[:, t, at],
                                                          ALU.add, ALU.add)
                        chain_y.then_inc(dve_took, 1)
                        taker_wait(dve, b, n)
                        ve.tensor_tensor(g.h[:, t, at], g.h[:, t, at], tmp[:], ALU.add).then_inc(added, 1)
                        dve.wait_ge(added, b * KD + (t + 1))
                chain.end(NB)


def delta_net(g):
    nc, dram = g.nc, g.dram
    H, DH, J = 8, 32, 2
    HJ = H * J
    tiles = [(s, min(P, S - s)) for s in range(0, S, P)]
    NTL = len(tiles)
    off = [sum(S - s for s, _ in tiles[:n]) for n in range(NTL)]
    DEC = off[-1] + S - tiles[-1][0]
    VG = D + H

    def cuts(lo, hi):
        return [(max(lo, a), min(hi, b)) for a, b in ((0, 512), (512, S)) if max(lo, a) < min(hi, b)]

    units = [("q", 0), ("q", 1), ("k", 0), ("k", 1)] + [("v", t) for t in range(NTL)] \
        + [("beta", 0), ("mix", 0), ("diff", 0)] + [("a", (n, t)) for n in range(H) for t in range(NTL)] \
        + [("coef", n) for n in range(H)]
    takers = {"q": "dve", "k": "dve", "v": "dve", "beta": "act", "mix": "act", "diff": "act", "a": "act",
              "coef": "dve"}
    NU = len(units)
    assert NU % 2 == 0
    dve_n, act_n, seen_d, seen_a = [], [], 0, 0
    for kind, _ in units:
        seen_d += takers[kind] == "dve"
        seen_a += takers[kind] == "act"
        dve_n.append(seen_d)
        act_n.append(seen_a)
    ND, NA = seen_d, seen_a
    first_a = units.index(("a", (0, 0)))
    first_c = units.index(("coef", 0))
    NB_USES = HJ + 3

    with ExitStack() as ctx:
        sc = Scope(nc, ctx, "dn")
        w_qk = sc.sb("w_qk", [P, KD, 2 * D])
        w_vg = sc.sb("w_vg", [P, KD, VG])
        w_bm = sc.sb("w_bm", [P, KD, 2 * HJ])
        w_o = sc.sb("w_o", [P, H, D])
        b_gate = sc.sb("b_gate", [P, H])
        vec16 = sc.sb("vec16", [HJ, 3])
        vec = sc.sb("vec", [P, 3, KD])
        diff = sc.sb("diff", [HJ, P])
        pick_den = sc.sb("pick_den", [P, H, HJ])
        eye = sc.sb("eye", [P, S])
        hres = sc.sb("hres", [P, KD, NT])
        loads = [(w_qk, "dn_wqk"), (w_vg, "dn_wvg"), (w_bm, "dn_wbm"), (w_o, "dn_wo"), (vec16, "dn_vec16"),
                 (vec, "dn_vec"), (diff, "c_diff"), (pick_den, "c_pick_den"),
                 (eye, "c_eye")]
        layer_norm(g, "dnn", g.h, g.xn, loads=[(a[:], dram[n]) for a, n in loads]
                   + [(b_gate[:], dram["L0_attn_bgate"].to_broadcast([P, H]))])

        def core(ctx):
            sc = Scope(nc, ctx, "dc")
            xb = sc.sb("xb", [P, KD, S])
            qz = sc.sb("qz", [P, H, NTL * P])
            kk = sc.sb("kk", [P, KD, NTL * P])
            hl = sc.sb("hl", [P, S + 1], F32R)
            pick = sc.sb("pick", [P, HJ, P], F32R)
            spread = sc.sb("spread", [P, H, P], F32R)
            ex = sc.sb("ex", [P, 4, S])
            gl = sc.sb("gl", [P, NTL, H])
            vr = sc.sb("vr", [P, NTL, D])
            vg = sc.sb("vg", [P, NTL, H, 2 * DH])
            beta = sc.sb("beta", [HJ, S])
            mix = sc.sb("mix", [HJ, S])
            den = sc.sb("den", [HJ, S])
            decay = sc.sb("decay", [P, 2, J, DEC])
            a_sb = sc.sb("a_sb", [P, 2, S])
            wt = sc.sb("wt", [P, 3, J, S])
            o_sb = sc.sb("o_sb", [P, H, S])
            ps_a = sc.ps("ps_a", [P, 2, 1024])
            ps_b = sc.ps("ps_b", [P, 1024])
            ps_o = sc.ps("ps_o", [P, 1024])
            xb_ready = sc.sem("xb_ready")
            filled = sc.sem("filled")
            dve_took = sc.sem("dve_took")
            act_took = sc.sem("act_took")
            low_ready = sc.sem("low_ready")
            exp_done = sc.sem("exp_done")
            gate_in = sc.sem("gate_in")
            gate_done = sc.sem("gate_done")
            v_done = sc.sem("v_done")
            beta_done = sc.sem("beta_done")
            b_filled = sc.sem("b_filled")
            b_took = sc.sem("b_took")
            w0_done = sc.sem("w0_done")
            w1_done = sc.sem("w1_done")
            o_ready = sc.sem("o_ready")
            o_took = sc.sem("o_took")
            den_done = sc.sem("den_done")
            own = sc.sem("own")
            zeroed = sc.sem("zeroed")
            landed_r = sc.sem("landed_r")
            block = ctx.enter_context(nc.Block())
            UA = H * NTL

            def slot(n):
                return ps_a[:, n % 2]

            even = ((0, 512), (512, S + 1))

            @block.gpsimd
            def _(pool):
                nc.gpsimd.dma_start(pick[:], dram["c_pick"]).then_inc(landed_r, 16)
                nc.gpsimd.dma_start(spread[:], dram["c_spread"]).then_inc(landed_r, 16)
                pool.wait_ge(zeroed, 1)
                nc.gpsimd.memset(a_sb[:, 0, 0:1], 0.0).then_inc(w1_done, 2)
                with nc.gpsimd.Fori(0, NB) as b:
                    pool.wait_ge(beta_done, b + 1)
                    nc.gpsimd.tensor_copy(xb[:], g.xn[:, :, bass.ds(b * S, S)]).then_inc(xb_ready, 1)
                    for h in range(H):
                        for t, (start, rows) in enumerate(tiles):
                            m, u = S - start, h * NTL + t
                            pool.wait_ge(act_took, b * NA + act_n[first_a + u])
                            pool.wait_ge(b_took, b * NB_USES + (h * J + 3))
                            nc.gpsimd.tensor_tensor(wt[0:rows, u % 3, 1, 0:m], a_sb[0:rows, u % 2, 0:m],
                                                    decay[0:rows, h % 2, 1, off[t]:off[t] + m], ALU.mult).then_inc(w1_done, 1)

            @block.tensor
            def _(pe):
                def dve_has(n, b):
                    pe.wait_ge(dve_took, b * ND + (dve_n[n] + 2))

                def fill(n, b):
                    kind, arg = units[n]
                    s = slot(n)
                    if n >= 2:
                        if takers[units[n - 2][0]] == "dve":
                            dve_has(n - 2, b)
                        else:
                            pe.wait_ge(act_took, b * NA + act_n[n - 2])
                    else:
                        pe.wait_ge(dve_took, b * ND + (n + 1))
                    if kind in "qk":
                        col = (0 if kind == "q" else D) + arg * P
                        for lo, hi in cuts(0, S):
                            for k in range(KD):
                                mm = nc.tensor.matmul(s[:, lo:hi], w_qk[:, k, col:col + P], xb[:, k, lo:hi],
                                                      start=(k == 0), stop=(k == KD - 1))
                    elif kind == "v":
                        start, rows = tiles[arg]
                        for k in range(KD):
                            mm = nc.tensor.matmul(s[0:rows, 0:VG], xb[:, k, start:start + rows], w_vg[:, k, :],
                                                  start=(k == 0), stop=(k == KD - 1))
                    elif kind in ("beta", "mix"):
                        col = 0 if kind == "beta" else HJ
                        for lo, hi in cuts(0, S):
                            for k in range(KD):
                                mm = nc.tensor.matmul(s[0:HJ, lo:hi], w_bm[:, k, col:col + HJ], xb[:, k, lo:hi],
                                                      start=(k == 0), stop=(k == KD - 1))
                    elif kind == "diff":
                        pe.wait_ge(act_took, b * NA + act_n[n - 1])
                        for lo, hi in cuts(0, S):
                            mm = nc.tensor.matmul(s[:, lo:hi], diff[:], mix[:, lo:hi], start=True, stop=True)
                    elif kind == "a":
                        h, t = arg
                        start, rows = tiles[t]
                        for lo, hi in cuts(0, S - start):
                            mm = nc.tensor.matmul(s[:, lo:hi], kk[:, h // 4, start:start + P],
                                                  qz[:, h, start + lo:start + hi], start=True, stop=True)
                    else:
                        for lo, hi in even:
                            mm = nc.tensor.matmul(s[:, lo:hi], spread[:, arg, :], hl[:, lo:hi], start=True, stop=True)
                    mm.then_inc(filled, 1)

                def betas(hj, b):
                    pe.wait_ge(b_took, b * NB_USES + (hj + 1))
                    for lo, hi in even:
                        mm = nc.tensor.matmul(ps_b[:, lo:hi], pick[:, hj, :], hl[:, lo:hi], start=True, stop=True)
                    mm.then_inc(b_filled, 1)

                def with_v(h, t, b):
                    start = tiles[t][0]
                    u = h * NTL + t
                    pe.wait_ge(w0_done, b * UA + (u + 3))
                    pe.wait_ge(w1_done, b * UA + (u + 3))
                    for j in range(J):
                        for lo, hi in cuts(start, S):
                            mm = nc.tensor.matmul(ps_o[j * 2 * DH:(j + 1) * 2 * DH, lo:hi], vg[:, t, h, :],
                                                  wt[:, u % 3, j, lo - start:hi - start], start=(t == 0),
                                                  stop=(t == NTL - 1), skip_group_check=True)
                    if t == NTL - 1:
                        mm.then_inc(o_ready, 1)

                pe.wait_ge(landed_r, 32)
                pe.wait_ge(zeroed, 1)
                with nc.tensor.Fori(0, NB) as b:
                    pe.wait_ge(xb_ready, b + 1)
                    for n in range(first_a):
                        fill(n, b)
                    pe.wait_ge(beta_done, b + 2)
                    betas(0, b)
                    betas(1, b)
                    pe.wait_ge(v_done, b + 1)
                    fill(first_a, b)
                    fill(first_a + 1, b)
                    for u in range(UA):
                        h, t = u // NTL, u % NTL
                        if u + 2 < UA:
                            fill(first_a + u + 2, b)
                        if t % 2 == 0 and t // 2 < J and h + 1 < H:
                            betas((h + 1) * J + t // 2, b)
                        if t == 0:
                            pe.wait_ge(o_took, b * H + (h + 1))
                        with_v(h, t, b)
                    pe.wait_ge(o_took, b * H + (H + 1))
                    pe.wait_ge(b_took, b * NB_USES + (HJ + 1))
                    for lo, hi in cuts(0, S):
                        for h in range(H):
                            mm = nc.tensor.matmul(ps_b[0:HJ, lo:hi], pick_den[:, h, :], o_sb[:, h, lo:hi],
                                                  start=(h == 0), stop=(h == H - 1))
                    mm.then_inc(b_filled, 1)
                    pe.wait_ge(den_done, b + 1)
                    for h in range(H):
                        fill(first_c + h, b)
                    dve_has(NU - 1, b)
                    for m in range(KD):
                        pe.wait_ge(b_took, b * NB_USES + (HJ + 2 + m))
                        for lo, hi in cuts(0, S):
                            for h in range(H):
                                mm = nc.tensor.matmul(ps_b[:, lo:hi], w_o[:, h, m * P:(m + 1) * P], o_sb[:, h, lo:hi],
                                                      start=(h == 0), stop=(h == H - 1))
                        mm.then_inc(b_filled, 1)

            @block.scalar
            def _(act):
                with nc.scalar.Fori(0, NB) as b:
                    for n in range(4):
                        act.wait_ge(low_ready, b * 4 + (n + 1))
                        nc.scalar.activation(ex[:, n, :], ex[:, n, :], ACT.Exp).then_inc(exp_done, 1)
                    act.wait_ge(gate_in, b + 1)
                    nc.scalar.activation(gl[:], gl[:], ACT.Sigmoid).then_inc(gate_done, 1)
                    for n, (kind, arg) in enumerate(units):
                        if takers[kind] != "act":
                            continue
                        s = slot(n)
                        act.wait_ge(filled, b * NU + (n + 1))
                        if kind == "beta":
                            last = nc.scalar.activation(beta[:], s[0:HJ, 0:S], ACT.Sigmoid, bias=vec16[:, 0:1])
                        elif kind == "mix":
                            last = nc.scalar.activation(mix[:], s[0:HJ, 0:S], ACT.Identity, bias=vec16[:, 1:2])
                        elif kind == "diff":
                            last = nc.scalar.activation(mix[:], s[0:HJ, 0:S], ACT.Sigmoid)
                        else:
                            h, t = arg
                            start, rows = tiles[t]
                            u = h * NTL + t
                            act.wait_ge(w0_done, b * UA + (u + 1))
                            act.wait_ge(w1_done, b * UA + (u + 1))
                            last = nc.scalar.copy(a_sb[0:rows, u % 2, 0:S - start], s[0:rows, 0:S - start])
                        last.then_inc(act_took, 1)
                        if kind == "a" and arg[1] == NTL - 1:
                            h = arg[0]
                            act.wait_ge(o_ready, b * H + (h + 1))
                            nc.scalar.copy(o_sb[:, h, :], ps_o[:, 0:S]).then_inc(o_took, 1)

            @block.vector
            def _(dve):
                ve = nc.vector
                chain = Chain(dve, own)
                ve.memset(vg[:], 0.0).then_inc(beta_done, 1)
                ve.memset(kk[:], 0.0)
                ve.memset(hl[:].bitcast(F32), 0.0)
                ve.memset(qz[:], 0.0).then_inc(dve_took, 2)
                ve.memset(wt[:], 0.0).then_inc(b_took, 1)
                ve.memset(beta[:, 0:1], 0.0).then_inc(o_took, 1)
                ve.memset(mix[:, 0:1], 0.0).then_inc(w0_done, 2)
                ve.memset(gl[:], 0.0).then_inc(zeroed, 1)
                dve.wait_ge(zeroed, 1)

                def scan(hj, b, first=0, end=NTL):
                    h, j = hj // 2, hj % 2
                    dve.wait_ge(b_filled, b * NB_USES + (hj + 1))
                    for t, (start, rows) in list(enumerate(tiles))[first:end]:
                        m = S - start
                        last = ve.tensor_tensor_scan(decay[0:rows, h % 2, j, off[t]:off[t] + m], ps_b[0:rows, start:S],
                                                     eye[0:rows, 0:m], 0.0, ALU.mult, ALU.add)
                    if end == NTL:
                        last.then_inc(b_took, 1)

                def halves(t, done):
                    chain.step(ve.tensor_copy(hl[0:HJ, 0:S], t[:]))
                    ve.tensor_tensor(hl[DH:DH + HJ, 0:S], t[:], hl[0:HJ, 0:S].bitcast(F32), ALU.subtract).then_inc(done, 1)

                with nc.vector.Fori(0, NB) as b:
                    chain.begin(b, 5)
                    for n in range(4):
                        dve.wait_ge(filled, b * NU + (n + 1))
                        ve.tensor_scalar(ex[:, n, :], slot(n)[:, 0:S], 0.0, None, ALU.min).then_inc(low_ready, 1)
                        if n % 2 == 1:
                            for m in (n - 1, n):
                                dve.wait_ge(exp_done, b * 4 + (m + 1))
                                rows_of = [slice(0, P)] if m >= KD else [slice(i * DH, (i + 1) * DH) for i in range(4)]
                                for i, r in enumerate(rows_of):
                                    o = kk[:, m - KD, 0:S] if m >= KD else qz[r, m * 4 + i, 0:S]
                                    last = ve.scalar_tensor_tensor(o, slot(m)[r, 0:S], 0.0, ex[r, m, :], ALU.max, ALU.add)
                                last.then_inc(dve_took, 1)
                    for t, (start, rows) in enumerate(tiles):
                        s = slot(4 + t)
                        dve.wait_ge(filled, b * NU + (4 + t + 1))
                        ve.tensor_tensor(gl[0:rows, t, :], s[0:rows, D:VG], b_gate[0:rows, :], ALU.add)
                        ve.tensor_copy(vr[0:rows, t, :], s[0:rows, 0:D]).then_inc(dve_took, 1)
                    ve.tensor_copy(ex[:, 0, 0:1], eye[:, 0:1]).then_inc(gate_in, 1)
                    dve.wait_ge(act_took, b * NA + act_n[units.index(("mix", 0))])
                    chain.step(ve.tensor_scalar(beta[:], beta[:], vec16[:, 2:3], 0.9999, ALU.mult, ALU.min))
                    halves(beta, beta_done)
                    dve.wait_ge(gate_done, b + 1)
                    dve.wait_ge(dve_took, b * ND + (9 + 2))
                    full = NTL - 1
                    for lo, hi, rows in ((0, full, P), (full, NTL, tiles[full][1])):
                        gb = gl[0:rows, lo:hi, :].rearrange("p t (h a) -> p (t h) a", a=1).to_broadcast(
                            [rows, (hi - lo) * H, DH])
                        o = vg[0:rows, lo:hi].rearrange("p t h d -> p (t h) d")
                        ve.tensor_tensor(o[:, :, 0:DH], vr[0:rows, lo:hi, :].rearrange("p t (h d) -> p (t h) d", d=DH),
                                         gb, ALU.mult)
                        last = ve.tensor_copy(o[:, :, DH:2 * DH], gb)
                    last.then_inc(v_done, 1)
                    scan(0, b)
                    scan(1, b)
                    for h in range(H):
                        dve.wait_ge(b_took, b * NB_USES + (h * J + 3))
                        for t, (start, rows) in enumerate(tiles):
                            m, u = S - start, h * NTL + t
                            dve.wait_ge(act_took, b * NA + act_n[first_a + u])
                            ve.tensor_tensor(wt[0:rows, u % 3, 0, 0:m], a_sb[0:rows, u % 2, 0:m],
                                             decay[0:rows, h % 2, 0, off[t]:off[t] + m], ALU.mult).then_inc(w0_done, 1)
                            if h + 1 < H and t < 4:
                                if t == 0 and h >= 1:
                                    dve.wait_ge(w0_done, b * UA + (h * NTL + 2))
                                    dve.wait_ge(w1_done, b * UA + (h * NTL + 2))
                                scan((h + 1) * J + t // 2, b, *((0, 1) if t % 2 == 0 else (1, NTL)))
                    dve.wait_ge(b_filled, b * NB_USES + (HJ + 1))
                    ve.tensor_scalar(den[:], ps_b[0:HJ, 0:S], 1.0e-6, None, ALU.add).then_inc(b_took, 1)
                    dve.wait_ge(b_took, b * NB_USES + (HJ + 2))
                    chain.step(ve.reciprocal(den[:], den[:]))
                    chain.step(ve.tensor_tensor(den[:], den[:], mix[:], ALU.mult))
                    halves(den, den_done)
                    for h in range(H):
                        dve.wait_ge(filled, b * NU + (first_c + h + 1))
                        ve.tensor_tensor(o_sb[:, h, :], o_sb[:, h, :], slot(first_c + h)[:, 0:S],
                                         ALU.mult).then_inc(dve_took, 1)
                    for m in range(KD):
                        dve.wait_ge(b_filled, b * NB_USES + (HJ + 2 + m))
                        at = bass.ds(b * S, S)
                        ve.scalar_tensor_tensor(hres[:, m, at], ps_b[:, 0:S], vec[:, 0, m:m + 1], g.xn[:, m, at],
                                                ALU.add, ALU.add).then_inc(b_took, 1)

        with ExitStack() as mid:
            core(mid)
        layer_norm(g, "dno", hres, hres, vec[:, 1, :], vec[:, 2, :], add_to=g.h)


def program(nc, dram, out):
    dram["s_gate"] = nc.dram_tensor("s_gate", (NE + 1, N_SEL), F32).ap()
    dram["s_rows"] = nc.dram_tensor("s_rows", (NT, D), F32).ap()
    dram["s_extra"] = nc.dram_tensor("s_extra", (NT + N_SEL, D), F32).ap()
    dram["s_y"] = nc.dram_tensor("s_y", (BLOCKS * CN, D), F32).ap()
    with ExitStack() as ctx:
        Scope.in_use.clear()
        g = Shared(nc, ctx, dram)
        load_constants(g)
        text_block(g)
        clear_semaphores(nc)
        delta_net(g)
        clear_semaphores(nc)
        selected_ffn(g)
        clear_semaphores(nc)
        gated_scan(g)
        clear_semaphores(nc)
        shared = ("L1_ffn_Wg_s", "L1_ffn_Wu_s", "L1_ffn_Wd_s")
        mixture(g, "m1", "m1_w", 192, "L1", "L1_ffn_W_gate_router", None,
                lambda tag, routes: add_choices(g, tag, routes, shared, 192))
        clear_semaphores(nc)
        query_attention(g)
        clear_semaphores(nc)
        three_matrices(g)
        clear_semaphores(nc)
        full_attention(g)
        clear_semaphores(nc)
        mixture(g, "m3", "m3_w", 688, "L3", "L3_ffn_Ws", "L3_ffn_bs",
                lambda tag, routes: store_sum(g, tag, routes, out))
        clear_semaphores(nc)



def _blocks(w):
    n = w.shape[-1]
    k = w.shape[-2] // P
    lead = w.shape[:-2]
    return w.reshape(*lead, k, P, n).swapaxes(-3, -2)


def _swap(np, stripe):
    half = stripe // 2
    to = np.arange(P)
    m = np.zeros((P, P), np.float32)
    m[to // stripe * stripe + half + to % half, to] = 1.0
    return m


def _stack_selection(np, dh):
    heads = P // dh
    m = np.zeros((P, 4, heads, P), np.float32)
    d = np.arange(dh)
    for h in range(heads):
        for part, places in enumerate(((0, 2), (1,), (0, 1), (2,))):
            for place in places:
                m[h * dh + d, part, h, place * dh + d] = 1.0
    return m


def _stripes(np, w, heads, dh):
    w = w.reshape(-1, heads, dh)
    return np.concatenate([w, np.zeros_like(w)], axis=2).reshape(w.shape[0], -1)


def _delta_constants(np):
    r = np.arange(16)
    diff = np.zeros((16, P), np.float32)
    diff[r, r], diff[r ^ 1, r] = 1.0, -1.0
    pick = np.zeros((P, 16, P), np.float32)
    pick[r, r], pick[32 + r, r] = 1.0, 1.0
    pick_den = np.zeros((P, 8, 16), np.float32)
    spread = np.zeros((P, 8, P), np.float32)
    for h in range(8):
        for j in range(2):
            pick_den[64 * j + 32, h, 2 * h + j] = 1.0
            for part in (0, 32):
                spread[part + 2 * h + j, h, 64 * j:64 * j + 32] = 1.0
    return {"c_diff": diff, "c_pick": pick, "c_pick_den": pick_den, "c_spread": spread}


def _decay_cap(np):
    slopes = np.array([0.5 ** (n + 1) for n in range(8)], dtype=np.float32)
    return np.repeat(np.exp(-slopes), 2)[:, None]


def _expert_rows(np, wg, wu, wd):
    e, f, _ = wd.shape
    n, starts, widths = hidden_tiles(f)
    down = np.zeros((e, P, n, D), wd.dtype)
    for i in range(n):
        down[:, :widths[i], i] = wd[:, starts[i]:starts[i] + widths[i]]
    parts = [_blocks(wg), _blocks(wu), down]
    return np.concatenate([p.reshape(e * P, -1) for p in parts], axis=1)


def _constants(np):
    at = np.arange(S_TXT, dtype=np.float32)[:, None]
    even = np.arange(0, D, 2, dtype=np.float32)[None]
    angle = at / np.power(np.float32(10000.0), np.float32(2.0) * even / np.float32(D))
    pos = np.zeros((S_TXT, D), np.float32)
    pos[:, 0::2], pos[:, 1::2] = np.sin(angle), np.cos(angle)
    freq = np.float32(1.0) / np.float32(10000.0) ** (np.arange(P, dtype=np.float32) / np.float32(P))
    turn = np.arange(S, dtype=np.float32)[:, None] * freq[None]
    rope = np.stack([np.round(np.cos(turn)), np.round(np.sin(turn))]).transpose(2, 0, 1)
    tok = np.arange(NT, dtype=np.float32).reshape(RT, RN).T
    return {
        "c_ident": np.eye(P, dtype=np.float32),
        "c_rank": np.broadcast_to(np.arange(NE, 0, -1, dtype=np.float32), (P, NE)),
        "c_tok": tok,
        "c_spare": NT + np.arange(N_SEL, dtype=np.float32).reshape(SEL_T, P).T,
        "c_keep": np.broadcast_to(np.arange(RT) > 0, (P, NE, RT)).astype(np.float32),
        "c_lower": np.triu(np.ones((P, P), np.float32), 1),
        "c_steps": np.broadcast_to(np.arange(BLOCKS, dtype=np.float32), (P, BLOCKS)),
        "c_tile_at": np.broadcast_to(np.arange(SLOT_TILES + 1, dtype=np.float32) * RN, (P, SLOT_TILES + 1)),
        "c_lanes": np.broadcast_to(np.arange(RN, dtype=np.float32), (P, RN)),
        "c_lane": np.arange(P, dtype=np.float32)[:, None] - P,
        "c_pos_txt": pos.reshape(S_TXT // P, P, D).swapaxes(0, 1),
        "c_rope": rope,
        "c_eye": np.eye(P, S, dtype=np.float32),
        **_delta_constants(np),
        "c_ones_row": (np.arange(P)[:, None] // 2 == 48).astype(np.float32),
        "c_sel16": _stack_selection(np, 16),
        "c_sel32": _stack_selection(np, 32),
        "c_mask_q": np.triu(np.full((P, P), -BIG, np.float32), 1),
        "c_mask_k": np.tril(np.full((P, P), -BIG, np.float32), -1),
        "c_swap32": _swap(np, 32),
        "c_swap64": _swap(np, 64),
    }


def _layouts(np, x):
    a = {}
    row = lambda n: x[n].reshape(1, -1)
    col = lambda n: x[n].reshape(-1, P).T
    a["L3_ffn_Ws"] = _blocks(x["L3_ffn_Ws"])
    a["L3_ffn_bs"] = row("L3_ffn_bs")
    for n in ("L1", "L3"):
        a[f"m{n[1]}_w"] = _expert_rows(np, *(x[f"{n}_ffn_W{m}"] for m in "gud"))
    for n in ("L1_ffn_Wg_s", "L1_ffn_Wu_s"):
        a[n] = _blocks(x[n])
    a["L1_ffn_Wd_s"] = x["L1_ffn_Wd_s"]
    a["L1_ffn_W_gate_router"] = _blocks(x["L1_ffn_W_gate_router"])
    a["L1_ffn_expert_bias"] = row("L1_ffn_expert_bias")
    cat = lambda e, s: np.concatenate([x["L0_ffn_" + e], x["L0_ffn_" + s][None]])
    a["f0_w1"] = _blocks(cat("ew1", "sw1").swapaxes(1, 2))
    a["f0_w2"] = _blocks(cat("ew2", "sw2").swapaxes(1, 2))
    a["f0_w3"] = cat("ew3", "sw3").swapaxes(1, 2)
    each = lambda n: np.broadcast_to(x["L0_ffn_" + n], (NE, P))
    b3 = cat("eb3", "sb3").reshape(NE + 1, KD, P)
    a["f0_vec"] = np.stack([
        cat("eb1", "sb1"), cat("eb2", "sb2"),
        np.concatenate([each("sel_ln_g"), x["L0_ffn_s_ln_g"][None]]),
        np.concatenate([each("sel_ln_b"), x["L0_ffn_s_ln_b"][None]]), b3[:, 0], b3[:, 1]], axis=-1)
    a["f0_router_w"] = _blocks(np.concatenate([x["L0_ffn_eg_w"], x["L0_ffn_sg_w"]]).T)
    a["f0_router_b"] = np.concatenate([x["L0_ffn_eg_b"], x["L0_ffn_sg_b"]])[None]
    a["L0_ffn_exp_bias"] = row("L0_ffn_exp_bias")
    a["f0_index"] = np.stack([x["L0_ffn_index_" + n].reshape(SEL_T, P).T for n in "bt"], axis=1)
    for n in ("L1_attn_W_in", "L1_attn_Wa", "L1_attn_Wb", "L1_attn_Wc", "L1_attn_Wo",
              "L2_ffn_weight", "L2_ffn_aux_weight1", "L2_ffn_aux_weight2"):
        a[n] = _blocks(x[n])
    a["s1_vec"] = np.concatenate([col("L1_attn_" + n) for n in ("b_in", "conv_b", "ba", "bb", "bc")], axis=1)
    for n in ("L1_attn_bo", "L1_attn_gamma", "L1_attn_beta", "L2_ffn_bias"):
        a[n] = col(n)
    a["L1_attn_conv_w"] = x["L1_attn_conv_w"].reshape(-1, P, 3).swapaxes(0, 1)
    wq = x["L2_attn_Wq"].swapaxes(0, 1).reshape(D, D)
    a["q2_wq"] = _blocks(wq)
    a["q2_wk"] = _blocks(np.pad(x["L2_attn_Wk"], ((0, 0), (0, P - 32))))
    a["q2_wv"] = _blocks(_stripes(np, x["L2_attn_Wv"], 1, 32))
    a["q2_wo"] = _stripes(np, x["L2_attn_Wp"].T, 8, 32).T.reshape(-1, P, D).swapaxes(0, 1)
    a["q2_bq"] = np.zeros((P, 2), np.float32)
    a["q2_bk"] = np.zeros((P, 1), np.float32)
    a["q2_bv"] = np.repeat(np.array([[0.0, 1.0]], np.float32), 32, axis=1)
    a["L2_attn_bp"] = col("L2_attn_bp")
    p = x["x"].reshape(NB, 3, 6, 16, 6, 16).transpose(1, 3, 5, 0, 2, 4).reshape(3 * 256, -1)
    a["patches"] = _blocks(p)
    a["L0_tok_W"] = _blocks(x["L0_tok_W"].T)
    a["tok_vec"] = np.stack([col("L0_tok_b"), col("L0_tok_cls_token")], axis=1)
    a["L0_tok_pos_embedding"] = x["L0_tok_pos_embedding"][0].T.reshape(KD, P, S_IMG).swapaxes(0, 1)
    a["x_txt"] = x["x_txt"].reshape(-1, P).T
    a["L0_txt_emb"] = x["L0_txt_emb"]
    w, b = x["L0_txt_in_proj_w"].T, x["L0_txt_in_proj_b"][None]
    part = lambda t, n: t[:, n * D:(n + 1) * D]
    a["ta_wq"], a["ta_wk"] = _blocks(part(w, 0)), _blocks(part(w, 1))
    a["ta_wv"] = _blocks(_stripes(np, part(w, 2), 16, 16))
    a["ta_bq"], a["ta_bk"] = (part(b, n).reshape(-1, P).T for n in range(2))
    a["ta_bv"] = np.where(np.arange(512)[None] % 32 >= 16, np.float32(1.0), _stripes(np, part(b, 2), 16, 16))
    a["ta_wo"] = _stripes(np, x["L0_txt_out_proj_w"], 16, 16).T.reshape(-1, P, D).swapaxes(0, 1)
    a["L0_txt_out_proj_b"] = col("L0_txt_out_proj_b")
    a["L0_txt_w1"] = _blocks(x["L0_txt_w1"].T)
    a["L0_txt_w2"] = _blocks(x["L0_txt_w2"].T)
    a["L0_txt_b1"] = col("L0_txt_b1")
    a["txt_vec"] = np.stack([col("L0_txt_" + n) for n in ("b2", "g1", "beta1", "g2", "beta2")], axis=1)
    t = lambda n: x["L0_attn_" + n].T
    a["dn_wqk"] = _blocks(np.concatenate([t("Wq"), t("Wk")], axis=1))
    a["dn_wvg"] = _blocks(np.concatenate([t("Wv"), t("Wgate")], axis=1))
    a["dn_wbm"] = _blocks(np.concatenate([t("Wbeta"), t("Wmix")], axis=1))
    wo = t("Wout").reshape(8, 32, D)
    z = np.zeros_like(wo)
    a["dn_wo"] = np.concatenate([wo, z, wo, z], axis=1).swapaxes(0, 1)
    a["dn_vec16"] = np.concatenate([x["L0_attn_bbeta"][:, None], x["L0_attn_bmix"][:, None], _decay_cap(np)], axis=1)
    a["dn_vec"] = np.stack([col("L0_attn_" + n) for n in ("bout", "ln_g", "ln_b")], axis=1)
    a["L0_attn_bgate"] = row("L0_attn_bgate")
    a["L3_attn_w_qkv"] = _blocks(x["L3_attn_w_qkv"])
    a["L3_attn_w_proj"] = _blocks(x["L3_attn_w_proj"])
    qkv_b = x["L3_attn_b_qkv"].reshape(3, KD, P)
    a["a3_vec"] = np.stack([col("L3_attn_g_norm"), qkv_b[0].T, qkv_b[1].T, col("L3_attn_b_proj")], axis=1)
    a["a3_bv"] = x["L3_attn_b_qkv"][None, 2 * D:]
    return a


def kernel(**inputs):
    import numpy as np
    import concourse.bacc as bacc
    from concourse.bass_utils import run_bass_kernel_spmd

    nc = bacc.Bacc("TRN2", target_bir_lowering=False, num_devices=1)
    laid = {**_layouts(np, inputs), **_constants(np)}
    arrays, dram = {}, {}
    for name, value in laid.items():
        value = np.ascontiguousarray(value)
        arrays[f"in_{name}"] = value
        dram[name] = nc.dram_tensor(f"in_{name}", value.shape, mybir.dt.from_np(value.dtype),
                                    kind="ExternalInput").ap()
    out = nc.dram_tensor("out_0", (NT, D), F32, kind="ExternalOutput").ap()
    program(nc, dram, out)
    result = run_bass_kernel_spmd(nc, [arrays], core_ids=[0]).results[0]["out_0"]
    return result.reshape(NB, S, D)
```
